# Optimizing a Trainium2 kernel written in Bass

```python
import numpy as np
import jax
import jax.numpy as jnp

def _softmax(x, axis=-1):
    return jax.nn.softmax(x, axis=axis)

def _gelu(x):
    return jax.nn.gelu(x, approximate=True)

def _silu(x):
    return jax.nn.silu(x)

def _sigmoid(x):
    return jax.nn.sigmoid(x)

def _layernorm(x, axis=-1, eps=1e-05):
    m = jnp.mean(x, axis=axis, keepdims=True)
    v = jnp.var(x, axis=axis, keepdims=True)
    return (x - m) / jnp.sqrt(v + eps)

def _scatter_add(tgt, idx, src, axis=0):
    return tgt.at[idx].add(src)

def _segment_sum(src, seg, n):
    return jax.ops.segment_sum(src, seg, n)
kernel_name = 'mk_perceiver_d4_seqx_r4_5959c8'

def setup_inputs(seed: int=0):
    np.random.seed(seed)
    _w = jnp.asarray

    def _rec_inputs():
        import jax
        import jax.numpy as jnp
        _rk = jax.random.key(seed)
        x = -0.0002928 + 1 * jax.random.normal(jax.random.fold_in(_rk, 1), (16, 64, 256), jnp.float32)
        _lenS = 64 - jax.random.randint(jax.random.fold_in(_rk, 7), (16,), 0, max(1, 64 // 4) + 1, jnp.int32)
        _lenS2 = 1601 - jax.random.randint(jax.random.fold_in(_rk, 8), (16,), 0, max(1, 1601 // 4) + 1, jnp.int32)
        _ctx_1024P = jax.random.normal(jax.random.fold_in(_rk, 11), (16, 16, 256), jnp.float32)
        _ctx_1024c = jax.random.dirichlet(jax.random.fold_in(_rk, 511), 0.3 * jnp.ones((16,), jnp.float32), (16, 1601))
        _ctx_1024t = jnp.einsum('bsk,bkd->bsd', _ctx_1024c, _ctx_1024P)
        _ctx_1024t = _ctx_1024t * jax.lax.rsqrt(jnp.mean(jnp.square(_ctx_1024t)) + 1e-12) * 0.953939
        ctx_1024 = -1.39393e-06 + 0.999914 * (_ctx_1024t + 0.3 * jax.random.normal(jax.random.fold_in(_rk, 611), (16, 1601, 256), jnp.float32))
        _validS = jnp.arange(64)[None, :] < _lenS[:, None]
        _validS2 = jnp.arange(1601)[None, :] < _lenS2[:, None]
        _causal = jnp.tril(jnp.ones((64, 64), dtype=bool))
        mask_BxSxS2_bk0 = jnp.logical_not(jnp.broadcast_to(_validS2[:, None, :], (16, 64, 1601)))
        return (x, ctx_1024, mask_BxSxS2_bk0)
    x, ctx_1024, mask_BxSxS2_bk0 = _rec_inputs()

    def _L0_xattn_setup():
        import jax, jax.numpy as jnp
        import numpy as np
        HEAD_NUM = 16
        PAD = 0.0
        MASKS_FUTURE = True

        def _split_head(x):
            B, S, D = x.shape
            return x.reshape(B, S, HEAD_NUM, D // HEAD_NUM).transpose(0, 2, 1, 3)
        key = jax.random.key(seed)
        ks = jax.random.split(key, 7)
        B, S, D = (2, 512, 256)
        scale = 0.02
        return {'q': jax.random.normal(ks[0], (B, S, D), dtype=jnp.float32), 'k': jax.random.normal(ks[1], (B, S, D), dtype=jnp.float32), 'v': jax.random.normal(ks[2], (B, S, D), dtype=jnp.float32), 'w_q': jax.random.normal(ks[3], (D, D), dtype=jnp.float32) * scale, 'w_k': jax.random.normal(ks[4], (D, D), dtype=jnp.float32) * scale, 'w_v': jax.random.normal(ks[5], (D, D), dtype=jnp.float32) * scale, 'w_o': jax.random.normal(ks[6], (D, D), dtype=jnp.float32) * scale}
    _L0_xattn_all = _L0_xattn_setup()
    _L0_xattn_in = {k: v for k, v in _L0_xattn_all.items() if k in ('w_q', 'w_k', 'w_v', 'w_o')}
    del _L0_xattn_all

    def _L0_attn_setup():
        import math
        import jax, jax.numpy as jnp
        import numpy as np
        B, T, D, H, L = (8, 512, 256, 16, 4)
        DK = D // H
        EPS_LN = 1e-05
        EPS_ATTN = 1e-06

        def _layernorm(x, scale, bias):
            mu = jnp.mean(x, axis=-1, keepdims=True)
            var = jnp.mean(jnp.square(x - mu), axis=-1, keepdims=True)
            return (x - mu) * jax.lax.rsqrt(var + EPS_LN) * scale + bias

        def _sinusoidal_pos_emb(t, d):
            half = d // 2
            freq = jnp.exp(jnp.arange(half, dtype=jnp.float32) * (-math.log(10000.0) / (half - 1)))
            pos = (jnp.arange(t, dtype=jnp.float32) + 1.0)[:, None] * freq[None, :]
            return jnp.concatenate([jnp.sin(pos), jnp.cos(pos)], axis=-1)

        def _linear_attention(q, k, v):
            qp = jax.nn.elu(q) + 1.0
            kp = jax.nn.elu(k) + 1.0
            kv = jnp.einsum('bshd,bshm->bhmd', kp, v)
            ksum = jnp.sum(kp, axis=1)
            z = 1.0 / (jnp.einsum('blhd,bhd->blh', qp, ksum) + EPS_ATTN)
            return jnp.einsum('blhd,bhmd,blh->blhm', qp, kv, z)

        def _encoder_layer(x, Wq, bq, Wk, bk, Wv, bv, Wo, bo, W1, b1, W2, b2, ln1_s, ln1_b, ln2_s, ln2_b):
            b, t, d = x.shape
            h = _layernorm(x, ln1_s, ln1_b)
            q = (h @ Wq + bq).reshape(b, t, H, DK)
            k = (h @ Wk + bk).reshape(b, t, H, DK)
            v = (h @ Wv + bv).reshape(b, t, H, DK)
            attn = _linear_attention(q, k, v).reshape(b, t, d)
            x = x + (attn @ Wo + bo)
            h = _layernorm(x, ln2_s, ln2_b)
            h = jax.nn.relu(h @ W1 + b1) @ W2 + b2
            return x + h
        key = jax.random.key(seed)
        ks = jax.random.split(key, 8)
        w = lambda k, shape: jax.random.normal(k, shape, dtype=jnp.float32) * 0.02
        return {'x_in': jax.random.normal(ks[0], (B, T, D), dtype=jnp.float32), 'Wq': w(ks[1], (L, D, D)), 'bq': jnp.zeros((L, D), jnp.float32), 'Wk': w(ks[2], (L, D, D)), 'bk': jnp.zeros((L, D), jnp.float32), 'Wv': w(ks[3], (L, D, D)), 'bv': jnp.zeros((L, D), jnp.float32), 'Wo': w(ks[4], (L, D, D)), 'bo': jnp.zeros((L, D), jnp.float32), 'W1': w(ks[5], (L, D, 4 * D)), 'b1': jnp.zeros((L, 4 * D), jnp.float32), 'W2': w(ks[6], (L, 4 * D, D)), 'b2': jnp.zeros((L, D), jnp.float32), 'ln1_s': jnp.ones((L, D), jnp.float32), 'ln1_b': jnp.zeros((L, D), jnp.float32), 'ln2_s': jnp.ones((L, D), jnp.float32), 'ln2_b': jnp.zeros((L, D), jnp.float32), 'lnf_s': jnp.ones((D,), jnp.float32), 'lnf_b': jnp.zeros((D,), jnp.float32)}
    _L0_attn_all = _L0_attn_setup()
    _L0_attn_in = {k: v for k, v in _L0_attn_all.items() if k in ('Wq', 'bq', 'Wk', 'bk', 'Wv', 'bv', 'Wo', 'bo', 'W1', 'b1', 'W2', 'b2', 'ln1_s', 'ln1_b', 'ln2_s', 'ln2_b', 'lnf_s', 'lnf_b')}
    del _L0_attn_all

    def _L0_ffn_setup():
        import jax, jax.numpy as jnp
        import numpy as np
        HIDDEN = 256
        NUM_EXPERTS = 8
        CAPACITY_FACTOR = 1.25
        key = jax.random.key(seed)
        k_tok, k_g, k_w1, k_b1, k_w2, k_b2 = jax.random.split(key, 6)
        B, S, H, E = (4, 512, HIDDEN, NUM_EXPERTS)
        tokens = jax.random.normal(k_tok, (B, S, H), dtype=jnp.float32)
        gate_w = jax.random.normal(k_g, (E, H), dtype=jnp.float32) * 0.02
        W1 = jax.random.normal(k_w1, (E, H, H), dtype=jnp.float32) * 0.02
        b1 = jax.random.normal(k_b1, (E, H), dtype=jnp.float32) * 0.02
        W2 = jax.random.normal(k_w2, (E, H, H), dtype=jnp.float32) * 0.02
        b2 = jax.random.normal(k_b2, (E, H), dtype=jnp.float32) * 0.02
        return {'tokens': tokens, 'gate_w': gate_w, 'W1': W1, 'b1': b1, 'W2': W2, 'b2': b2}
    _L0_ffn_all = _L0_ffn_setup()
    _L0_ffn_in = {k: v for k, v in _L0_ffn_all.items() if k in ('gate_w', 'W1', 'b1', 'W2', 'b2')}
    del _L0_ffn_all

    def _L1_xattn_setup():
        import jax, jax.numpy as jnp
        import numpy as np
        D = 256
        NUM_ITERS = 3
        EPS = 1e-06
        SCALE = D ** (-0.5)

        def rmsnorm(x, w, eps=EPS):
            return x * jax.lax.rsqrt(jnp.mean(x * x, axis=-1, keepdims=True) + eps) * w

        def gru_cell(x, h, wih, whh, bih, bhh):
            gx = x @ wih.T + bih
            gh = h @ whh.T + bhh
            xr, xz, xn = jnp.split(gx, 3, axis=-1)
            hr, hz, hn = jnp.split(gh, 3, axis=-1)
            r = jax.nn.sigmoid(xr + hr)
            z = jax.nn.sigmoid(xz + hz)
            n = jnp.tanh(xn + r * hn)
            return (1.0 - z) * n + z * h
        key = jax.random.key(seed)
        ks = jax.random.split(key, 8)
        B, K, M, d = (8, 64, 1024, D)
        w_std = d ** (-0.5)
        return {'slots': jax.random.normal(ks[0], (B, K, d), jnp.float32), 'P': jax.random.normal(ks[1], (B, M, d), jnp.float32), 'Wq': jax.random.normal(ks[2], (d, d), jnp.float32) * w_std, 'Wk': jax.random.normal(ks[3], (d, d), jnp.float32) * w_std, 'Wv': jax.random.normal(ks[4], (d, d), jnp.float32) * w_std, 'gru_wih': jax.random.normal(ks[5], (3 * d, d), jnp.float32) * w_std, 'gru_whh': jax.random.normal(ks[6], (3 * d, d), jnp.float32) * w_std, 'gru_bih': jnp.zeros((3 * d,), jnp.float32), 'gru_bhh': jnp.zeros((3 * d,), jnp.float32), 'slot_norm_w': jnp.ones((d,), jnp.float32), 'input_norm_w': jnp.ones((d,), jnp.float32)}
    _L1_xattn_all = _L1_xattn_setup()
    _L1_xattn_in = {k: v for k, v in _L1_xattn_all.items() if k in ('Wq', 'Wk', 'Wv', 'gru_wih', 'gru_whh', 'gru_bih', 'gru_bhh', 'slot_norm_w', 'input_norm_w')}
    del _L1_xattn_all

    def _L1_attn_setup():
        import jax, jax.numpy as jnp
        import numpy as np
        B, L, D, H = (2, 512, 256, 16)
        C = D // H
        SCALE = 1.0 / np.sqrt(D).astype(np.float32)
        key = jax.random.key(seed)
        ks = jax.random.split(key, 5)
        return {'x': jax.random.normal(ks[0], (B, L, D), dtype=jnp.float32), 'w_qkv': jax.random.normal(ks[1], (3 * D, D), dtype=jnp.float32) * (1.0 / np.sqrt(D)), 'b_qkv': jax.random.normal(ks[2], (3 * D,), dtype=jnp.float32) * 0.02, 'w_o': jax.random.normal(ks[3], (D, D), dtype=jnp.float32) * (1.0 / np.sqrt(D)), 'b_o': jax.random.normal(ks[4], (D,), dtype=jnp.float32) * 0.02}
    _L1_attn_all = _L1_attn_setup()
    _L1_attn_in = {k: v for k, v in _L1_attn_all.items() if k in ('w_qkv', 'b_qkv', 'w_o', 'b_o')}
    del _L1_attn_all

    def _L1_ffn_setup():
        import jax, jax.numpy as jnp
        import numpy as np
        B, N, D = (4, 1024, 256)
        E, K, H, ITERS = (8, 2, 64, 2)
        DT = 0.1
        C = 2 * D

        def _gelu(x):
            return jax.nn.gelu(x, approximate=False)

        def _inl(ctrl, xs, vs, mu):
            a, b, g = jnp.split(ctrl, 3, axis=-1)
            v_next = jax.nn.sigmoid(a) * vs - jax.nn.softplus(b) * (xs - mu)
            x_next = xs + DT * jax.nn.sigmoid(g) * v_next
            return (x_next, v_next)

        def _experts(ctx, idx, w1, b1, w2, b2):
            out = jnp.zeros((ctx.shape[0], w2.shape[2]), ctx.dtype)
            for e in range(E):
                h = _gelu(ctx @ w1[e] + b1[e])
                o = h @ w2[e] + b2[e]
                out = out + jnp.where((idx == e)[:, None], o, jnp.float32(0))
            return out

        def _forward(x, integration_weight, mu, router_w1, router_b1, router_w2, router_b2, halt_w1, halt_b1, halt_w2, halt_b2, expert_w1, expert_b1, expert_w2, expert_b2, shared_w1, shared_b1, shared_w2, shared_b2, shared_weight, refine_w1, refine_b1, refine_w2, refine_b2):
            b, n, d = x.shape
            xf = x.reshape(b * n, d)
            logits = _gelu(xf @ router_w1 + router_b1) @ router_w2 + router_b2
            probs = jax.nn.softmax(logits, axis=-1)
            topk_p, topk_i = jax.lax.top_k(probs, K)
            topk_p = topk_p / jnp.sum(topk_p, axis=-1, keepdims=True)
            flat_idx = topk_i.reshape(-1)
            flat_w = topk_p.reshape(-1, 1)
            v = jnp.zeros_like(xf)
            integrated = xf
            for _ in range(ITERS):
                ctx = jnp.concatenate([integrated, v], axis=-1)
                shared_ctrl = _gelu(ctx @ shared_w1 + shared_b1) @ shared_w2 + shared_b2
                x_sh, v_sh = _inl(shared_ctrl, integrated, v, mu)
                sw = jax.nn.sigmoid(shared_weight)
                ctx_e = jnp.repeat(ctx, K, axis=0)
                x_e = jnp.repeat(integrated, K, axis=0)
                v_e = jnp.repeat(v, K, axis=0)
                ctrl = _experts(ctx_e, flat_idx, expert_w1, expert_b1, expert_w2, expert_b2)
                x_r, v_r = _inl(ctrl, x_e, v_e, mu)
                x_r = (x_r * flat_w).reshape(-1, K, d).sum(axis=1)
                v_r = (v_r * flat_w).reshape(-1, K, d).sum(axis=1)
                x_next = sw * x_sh + (1.0 - sw) * x_r
                v_next = sw * v_sh + (1.0 - sw) * v_r
                halt = jax.nn.sigmoid(_gelu(integrated @ halt_w1 + halt_b1) @ halt_w2 + halt_b2)
                integrated = integrated + halt * (x_next - integrated)
                v = v + halt * (v_next - v)
            refined = _gelu(integrated @ refine_w1 + refine_b1) @ refine_w2 + refine_b2
            out = xf + integration_weight * refined
            return out.reshape(b, n, d)
        key = jax.random.key(seed)
        ks = jax.random.split(key, 12)
        rn = lambda k, s, sc=0.02: jax.random.normal(k, s, dtype=jnp.float32) * sc
        z = lambda s: jnp.zeros(s, jnp.float32)
        return {'x': jax.random.normal(ks[0], (B, N, D), dtype=jnp.float32), 'integration_weight': jnp.full((D,), 0.5, jnp.float32), 'mu': z((D,)), 'router_w1': rn(ks[1], (D, D // 4)), 'router_b1': z((D // 4,)), 'router_w2': rn(ks[2], (D // 4, E)), 'router_b2': z((E,)), 'halt_w1': rn(ks[3], (D, D // 4)), 'halt_b1': z((D // 4,)), 'halt_w2': rn(ks[4], (D // 4, 1)), 'halt_b2': z((1,)), 'expert_w1': rn(ks[5], (E, C, H)), 'expert_b1': z((E, H)), 'expert_w2': rn(ks[6], (E, H, 3 * D)), 'expert_b2': z((E, 3 * D)), 'shared_w1': rn(ks[7], (C, H)), 'shared_b1': z((H,)), 'shared_w2': rn(ks[8], (H, 3 * D)), 'shared_b2': z((3 * D,)), 'shared_weight': jnp.float32(0.5), 'refine_w1': rn(ks[9], (D, 2 * D)), 'refine_b1': z((2 * D,)), 'refine_w2': rn(ks[10], (2 * D, D)), 'refine_b2': z((D,))}
    _L1_ffn_all = _L1_ffn_setup()
    _L1_ffn_in = {k: v for k, v in _L1_ffn_all.items() if k in ('integration_weight', 'mu', 'router_w1', 'router_b1', 'router_w2', 'router_b2', 'halt_w1', 'halt_b1', 'halt_w2', 'halt_b2', 'expert_w1', 'expert_b1', 'expert_w2', 'expert_b2', 'shared_w1', 'shared_b1', 'shared_w2', 'shared_b2', 'shared_weight', 'refine_w1', 'refine_b1', 'refine_w2', 'refine_b2')}
    del _L1_ffn_all

    def _L2_xattn_setup():
        import jax, jax.numpy as jnp
        import numpy as np
        from math import sqrt
        B, Q, S, D, H = (2, 512, 512, 256, 16)
        ADIM = D // H
        IEPS = 1e-32

        def sparse_norm(scores, nbias):
            t = jax.nn.relu(scores + nbias[0])
            t = t * t
            return t / (t.sum(-1, keepdims=True) + IEPS)
        key = jax.random.key(seed)
        ks = jax.random.split(key, 7)
        sc = 0.02
        return {'iQ': jax.random.normal(ks[0], (B, Q, D), jnp.float32), 'iK': jax.random.normal(ks[1], (B, S, D), jnp.float32), 'mask': jax.random.randint(ks[2], (B, Q, S), 0, 2) > 0, 'Wq': jax.random.normal(ks[3], (D, D), jnp.float32) * sc, 'Wkv': jax.random.normal(ks[4], (2 * D, D), jnp.float32) * sc, 'Wo': jax.random.normal(ks[5], (D, D), jnp.float32) * sc, 'nbias': jnp.zeros((1,), jnp.float32)}
    _L2_xattn_all = _L2_xattn_setup()
    _L2_xattn_in = {k: v for k, v in _L2_xattn_all.items() if k in ('Wq', 'Wkv', 'Wo', 'nbias')}
    del _L2_xattn_all

    def _L2_attn_setup():
        import jax, jax.numpy as jnp
        import numpy as np
        EMBED_DIM = 256
        NUM_HEADS = 16
        HEAD_DIM = EMBED_DIM // NUM_HEADS
        NUM_FEATS = 64
        YAT_EPS = 0.1
        BATCH = 4
        SEQ = 1024

        def _spherical_features(x, projection):
            x_norm = x / (jnp.linalg.norm(x, axis=-1, keepdims=True) + 1e-08)
            proj = jnp.einsum('bhsd,hfd->bhsf', x_norm, projection)
            return jax.nn.relu(proj) + YAT_EPS
        key = jax.random.key(seed)
        ks = jax.random.split(key, 6)
        s = 1.0 / np.sqrt(EMBED_DIM)
        return {'x': jax.random.normal(ks[0], (BATCH, SEQ, EMBED_DIM), jnp.float32), 'Wq': jax.random.normal(ks[1], (EMBED_DIM, EMBED_DIM), jnp.float32) * s, 'bq': jnp.zeros((EMBED_DIM,), jnp.float32), 'Wk': jax.random.normal(ks[2], (EMBED_DIM, EMBED_DIM), jnp.float32) * s, 'bk': jnp.zeros((EMBED_DIM,), jnp.float32), 'Wv': jax.random.normal(ks[3], (EMBED_DIM, EMBED_DIM), jnp.float32) * s, 'bv': jnp.zeros((EMBED_DIM,), jnp.float32), 'Wo': jax.random.normal(ks[4], (EMBED_DIM, EMBED_DIM), jnp.float32) * s, 'bo': jnp.zeros((EMBED_DIM,), jnp.float32), 'projection': jax.random.normal(ks[5], (NUM_HEADS, NUM_FEATS, HEAD_DIM), jnp.float32)}
    _L2_attn_all = _L2_attn_setup()
    _L2_attn_in = {k: v for k, v in _L2_attn_all.items() if k in ('Wq', 'bq', 'Wk', 'bk', 'Wv', 'bv', 'Wo', 'bo', 'projection')}
    del _L2_attn_all

    def _L2_ffn_setup():
        import jax, jax.numpy as jnp
        import numpy as np
        B, S, D = (2, 128, 256)
        E, K, I = (16, 8, 256)
        I_SH = 256
        ROUTE_SCALE = 2.826
        key = jax.random.key(seed)
        ks = jax.random.split(key, 8)
        s = 0.02
        return {'x': jax.random.normal(ks[0], (B, S, D), dtype=jnp.float32), 'gate_w': jax.random.normal(ks[1], (E, D), dtype=jnp.float32) * s, 'expert_bias': jnp.zeros((E,), dtype=jnp.float32), 'w_gate': jax.random.normal(ks[2], (E, I, D), dtype=jnp.float32) * s, 'w_up': jax.random.normal(ks[3], (E, I, D), dtype=jnp.float32) * s, 'w_down': jax.random.normal(ks[4], (E, D, I), dtype=jnp.float32) * s, 'shared_gate_w': jax.random.normal(ks[5], (I_SH, D), dtype=jnp.float32) * s, 'shared_up_w': jax.random.normal(ks[6], (I_SH, D), dtype=jnp.float32) * s, 'shared_down_w': jax.random.normal(ks[7], (D, I_SH), dtype=jnp.float32) * s}
    _L2_ffn_all = _L2_ffn_setup()
    _L2_ffn_in = {k: v for k, v in _L2_ffn_all.items() if k in ('gate_w', 'expert_bias', 'w_gate', 'w_up', 'w_down', 'shared_gate_w', 'shared_up_w', 'shared_down_w')}
    del _L2_ffn_all

    def _L3_xattn_setup():
        import jax, jax.numpy as jnp
        import numpy as np
        B, SQ, SK, D, H = (4, 512, 512, 256, 16)
        SCALE = (D / H) ** 0.5
        key = jax.random.key(seed)
        ks = jax.random.split(key, 8)
        s = 1.0 / np.sqrt(D)
        return {'x1': jax.random.normal(ks[0], (B, SQ, D), dtype=jnp.float32), 'x2': jax.random.normal(ks[1], (B, SK, D), dtype=jnp.float32), 'Wq': jax.random.uniform(ks[2], (D, D), jnp.float32, -s, s), 'bq': jax.random.uniform(ks[3], (D,), jnp.float32, -s, s), 'Wk': jax.random.uniform(ks[4], (D, D), jnp.float32, -s, s), 'bk': jax.random.uniform(ks[5], (D,), jnp.float32, -s, s), 'Wv': jax.random.uniform(ks[6], (D, D), jnp.float32, -s, s), 'bv': jax.random.uniform(ks[7], (D,), jnp.float32, -s, s)}
    _L3_xattn_all = _L3_xattn_setup()
    _L3_xattn_in = {k: v for k, v in _L3_xattn_all.items() if k in ('Wq', 'bq', 'Wk', 'bk', 'Wv', 'bv')}
    del _L3_xattn_all

    def _L3_attn_setup():
        import math
        import jax, jax.numpy as jnp
        import numpy as np
        N_EMBD = 256
        N_HEAD = 16
        NUM_BUCKETS = 32
        MAX_DISTANCE = 128

        def _relative_position_bucket(relative_position, num_buckets=NUM_BUCKETS, max_distance=MAX_DISTANCE):
            rp = -jnp.minimum(relative_position, 0)
            max_exact = num_buckets // 2
            is_small = rp < max_exact
            rp_large = max_exact + (jnp.log(rp.astype(jnp.float32) / max_exact + 1e-10) / math.log(max_distance / max_exact) * (num_buckets - max_exact)).astype(jnp.int32)
            rp_large = jnp.minimum(rp_large, num_buckets - 1)
            return jnp.where(is_small, rp, rp_large)
        key = jax.random.key(seed)
        ks = jax.random.split(key, 6)
        B, T, C = (4, 512, N_EMBD)
        s_in = 1.0 / math.sqrt(C)
        x = jax.random.normal(ks[0], (B, T, C), dtype=jnp.float32)
        W_attn = jax.random.normal(ks[1], (3 * C, C), dtype=jnp.float32) * s_in
        b_attn = jnp.zeros((3 * C,), dtype=jnp.float32)
        W_proj = jax.random.normal(ks[2], (C, C), dtype=jnp.float32) * s_in
        b_proj = jnp.zeros((C,), dtype=jnp.float32)
        rel_emb = jax.random.normal(ks[3], (NUM_BUCKETS, N_HEAD), dtype=jnp.float32) * 0.02
        return {'x': x, 'W_attn': W_attn, 'b_attn': b_attn, 'W_proj': W_proj, 'b_proj': b_proj, 'rel_emb': rel_emb}
    _L3_attn_all = _L3_attn_setup()
    _L3_attn_in = {k: v for k, v in _L3_attn_all.items() if k in ('W_attn', 'b_attn', 'W_proj', 'b_proj', 'rel_emb')}
    del _L3_attn_all

    def _L3_ffn_setup():
        import jax, jax.numpy as jnp
        import numpy as np
        B, S, IN, OUT = (4, 2048, 256, 256)
        EPS = 1e-06

        def _xla_quantized_matmul(x2d, weight_q, weight_scale):
            amax = jnp.max(jnp.abs(x2d), axis=-1, keepdims=True)
            x_scale = jnp.maximum(amax, EPS) / 127.0
            x_q = jnp.clip(jnp.round(x2d / x_scale), -128, 127).astype(jnp.int8)
            acc = jax.lax.dot_general(x_q, weight_q, (((1,), (1,)), ((), ())), preferred_element_type=jnp.int32)
            return acc.astype(jnp.float32) * x_scale * weight_scale[None, :]
        key = jax.random.key(seed)
        k1, k2, k3, k4 = jax.random.split(key, 4)
        x = jax.random.normal(k1, (B, S, IN), dtype=jnp.float32)
        weight_q = jax.random.randint(k2, (OUT, IN), -128, 128, dtype=jnp.int32).astype(jnp.int8)
        weight_scale = jax.random.uniform(k3, (OUT,), dtype=jnp.float32, minval=0.001, maxval=0.01)
        bias = jax.random.normal(k4, (OUT,), dtype=jnp.float32) * 0.01
        return {'x': x, 'weight_q': weight_q, 'weight_scale': weight_scale, 'bias': bias}
    _L3_ffn_all = _L3_ffn_setup()
    _L3_ffn_in = {k: v for k, v in _L3_ffn_all.items() if k in ('weight_q', 'weight_scale', 'bias')}
    del _L3_ffn_all
    return {'x': x, 'ctx_1024': ctx_1024, 'mask_BxSxS2_bk0': mask_BxSxS2_bk0, 'L0_xattn_w_q': _L0_xattn_in['w_q'], 'L0_xattn_w_k': _L0_xattn_in['w_k'], 'L0_xattn_w_v': _L0_xattn_in['w_v'], 'L0_xattn_w_o': _L0_xattn_in['w_o'], 'L0_attn_Wq': _L0_attn_in['Wq'], 'L0_attn_bq': _L0_attn_in['bq'], 'L0_attn_Wk': _L0_attn_in['Wk'], 'L0_attn_bk': _L0_attn_in['bk'], 'L0_attn_Wv': _L0_attn_in['Wv'], 'L0_attn_bv': _L0_attn_in['bv'], 'L0_attn_Wo': _L0_attn_in['Wo'], 'L0_attn_bo': _L0_attn_in['bo'], 'L0_attn_W1': _L0_attn_in['W1'], 'L0_attn_b1': _L0_attn_in['b1'], 'L0_attn_W2': _L0_attn_in['W2'], 'L0_attn_b2': _L0_attn_in['b2'], 'L0_attn_ln1_s': _L0_attn_in['ln1_s'], 'L0_attn_ln1_b': _L0_attn_in['ln1_b'], 'L0_attn_ln2_s': _L0_attn_in['ln2_s'], 'L0_attn_ln2_b': _L0_attn_in['ln2_b'], 'L0_attn_lnf_s': _L0_attn_in['lnf_s'], 'L0_attn_lnf_b': _L0_attn_in['lnf_b'], 'L0_ffn_gate_w': _L0_ffn_in['gate_w'], 'L0_ffn_W1': _L0_ffn_in['W1'], 'L0_ffn_b1': _L0_ffn_in['b1'], 'L0_ffn_W2': _L0_ffn_in['W2'], 'L0_ffn_b2': _L0_ffn_in['b2'], 'L1_xattn_Wq': _L1_xattn_in['Wq'], 'L1_xattn_Wk': _L1_xattn_in['Wk'], 'L1_xattn_Wv': _L1_xattn_in['Wv'], 'L1_xattn_gru_wih': _L1_xattn_in['gru_wih'], 'L1_xattn_gru_whh': _L1_xattn_in['gru_whh'], 'L1_xattn_gru_bih': _L1_xattn_in['gru_bih'], 'L1_xattn_gru_bhh': _L1_xattn_in['gru_bhh'], 'L1_xattn_slot_norm_w': _L1_xattn_in['slot_norm_w'], 'L1_xattn_input_norm_w': _L1_xattn_in['input_norm_w'], 'L1_attn_w_qkv': _L1_attn_in['w_qkv'], 'L1_attn_b_qkv': _L1_attn_in['b_qkv'], 'L1_attn_w_o': _L1_attn_in['w_o'], 'L1_attn_b_o': _L1_attn_in['b_o'], 'L1_ffn_integration_weight': _L1_ffn_in['integration_weight'], 'L1_ffn_mu': _L1_ffn_in['mu'], 'L1_ffn_router_w1': _L1_ffn_in['router_w1'], 'L1_ffn_router_b1': _L1_ffn_in['router_b1'], 'L1_ffn_router_w2': _L1_ffn_in['router_w2'], 'L1_ffn_router_b2': _L1_ffn_in['router_b2'], 'L1_ffn_halt_w1': _L1_ffn_in['halt_w1'], 'L1_ffn_halt_b1': _L1_ffn_in['halt_b1'], 'L1_ffn_halt_w2': _L1_ffn_in['halt_w2'], 'L1_ffn_halt_b2': _L1_ffn_in['halt_b2'], 'L1_ffn_expert_w1': _L1_ffn_in['expert_w1'], 'L1_ffn_expert_b1': _L1_ffn_in['expert_b1'], 'L1_ffn_expert_w2': _L1_ffn_in['expert_w2'], 'L1_ffn_expert_b2': _L1_ffn_in['expert_b2'], 'L1_ffn_shared_w1': _L1_ffn_in['shared_w1'], 'L1_ffn_shared_b1': _L1_ffn_in['shared_b1'], 'L1_ffn_shared_w2': _L1_ffn_in['shared_w2'], 'L1_ffn_shared_b2': _L1_ffn_in['shared_b2'], 'L1_ffn_shared_weight': _L1_ffn_in['shared_weight'], 'L1_ffn_refine_w1': _L1_ffn_in['refine_w1'], 'L1_ffn_refine_b1': _L1_ffn_in['refine_b1'], 'L1_ffn_refine_w2': _L1_ffn_in['refine_w2'], 'L1_ffn_refine_b2': _L1_ffn_in['refine_b2'], 'L2_xattn_Wq': _L2_xattn_in['Wq'], 'L2_xattn_Wkv': _L2_xattn_in['Wkv'], 'L2_xattn_Wo': _L2_xattn_in['Wo'], 'L2_xattn_nbias': _L2_xattn_in['nbias'], 'L2_attn_Wq': _L2_attn_in['Wq'], 'L2_attn_bq': _L2_attn_in['bq'], 'L2_attn_Wk': _L2_attn_in['Wk'], 'L2_attn_bk': _L2_attn_in['bk'], 'L2_attn_Wv': _L2_attn_in['Wv'], 'L2_attn_bv': _L2_attn_in['bv'], 'L2_attn_Wo': _L2_attn_in['Wo'], 'L2_attn_bo': _L2_attn_in['bo'], 'L2_attn_projection': _L2_attn_in['projection'], 'L2_ffn_gate_w': _L2_ffn_in['gate_w'], 'L2_ffn_expert_bias': _L2_ffn_in['expert_bias'], 'L2_ffn_w_gate': _L2_ffn_in['w_gate'], 'L2_ffn_w_up': _L2_ffn_in['w_up'], 'L2_ffn_w_down': _L2_ffn_in['w_down'], 'L2_ffn_shared_gate_w': _L2_ffn_in['shared_gate_w'], 'L2_ffn_shared_up_w': _L2_ffn_in['shared_up_w'], 'L2_ffn_shared_down_w': _L2_ffn_in['shared_down_w'], 'L3_xattn_Wq': _L3_xattn_in['Wq'], 'L3_xattn_bq': _L3_xattn_in['bq'], 'L3_xattn_Wk': _L3_xattn_in['Wk'], 'L3_xattn_bk': _L3_xattn_in['bk'], 'L3_xattn_Wv': _L3_xattn_in['Wv'], 'L3_xattn_bv': _L3_xattn_in['bv'], 'L3_attn_W_attn': _L3_attn_in['W_attn'], 'L3_attn_b_attn': _L3_attn_in['b_attn'], 'L3_attn_W_proj': _L3_attn_in['W_proj'], 'L3_attn_b_proj': _L3_attn_in['b_proj'], 'L3_attn_rel_emb': _L3_attn_in['rel_emb'], 'L3_ffn_weight_q': _L3_ffn_in['weight_q'], 'L3_ffn_weight_scale': _L3_ffn_in['weight_scale'], 'L3_ffn_bias': _L3_ffn_in['bias']}

def reference(x, ctx_1024, mask_BxSxS2_bk0, L0_xattn_w_q, L0_xattn_w_k, L0_xattn_w_v, L0_xattn_w_o, L0_attn_Wq, L0_attn_bq, L0_attn_Wk, L0_attn_bk, L0_attn_Wv, L0_attn_bv, L0_attn_Wo, L0_attn_bo, L0_attn_W1, L0_attn_b1, L0_attn_W2, L0_attn_b2, L0_attn_ln1_s, L0_attn_ln1_b, L0_attn_ln2_s, L0_attn_ln2_b, L0_attn_lnf_s, L0_attn_lnf_b, L0_ffn_gate_w, L0_ffn_W1, L0_ffn_b1, L0_ffn_W2, L0_ffn_b2, L1_xattn_Wq, L1_xattn_Wk, L1_xattn_Wv, L1_xattn_gru_wih, L1_xattn_gru_whh, L1_xattn_gru_bih, L1_xattn_gru_bhh, L1_xattn_slot_norm_w, L1_xattn_input_norm_w, L1_attn_w_qkv, L1_attn_b_qkv, L1_attn_w_o, L1_attn_b_o, L1_ffn_integration_weight, L1_ffn_mu, L1_ffn_router_w1, L1_ffn_router_b1, L1_ffn_router_w2, L1_ffn_router_b2, L1_ffn_halt_w1, L1_ffn_halt_b1, L1_ffn_halt_w2, L1_ffn_halt_b2, L1_ffn_expert_w1, L1_ffn_expert_b1, L1_ffn_expert_w2, L1_ffn_expert_b2, L1_ffn_shared_w1, L1_ffn_shared_b1, L1_ffn_shared_w2, L1_ffn_shared_b2, L1_ffn_shared_weight, L1_ffn_refine_w1, L1_ffn_refine_b1, L1_ffn_refine_w2, L1_ffn_refine_b2, L2_xattn_Wq, L2_xattn_Wkv, L2_xattn_Wo, L2_xattn_nbias, L2_attn_Wq, L2_attn_bq, L2_attn_Wk, L2_attn_bk, L2_attn_Wv, L2_attn_bv, L2_attn_Wo, L2_attn_bo, L2_attn_projection, L2_ffn_gate_w, L2_ffn_expert_bias, L2_ffn_w_gate, L2_ffn_w_up, L2_ffn_w_down, L2_ffn_shared_gate_w, L2_ffn_shared_up_w, L2_ffn_shared_down_w, L3_xattn_Wq, L3_xattn_bq, L3_xattn_Wk, L3_xattn_bk, L3_xattn_Wv, L3_xattn_bv, L3_attn_W_attn, L3_attn_b_attn, L3_attn_W_proj, L3_attn_b_proj, L3_attn_rel_emb, L3_ffn_weight_q, L3_ffn_weight_scale, L3_ffn_bias):
    import jax
    import jax.numpy as jnp

    def _L0_xattn_ref(q, k, v, w_q, w_k, w_v, w_o):
        import jax, jax.numpy as jnp
        import numpy as np
        HEAD_NUM = 16
        PAD = 0.0
        MASKS_FUTURE = True

        def _split_head(x):
            B, S, D = x.shape
            return x.reshape(B, S, HEAD_NUM, D // HEAD_NUM).transpose(0, 2, 1, 3)
        qp = _split_head(q @ w_q)
        kp = _split_head(k @ w_k)
        vp = _split_head(v @ w_v)
        d_k = qp.shape[-1]
        scores = jnp.einsum('bhqd,bhkd->bhqk', qp, kp) / jnp.sqrt(jnp.float32(d_k))
        mask = scores == PAD
        if MASKS_FUTURE:
            Sq, Sk = (scores.shape[-2], scores.shape[-1])
            tril = jnp.tril(jnp.ones((Sq, Sk), dtype=bool))
            mask = mask & tril
        neg = jnp.finfo(jnp.float32).min
        scores = jnp.where(mask, neg, scores)
        attn = jax.nn.softmax(scores, axis=-1)
        attn = jnp.where(mask, PAD, attn)
        out = jnp.einsum('bhqk,bhkd->bhqd', attn, vp)
        B, H, S, dh = out.shape
        concat = out.transpose(0, 2, 1, 3).reshape(B, S, H * dh)
        return concat @ w_o

    def _L0_attn_ref(x_in, Wq, bq, Wk, bk, Wv, bv, Wo, bo, W1, b1, W2, b2, ln1_s, ln1_b, ln2_s, ln2_b, lnf_s, lnf_b):
        import math
        import jax, jax.numpy as jnp
        import numpy as np
        B, T, D, H, L = (8, 512, 256, 16, 4)
        DK = D // H
        EPS_LN = 1e-05
        EPS_ATTN = 1e-06

        def _layernorm(x, scale, bias):
            mu = jnp.mean(x, axis=-1, keepdims=True)
            var = jnp.mean(jnp.square(x - mu), axis=-1, keepdims=True)
            return (x - mu) * jax.lax.rsqrt(var + EPS_LN) * scale + bias

        def _sinusoidal_pos_emb(t, d):
            half = d // 2
            freq = jnp.exp(jnp.arange(half, dtype=jnp.float32) * (-math.log(10000.0) / (half - 1)))
            pos = (jnp.arange(t, dtype=jnp.float32) + 1.0)[:, None] * freq[None, :]
            return jnp.concatenate([jnp.sin(pos), jnp.cos(pos)], axis=-1)

        def _linear_attention(q, k, v):
            qp = jax.nn.elu(q) + 1.0
            kp = jax.nn.elu(k) + 1.0
            kv = jnp.einsum('bshd,bshm->bhmd', kp, v)
            ksum = jnp.sum(kp, axis=1)
            z = 1.0 / (jnp.einsum('blhd,bhd->blh', qp, ksum) + EPS_ATTN)
            return jnp.einsum('blhd,bhmd,blh->blhm', qp, kv, z)

        def _encoder_layer(x, Wq, bq, Wk, bk, Wv, bv, Wo, bo, W1, b1, W2, b2, ln1_s, ln1_b, ln2_s, ln2_b):
            b, t, d = x.shape
            h = _layernorm(x, ln1_s, ln1_b)
            q = (h @ Wq + bq).reshape(b, t, H, DK)
            k = (h @ Wk + bk).reshape(b, t, H, DK)
            v = (h @ Wv + bv).reshape(b, t, H, DK)
            attn = _linear_attention(q, k, v).reshape(b, t, d)
            x = x + (attn @ Wo + bo)
            h = _layernorm(x, ln2_s, ln2_b)
            h = jax.nn.relu(h @ W1 + b1) @ W2 + b2
            return x + h
        b, t, d = x_in.shape
        x = math.sqrt(d) * x_in + _sinusoidal_pos_emb(t, d)[None, :, :]
        for i in range(L):
            x = _encoder_layer(x, Wq[i], bq[i], Wk[i], bk[i], Wv[i], bv[i], Wo[i], bo[i], W1[i], b1[i], W2[i], b2[i], ln1_s[i], ln1_b[i], ln2_s[i], ln2_b[i])
        return _layernorm(x, lnf_s, lnf_b)

    def _L0_ffn_ref(tokens, gate_w, W1, b1, W2, b2):
        import jax, jax.numpy as jnp
        import numpy as np
        HIDDEN = 256
        NUM_EXPERTS = 8
        CAPACITY_FACTOR = 1.25
        B, S, H = tokens.shape
        E = gate_w.shape[0]
        T = B * S
        x = tokens.reshape(T, H)
        logits = x @ gate_w.T
        probs = jax.nn.softmax(logits, axis=-1)
        top2_w, top2_idx = jax.lax.top_k(probs, 2)
        cap = int(CAPACITY_FACTOR * T / E)
        counts = jnp.bincount(top2_idx.reshape(-1), length=E)
        keep = (counts <= cap).astype(x.dtype)
        comb = jnp.zeros((T, E), dtype=x.dtype).at[jnp.arange(T)[:, None], top2_idx].add(top2_w)
        comb = comb * keep[None, :]
        h = jax.nn.relu(jnp.einsum('th,ehf->tef', x, W1) + b1[None, :, :])
        y = jnp.einsum('teh,ehf->tef', h, W2) + b2[None, :, :]
        out = jnp.einsum('te,tef->tf', comb, y)
        return out.reshape(B, S, H)

    def _L1_xattn_ref(slots, P, Wq, Wk, Wv, gru_wih, gru_whh, gru_bih, gru_bhh, slot_norm_w, input_norm_w):
        import jax, jax.numpy as jnp
        import numpy as np
        D = 256
        NUM_ITERS = 3
        EPS = 1e-06
        SCALE = D ** (-0.5)

        def rmsnorm(x, w, eps=EPS):
            return x * jax.lax.rsqrt(jnp.mean(x * x, axis=-1, keepdims=True) + eps) * w

        def gru_cell(x, h, wih, whh, bih, bhh):
            gx = x @ wih.T + bih
            gh = h @ whh.T + bhh
            xr, xz, xn = jnp.split(gx, 3, axis=-1)
            hr, hz, hn = jnp.split(gh, 3, axis=-1)
            r = jax.nn.sigmoid(xr + hr)
            z = jax.nn.sigmoid(xz + hz)
            n = jnp.tanh(xn + r * hn)
            return (1.0 - z) * n + z * h
        Pn = rmsnorm(P, input_norm_w)
        k_proj = Pn @ Wk.T
        v_proj = Pn @ Wv.T
        for _ in range(NUM_ITERS):
            sn = rmsnorm(slots, slot_norm_w)
            q_proj = sn @ Wq.T
            scores = jnp.einsum('bkd,bmd->bkm', q_proj, k_proj) * SCALE
            attn = jax.nn.softmax(scores, axis=-2)
            attn = attn / (jnp.sum(attn, axis=-1, keepdims=True) + EPS)
            updates = jnp.einsum('bkm,bmd->bkd', attn, v_proj)
            slots = gru_cell(updates, slots, gru_wih, gru_whh, gru_bih, gru_bhh)
        return slots

    def _L1_attn_ref(x, w_qkv, b_qkv, w_o, b_o):
        import jax, jax.numpy as jnp
        import numpy as np
        B, L, D, H = (2, 512, 256, 16)
        C = D // H
        SCALE = 1.0 / np.sqrt(D).astype(np.float32)
        b, l, d = x.shape
        h, c = (H, d // H)
        qkv = jnp.einsum('bld,ed->ble', x, w_qkv) + b_qkv
        q, k, v = jnp.split(qkv, 3, axis=-1)
        q = q.reshape(b, l, h, c)
        k = k.reshape(b, l, h, c)
        v = v.reshape(b, l, h, c)
        attn = jax.nn.softmax(jnp.einsum('blhc,bmhc->bhlm', q, k) * SCALE, axis=-1)
        heads = jnp.einsum('bhlm,bmhc->blhc', attn, v).reshape(b, l, d)
        return jnp.einsum('bld,ed->ble', heads, w_o) + b_o + x

    def _L1_ffn_ref(x, integration_weight, mu, router_w1, router_b1, router_w2, router_b2, halt_w1, halt_b1, halt_w2, halt_b2, expert_w1, expert_b1, expert_w2, expert_b2, shared_w1, shared_b1, shared_w2, shared_b2, shared_weight, refine_w1, refine_b1, refine_w2, refine_b2):
        import jax, jax.numpy as jnp
        import numpy as np
        B, N, D = (4, 1024, 256)
        E, K, H, ITERS = (8, 2, 64, 2)
        DT = 0.1
        C = 2 * D

        def _gelu(x):
            return jax.nn.gelu(x, approximate=False)

        def _inl(ctrl, xs, vs, mu):
            a, b, g = jnp.split(ctrl, 3, axis=-1)
            v_next = jax.nn.sigmoid(a) * vs - jax.nn.softplus(b) * (xs - mu)
            x_next = xs + DT * jax.nn.sigmoid(g) * v_next
            return (x_next, v_next)

        def _experts(ctx, idx, w1, b1, w2, b2):
            out = jnp.zeros((ctx.shape[0], w2.shape[2]), ctx.dtype)
            for e in range(E):
                h = _gelu(ctx @ w1[e] + b1[e])
                o = h @ w2[e] + b2[e]
                out = out + jnp.where((idx == e)[:, None], o, jnp.float32(0))
            return out

        def _forward(x, integration_weight, mu, router_w1, router_b1, router_w2, router_b2, halt_w1, halt_b1, halt_w2, halt_b2, expert_w1, expert_b1, expert_w2, expert_b2, shared_w1, shared_b1, shared_w2, shared_b2, shared_weight, refine_w1, refine_b1, refine_w2, refine_b2):
            b, n, d = x.shape
            xf = x.reshape(b * n, d)
            logits = _gelu(xf @ router_w1 + router_b1) @ router_w2 + router_b2
            probs = jax.nn.softmax(logits, axis=-1)
            topk_p, topk_i = jax.lax.top_k(probs, K)
            topk_p = topk_p / jnp.sum(topk_p, axis=-1, keepdims=True)
            flat_idx = topk_i.reshape(-1)
            flat_w = topk_p.reshape(-1, 1)
            v = jnp.zeros_like(xf)
            integrated = xf
            for _ in range(ITERS):
                ctx = jnp.concatenate([integrated, v], axis=-1)
                shared_ctrl = _gelu(ctx @ shared_w1 + shared_b1) @ shared_w2 + shared_b2
                x_sh, v_sh = _inl(shared_ctrl, integrated, v, mu)
                sw = jax.nn.sigmoid(shared_weight)
                ctx_e = jnp.repeat(ctx, K, axis=0)
                x_e = jnp.repeat(integrated, K, axis=0)
                v_e = jnp.repeat(v, K, axis=0)
                ctrl = _experts(ctx_e, flat_idx, expert_w1, expert_b1, expert_w2, expert_b2)
                x_r, v_r = _inl(ctrl, x_e, v_e, mu)
                x_r = (x_r * flat_w).reshape(-1, K, d).sum(axis=1)
                v_r = (v_r * flat_w).reshape(-1, K, d).sum(axis=1)
                x_next = sw * x_sh + (1.0 - sw) * x_r
                v_next = sw * v_sh + (1.0 - sw) * v_r
                halt = jax.nn.sigmoid(_gelu(integrated @ halt_w1 + halt_b1) @ halt_w2 + halt_b2)
                integrated = integrated + halt * (x_next - integrated)
                v = v + halt * (v_next - v)
            refined = _gelu(integrated @ refine_w1 + refine_b1) @ refine_w2 + refine_b2
            out = xf + integration_weight * refined
            return out.reshape(b, n, d)
        return _forward(x, integration_weight, mu, router_w1, router_b1, router_w2, router_b2, halt_w1, halt_b1, halt_w2, halt_b2, expert_w1, expert_b1, expert_w2, expert_b2, shared_w1, shared_b1, shared_w2, shared_b2, shared_weight, refine_w1, refine_b1, refine_w2, refine_b2)

    def _L2_xattn_ref(iQ, iK, mask, Wq, Wkv, Wo, nbias):
        import jax, jax.numpy as jnp
        import numpy as np
        from math import sqrt
        B, Q, S, D, H = (2, 512, 512, 256, 16)
        ADIM = D // H
        IEPS = 1e-32

        def sparse_norm(scores, nbias):
            t = jax.nn.relu(scores + nbias[0])
            t = t * t
            return t / (t.sum(-1, keepdims=True) + IEPS)
        b, q, _ = iQ.shape
        s = iK.shape[1]
        rq = (iQ @ Wq.T).reshape(b, q, H, ADIM)
        kv = (iK @ Wkv.T).reshape(b, s, 2, H, ADIM)
        rk, rv = (kv[:, :, 0], kv[:, :, 1])
        scores = jnp.einsum('bqhd,bshd->bhqs', rq, rk) / sqrt(ADIM)
        scores = jnp.where(mask[:, None, :, :], jnp.float32(-1e+32), scores)
        attn = sparse_norm(scores, nbias)
        o = jnp.einsum('bhqs,bshd->bqhd', attn, rv).reshape(b, q, H * ADIM)
        return o @ Wo.T

    def _L2_attn_ref(x, Wq, bq, Wk, bk, Wv, bv, Wo, bo, projection):
        import jax, jax.numpy as jnp
        import numpy as np
        EMBED_DIM = 256
        NUM_HEADS = 16
        HEAD_DIM = EMBED_DIM // NUM_HEADS
        NUM_FEATS = 64
        YAT_EPS = 0.1
        BATCH = 4
        SEQ = 1024

        def _spherical_features(x, projection):
            x_norm = x / (jnp.linalg.norm(x, axis=-1, keepdims=True) + 1e-08)
            proj = jnp.einsum('bhsd,hfd->bhsf', x_norm, projection)
            return jax.nn.relu(proj) + YAT_EPS
        b, s, _ = x.shape

        def heads(t):
            return jnp.transpose(t.reshape(b, s, NUM_HEADS, HEAD_DIM), (0, 2, 1, 3))
        Q = heads(x @ Wq + bq)
        K = heads(x @ Wk + bk)
        V = heads(x @ Wv + bv)
        Qp = _spherical_features(Q, projection)
        Kp = _spherical_features(K, projection)
        KV = jnp.einsum('bhsf,bhsd->bhfd', Kp, V)
        QKV = jnp.einsum('bhsf,bhfd->bhsd', Qp, KV)
        K_sum = jnp.sum(Kp, axis=2)
        normalizer = jnp.einsum('bhsf,bhf->bhs', Qp, K_sum)[..., None]
        normalizer = jnp.maximum(normalizer, 1e-06)
        out = QKV / normalizer
        out = jnp.transpose(out, (0, 2, 1, 3)).reshape(b, s, EMBED_DIM)
        return out @ Wo + bo

    def _L2_ffn_ref(x, gate_w, expert_bias, w_gate, w_up, w_down, shared_gate_w, shared_up_w, shared_down_w):
        import jax, jax.numpy as jnp
        import numpy as np
        B, S, D = (2, 128, 256)
        E, K, I = (16, 8, 256)
        I_SH = 256
        ROUTE_SCALE = 2.826
        gates = jnp.einsum('bsd,ed->bse', x, gate_w)
        scores = jax.nn.sigmoid(gates.astype(jnp.float32))
        sel_scores = scores + expert_bias
        _, inds = jax.lax.top_k(sel_scores, K)
        selected = jnp.take_along_axis(scores, inds, axis=-1)
        selected = selected / selected.sum(axis=-1, keepdims=True)
        selected = selected * ROUTE_SCALE
        onehot = jax.nn.one_hot(inds, E, dtype=selected.dtype)
        combine = jnp.einsum('bske,bsk->bse', onehot, selected)
        hg = jnp.einsum('bsd,eid->bsei', x, w_gate)
        hu = jnp.einsum('bsd,eid->bsei', x, w_up)
        h = jax.nn.silu(hg) * hu
        ye = jnp.einsum('bsei,edi->bsed', h, w_down)
        y = jnp.einsum('bsed,bse->bsd', ye, combine).astype(x.dtype)
        g = jnp.einsum('bsd,id->bsi', x, shared_gate_w)
        u = jnp.einsum('bsd,id->bsi', x, shared_up_w)
        y = y + jnp.einsum('bsi,di->bsd', jax.nn.silu(g) * u, shared_down_w)
        return y

    def _L3_xattn_ref(x1, x2, Wq, bq, Wk, bk, Wv, bv):
        import jax, jax.numpy as jnp
        import numpy as np
        B, SQ, SK, D, H = (4, 512, 512, 256, 16)
        SCALE = (D / H) ** 0.5
        q = x1 @ Wq.T + bq
        k = x2 @ Wk.T + bk
        v = x2 @ Wv.T + bv
        qk = jnp.einsum('bqd,bkd->bqk', q, k) * SCALE
        attn = jax.nn.softmax(qk, axis=-1)
        return jnp.einsum('bqk,bkd->bqd', attn, v)

    def _L3_attn_ref(x, W_attn, b_attn, W_proj, b_proj, rel_emb):
        import math
        import jax, jax.numpy as jnp
        import numpy as np
        N_EMBD = 256
        N_HEAD = 16
        NUM_BUCKETS = 32
        MAX_DISTANCE = 128

        def _relative_position_bucket(relative_position, num_buckets=NUM_BUCKETS, max_distance=MAX_DISTANCE):
            rp = -jnp.minimum(relative_position, 0)
            max_exact = num_buckets // 2
            is_small = rp < max_exact
            rp_large = max_exact + (jnp.log(rp.astype(jnp.float32) / max_exact + 1e-10) / math.log(max_distance / max_exact) * (num_buckets - max_exact)).astype(jnp.int32)
            rp_large = jnp.minimum(rp_large, num_buckets - 1)
            return jnp.where(is_small, rp, rp_large)
        B, T, C = x.shape
        H = N_HEAD
        D = C // H
        qkv = x @ W_attn.T + b_attn
        q, k, v = jnp.split(qkv, 3, axis=-1)
        q = q.reshape(B, T, H, D).transpose(0, 2, 1, 3)
        k = k.reshape(B, T, H, D).transpose(0, 2, 1, 3)
        v = v.reshape(B, T, H, D).transpose(0, 2, 1, 3)
        pos = jnp.arange(T)
        rel_pos = pos[None, :] - pos[:, None]
        buckets = _relative_position_bucket(rel_pos)
        rel_bias = rel_emb[buckets]
        rel_bias = rel_bias.transpose(2, 0, 1)[None]
        att = jnp.einsum('bhqd,bhkd->bhqk', q, k) * (1.0 / math.sqrt(D))
        att = att + rel_bias
        causal = jnp.tril(jnp.ones((T, T), dtype=bool))
        att = jnp.where(causal[None, None], att, -jnp.inf)
        att = jax.nn.softmax(att, axis=-1)
        y = jnp.einsum('bhqk,bhkd->bhqd', att, v)
        y = y.transpose(0, 2, 1, 3).reshape(B, T, C)
        y = y @ W_proj.T + b_proj
        return y

    def _L3_ffn_ref(x, weight_q, weight_scale, bias):
        import jax, jax.numpy as jnp
        import numpy as np
        B, S, IN, OUT = (4, 2048, 256, 256)
        EPS = 1e-06

        def _xla_quantized_matmul(x2d, weight_q, weight_scale):
            amax = jnp.max(jnp.abs(x2d), axis=-1, keepdims=True)
            x_scale = jnp.maximum(amax, EPS) / 127.0
            x_q = jnp.clip(jnp.round(x2d / x_scale), -128, 127).astype(jnp.int8)
            acc = jax.lax.dot_general(x_q, weight_q, (((1,), (1,)), ((), ())), preferred_element_type=jnp.int32)
            return acc.astype(jnp.float32) * x_scale * weight_scale[None, :]
        orig_shape = x.shape
        x2d = x.reshape(-1, orig_shape[-1])
        out = _xla_quantized_matmul(x2d, weight_q, weight_scale)
        out = out.reshape(*orig_shape[:-1], out.shape[-1])
        out = out + bias
        return out
    x = x + _L0_xattn_ref(_layernorm(x, axis=-1), ctx_1024, ctx_1024, L0_xattn_w_q, L0_xattn_w_k, L0_xattn_w_v, L0_xattn_w_o)
    x = x + _L0_attn_ref(_layernorm(x, axis=-1), L0_attn_Wq, L0_attn_bq, L0_attn_Wk, L0_attn_bk, L0_attn_Wv, L0_attn_bv, L0_attn_Wo, L0_attn_bo, L0_attn_W1, L0_attn_b1, L0_attn_W2, L0_attn_b2, L0_attn_ln1_s, L0_attn_ln1_b, L0_attn_ln2_s, L0_attn_ln2_b, L0_attn_lnf_s, L0_attn_lnf_b)
    x = x + _L0_ffn_ref(_layernorm(x, axis=-1), L0_ffn_gate_w, L0_ffn_W1, L0_ffn_b1, L0_ffn_W2, L0_ffn_b2)
    x = x + _L1_xattn_ref(_layernorm(x, axis=-1), ctx_1024, L1_xattn_Wq, L1_xattn_Wk, L1_xattn_Wv, L1_xattn_gru_wih, L1_xattn_gru_whh, L1_xattn_gru_bih, L1_xattn_gru_bhh, L1_xattn_slot_norm_w, L1_xattn_input_norm_w)
    x = x + _L1_attn_ref(_layernorm(x, axis=-1), L1_attn_w_qkv, L1_attn_b_qkv, L1_attn_w_o, L1_attn_b_o)
    x = x + _L1_ffn_ref(_layernorm(x, axis=-1), L1_ffn_integration_weight, L1_ffn_mu, L1_ffn_router_w1, L1_ffn_router_b1, L1_ffn_router_w2, L1_ffn_router_b2, L1_ffn_halt_w1, L1_ffn_halt_b1, L1_ffn_halt_w2, L1_ffn_halt_b2, L1_ffn_expert_w1, L1_ffn_expert_b1, L1_ffn_expert_w2, L1_ffn_expert_b2, L1_ffn_shared_w1, L1_ffn_shared_b1, L1_ffn_shared_w2, L1_ffn_shared_b2, L1_ffn_shared_weight, L1_ffn_refine_w1, L1_ffn_refine_b1, L1_ffn_refine_w2, L1_ffn_refine_b2)
    x = x + _L2_xattn_ref(_layernorm(x, axis=-1), ctx_1024, mask_BxSxS2_bk0, L2_xattn_Wq, L2_xattn_Wkv, L2_xattn_Wo, L2_xattn_nbias)
    x = x + _L2_attn_ref(_layernorm(x, axis=-1), L2_attn_Wq, L2_attn_bq, L2_attn_Wk, L2_attn_bk, L2_attn_Wv, L2_attn_bv, L2_attn_Wo, L2_attn_bo, L2_attn_projection)
    x = x + _L2_ffn_ref(_layernorm(x, axis=-1), L2_ffn_gate_w, L2_ffn_expert_bias, L2_ffn_w_gate, L2_ffn_w_up, L2_ffn_w_down, L2_ffn_shared_gate_w, L2_ffn_shared_up_w, L2_ffn_shared_down_w)
    x = x + _L3_xattn_ref(_layernorm(x, axis=-1), ctx_1024, L3_xattn_Wq, L3_xattn_bq, L3_xattn_Wk, L3_xattn_bk, L3_xattn_Wv, L3_xattn_bv)
    x = x + _L3_attn_ref(_layernorm(x, axis=-1), L3_attn_W_attn, L3_attn_b_attn, L3_attn_W_proj, L3_attn_b_proj, L3_attn_rel_emb)
    x = x + _L3_ffn_ref(_layernorm(x, axis=-1), L3_ffn_weight_q, L3_ffn_weight_scale, L3_ffn_bias)
    return x

_drawn_inputs = setup_inputs


def setup_inputs(seed=0):
    import zlib

    import numpy as np

    out = dict(_drawn_inputs(seed))
    spreads = {'L0_attn_bq': (0.0, 2.0),
     'L0_attn_bk': (0.0, 2.0),
     'L0_attn_bv': (0.0, 0.8),
     'L0_attn_bo': (0.0, 0.711),
     'L0_attn_b1': (0.0, 0.8),
     'L0_attn_b2': (0.0, 0.672),
     'L0_attn_ln1_s': (1.0, 0.6),
     'L0_attn_ln1_b': (0.0, 0.8),
     'L0_attn_ln2_s': (1.0, 0.6),
     'L0_attn_ln2_b': (0.0, 0.8),
     'L0_attn_lnf_s': (1.0, 0.2),
     'L0_attn_lnf_b': (0.0, 0.1),
     'L1_xattn_gru_bih': (0.0, 0.1),
     'L1_xattn_gru_bhh': (0.0, 0.314),
     'L1_xattn_slot_norm_w': (1.0, 0.6),
     'L1_xattn_input_norm_w': (1.0, 0.2),
     'L1_ffn_integration_weight': (0.5, 0.6),
     'L1_ffn_mu': (0.0, 0.8),
     'L1_ffn_router_b1': (0.0, 2.0),
     'L1_ffn_router_b2': (0.0, 2.0),
     'L1_ffn_halt_b1': (0.0, 0.8),
     'L1_ffn_expert_b1': (0.0, 0.8),
     'L1_ffn_expert_b2': (0.0, 2.0),
     'L1_ffn_shared_b1': (0.0, 0.8),
     'L1_ffn_shared_b2': (0.0, 0.8),
     'L1_ffn_refine_b1': (0.0, 0.8),
     'L1_ffn_refine_b2': (0.0, 0.463),
     'L2_attn_bq': (0.0, 2.0),
     'L2_attn_bk': (0.0, 2.0),
     'L2_attn_bv': (0.0, 0.1),
     'L2_attn_bo': (0.0, 0.282),
     'L2_ffn_expert_bias': (0.0, 0.8),
     'L3_attn_b_attn': (0.0, 1.259),
     'L3_attn_b_proj': (0.0, 1.211)}
    factors = {'L0_xattn_w_q': 8.0,
     'L0_xattn_w_k': 8.0,
     'L0_attn_Wq': 8.0,
     'L0_attn_Wk': 8.0,
     'L0_attn_Wv': 8.0,
     'L0_attn_Wo': 8.0,
     'L0_attn_W1': 4.953,
     'L0_attn_W2': 4.032,
     'L1_attn_b_qkv': 5.016,
     'L1_attn_b_o': 5.743,
     'L1_ffn_router_w1': 8.0,
     'L1_ffn_router_w2': 8.0,
     'L1_ffn_halt_w1': 8.0,
     'L1_ffn_halt_w2': 8.0,
     'L1_ffn_expert_w1': 8.0,
     'L1_ffn_expert_w2': 8.0,
     'L1_ffn_shared_w1': 8.0,
     'L1_ffn_shared_w2': 8.0,
     'L1_ffn_refine_w1': 4.633,
     'L1_ffn_refine_w2': 4.459,
     'L2_xattn_Wq': 4.377,
     'L2_xattn_Wkv': 2.869,
     'L2_xattn_Wo': 2.838,
     'L2_attn_Wq': 4.608,
     'L2_attn_Wk': 4.216,
     'L2_attn_projection': 5.757,
     'L2_ffn_gate_w': 8.0,
     'L2_ffn_w_gate': 7.819,
     'L2_ffn_w_up': 7.658,
     'L2_ffn_w_down': 7.71,
     'L2_ffn_shared_gate_w': 7.837,
     'L2_ffn_shared_up_w': 7.763,
     'L2_ffn_shared_down_w': 7.749,
     'L3_xattn_bk': 200.0,
     'L3_xattn_bv': 24.786,
     'L3_attn_rel_emb': 198.375,
     'L3_ffn_bias': 64.0,
     'L0_ffn_gate_w': 4.755,
     'L0_ffn_W1': 4.231,
     'L0_ffn_b1': 8.0,
     'L0_ffn_W2': 4.311,
     'L0_ffn_b2': 8.0,
     'L3_xattn_bq': 6.782}
    for name, (base, spread) in spreads.items():
        noise = np.random.default_rng([zlib.crc32(name.encode()), seed]).standard_normal(out[name].shape)
        drawn = base * np.exp(spread * noise) if base else spread * noise
        out[name] = jnp.asarray(drawn.astype(out[name].dtype))
    for name, factor in factors.items():
        out[name] = (out[name] * factor).astype(out[name].dtype)
    return out
```

```python
from contextlib import ExitStack, contextmanager

import numpy as np

import concourse.bass as bass
from concourse import mybir

F32 = mybir.dt.float32
BF16 = mybir.dt.bfloat16
U8 = mybir.dt.uint8
I8 = mybir.dt.int8
I32 = mybir.dt.int32
U32 = mybir.dt.uint32
ACT = mybir.ActivationFunctionType
ALU = mybir.AluOpType
AX = mybir.AxisListType.X

P = 128
B = 16
S = 64
D = 256
KT = D // P
T = B * S // P
N = B * S
NH = 512
H = 16
DH = D // H
HPT = P // DH
PAIRS = H // 2
SK = 1601
CT = -(-SK // P)
LAST = SK - (CT - 1) * P
CHUNKS = [(c, min(NH, SK - c)) for c in range(0, SK, NH)]


@contextmanager
def signals(nc, stage, names):
    held = [nc.alloc_semaphore(f"{stage}_{n}") for n in names.split()]
    yield held
    nc.clear_and_free_semaphores(held)
    nc.all_engine_barrier()


class Steps:

    def __init__(self, eng, sem):
        self.eng, self.sem, self.n = eng, sem, 0

    def done(self, ins):
        self.n += 1
        ins.then_inc(self.sem, 1)

    def wait(self):
        self.eng.wait_ge(self.sem, self.n)


class Env:
    pass


def keys_of(k):
    return P if k < CT - 1 else LAST


def load_all(sp, loads, sem):
    for dst, src in loads:
        sp.dma_start(dst, src).then_inc(sem, 16)
    if loads:
        sp.wait_ge(sem, 16 * len(loads))


def wview(ap):
    return ap.rearrange("(k p) n -> p k n", p=P)


def layernorm(nc, env, stage, src, nat, dst_T, affine=None, early=(), loads=()):
    with signals(nc, stage, "loaded early own stats std rows turned act_out dve_out") as (
            loaded, affine_in, own, stats, std_ready, rows_ready, turned, act_out, dve_out):
        with nc.Block() as block:

            @block.sync
            def _(sp):
                load_all(sp, early, affine_in)
                load_all(sp, loads, loaded)

            @block.vector
            def _(dve):
                steps = Steps(dve, own)
                for t in range(T):
                    steps.done(nc.vector.bn_stats(env.bn[:, t, :], src[:, t, :]))
                steps.wait()
                for t in range(T):
                    nc.vector.bn_aggr(env.mv[:, t, :], env.bn[:, t, :]).then_inc(stats, 1)
                dve.wait_ge(std_ready, 1)
                steps.done(nc.vector.reciprocal(env.rstd[:, :], env.std[:, :]))
                steps.wait()
                for t in range(T):
                    nc.vector.tensor_scalar(nat[:, t, :], src[:, t, :], env.mv[:, t, 0:1],
                                            env.rstd[:, t:t + 1], ALU.subtract,
                                            ALU.mult).then_inc(rows_ready, 1)
                if early:
                    dve.wait_ge(affine_in, 16 * len(early))
                for half in range(2 if dst_T is not None else 0):
                    dve.wait_ge(turned, 2 * half + 2)
                    out, put = dst_T[:, 1, half * NH:(half + 1) * NH], env.ps[:, 2 * half + 1, :]
                    if affine is None:
                        nc.vector.tensor_copy(out, put).then_inc(dve_out, 1)
                    else:
                        nc.vector.tensor_scalar(out, put, affine[0][:, 1:2], affine[1][:, 1:2],
                                                ALU.mult, ALU.add).then_inc(dve_out, 1)

            @block.scalar
            def _(act):
                act.wait_ge(stats, T)
                nc.scalar.activation(env.std[:, :], env.mv[:, :, 1], ACT.Sqrt,
                                     bias=env.eps5[:, 0:1]).then_inc(std_ready, 1)
                if early:
                    act.wait_ge(affine_in, 16 * len(early))
                for half in range(2 if dst_T is not None else 0):
                    act.wait_ge(turned, 2 * half + 1)
                    out, put = dst_T[:, 0, half * NH:(half + 1) * NH], env.ps[:, 2 * half, :]
                    if affine is None:
                        nc.scalar.copy(out, put).then_inc(act_out, 1)
                    else:
                        nc.scalar.activation(out, put, ACT.Identity, scale=affine[0][:, 0:1],
                                             bias=affine[1][:, 0:1]).then_inc(act_out, 1)

            @block.tensor
            def _(pe):
                for half in range(2 if dst_T is not None else 0):
                    pe.wait_ge(rows_ready, 4 * half + 4)
                    for f in range(KT):
                        for t in range(4):
                            last = nc.tensor.transpose(
                                env.ps[:, 2 * half + f, t * P:(t + 1) * P],
                                nat[:, 4 * half + t, f * P:(f + 1) * P], env.ident)
                        last.then_inc(turned, 1)


def turn_rows(nc, env, stage, nat, dst_T, loads=()):
    with signals(nc, stage, "loaded turned act_out dve_out") as (loaded, turned, act_out, dve_out):
        with nc.Block() as block:

            @block.sync
            def _(sp):
                load_all(sp, loads, loaded)

            @block.tensor
            def _(pe):
                for half in range(2):
                    for f in range(KT):
                        for t in range(4):
                            last = nc.tensor.transpose(
                                env.ps[:, 2 * half + f, t * P:(t + 1) * P],
                                nat[:, 4 * half + t, f * P:(f + 1) * P], env.ident)
                        last.then_inc(turned, 1)

            @block.vector
            def _(dve):
                for half in range(2):
                    dve.wait_ge(turned, 2 * half + 2)
                    nc.vector.tensor_copy(dst_T[:, 1, half * NH:(half + 1) * NH],
                                          env.ps[:, 2 * half + 1, :]).then_inc(dve_out, 1)

            @block.scalar
            def _(act):
                for half in range(2):
                    act.wait_ge(turned, 2 * half + 1)
                    nc.scalar.copy(dst_T[:, 0, half * NH:(half + 1) * NH],
                                   env.ps[:, 2 * half, :]).then_inc(act_out, 1)


def add_turned(nc, env, stage, src_T, dst):
    with signals(nc, stage, "turned added") as (turned, added):
        with nc.Block() as block:

            @block.tensor
            def _(pe):
                for t in range(T):
                    for f in range(KT):
                        last = nc.tensor.transpose(env.ps[:, t, f * P:(f + 1) * P],
                                                   src_T[:, f, t * P:(t + 1) * P], env.ident)
                    last.then_inc(turned, 1)

            @block.vector
            def _(dve):
                for t in range(T):
                    dve.wait_ge(turned, t + 1)
                    nc.vector.tensor_tensor(dst[:, t, :], dst[:, t, :], env.ps[:, t, 0:D],
                                            ALU.add).then_inc(added, 1)


def linear_T(nc, env, stage, parts, loads=()):
    groups = []
    for in_T, w, out_T, bias, func in parts:
        n_out = w.shape[2]
        for m in range(-(-n_out // P)):
            rows = min(P, n_out - m * P)
            for c in range(2):
                groups.append((in_T, w, out_T, bias, func, m, rows, c))
    on_act = [func not in (None, "relu") or g % 2 == 0
              for g, (_, _, _, _, func, _, _, _) in enumerate(groups)]
    act_before = [sum(on_act[:g]) for g in range(len(groups) + 1)]
    dve_before = [g - a for g, a in enumerate(act_before)]
    with signals(nc, stage, "loaded product act_out dve_out") as (
            loaded, product, act_out, dve_out):
        with nc.Block() as block:

            @block.sync
            def _(sp):
                load_all(sp, loads, loaded)

            @block.tensor
            def _(pe):
                for g, (in_T, w, out_T, bias, func, m, rows, c) in enumerate(groups):
                    if g >= 8:
                        if on_act[g - 8]:
                            pe.wait_ge(act_out, act_before[g - 7])
                        else:
                            pe.wait_ge(dve_out, dve_before[g - 7])
                    kts = w.shape[1]
                    for k in range(kts):
                        last = nc.tensor.matmul(env.ps[0:rows, g % 8, :],
                                                w[:, k, m * P:m * P + rows],
                                                in_T[:, k, c * NH:(c + 1) * NH],
                                                start=(k == 0), stop=(k == kts - 1))
                    last.then_inc(product, 1)

            @block.scalar
            def _(act):
                for g, (in_T, w, out_T, bias, func, m, rows, c) in enumerate(groups):
                    if not on_act[g]:
                        continue
                    act.wait_ge(product, g + 1)
                    kind = {None: ACT.Identity, "relu": ACT.Relu, "gelu": ACT.Gelu}[func]
                    nc.scalar.activation(
                        out_T[0:rows, m, c * NH:(c + 1) * NH], env.ps[0:rows, g % 8, :], kind,
                        bias=bias[0:rows, m:m + 1] if bias is not None else env.zero[0:rows, 0:1],
                    ).then_inc(act_out, 1)

            @block.vector
            def _(dve):
                for g, (in_T, w, out_T, bias, func, m, rows, c) in enumerate(groups):
                    if on_act[g]:
                        continue
                    dve.wait_ge(product, g + 1)
                    out, put = out_T[0:rows, m, c * NH:(c + 1) * NH], env.ps[0:rows, g % 8, :]
                    if func == "relu":
                        ins = nc.vector.tensor_scalar(
                            out, put, bias[0:rows, m:m + 1] if bias is not None else 0.0, 0.0,
                            ALU.add, ALU.max)
                    elif bias is not None:
                        ins = nc.vector.tensor_scalar(out, put, bias[0:rows, m:m + 1], None, ALU.add)
                    else:
                        ins = nc.vector.tensor_copy(out, put)
                    ins.then_inc(dve_out, 1)


def linear_rows(nc, env, stage, in_T, parts, loads=()):
    groups = [(t, w, bias, dst) for w, bias, dst in parts for t in range(T)]
    with signals(nc, stage, "loaded product act_out dve_out") as (
            loaded, product, act_out, dve_out):
        with nc.Block() as block:

            @block.sync
            def _(sp):
                load_all(sp, loads, loaded)

            @block.tensor
            def _(pe):
                for g, (t, w, bias, dst) in enumerate(groups):
                    if g >= 8:
                        pe.wait_ge((act_out, dve_out)[g % 2], (g - 8) // 2 + 1)
                    kts = w.shape[1]
                    for k in range(kts):
                        last = nc.tensor.matmul(env.ps[:, g % 8, 0:D], in_T[:, k, t * P:(t + 1) * P],
                                                w[:, k, :], start=(k == 0),
                                                stop=(k == kts - 1 and bias is None))
                    if bias is not None:
                        last = nc.tensor.matmul(env.ps[:, g % 8, 0:D], env.ones[0:1, :], bias,
                                                start=False, stop=True)
                    last.then_inc(product, 1)

            def source(g, dst):
                put = env.ps[:, g % 8, 0:D]
                return put if len(dst.shape) == 2 else put.rearrange("p (a b) -> p a b",
                                                                     a=dst.shape[1])

            @block.scalar
            def _(act):
                for g in range(0, len(groups), 2):
                    dst = groups[g][3](groups[g][0])
                    act.wait_ge(product, g + 1)
                    nc.scalar.copy(dst, source(g, dst)).then_inc(act_out, 1)

            @block.vector
            def _(dve):
                for g in range(1, len(groups), 2):
                    dst = groups[g][3](groups[g][0])
                    dve.wait_ge(product, g + 1)
                    nc.vector.tensor_copy(dst, source(g, dst)).then_inc(dve_out, 1)


def project_add(nc, env, stage, act_T, w, bias_row, dst, loads=(), also=None, scale=None,
                weigh=None):
    kts = w.shape[1]
    with signals(nc, stage, "loaded own product added") as (loaded, own, product, added):
        with nc.Block() as block:

            @block.sync
            def _(sp):
                load_all(sp, loads, loaded)

            @block.tensor
            def _(pe):
                for t in range(T):
                    for k in range(kts):
                        last = nc.tensor.matmul(env.ps[:, t, 0:D], act_T[:, k, t * P:(t + 1) * P],
                                                w[:, k, :], start=(k == 0),
                                                stop=(k == kts - 1 and bias_row is None))
                    if bias_row is not None:
                        last = nc.tensor.matmul(env.ps[:, t, 0:D], env.ones[0:1, :], bias_row,
                                                start=False, stop=True)
                    last.then_inc(product, 1)

            @block.vector
            def _(dve):
                steps = Steps(dve, own)
                for t in range(T):
                    dve.wait_ge(product, t + 1)
                    if weigh is not None:
                        nc.vector.scalar_tensor_tensor(
                            out=dst[:, t, :], in0=env.ps[:, t, 0:D], scalar=weigh(t),
                            in1=dst[:, t, :], op0=ALU.mult, op1=ALU.add).then_inc(added, 1)
                        continue
                    put = env.ps[:, t, 0:D]
                    if scale is not None:
                        steps.done(nc.vector.tensor_tensor(env.rows[:, t, :], put, scale, ALU.mult))
                        steps.wait()
                        put = env.rows[:, t, :]
                    if also is not None:
                        steps.done(nc.vector.tensor_tensor(dst[:, t, :], dst[:, t, :],
                                                           also[:, t, :], ALU.add))
                        steps.wait()
                    nc.vector.tensor_tensor(dst[:, t, :], dst[:, t, :], put,
                                            ALU.add).then_inc(added, 1)


def context_heads(nc, env, stage, ctx, q_T, att_T, w_k, w_v, softmax, notmask=None, nb=None):
    with ExitStack() as mem:
        def sb(name, shape, dt=F32):
            return mem.enter_context(nc.sbuf_tensor(f"{stage}_{name}", shape, dt))

        RING = 3
        ctx_T = sb("ctx_T", [P, KT, SK])
        k_T = sb("k_T", [P, KT, SK])
        v_aug = sb("v_aug", [P, CT, PAIRS, 2 * DH + 1])
        q_own = sb("q_own", [P, KT, S])
        q_bd = sb("q_bd", [P, KT, HPT, S])
        shifted = sb("shifted", [P, RING, H, S])
        probs = sb("probs", [P, RING, H, S])
        o_nat = sb("o_nat", [P, PAIRS, 2 * DH])
        r_mask = sb("r_mask", [P, PAIRS, 2 * DH])
        den = sb("den", [P, PAIRS])
        if softmax:
            zero_min = sb("zero_min", [P, PAIRS, S])
            first = sb("first", [P, PAIRS, S])
            top = sb("top", [P, 3, PAIRS])
            diag = sb("diag", [P, PAIRS, P])
            top_bc = sb("top_bc", [P, H, S])
            zeros = sb("zeros", [S, H, S])
        else:
            mask_in4 = sb("mask_in4", [P, CT, S // 4], I32)
            mask_u8 = mask_in4[:, :, :].bitcast(U8)
            cap = sb("cap", [P, CT, S])
        ps = env.ps

        with signals(nc, stage + "_pre", "loaded ones") as (loaded, ones_set):
            with nc.Block() as block:

                @block.sync
                def _(sp):
                    sp.dma_start(ctx_T[:, :, :], ctx[0].rearrange("(k p) n -> p k n", p=P)
                                 ).then_inc(loaded, 16)
                    sp.wait_ge(loaded, 16)

                @block.vector
                def _(dve):
                    nc.vector.memset(v_aug[:, :, :, 2 * DH:2 * DH + 1], 1.0).then_inc(ones_set, 1)

        with nc.Fori(0, B) as b:
            with signals(nc, stage, "next_ctx mask_in own q_in q_ready k_product k_out v_product v_out "
                         "n_product n_taken diag_ready bc_product bc_ready t_product t_taken "
                         "p_ready kept pv_done o_ready o_turned o_out cap_ready") as (
                    next_ctx, mask_in, own, q_in, q_ready, k_product, k_out, v_product, v_out,
                    n_product, n_taken, diag_ready, bc_product, bc_ready, t_product, t_taken,
                    p_ready, kept, pv_done, o_ready, o_turned, o_out, cap_ready):
                with nc.Block() as block:

                    @block.sync
                    def _(sp):
                        if not softmax:
                            sp.dma_start(mask_in4[:, 0:CT - 1, :],
                                         notmask[b, 0:(CT - 1) * P, :].rearrange(
                                             "(t p) s -> p t s", p=P)).then_inc(mask_in, 16)
                            sp.dma_start(mask_in4[0:LAST, CT - 1, :],
                                         notmask[b, (CT - 1) * P:SK, :]).then_inc(mask_in, 16)
                        sp.wait_ge(k_product, 8)
                        sp.wait_ge(v_product, CT)
                        sp.dma_start(ctx_T[:, :, :], ctx[(b + 1) % B].rearrange(
                            "(k p) n -> p k n", p=P)).then_inc(next_ctx, 16)
                        sp.wait_ge(next_ctx, 16)

                    @block.tensor
                    def _(pe):
                        for m in range(KT):
                            for c, (at, n) in enumerate(CHUNKS):
                                for k in range(KT):
                                    last = nc.tensor.matmul(
                                        ps[:, 4 * m + c, 0:n], w_k[:, k, m * P:(m + 1) * P],
                                        ctx_T[:, k, at:at + n], start=(k == 0), stop=(k == KT - 1))
                                last.then_inc(k_product, 1)
                        for t in range(CT):
                            if t < 8:
                                pe.wait_ge(k_out, t + 1)
                            else:
                                pe.wait_ge(v_out, t - 7)
                            n = keys_of(t)
                            for k in range(KT):
                                last = nc.tensor.matmul(ps[0:n, t % 8, 0:D],
                                                        ctx_T[:, k, t * P:t * P + n],
                                                        w_v[:, k, :], start=(k == 0),
                                                        stop=(k == KT - 1))
                            last.then_inc(v_product, 1)
                        pe.wait_ge(q_ready, KT)
                        pe.wait_ge(v_out, CT)
                        if softmax:
                            for j in range(PAIRS):
                                if j >= 2:
                                    pe.wait_ge(n_taken, j - 1)
                                lhs = q_bd[:, j // 4, 2 * (j % 4):2 * (j % 4) + 2, :]
                                for c, (at, n) in enumerate(CHUNKS):
                                    last = nc.tensor.matmul(ps[:, 4 * (j % 2) + c, 0:n], lhs,
                                                            k_T[:, j // 4, at:at + n],
                                                            start=True, stop=True)
                                last.then_inc(n_product, 1)
                            pe.wait_ge(n_taken, PAIRS)
                            pe.wait_ge(diag_ready, PAIRS)
                            for half in range(2):
                                nc.tensor.matmul(ps[:, half, :], env.ones,
                                                 diag[:, 4 * half:4 * half + 4, :],
                                                 start=True, stop=True).then_inc(bc_product, 1)
                            pe.wait_ge(bc_ready, 2)

                        def scores(t):
                            if t >= 3:
                                pe.wait_ge(t_taken, 2 * (t - 2))
                            n = keys_of(t)
                            for half in range(2):
                                last = nc.tensor.matmul(ps[0:n, 2 * (t % 3) + half, :],
                                                        k_T[:, half, t * P:t * P + n],
                                                        q_bd[:, half, :, :], start=True, stop=True)
                            last.then_inc(t_product, 1)

                        def values(t):
                            pe.wait_ge(p_ready, 2 * t + 2)
                            if t == 0 and softmax:
                                pe.wait_ge(kept, 2)
                            n = keys_of(t)
                            for j in range(PAIRS):
                                last = nc.tensor.matmul(
                                    ps[:, 6, (2 * DH + 1) * j:(2 * DH + 1) * (j + 1)],
                                    probs[0:n, t % RING, 2 * j:2 * j + 2, :],
                                    v_aug[0:n, t, j, :], start=(t == 0 and j == 0),
                                    stop=(t == CT - 1), skip_group_check=True)
                            last.then_inc(pv_done, 1)

                        for t in range(CT + 1):
                            if t < CT:
                                scores(t)
                            if t >= 1:
                                values(t - 1)
                        pe.wait_ge(o_ready, 1)
                        for f in range(KT):
                            last = nc.tensor.matmul(ps[:, 7, f * S:(f + 1) * S],
                                                    o_nat[:, 4 * f:4 * f + 4, :], env.fold,
                                                    start=True, stop=True)
                        last.then_inc(o_turned, 1)

                    @block.scalar
                    def _(act):
                        for m in range(KT):
                            for c, (at, n) in enumerate(CHUNKS):
                                act.wait_ge(k_product, 4 * m + c + 1)
                                nc.scalar.copy(k_T[:, m, at:at + n],
                                               ps[:, 4 * m + c, 0:n]).then_inc(k_out, 1)
                        if softmax:
                            for half in range(2):
                                act.wait_ge(bc_product, half + 1)
                                nc.scalar.copy(top_bc[:, 8 * half:8 * half + 8, :].rearrange(
                                    "p h s -> p (h s)"), ps[:, half, :]).then_inc(bc_ready, 1)
                        for t in range(CT):
                            n = keys_of(t)
                            if t >= RING:
                                act.wait_ge(pv_done, t - RING + 1)
                            for half in range(2):
                                act.wait_ge(t_taken, 2 * t + half + 1)
                                hs = slice(8 * half, 8 * half + 8)
                                if softmax:
                                    ins = nc.scalar.activation(probs[0:n, t % RING, hs, :],
                                                               shifted[0:n, t % RING, hs, :],
                                                               ACT.Exp, scale=DH ** -0.5)
                                else:
                                    ins = nc.scalar.activation(probs[0:n, t % RING, hs, :],
                                                               shifted[0:n, t % RING, hs, :],
                                                               ACT.Square, scale=DH ** -0.5,
                                                               bias=nb[0:n, 0:1])
                                ins.then_inc(p_ready, 1)
                        act.wait_ge(o_turned, 1)
                        nc.scalar.copy(att_T[:, :, bass.ds(b * S, S)],
                                       ps[:, 7, 0:KT * S].rearrange("p (k s) -> p k s", k=KT)
                                       ).then_inc(o_out, 1)

                    @block.vector
                    def _(dve):
                        steps = Steps(dve, own)
                        nc.vector.tensor_copy(q_own[:, :, :],
                                              q_T[:, :, bass.ds(b * S, S)]).then_inc(q_in, 1)
                        dve.wait_ge(q_in, 1)
                        for half in range(2):
                            nc.vector.tensor_tensor(
                                q_bd[:, half, :, :],
                                q_own[:, half, :].unsqueeze(1).broadcast_to([P, HPT, S]),
                                env.head_of.unsqueeze(2).broadcast_to([P, HPT, S]),
                                ALU.mult).then_inc(q_ready, 1)
                        if not softmax:
                            dve.wait_ge(mask_in, 32)
                            for rows, ts in ((P, slice(0, CT - 1)), (LAST, slice(CT - 1, CT))):
                                steps.done(nc.vector.tensor_scalar(
                                    cap[0:rows, ts, :], mask_u8[0:rows, ts, :], -3e38, 3e38,
                                    ALU.mult, ALU.add))
                                steps.wait()
                                steps.done(nc.vector.tensor_scalar(
                                    cap[0:rows, ts, :], cap[0:rows, ts, :], nb[0:rows, 1:2], None,
                                    ALU.add))
                            steps.wait()
                        for t in range(CT):
                            dve.wait_ge(v_product, t + 1)
                            n = keys_of(t)
                            nc.vector.tensor_copy(
                                v_aug[0:n, t, :, 0:2 * DH],
                                ps[0:n, t % 8, 0:D].rearrange("p (j d) -> p j d", j=PAIRS)
                            ).then_inc(v_out, 1)
                        if softmax:
                            for j in range(PAIRS):
                                dve.wait_ge(n_product, j + 1)
                                bank = ps[:, 4 * (j % 2):4 * (j % 2) + 4, :].rearrange(
                                    "p c n -> p (c n)")
                                steps.done(nc.vector.scalar_tensor_tensor(
                                    out=zero_min[:, j, :], in0=bank[:, 0:S], scalar=0.0,
                                    in1=env.tril_min, op0=ALU.is_equal, op1=ALU.mult))
                                steps.done(nc.vector.tensor_reduce(
                                    top[:, 1, j:j + 1], bank[:, S:SK], AX, ALU.max))
                                steps.wait()
                                nc.vector.tensor_tensor(first[:, j, :], zero_min[:, j, :],
                                                        bank[:, 0:S], ALU.add).then_inc(n_taken, 1)
                            dve.wait_ge(n_taken, PAIRS)
                            steps.done(nc.vector.tensor_reduce(top[:, 0, :], first[:, :, :], AX,
                                                               ALU.max))
                            steps.wait()
                            steps.done(nc.vector.tensor_tensor(top[:, 2, :], top[:, 0, :],
                                                               top[:, 1, :], ALU.max))
                            steps.wait()
                            for j in range(PAIRS):
                                nc.vector.tensor_scalar(diag[:, j, :], env.ident,
                                                        top[:, 2, j:j + 1], None,
                                                        ALU.mult).then_inc(diag_ready, 1)
                            dve.wait_ge(bc_ready, 2)
                        for t in range(CT):
                            n = keys_of(t)
                            dve.wait_ge(t_product, t + 1)
                            if t >= RING:
                                dve.wait_ge(p_ready, 2 * (t - RING) + 2)
                            for half in range(2):
                                put = ps[0:n, 2 * (t % 3) + half, :].rearrange(
                                    "p (h s) -> p h s", h=HPT)
                                hs = slice(8 * half, 8 * half + 8)
                                if softmax:
                                    if t == 0:
                                        steps.done(nc.vector.scalar_tensor_tensor(
                                            out=zeros[:, hs, :], in0=put[0:S], scalar=0.0,
                                            in1=env.key_le_q[0:S, :].unsqueeze(1).broadcast_to(
                                                [S, HPT, S]), op0=ALU.is_equal, op1=ALU.mult))
                                    ins = nc.vector.tensor_tensor(
                                        shifted[0:n, t % RING, hs, :], put, top_bc[0:n, hs, :],
                                        ALU.subtract)
                                else:
                                    ins = nc.vector.scalar_tensor_tensor(
                                        out=shifted[0:n, t % RING, hs, :], in0=put,
                                        scalar=nb[0:n, 1:2],
                                        in1=cap[0:n, t, :].unsqueeze(1).broadcast_to([n, HPT, S]),
                                        op0=ALU.max, op1=ALU.min)
                                ins.then_inc(t_taken, 1)
                            if t == 1 and softmax:
                                dve.wait_ge(p_ready, 2)
                                steps.wait()
                                for half in range(2):
                                    hs = slice(8 * half, 8 * half + 8)
                                    nc.vector.scalar_tensor_tensor(
                                        out=probs[0:S, 0, hs, :], in0=zeros[:, hs, :],
                                        scalar=0.0, in1=probs[0:S, 0, hs, :],
                                        op0=ALU.is_equal, op1=ALU.mult).then_inc(kept, 1)
                        dve.wait_ge(pv_done, CT)
                        o_ps = ps[:, 6, 0:(2 * DH + 1) * PAIRS].rearrange("p (j d) -> p j d",
                                                                          j=PAIRS)
                        if not softmax:
                            steps.done(nc.vector.tensor_scalar(
                                den[:, :], o_ps[:, :, 2 * DH], 1e-32, None, ALU.add))
                        else:
                            steps.done(nc.vector.tensor_copy(den[:, :], o_ps[:, :, 2 * DH]))
                        steps.wait()
                        steps.done(nc.vector.reciprocal(den[:, :], den[:, :]))
                        steps.wait()
                        steps.done(nc.vector.tensor_tensor(
                            r_mask[:, :, :], env.own_head.unsqueeze(1).broadcast_to([P, PAIRS, 32]),
                            den[:, :].unsqueeze(2).broadcast_to([P, PAIRS, 32]), ALU.mult))
                        steps.wait()
                        nc.vector.tensor_tensor(o_nat[:, :, :], o_ps[:, :, 0:2 * DH],
                                                r_mask[:, :, :], ALU.mult).then_inc(o_ready, 1)


def scoped(nc, name):
    mem = ExitStack()

    def sb(n, shape, dt=F32):
        return mem.enter_context(nc.sbuf_tensor(f"{name}_{n}", shape, dt))

    return mem, sb


def l0_xattn(nc, env, d):
    mem, sb = scoped(nc, "x0")
    with mem:
        wq, wk, wv, wo = (sb(n, [P, KT, D]) for n in ("wq", "wk", "wv", "wo"))
        q_T, att_T = sb("q_T", [P, KT, N]), sb("att_T", [P, KT, N])
        layernorm(nc, env, "x0_ln", env.x, env.h, env.h_T, loads=[
            (wq[:, :, :], wview(d["L0_xattn_w_q"])), (wk[:, :, :], wview(d["L0_xattn_w_k"])),
            (wv[:, :, :], wview(d["L0_xattn_w_v"])), (wo[:, :, :], wview(d["L0_xattn_w_o"]))])
        linear_T(nc, env, "x0_q", [(env.h_T, wq, q_T, None, None)])
        context_heads(nc, env, "x0", d["ctx_T"], q_T, att_T, wk, wv, softmax=True)
        project_add(nc, env, "x0_o", att_T, wo, None, env.x)


def l0_attn(nc, env, d):
    mem, sb = scoped(nc, "e0")
    FF = 4 * D
    with mem:
        y = sb("y", [P, T, D])
        wq, wk, wv, wo = (sb(n, [P, KT, D]) for n in ("wq", "wk", "wv", "wo"))
        w1, w2 = sb("w1", [P, KT, FF]), sb("w2", [P, FF // P, D])
        ln1, ln2 = sb("ln1", [P, 2, KT]), sb("ln2", [P, 2, KT])
        bq, b1 = sb("bq", [P, KT]), sb("b1", [P, FF // P])
        rows_b = sb("rows_b", [1, 4, D])
        pos, lnf = sb("pos", [P, D]), sb("lnf", [P, 2, D])
        q_T, num_T, den_T = sb("q_T", [P, KT, N]), sb("num_T", [P, KT, N]), sb("den_T", [P, KT, N])
        k_nat, v_nat = sb("k_nat", [P, T, D]), sb("v_nat", [P, T, KT, P + 1])
        hid_T = sb("hid_T", [P, FF // P, N])
        kv_bd, ks_bd = sb("kv_bd", [P, KT, 2, P]), sb("ks_bd", [P, KT, 2, P])
        ksum = sb("ksum", [P, KT, 2])
        layernorm(nc, env, "e0_in", env.x, env.h, None, loads=[
            (pos[:, :], d["pos"]),
            (lnf[:, 0, :], d["L0_attn_lnf_s"].partition_broadcast(P)),
            (lnf[:, 1, :], d["L0_attn_lnf_b"].partition_broadcast(P))])
        with signals(nc, "e0_pos", "own set") as (own, y_set):
            with nc.Block() as block:

                @block.vector
                def _(dve):
                    for t in range(T):
                        nc.vector.scalar_tensor_tensor(
                            out=y[:, t, :], in0=env.h[:, t, :], scalar=float(D) ** 0.5,
                            in1=pos[:, :], op0=ALU.mult, op1=ALU.add).then_inc(y_set, 1)
                    nc.vector.memset(v_nat[:, :, :, P:P + 1], 1.0).then_inc(y_set, 1)

        with nc.Fori(0, 4) as i:
            layernorm(nc, env, "e0_ln1", y, env.h, env.h_T, affine=(ln1[:, 0, :], ln1[:, 1, :]),
                      early=[(ln1[:, 0, :], d["L0_attn_ln1_s"][i]),
                             (ln1[:, 1, :], d["L0_attn_ln1_b"][i])],
                      loads=[(wq[:, :, :], wview(d["L0_attn_Wq"][i])),
                             (wk[:, :, :], wview(d["L0_attn_Wk"][i])),
                             (wv[:, :, :], wview(d["L0_attn_Wv"][i])),
                             (wo[:, :, :], wview(d["L0_attn_Wo"][i])),
                             (bq[:, :], d["L0_attn_bq"][i]),
                             (rows_b[:, 0, :], d["L0_attn_bk"][i].unsqueeze(0)),
                             (rows_b[:, 1, :], d["L0_attn_bv"][i].unsqueeze(0)),
                             (rows_b[:, 2, :], d["L0_attn_bo"][i].unsqueeze(0)),
                             (rows_b[:, 3, :], d["L0_attn_b2"][i].unsqueeze(0))])
            linear_T(nc, env, "e0_q", [(env.h_T, wq, q_T, bq, None)],
                     loads=[(ln2[:, 0, :], d["L0_attn_ln2_s"][i]),
                            (ln2[:, 1, :], d["L0_attn_ln2_b"][i]),
                            (b1[:, :], d["L0_attn_b1"][i]),
                            (w1[:, :, :], wview(d["L0_attn_W1"][i])),
                            (w2[:, :, :], wview(d["L0_attn_W2"][i]))])
            linear_rows(nc, env, "e0_kv", env.h_T, [
                (wk, rows_b[:, 0, :], lambda t: k_nat[:, t, :]),
                (wv, rows_b[:, 1, :], lambda t: v_nat[:, t, :, 0:P])])
            with signals(nc, "e0_elu", "low exp high") as (low, exped, high):
                with nc.Block() as block:

                    @block.vector
                    def _(dve):
                        nc.vector.tensor_scalar(num_T[:, :, :], q_T[:, :, :], 0.0, None,
                                                ALU.min).then_inc(low, 1)
                        nc.vector.tensor_scalar(env.rows[:, :, :], k_nat[:, :, :], 0.0, None,
                                                ALU.min).then_inc(low, 1)
                        dve.wait_ge(exped, 1)
                        nc.vector.scalar_tensor_tensor(
                            out=q_T[:, :, :], in0=q_T[:, :, :], scalar=0.0, in1=num_T[:, :, :],
                            op0=ALU.max, op1=ALU.add).then_inc(high, 1)
                        dve.wait_ge(exped, 2)
                        nc.vector.scalar_tensor_tensor(
                            out=k_nat[:, :, :], in0=k_nat[:, :, :], scalar=0.0,
                            in1=env.rows[:, :, :], op0=ALU.max, op1=ALU.add).then_inc(high, 1)

                    @block.scalar
                    def _(act):
                        act.wait_ge(low, 1)
                        nc.scalar.activation(num_T[:, :, :], num_T[:, :, :],
                                             ACT.Exp).then_inc(exped, 1)
                        act.wait_ge(low, 2)
                        nc.scalar.activation(env.rows[:, :, :], env.rows[:, :, :],
                                             ACT.Exp).then_inc(exped, 1)

            with signals(nc, "e0_lin", "own kv_product sums masked out_product out_taken") as (
                    own, kv_product, sums, masked, out_product, out_taken):
                with nc.Block() as block:

                    @block.tensor
                    def _(pe):
                        def key_values(t):
                            if t >= 2:
                                pe.wait_ge(masked, 8 * (t - 1))
                            for g in range(4):
                                f, b = g // 2, g % 2
                                rows = slice(b * S, b * S + S)
                                last = nc.tensor.matmul(
                                    env.ps[:, 2 * (t % 2) + b, f * 256:f * 256 + P + 1],
                                    k_nat[rows, t, f * P:(f + 1) * P], v_nat[rows, t, f, :],
                                    start=True, stop=True)
                            last.then_inc(kv_product, 1)

                        def outputs(t):
                            pe.wait_ge(masked, 8 * (t + 1))
                            if t >= 2:
                                pe.wait_ge(out_taken, 2 * (t - 1))
                            for g in range(4):
                                f, b = g // 2, g % 2
                                cols = slice(t * P + b * S, t * P + b * S + S)
                                for kind, m in ((0, kv_bd), (1, ks_bd)):
                                    at = (2 * kind + f) * P + b * S
                                    last = nc.tensor.matmul(
                                        env.ps[:, 4 + t % 2, at:at + S], m[:, f, b, :],
                                        q_T[:, f, cols], start=True, stop=True)
                            last.then_inc(out_product, 1)

                        for t in range(T):
                            key_values(t)
                            outputs(t)

                    @block.vector
                    def _(dve):
                        steps = Steps(dve, own)
                        for t in range(T):
                            dve.wait_ge(kv_product, t + 1)
                            if t >= 1:
                                dve.wait_ge(out_product, t)
                            for b in range(2):
                                nc.vector.tensor_copy(
                                    ksum[:, :, b], env.ps[:, 2 * (t % 2) + b, :].rearrange(
                                        "p (f c) -> p f c", f=2)[:, :, P]).then_inc(sums, 1)
                            for f in range(KT):
                                for b in range(2):
                                    nc.vector.tensor_tensor(
                                        kv_bd[:, f, b, :],
                                        env.ps[:, 2 * (t % 2) + b, f * 256:f * 256 + P],
                                        env.same_head, ALU.mult).then_inc(masked, 1)
                            dve.wait_ge(sums, 2 * t + 2)
                            for f in range(KT):
                                for b in range(2):
                                    nc.vector.tensor_scalar(
                                        ks_bd[:, f, b, :], env.same_head, ksum[:, f, b:b + 1],
                                        None, ALU.mult).then_inc(masked, 1)
                        dve.wait_ge(out_taken, 2 * T)
                        steps.done(nc.vector.tensor_scalar(den_T[:, :, :], den_T[:, :, :], 1e-6,
                                                           None, ALU.add))
                        steps.wait()
                        steps.done(nc.vector.reciprocal(den_T[:, :, :], den_T[:, :, :]))
                        steps.wait()
                        steps.done(nc.vector.tensor_tensor(num_T[:, :, :], num_T[:, :, :],
                                                           den_T[:, :, :], ALU.mult))

                    @block.scalar
                    def _(act):
                        for t in range(T):
                            act.wait_ge(out_product, t + 1)
                            for kind, dst in ((0, num_T), (1, den_T)):
                                nc.scalar.copy(
                                    dst[:, :, t * P:(t + 1) * P],
                                    env.ps[:, 4 + t % 2, 2 * kind * P:(2 * kind + 2) * P].rearrange(
                                        "p (f c) -> p f c", f=2)).then_inc(out_taken, 1)

            project_add(nc, env, "e0_o", num_T, wo, rows_b[:, 2, :], y)
            layernorm(nc, env, "e0_ln2", y, env.h, env.h_T, affine=(ln2[:, 0, :], ln2[:, 1, :]))
            linear_T(nc, env, "e0_up", [(env.h_T, w1, hid_T, b1, "relu")])
            project_add(nc, env, "e0_down", hid_T, w2, rows_b[:, 3, :], y)

        layernorm(nc, env, "e0_lnf", y, env.h, None)
        with signals(nc, "e0_add", "scaled moved added") as (scaled, moved, added):
            with nc.Block() as block:

                @block.vector
                def _(dve):
                    for t in range(T):
                        nc.vector.tensor_tensor(env.h[:, t, :], env.h[:, t, :], lnf[:, 0, :],
                                                ALU.mult).then_inc(scaled, 1)
                    for t in range(T):
                        dve.wait_ge(scaled, t + 1)
                        nc.vector.tensor_tensor(env.h[:, t, :], env.h[:, t, :], lnf[:, 1, :],
                                                ALU.add).then_inc(moved, 1)
                    for t in range(T):
                        dve.wait_ge(moved, t + 1)
                        nc.vector.tensor_tensor(env.x[:, t, :], env.x[:, t, :], env.h[:, t, :],
                                                ALU.add).then_inc(added, 1)


def top2(nc, env, dve, probs, experts, weights, chosen, m8, i8, i_f, steps):
    for t in range(T):
        steps.done(nc.vector.max(m8[:, t, :], probs[:, t, :]))
    steps.wait()
    for t in range(T):
        steps.done(nc.vector.max_index(i8[:, t, :], m8[:, t, :], probs[:, t, :]))
    steps.done(nc.vector.tensor_copy(weights, m8[:, :, 0:2]))
    steps.wait()
    steps.done(nc.vector.tensor_copy(i_f[:, :, :], i8[:, :, 0:2]))
    steps.wait()
    for k in range(2):
        steps.done(nc.vector.tensor_tensor(
            chosen[:, :, k, :], env.iota8.unsqueeze(1).broadcast_to([P, T, experts]),
            i_f[:, :, k:k + 1].broadcast_to([P, T, experts]), ALU.is_equal))
    steps.wait()


def row_softmax(nc, dve, logits, top, total, n, exped, shifted, steps):
    steps.done(nc.vector.tensor_reduce(top, logits, AX, ALU.max))
    steps.wait()
    nc.vector.tensor_tensor(logits, logits, top.unsqueeze(2).broadcast_to([P, T, n]),
                            ALU.subtract).then_inc(shifted, 1)
    dve.wait_ge(exped, 1)
    steps.done(nc.vector.tensor_reduce(total, logits, AX, ALU.add))
    steps.wait()
    steps.done(nc.vector.reciprocal(total, total))
    steps.wait()
    steps.done(nc.vector.tensor_tensor(logits, logits, total.unsqueeze(2).broadcast_to([P, T, n]),
                                       ALU.mult))
    steps.wait()


def l0_ffn(nc, env, d):
    E = 8
    CAP = int(1.25 * N / E)
    mem, sb = scoped(nc, "f0")
    with mem:
        gate = sb("gate", [P, KT, E])
        w1, w2 = sb("w1", [P, 2, KT, D]), sb("w2", [P, 2, KT, D])
        b1, b2 = sb("b1", [P, E, KT]), sb("b2", [1, E, D])
        probs, comb = sb("probs", [P, T, E]), sb("comb", [P, T, E])
        chosen, weights = sb("chosen", [P, T, 2, E]), sb("weights", [P, T, 2])
        m8, i8, i_f = sb("m8", [P, T, 8]), sb("i8", [P, T, 8], U32), sb("i_f", [P, T, 2])
        top, total, keep = sb("top", [P, T]), sb("total", [P, T]), sb("keep", [P, E])
        both, tmp = sb("both", [P, T, E]), sb("tmp", [P, T, E])
        hid_T = sb("hid_T", [P, KT, N])
        layernorm(nc, env, "f0_ln", env.x, env.h, env.h_T, loads=[
            (gate[:, :, :], wview(d["L0_ffn_gate_w"])), (b1[:, :, :], d["L0_ffn_b1"]),
            (b2[:, :, :], d["L0_ffn_b2"].unsqueeze(0)),
            (w1[:, 0, :, :], wview(d["L0_ffn_W1"][0])), (w2[:, 0, :, :], wview(d["L0_ffn_W2"][0]))])
        with signals(nc, "f0_route", "logits own shifted exped picked counted") as (
                logits, own, shifted, exped, picked, counted):
            with nc.Block() as block:

                @block.tensor
                def _(pe):
                    for t in range(T):
                        for k in range(KT):
                            last = nc.tensor.matmul(env.ps[:, 0, t * E:(t + 1) * E],
                                                    env.h_T[:, k, t * P:(t + 1) * P],
                                                    gate[:, k, :], start=(k == 0),
                                                    stop=(k == KT - 1))
                    last.then_inc(logits, 1)
                    pe.wait_ge(picked, 1)
                    for t in range(T):
                        last = nc.tensor.matmul(env.ps[:, 1, 0:E], env.ones, both[:, t, :],
                                                start=(t == 0), stop=(t == T - 1))
                    last.then_inc(counted, 1)

                @block.scalar
                def _(act):
                    act.wait_ge(shifted, 1)
                    nc.scalar.activation(probs[:, :, :], probs[:, :, :], ACT.Exp).then_inc(exped, 1)

                @block.vector
                def _(dve):
                    steps = Steps(dve, own)
                    dve.wait_ge(logits, 1)
                    steps.done(nc.vector.tensor_copy(
                        probs[:, :, :], env.ps[:, 0, 0:T * E].rearrange("p (t e) -> p t e", t=T)))
                    steps.wait()
                    row_softmax(nc, dve, probs[:, :, :], top[:, :], total[:, :], E, exped, shifted,
                                steps)
                    top2(nc, env, dve, probs, E, weights[:, :, :], chosen, m8, i8, i_f, steps)
                    nc.vector.tensor_tensor(both[:, :, :], chosen[:, :, 0, :], chosen[:, :, 1, :],
                                            ALU.add).then_inc(picked, 1)
                    for k, dst in ((0, comb), (1, tmp)):
                        steps.done(nc.vector.tensor_tensor(
                            dst[:, :, :], chosen[:, :, k, :],
                            weights[:, :, k:k + 1].broadcast_to([P, T, E]), ALU.mult))
                    steps.wait()
                    steps.done(nc.vector.tensor_tensor(comb[:, :, :], comb[:, :, :], tmp[:, :, :],
                                                       ALU.add))
                    dve.wait_ge(counted, 1)
                    steps.done(nc.vector.tensor_scalar(keep[:, :], env.ps[:, 1, 0:E], float(CAP),
                                                       None, ALU.is_le))
                    steps.wait()
                    steps.done(nc.vector.tensor_tensor(
                        comb[:, :, :], comb[:, :, :],
                        keep[:, :].unsqueeze(1).broadcast_to([P, T, E]), ALU.mult))

        with nc.Fori(0, E // 2) as i:
            for r in range(2):
                e = 2 * i + r
                nxt = (e + 1) % E
                experts = [(w1[:, 1 - r, :, :], wview(d["L0_ffn_W1"][nxt])),
                           (w2[:, 1 - r, :, :], wview(d["L0_ffn_W2"][nxt]))]
                expert_bias = b1[:, bass.ds(e, 1), :].squeeze(1)
                linear_T(nc, env, f"f0_up{r}", [(env.h_T, w1[:, r], hid_T, expert_bias, "relu")],
                         loads=experts)
                project_add(nc, env, f"f0_down{r}", hid_T, w2[:, r],
                            b2[:, bass.ds(e, 1), :].squeeze(1), env.x,
                            weigh=lambda t, e=e: comb[:, t, bass.ds(e, 1)])


def l1_xattn(nc, env, d):
    G3 = 3 * KT
    PAD = CT * P
    mem, sb = scoped(nc, "s1")
    with mem:
        wq, wk, wv = (sb(n, [P, KT, D]) for n in ("wq", "wk", "wv"))
        wih, whh = sb("wih", [P, KT, 3 * D]), sb("whh", [P, KT, 3 * D])
        norm = sb("norm", [P, 2, KT])
        gb = sb("gb", [P, 2, G3])
        gb2 = sb("gb2", [P, 4])
        res_T = sb("res_T", [P, KT, N])
        ctx_T = [sb(f"ctx_T{r}", [P, 2, KT, PAD]) for r in range(2)]
        ctx_n = [sb(f"ctx_n{r}", [P, 2, CT, D]) for r in range(2)]
        ssq, rs_c = sb("ssq", [P, 2, CT]), sb("rs_c", [P, 2, CT])
        junk = sb("junk", [P, 2, D])
        sl = sb("sl", [P, KT, P])
        sq, sn, q1, q2, upd = (sb(n, [P, KT, P]) for n in ("sq", "sn", "q1", "q2", "upd"))
        std, rs = sb("std", [P, P]), sb("rs", [P, P])
        att = sb("att", [P, 2, CT, S])
        top, tot = sb("top", [P, 2, CT]), sb("tot", [P, 2, CT])
        rden = sb("rden", [P, 2, S])
        u_T = sb("u_T", [P, KT, 2, S])
        rz, n_T, hn = sb("rz", [P, 4, P]), sb("n_T", [P, KT, P]), sb("hn", [P, KT, P])
        ps = env.ps
        layernorm(nc, env, "s1_ln", env.x, env.h, env.h_T, loads=[
            (wq[:, :, :], wview(d["L1_xattn_Wq"])), (wk[:, :, :], wview(d["L1_xattn_Wk"])),
            (wv[:, :, :], wview(d["L1_xattn_Wv"])), (wih[:, :, :], wview(d["L1_xattn_gru_wih"])),
            (whh[:, :, :], wview(d["L1_xattn_gru_whh"])),
            (norm[:, 0, :], d["L1_xattn_slot_norm_w"]), (norm[:, 1, :], d["L1_xattn_input_norm_w"]),
            (gb[:, 0, :], d["L1_xattn_gru_bih"]), (gb[:, 1, :], d["L1_xattn_gru_bhh"])])

        def load_context(sp, r, pair, sem):
            for b in range(2):
                row = 2 * pair + b
                sp.dma_start(ctx_T[r][:, b, :, 0:SK],
                             d["ctx_T"][row].rearrange("(k p) n -> p k n", p=P)).then_inc(sem, 16)
                sp.dma_start(ctx_n[r][:, b, 0:CT - 1, :],
                             d["ctx"][row, 0:(CT - 1) * P, :].rearrange(
                                 "(t p) f -> p t f", p=P)).then_inc(sem, 16)
                sp.dma_start(ctx_n[r][0:LAST, b, CT - 1, :],
                             d["ctx"][row, (CT - 1) * P:SK, :]).then_inc(sem, 16)

        with signals(nc, "s1_pre", "cleared loaded own") as (cleared, loaded, own):
            with nc.Block() as block:

                @block.vector
                def _(dve):
                    for r in range(2):
                        nc.vector.memset(ctx_T[r][:, :, :, SK:PAD], 0.0).then_inc(cleared, 1)
                        nc.vector.memset(ctx_n[r][S:P, :, CT - 1, :], 0.0).then_inc(cleared, 1)
                    steps = Steps(dve, own)
                    steps.done(nc.vector.tensor_tensor(gb2[:, :], gb[:, 0, 0:4], gb[:, 1, 0:4],
                                                       ALU.add))
                    steps.wait()
                    steps.done(nc.vector.tensor_scalar(gb2[:, :], gb2[:, :], 0.5, None, ALU.mult))

                @block.sync
                def _(sp):
                    sp.wait_ge(cleared, 4)
                    load_context(sp, 0, 0, loaded)
                    sp.wait_ge(loaded, 6 * 16)

        def prepare(r, pair, loads):
            with signals(nc, f"s1_prep{r}", "squared std scaled taken own") as (
                    squared, std_ready, scaled, taken, own):
                with nc.Block() as block:

                    @block.sync
                    def _(sp):
                        loads(sp)

                    @block.scalar
                    def _(act):
                        for t in range(CT):
                            nc.scalar.activation(junk[:, 0, :], ctx_n[r][:, 0, t, :], ACT.Square,
                                                 accum_out=ssq[:, 0, t:t + 1]).then_inc(squared, 1)
                            act.wait_ge(squared, t + 1)
                        act.wait_ge(own, CT)
                        nc.scalar.activation(rs_c[:, :, :], ssq[:, :, :], ACT.Sqrt, scale=1.0 / D,
                                             bias=env.eps6[:, 0:1]).then_inc(std_ready, 1)

                    @block.vector
                    def _(dve):
                        steps = Steps(dve, own)
                        for t in range(CT):
                            steps.done(nc.vector.tensor_tensor_reduce(
                                junk[:, 1, :], ctx_n[r][:, 1, t, :], ctx_n[r][:, 1, t, :], 1.0, 0.0,
                                ALU.mult, ALU.add, ssq[:, 1, t:t + 1]))
                            steps.wait()
                        nc.vector.tensor_copy(sl[:, :, :], env.h_T[:, :, bass.ds(pair * P, P)]
                                              ).then_inc(taken, 1)
                        dve.wait_ge(std_ready, 1)
                        steps.done(nc.vector.reciprocal(rs_c[:, :, :], rs_c[:, :, :]))
                        steps.wait()
                        for b in range(2):
                            for t in range(CT):
                                nc.vector.tensor_scalar(ctx_n[r][:, b, t, :], ctx_n[r][:, b, t, :],
                                                        rs_c[:, b, t:t + 1], None,
                                                        ALU.mult).then_inc(scaled, 1)

        def attend(r):
            with signals(nc, f"s1_it{r}", "own squares ssq_done std normed q1_done q1_out q2_done "
                         "q2_out s_done shifted exped weights u_done u_ready upd_done upd_out "
                         "g_done rz_half n_in n_out") as (
                    own, squares, ssq_done, std_ready, normed, q1_done, q1_out, q2_done, q2_out,
                    s_done, shifted, exped, weights, u_done, u_ready, upd_done, upd_out, g_done,
                    rz_half, n_in, n_out):
                with nc.Block() as block:

                    @block.tensor
                    def _(pe):
                        def project(put, w, in_T, m):
                            for k in range(KT):
                                last = nc.tensor.matmul(put, w[:, k, m * P:(m + 1) * P],
                                                        in_T[:, k, :], start=(k == 0),
                                                        stop=(k == KT - 1))
                            return last

                        pe.wait_ge(squares, 1)
                        for k in range(KT):
                            last = nc.tensor.matmul(ps[:, 7, 0:P], env.ones, sq[:, k, :],
                                                    start=(k == 0), stop=(k == KT - 1))
                        last.then_inc(ssq_done, 1)
                        pe.wait_ge(normed, KT)
                        for m in range(KT):
                            last = project(ps[:, 6, m * P:(m + 1) * P], wq, sn, m)
                        last.then_inc(q1_done, 1)
                        pe.wait_ge(q1_out, 1)
                        for m in range(KT):
                            last = project(ps[:, 5, m * P:(m + 1) * P], wk, q1, m)
                        last.then_inc(q2_done, 1)
                        pe.wait_ge(q2_out, KT)
                        for b in range(2):
                            for t in range(CT):
                                at = (t % 8) * S
                                for k in range(KT):
                                    last = nc.tensor.matmul(
                                        ps[:, 2 * b + t // 8, at:at + S],
                                        ctx_T[r][:, b, k, t * P:(t + 1) * P],
                                        q2[:, k, b * S:(b + 1) * S], start=(k == 0),
                                        stop=(k == KT - 1))
                            last.then_inc(s_done, 1)
                        for b in range(2):
                            pe.wait_ge(weights, b + 1)
                            for f in range(KT):
                                for t in range(CT):
                                    nc.tensor.matmul(ps[:, 4 + b, f * S:(f + 1) * S],
                                                     ctx_n[r][:, b, t, f * P:(f + 1) * P],
                                                     att[:, b, t, :], start=(t == 0),
                                                     stop=(t == CT - 1))
                            for t in range(CT):
                                last = nc.tensor.matmul(
                                    ps[:, 4 + b, 2 * S:3 * S],
                                    env.ones if t < CT - 1 else env.valid_last, att[:, b, t, :],
                                    start=(t == 0), stop=(t == CT - 1))
                            last.then_inc(u_done, 1)
                        pe.wait_ge(u_ready, 2 * KT)
                        u2 = u_T[:, :, :, :].rearrange("p k b s -> p k (b s)")
                        for m in range(KT):
                            last = project(ps[:, 6, m * P:(m + 1) * P], wv, u2, m)
                        last.then_inc(upd_done, 1)
                        pe.wait_ge(upd_out, 1)
                        for m in range(4):
                            for g, (w, v) in enumerate(((wih, upd), (whh, sl))):
                                for k in range(KT):
                                    last = nc.tensor.matmul(ps[:, 0, m * P:(m + 1) * P],
                                                            w[:, k, m * P:(m + 1) * P], v[:, k, :],
                                                            start=(g == 0 and k == 0),
                                                            stop=(g == 1 and k == KT - 1))
                        last.then_inc(g_done, 1)
                        for g, (w, v) in enumerate(((wih, upd), (whh, sl))):
                            for m in range(KT):
                                last = project(ps[:, 1, (2 * g + m) * P:(2 * g + m + 1) * P], w, v,
                                               4 + m)
                        last.then_inc(g_done, 1)

                    @block.scalar
                    def _(act):
                        act.wait_ge(ssq_done, 1)
                        nc.scalar.activation(std[:, :], ps[:, 7, 0:P], ACT.Sqrt, scale=1.0 / D,
                                             bias=env.eps6[:, 0:1]).then_inc(std_ready, 1)
                        act.wait_ge(q1_done, 1)
                        nc.scalar.copy(q1[:, :, :].rearrange("p k n -> p (k n)"),
                                       ps[:, 6, 0:2 * P]).then_inc(q1_out, 1)
                        act.wait_ge(q2_done, 1)
                        for m in range(KT):
                            nc.scalar.activation(q2[:, m, :], ps[:, 5, m * P:(m + 1) * P],
                                                 ACT.Identity, scale=norm[:, 1, m:m + 1],
                                                 bias=env.zero[:, 0:1]).then_inc(q2_out, 1)
                        for b in range(2):
                            act.wait_ge(shifted, b + 1)
                            nc.scalar.activation(att[:, b, :, :], att[:, b, :, :], ACT.Exp,
                                                 scale=D ** -0.5).then_inc(exped, 1)
                        act.wait_ge(upd_done, 1)
                        nc.scalar.copy(upd[:, :, :].rearrange("p k n -> p (k n)"),
                                       ps[:, 6, 0:2 * P]).then_inc(upd_out, 1)
                        act.wait_ge(g_done, 1)
                        for m in range(4):
                            nc.scalar.activation(rz[:, m, :], ps[:, 0, m * P:(m + 1) * P], ACT.Tanh,
                                                 scale=0.5, bias=gb2[:, m:m + 1]
                                                 ).then_inc(rz_half, 1)
                        act.wait_ge(n_in, 1)
                        for m in range(KT):
                            nc.scalar.activation(n_T[:, m, :], n_T[:, m, :], ACT.Tanh,
                                                 bias=gb[:, 0, 4 + m:5 + m]).then_inc(n_out, 1)

                    @block.vector
                    def _(dve):
                        steps = Steps(dve, own)
                        nc.vector.tensor_tensor(sq[:, :, :], sl[:, :, :], sl[:, :, :],
                                                ALU.mult).then_inc(squares, 1)
                        dve.wait_ge(std_ready, 1)
                        steps.done(nc.vector.reciprocal(rs[:, :], std[:, :]))
                        steps.wait()
                        for k in range(KT):
                            nc.vector.scalar_tensor_tensor(
                                out=sn[:, k, :], in0=sl[:, k, :], scalar=norm[:, 0, k:k + 1],
                                in1=rs[:, :], op0=ALU.mult, op1=ALU.mult).then_inc(normed, 1)
                        s_of = [ps[:, 2 * b:2 * b + 2, :].rearrange("p c n -> p (c n)")
                                [:, 0:CT * S].rearrange("p (t s) -> p t s", t=CT) for b in range(2)]

                        def over_slots(x):
                            return x.unsqueeze(2).broadcast_to([P, CT, S])

                        for b in range(2):
                            dve.wait_ge(s_done, b + 1)
                            steps.done(nc.vector.tensor_reduce(top[:, b, :], s_of[b], AX, ALU.max))
                            steps.wait()
                            steps.done(nc.vector.tensor_tensor(att[:, b, :, :], s_of[b],
                                                               over_slots(top[:, b, :]),
                                                               ALU.subtract))
                            steps.wait()
                            nc.vector.tensor_tensor(att[:, b, :, :], att[:, b, :, :],
                                                    over_slots(rs_c[:, b, :]),
                                                    ALU.mult).then_inc(shifted, 1)
                        for b in range(2):
                            dve.wait_ge(exped, b + 1)
                            steps.done(nc.vector.tensor_reduce(tot[:, b, :], att[:, b, :, :], AX,
                                                               ALU.add))
                            steps.wait()
                            steps.done(nc.vector.reciprocal(tot[:, b, :], tot[:, b, :]))
                            steps.wait()
                            nc.vector.tensor_tensor(att[:, b, :, :], att[:, b, :, :],
                                                    over_slots(tot[:, b, :]),
                                                    ALU.mult).then_inc(weights, 1)
                        for b in range(2):
                            dve.wait_ge(u_done, b + 1)
                            steps.done(nc.vector.tensor_scalar(
                                rden[:, b, :], ps[:, 4 + b, 2 * S:3 * S], 1e-6, None, ALU.add))
                            steps.wait()
                            steps.done(nc.vector.reciprocal(rden[:, b, :], rden[:, b, :]))
                            steps.wait()
                            for f in range(KT):
                                nc.vector.scalar_tensor_tensor(
                                    out=u_T[:, f, b, :], in0=ps[:, 4 + b, f * S:(f + 1) * S],
                                    scalar=norm[:, 1, f:f + 1], in1=rden[:, b, :], op0=ALU.mult,
                                    op1=ALU.mult).then_inc(u_ready, 1)
                        dve.wait_ge(g_done, 2)
                        for m in range(KT):
                            steps.done(nc.vector.tensor_scalar(
                                hn[:, m, :], ps[:, 1, (2 + m) * P:(3 + m) * P],
                                gb[:, 1, 4 + m:5 + m], None, ALU.add))
                        dve.wait_ge(rz_half, 4)
                        steps.done(nc.vector.tensor_scalar(rz[:, :, :], rz[:, :, :], 0.5, 0.5,
                                                           ALU.mult, ALU.add))
                        steps.wait()
                        steps.done(nc.vector.tensor_tensor(hn[:, :, :], hn[:, :, :],
                                                           rz[:, 0:2, :], ALU.mult))
                        steps.wait()
                        nc.vector.tensor_tensor(
                            n_T[:, :, :], hn[:, :, :],
                            ps[:, 1, 0:2 * P].rearrange("p (m n) -> p m n", m=KT),
                            ALU.add).then_inc(n_in, 1)
                        dve.wait_ge(n_out, KT)
                        steps.done(nc.vector.tensor_tensor(hn[:, :, :], sl[:, :, :], n_T[:, :, :],
                                                           ALU.subtract))
                        steps.wait()
                        steps.done(nc.vector.tensor_tensor(hn[:, :, :], hn[:, :, :], rz[:, 2:4, :],
                                                           ALU.mult))
                        steps.wait()
                        steps.done(nc.vector.tensor_tensor(sl[:, :, :], n_T[:, :, :], hn[:, :, :],
                                                           ALU.add))

        def keep_slots(r, pair, loads):
            with signals(nc, f"s1_keep{r}", "kept") as (kept,):
                with nc.Block() as block:

                    @block.sync
                    def _(sp):
                        loads(sp)

                    @block.vector
                    def _(dve):
                        nc.vector.tensor_copy(res_T[:, :, bass.ds(pair * P, P)],
                                              sl[:, :, :]).then_inc(kept, 1)

        with nc.Fori(0, T // 2) as i:
            with signals(nc, "s1_ctx", "second_in first_in") as (second_in, first_in):
                prepare(0, 2 * i, lambda sp: load_context(sp, 1, 2 * i + 1, second_in))
                with nc.Fori(0, 3):
                    attend(0)
                keep_slots(0, 2 * i, lambda sp: sp.wait_ge(second_in, 6 * 16))
                prepare(1, 2 * i + 1, lambda sp: load_context(sp, 0, (2 * i + 2) % T, first_in))
                with nc.Fori(0, 3):
                    attend(1)
                keep_slots(1, 2 * i + 1, lambda sp: sp.wait_ge(first_in, 6 * 16))
        add_turned(nc, env, "s1_add", res_T, env.x)


def self_attention(nc, env, stage, w, b_col, b_row, att_T, scale, bias, per_head, sb):
    q_T, k_T, v_nat = sb("q_T", [P, KT, N]), sb("k_T", [P, KT, N]), sb("v_nat", [P, T, D])
    q_own, k_bd = sb("q_own", [P, KT, P]), sb("k_bd", [P, KT, HPT, P])
    sc, p_T = sb("sc", [P, H, P]), sb("p_T", [P, H, P])
    top, tot = sb("top", [P, H]), sb("tot", [P, H])
    ps = env.ps
    linear_T(nc, env, f"{stage}_qk", [(env.h_T, w[:, :, 0:D], q_T, b_col[:, 0:KT], None),
                                      (env.h_T, w[:, :, D:2 * D], k_T, b_col[:, KT:2 * KT], None)])
    linear_rows(nc, env, f"{stage}_v", env.h_T, [(w[:, :, 2 * D:3 * D], b_row,
                                                  lambda t: v_nat[:, t, :])])
    with nc.Fori(0, T) as t:
        with signals(nc, f"{stage}_at", "own q_in k_in s_done shifted exped p_turned act_out "
                     "dve_out o_done o_out") as (
                own, q_in, k_in, s_done, shifted, exped, p_turned, act_out, dve_out, o_done, o_out):
            with nc.Block() as block:

                @block.tensor
                def _(pe):
                    pe.wait_ge(q_in, 1)
                    for g in range(4):
                        if g % 2 == 0:
                            pe.wait_ge(k_in, g // 2 + 1)
                        nc.tensor.matmul(ps[:, g, :], q_own[:, g // 2, :],
                                         k_bd[:, g // 2, 4 * (g % 2):4 * (g % 2) + 4, :],
                                         start=True, stop=True).then_inc(s_done, 1)
                    for g in range(4):
                        pe.wait_ge(exped, g + 1)
                        for h in range(4 * g, 4 * g + 4):
                            last = nc.tensor.transpose(ps[:, 4 + g, (h % 4) * P:(h % 4 + 1) * P],
                                                       sc[:, h, :], env.ident)
                        last.then_inc(p_turned, 1)
                    pe.wait_ge(act_out, 2)
                    pe.wait_ge(dve_out, 2)
                    for h in range(H):
                        last = nc.tensor.matmul(
                            ps[:, 0, h * DH:(h + 1) * DH], p_T[:, h, :],
                            v_nat[:, bass.ds(t, 1), h * DH:(h + 1) * DH].squeeze(1),
                            start=True, stop=True)
                    last.then_inc(o_done, 1)

                @block.scalar
                def _(act):
                    nc.scalar.copy(q_own[:, :, :], q_T[:, :, bass.ds(t * P, P)]).then_inc(q_in, 1)
                    for g in range(4):
                        act.wait_ge(shifted, g + 1)
                        nc.scalar.activation(sc[:, 4 * g:4 * g + 4, :], sc[:, 4 * g:4 * g + 4, :],
                                             ACT.Exp).then_inc(exped, 1)
                    for g in (0, 2):
                        act.wait_ge(p_turned, g + 1)
                        nc.scalar.copy(p_T[:, 4 * g:4 * g + 4, :].rearrange("p h n -> p (h n)"),
                                       ps[:, 4 + g, :]).then_inc(act_out, 1)

                @block.vector
                def _(dve):
                    steps = Steps(dve, own)
                    for half in range(2):
                        nc.vector.tensor_tensor(
                            k_bd[:, half, :, :],
                            k_T[:, half, bass.ds(t * P, P)].unsqueeze(1).broadcast_to([P, HPT, P]),
                            env.head_of.unsqueeze(2).broadcast_to([P, HPT, P]),
                            ALU.mult).then_inc(k_in, 1)
                    for g in range(4):
                        hs = slice(4 * g, 4 * g + 4)
                        dve.wait_ge(s_done, g + 1)
                        steps.done(nc.vector.scalar_tensor_tensor(
                            out=sc[:, hs, :], in0=ps[:, g, :].rearrange("p (h n) -> p h n", h=4),
                            scalar=scale,
                            in1=bias[:, hs, :] if per_head else
                            bias.unsqueeze(1).broadcast_to([P, 4, P]),
                            op0=ALU.mult, op1=ALU.add))
                    for g in range(4):
                        hs = slice(4 * g, 4 * g + 4)
                        dve.wait_ge(own, g + 1)
                        steps.done(nc.vector.tensor_reduce(top[:, hs], sc[:, hs, :], AX, ALU.max))
                    for g in range(4):
                        hs = slice(4 * g, 4 * g + 4)
                        dve.wait_ge(own, 4 + g + 1)
                        nc.vector.tensor_tensor(
                            sc[:, hs, :], sc[:, hs, :],
                            top[:, hs].unsqueeze(2).broadcast_to([P, 4, P]),
                            ALU.subtract).then_inc(shifted, 1)
                    dve.wait_ge(exped, 4)
                    steps.done(nc.vector.tensor_reduce(tot[:, :], sc[:, :, :], AX, ALU.add))
                    steps.wait()
                    steps.done(nc.vector.reciprocal(tot[:, :], tot[:, :]))
                    for g in (1, 3):
                        dve.wait_ge(p_turned, g + 1)
                        nc.vector.tensor_copy(
                            p_T[:, 4 * g:4 * g + 4, :].rearrange("p h n -> p (h n)"),
                            ps[:, 4 + g, :]).then_inc(dve_out, 1)
                    dve.wait_ge(o_done, 1)
                    steps.wait()
                    nc.vector.tensor_tensor(
                        env.rows[:, bass.ds(t, 1), :].squeeze(1).rearrange(
                            "p (h d) -> p h d", h=H),
                        ps[:, 0, 0:D].rearrange("p (h d) -> p h d", h=H),
                        tot[:, :].unsqueeze(2).broadcast_to([P, H, DH]), ALU.mult).then_inc(o_out, 1)
    turn_rows(nc, env, f"{stage}_turn", env.rows, att_T)


def l1_attn(nc, env, d):
    mem, sb = scoped(nc, "a1")
    with mem:
        w, wo = sb("w", [P, KT, 3 * D]), sb("wo", [P, KT, D])
        b_col, b_row = sb("b_col", [P, 2 * KT]), sb("b_row", [1, 2, D])
        att_T = sb("att_T", [P, KT, N])
        layernorm(nc, env, "a1_ln", env.x, env.h, env.h_T, loads=[
            (w[:, :, :], wview(d["L1_attn_w_qkv"])), (wo[:, :, :], wview(d["L1_attn_w_o"])),
            (b_col[:, :], d["L1_attn_b_qk"]),
            (b_row[:, 0, :], d["L1_attn_b_qkv"][2 * D:3 * D].unsqueeze(0)),
            (b_row[:, 1, :], d["L1_attn_b_o"].unsqueeze(0))])
        self_attention(nc, env, "a1", w, b_col, b_row[:, 0, :], att_T, D ** -0.5, env.cross, False,
                       sb)
        project_add(nc, env, "a1_o", att_T, wo, b_row[:, 1, :], env.x, also=env.h)


def l1_ffn(nc, env, d):
    E, HD, ITERS, G = 8, 64, 2, 4
    mem, sb = scoped(nc, "g1")
    with mem:
        rw1, hw1 = sb("rw1", [P, KT, HD]), sb("hw1", [P, KT, HD])
        rw2, hw2 = sb("rw2", [HD, 1, E]), sb("hw2", [HD, 1, 1])
        rb1, hb1, sb1 = (sb(n, [HD, 1]) for n in ("rb1", "hb1", "sb1"))
        rb2, sb2, fb2 = sb("rb2", [1, E]), sb("sb2", [1, 3 * D]), sb("fb2", [1, D])
        hb2 = sb("hb2", [P, 1])
        ew1, eb1 = sb("ew1", [P, 2 * KT, E * HD]), sb("eb1", [P, G])
        ew2, eb2 = sb("ew2", [P, G, 3 * D]), sb("eb2", [E, 3 * D])
        sw1, sw2 = sb("sw1", [P, 2 * KT, HD]), sb("sw2", [HD, 3 * D])
        fw1, fb1, fw2 = sb("fw1", [P, KT, 2 * D]), sb("fb1", [P, 2 * KT]), sb("fw2", [P, 2 * KT, D])
        mu, iw, sw = sb("mu", [P, D]), sb("iw", [P, D]), sb("sw", [P, 2])
        r_T, sh_T = sb("r_T", [HD, 1, N]), sb("sh_T", [HD, 1, N])
        hid_T = sb("hid_T", [P, G, N])
        sel = sb("sel", [E, G, P])
        masks = sb("masks", [P, 2, G, N], BF16)
        probs, chosen = sb("probs", [P, T, E]), sb("chosen", [P, T, 2, E])
        chosen_T = sb("chosen_T", [E, 2, N])
        weights, coef, wsum = sb("weights", [P, T, 2]), sb("coef", [P, T, 3]), sb("wsum", [P, T])
        m8, i8, i_f = sb("m8", [P, T, 8]), sb("i8", [P, T, 8], U32), sb("i_f", [P, T, 2])
        top, total, halt = sb("top", [P, T]), sb("total", [P, T]), sb("halt", [P, T])
        cur, vel = sb("cur", [P, T, D]), sb("vel", [P, T, D])
        cv_T = sb("cv_T", [P, 2 * KT, N])
        hm, sh_own, ch_own = sb("hm", [P, 2, G, P]), sb("sh_own", [HD, P]), sb("ch_own", [E, 2, P])
        cur_own, vel_own = sb("cur_own", [P, D]), sb("vel_own", [P, D])
        ea, sp_ = sb("ea", [P, 2, 3, D]), sb("sp", [P, 3, D])
        absb = sb("absb", [P, 3, D])
        v3, x3 = sb("v3", [P, 3, D]), sb("x3", [P, 3, D])
        away, acc = sb("away", [P, D]), sb("acc", [P, 2, D])
        ps = env.ps
        layernorm(nc, env, "g1_ln", env.x, env.h, env.h_T, loads=[
            (rw1[:, :, :], wview(d["L1_ffn_router_w1"])), (hw1[:, :, :], wview(d["L1_ffn_halt_w1"])),
            (rw2[:, 0, :], d["L1_ffn_router_w2"]), (hw2[:, 0, :], d["L1_ffn_halt_w2"]),
            (rb1[:, :], d["L1_ffn_router_b1"].unsqueeze(1)),
            (hb1[:, :], d["L1_ffn_halt_b1"].unsqueeze(1)),
            (sb1[:, :], d["L1_ffn_shared_b1"].unsqueeze(1)),
            (rb2[:, :], d["L1_ffn_router_b2"].unsqueeze(0)),
            (sb2[:, :], d["L1_ffn_shared_b2"].unsqueeze(0)),
            (fb2[:, :], d["L1_ffn_refine_b2"].unsqueeze(0)),
            (hb2[:, :], d["L1_ffn_halt_b2"].partition_broadcast(P)),
            (sw[:, 0:1], d["L1_ffn_shared_weight"].partition_broadcast(P)),
            (ew1[:, :, :], wview(d["L1_ffn_expert_w1"])), (eb1[:, :], d["L1_ffn_expert_b1"]),
            (ew2[:, :, :], wview(d["L1_ffn_expert_w2"])), (eb2[:, :], d["L1_ffn_expert_b2"]),
            (sw1[:, :, :], wview(d["L1_ffn_shared_w1"])), (sw2[:, :], d["L1_ffn_shared_w2"]),
            (fw1[:, :, :], wview(d["L1_ffn_refine_w1"])), (fb1[:, :], d["L1_ffn_refine_b1"]),
            (fw2[:, :, :], wview(d["L1_ffn_refine_w2"])),
            (mu[:, :], d["L1_ffn_mu"].partition_broadcast(P)),
            (iw[:, :], d["L1_ffn_integration_weight"].partition_broadcast(P)),
            (sel[:, :, :], d["expert_sel"])])
        linear_T(nc, env, "g1_r", [(env.h_T, rw1, r_T, rb1, "gelu")])
        with signals(nc, "g1_route", "own logits shifted exped neg state picked turned turned_out "
                     "spread spread_out") as (own, logits, shifted, exped, neg, state, picked,
                                              turned, turned_out, spread, spread_out):
            with nc.Block() as block:

                @block.gpsimd
                def _(pool):
                    nc.gpsimd.memset(vel[:, :, :], 0.0).then_inc(state, 1)
                    nc.gpsimd.memset(cv_T[:, KT:2 * KT, :], 0.0).then_inc(state, 1)
                    nc.gpsimd.tensor_copy(cur[:, :, :], env.h[:, :, :]).then_inc(state, 1)
                    nc.gpsimd.tensor_copy(cv_T[:, 0:KT, :], env.h_T[:, :, :]).then_inc(state, 1)

                @block.tensor
                def _(pe):
                    for t in range(T):
                        put = ps[:, 0, t * E:(t + 1) * E]
                        nc.tensor.matmul(put, r_T[:, 0, t * P:(t + 1) * P], rw2[:, 0, :],
                                         start=True, stop=False)
                        last = nc.tensor.matmul(put, env.ones[0:1, :], rb2[:, :],
                                                start=False, stop=True)
                    last.then_inc(logits, 1)
                    pe.wait_ge(picked, 1)
                    for k in range(2):
                        for t in range(T):
                            last = nc.tensor.transpose(
                                ps[0:E, 1 + 2 * k + t // 4, (t % 4) * P:(t % 4 + 1) * P],
                                chosen[:, t, k, :], env.ident)
                        last.then_inc(turned, 1)
                    pe.wait_ge(turned_out, 2)
                    n = 0
                    for k in range(2):
                        for g in range(G):
                            for c in range(2):
                                if n >= 8:
                                    pe.wait_ge(spread_out, n - 7)
                                nc.tensor.matmul(ps[:, n % 8, :], sel[:, g, :],
                                                 chosen_T[:, k, c * NH:(c + 1) * NH], start=True,
                                                 stop=True).then_inc(spread, 1)
                                n += 1

                @block.scalar
                def _(act):
                    act.wait_ge(shifted, 1)
                    nc.scalar.activation(probs[:, :, :], probs[:, :, :], ACT.Exp).then_inc(exped, 1)
                    nc.scalar.activation(sw[:, 1:2], sw[:, 0:1], ACT.Exp, scale=-1.0
                                         ).then_inc(neg, 1)

                @block.vector
                def _(dve):
                    steps = Steps(dve, own)
                    dve.wait_ge(logits, 1)
                    steps.done(nc.vector.tensor_copy(
                        probs[:, :, :], ps[:, 0, 0:T * E].rearrange("p (t e) -> p t e", t=T)))
                    steps.wait()
                    row_softmax(nc, dve, probs[:, :, :], top[:, :], total[:, :], E, exped, shifted,
                                steps)
                    top2(nc, env, dve, probs, E, weights[:, :, :], chosen, m8, i8, i_f, steps)
                    steps.done(nc.vector.tensor_reduce(wsum[:, :], weights[:, :, :], AX, ALU.add))
                    steps.wait()
                    steps.done(nc.vector.reciprocal(wsum[:, :], wsum[:, :]))
                    dve.wait_ge(neg, 1)
                    steps.done(nc.vector.tensor_scalar(sw[:, 1:2], sw[:, 1:2], 1.0, None, ALU.add))
                    steps.wait()
                    steps.done(nc.vector.reciprocal(sw[:, 0:1], sw[:, 1:2]))
                    steps.wait()
                    steps.done(nc.vector.tensor_scalar(sw[:, 1:2], sw[:, 0:1], -1.0, 1.0, ALU.mult,
                                                       ALU.add))
                    steps.done(nc.vector.tensor_copy(
                        coef[:, :, 0:1], sw[:, 0:1].unsqueeze(1).broadcast_to([P, T, 1])))
                    steps.done(nc.vector.tensor_tensor(
                        weights[:, :, :], weights[:, :, :],
                        wsum[:, :].unsqueeze(2).broadcast_to([P, T, 2]), ALU.mult))
                    steps.wait()
                    nc.vector.tensor_scalar(coef[:, :, 1:3], weights[:, :, :], sw[:, 1:2], None,
                                            ALU.mult).then_inc(picked, 1)
                    for k in range(2):
                        dve.wait_ge(turned, k + 1)
                        nc.vector.tensor_copy(
                            chosen_T[:, k, :].rearrange("e (c n) -> e c n", c=2),
                            ps[0:E, 1 + 2 * k:3 + 2 * k, :]).then_inc(turned_out, 1)
                    n = 0
                    for k in range(2):
                        for g in range(G):
                            for c in range(2):
                                dve.wait_ge(spread, n + 1)
                                nc.vector.tensor_copy(masks[:, k, g, c * NH:(c + 1) * NH],
                                                      ps[:, n % 8, :]).then_inc(spread_out, 1)
                                n += 1

        with nc.Fori(0, ITERS):
            linear_T(nc, env, "g1_hid", [(cv_T, ew1, hid_T, eb1, "gelu"),
                                         (cv_T, sw1, sh_T, sb1, "gelu"),
                                         (cv_T[:, 0:KT], hw1, r_T, hb1, "gelu")])
            with signals(nc, "g1_halt", "own product exped") as (own, product, exped):
                with nc.Block() as block:

                    @block.tensor
                    def _(pe):
                        for t in range(T):
                            last = nc.tensor.matmul(ps[:, 0, t:t + 1], r_T[:, 0, t * P:(t + 1) * P],
                                                    hw2[:, 0, :], start=True, stop=True)
                        last.then_inc(product, 1)

                    @block.scalar
                    def _(act):
                        act.wait_ge(own, 1)
                        nc.scalar.activation(halt[:, :], halt[:, :], ACT.Tanh, scale=0.5
                                             ).then_inc(exped, 1)

                    @block.vector
                    def _(dve):
                        steps = Steps(dve, own)
                        dve.wait_ge(product, 1)
                        steps.done(nc.vector.tensor_scalar(halt[:, :], ps[:, 0, 0:T], hb2[:, 0:1],
                                                           None, ALU.add))
                        dve.wait_ge(exped, 1)
                        steps.done(nc.vector.tensor_scalar(halt[:, :], halt[:, :], 0.5, 0.5,
                                                           ALU.mult, ALU.add))

            with nc.Fori(0, T) as t:
                with signals(nc, "g1_step", "own taken masked ctrl e_done sp_done new_state") as (
                        own, taken, masked, ctrl, e_done, sp_done, new_state):
                    tile = bass.ds(t * P, P)
                    with nc.Block() as block:

                        @block.gpsimd
                        def _(pool):
                            nc.gpsimd.tensor_copy(sh_own[:, :], sh_T[:, 0, tile]).then_inc(taken, 1)
                            nc.gpsimd.tensor_copy(ch_own[:, :, :], chosen_T[:, :, tile]
                                                  ).then_inc(taken, 1)

                        @block.tensor
                        def _(pe):
                            pe.wait_ge(taken, 2)
                            for s in range(3):
                                if s:
                                    pe.wait_ge(masked, s)
                                for bank, cols in ((2 * s, slice(0, 2 * D)),
                                                   (2 * s + 1, slice(2 * D, 3 * D))):
                                    put = ps[:, bank, 0:cols.stop - cols.start]
                                    if s == 0:
                                        nc.tensor.matmul(put, sh_own[:, :], sw2[:, cols],
                                                         start=True, stop=False)
                                        last = nc.tensor.matmul(put, env.ones[0:1, :],
                                                                sb2[:, cols], start=False,
                                                                stop=True)
                                        continue
                                    for g in range(G):
                                        nc.tensor.matmul(put, hm[:, s - 1, g, :], ew2[:, g, cols],
                                                         start=(g == 0), stop=False)
                                    last = nc.tensor.matmul(put, ch_own[:, s - 1, :], eb2[:, cols],
                                                            start=False, stop=True)
                            last.then_inc(ctrl, 1)

                        @block.scalar
                        def _(act):
                            act.wait_ge(ctrl, 1)
                            ab = ps[:, 0:6, :].rearrange("p (s two) n -> p s two n", two=2)
                            nc.scalar.activation(ea[:, 0, :, :], ab[:, :, 0, 0:D], ACT.Exp,
                                                 scale=-1.0).then_inc(e_done, 1)
                            nc.scalar.activation(ea[:, 1, :, :], ab[:, :, 1, 0:D], ACT.Exp,
                                                 scale=-1.0).then_inc(e_done, 1)
                            nc.scalar.activation(absb[:, :, :], ab[:, :, 0, D:2 * D], ACT.Abs
                                                 ).then_inc(e_done, 1)
                            act.wait_ge(e_done, 3)
                            nc.scalar.activation(absb[:, :, :], absb[:, :, :], ACT.Exp, scale=-1.0
                                                 ).then_inc(sp_done, 1)
                            act.wait_ge(sp_done, 1)
                            nc.scalar.activation(absb[:, :, :], absb[:, :, :], ACT.Ln,
                                                 bias=env.ones[:, 0:1]).then_inc(sp_done, 1)

                        @block.vector
                        def _(dve):
                            steps = Steps(dve, own)
                            for k in range(2):
                                nc.vector.tensor_tensor(hm[:, k, :, :], hid_T[:, :, tile],
                                                        masks[:, k, :, tile],
                                                        ALU.mult).then_inc(masked, 1)
                            steps.done(nc.vector.tensor_copy(cur_own[:, :],
                                                             cur[:, bass.ds(t, 1), :].squeeze(1)))
                            steps.done(nc.vector.tensor_copy(vel_own[:, :],
                                                             vel[:, bass.ds(t, 1), :].squeeze(1)))
                            steps.wait()
                            steps.done(nc.vector.tensor_tensor(away[:, :], cur_own[:, :], mu[:, :],
                                                               ALU.subtract))

                            def three(x):
                                return x.unsqueeze(1).broadcast_to([P, 3, D])

                            dve.wait_ge(e_done, 2)
                            steps.done(nc.vector.tensor_scalar(ea[:, :, :, :], ea[:, :, :, :], 1.0,
                                                               None, ALU.add))
                            steps.wait()
                            steps.done(nc.vector.reciprocal(ea[:, :, :, :], ea[:, :, :, :]))
                            steps.wait()
                            steps.done(nc.vector.tensor_tensor(v3[:, :, :], ea[:, 0, :, :],
                                                               three(vel_own[:, :]), ALU.mult))
                            dve.wait_ge(sp_done, 2)
                            steps.done(nc.vector.scalar_tensor_tensor(
                                out=sp_[:, :, :],
                                in0=ps[:, 0:6, :].rearrange("p (s two) n -> p s two n", two=2)
                                [:, :, 0, D:2 * D], scalar=0.0, in1=absb[:, :, :], op0=ALU.max,
                                op1=ALU.add))
                            steps.wait()
                            steps.done(nc.vector.tensor_tensor(sp_[:, :, :], sp_[:, :, :],
                                                               three(away[:, :]), ALU.mult))
                            steps.wait()
                            steps.done(nc.vector.tensor_tensor(v3[:, :, :], v3[:, :, :],
                                                               sp_[:, :, :], ALU.subtract))
                            steps.wait()
                            steps.done(nc.vector.tensor_tensor(x3[:, :, :], ea[:, 1, :, :],
                                                               v3[:, :, :], ALU.mult))
                            steps.wait()
                            steps.done(nc.vector.scalar_tensor_tensor(
                                out=x3[:, :, :], in0=x3[:, :, :], scalar=0.1,
                                in1=three(cur_own[:, :]), op0=ALU.mult, op1=ALU.add))
                            steps.wait()
                            for s in range(3):
                                c = coef[:, bass.ds(t, 1), s:s + 1].squeeze(1)
                                for n, src in ((0, x3), (1, v3)):
                                    if s == 0:
                                        steps.done(nc.vector.tensor_scalar(
                                            acc[:, n, :], src[:, s, :], c, None, ALU.mult))
                                    else:
                                        steps.done(nc.vector.scalar_tensor_tensor(
                                            out=acc[:, n, :], in0=src[:, s, :], scalar=c,
                                            in1=acc[:, n, :], op0=ALU.mult, op1=ALU.add))
                                steps.wait()
                            for n, own_state in ((0, cur_own), (1, vel_own)):
                                steps.done(nc.vector.tensor_tensor(
                                    acc[:, n, :], acc[:, n, :], own_state[:, :], ALU.subtract))
                            steps.wait()
                            for n, own_state, state in ((0, cur_own, cur), (1, vel_own, vel)):
                                nc.vector.scalar_tensor_tensor(
                                    out=state[:, bass.ds(t, 1), :].squeeze(1), in0=acc[:, n, :],
                                    scalar=halt[:, bass.ds(t, 1)], in1=own_state[:, :],
                                    op0=ALU.mult, op1=ALU.add).then_inc(new_state, 1)
            turn_rows(nc, env, "g1_cur", cur, cv_T[:, 0:KT])
            turn_rows(nc, env, "g1_vel", vel, cv_T[:, KT:2 * KT])
        linear_T(nc, env, "g1_ref", [(cv_T[:, 0:KT], fw1, hid_T, fb1, "gelu")])
        project_add(nc, env, "g1_out", hid_T, fw2, fb2[:, :], env.x, also=env.h, scale=iw[:, :])



def l2_xattn(nc, env, d):
    mem, sb = scoped(nc, "x2")
    with mem:
        wq, wk, wv, wo = (sb(n, [P, KT, D]) for n in ("wq", "wk", "wv", "wo"))
        q_T, att_T, nb = sb("q_T", [P, KT, N]), sb("att_T", [P, KT, N]), sb("nb", [P, 2])
        kv = wview(d["L2_xattn_Wkv"])
        layernorm(nc, env, "x2_ln", env.x, env.h, env.h_T, loads=[
            (wq[:, :, :], wview(d["L2_xattn_Wq"])), (wk[:, :, :], kv[:, :, 0:D]),
            (wv[:, :, :], kv[:, :, D:2 * D]), (wo[:, :, :], wview(d["L2_xattn_Wo"])),
            (nb[:, 0:1], d["L2_xattn_nbias"].partition_broadcast(P))])
        with signals(nc, "x2_nb", "ready") as (ready,):
            with nc.Block() as block:

                @block.vector
                def _(dve):
                    nc.vector.tensor_scalar(nb[:, 1:2], nb[:, 0:1], -float(DH) ** 0.5, None,
                                            ALU.mult).then_inc(ready, 1)
        linear_T(nc, env, "x2_q", [(env.h_T, wq, q_T, None, None)])
        context_heads(nc, env, "x2", d["ctx_T"], q_T, att_T, wk, wv, softmax=False,
                      notmask=d["mask_T"], nb=nb)
        project_add(nc, env, "x2_o", att_T, wo, None, env.x)


def l2_attn(nc, env, d):
    F = 64
    mem, sb = scoped(nc, "a2")
    with mem:
        wq, wk, wv, wo = (sb(n, [P, KT, D]) for n in ("wq", "wk", "wv", "wo"))
        b_rows = sb("b_rows", [1, 4, D])
        proj = sb("proj", [P, KT, HPT, F])
        qk, v_aug = sb("qk", [P, 2, T, D]), sb("v_aug", [P, T, PAIRS, 2 * DH + 1])
        sq, ssq = sb("sq", [P, 2, T, D]), sb("ssq", [P, 2, T * H])
        q_T, k_T = sb("q_T", [P, KT, N]), sb("k_T", [P, KT, N])
        qf_T, kf = sb("qf_T", [P, PAIRS, N]), sb("kf", [P, T, H * F])
        kv = sb("kv", [P, 2, 2, PAIRS, 2 * DH + 2])
        nrm, att_T = sb("nrm", [P, T, H]), sb("att_T", [P, KT, N])
        o_own = sb("o_own", [P, H])
        ps = env.ps
        layernorm(nc, env, "a2_ln", env.x, env.h, env.h_T, loads=[
            (wq[:, :, :], wview(d["L2_attn_Wq"])), (wk[:, :, :], wview(d["L2_attn_Wk"])),
            (wv[:, :, :], wview(d["L2_attn_Wv"])), (wo[:, :, :], wview(d["L2_attn_Wo"])),
            (b_rows[:, 0, :], d["L2_attn_bq"].unsqueeze(0)),
            (b_rows[:, 1, :], d["L2_attn_bk"].unsqueeze(0)),
            (b_rows[:, 2, :], d["L2_attn_bv"].unsqueeze(0)),
            (b_rows[:, 3, :], d["L2_attn_bo"].unsqueeze(0)),
            (proj[:, :, :, :], d["proj_rows"])])
        linear_rows(nc, env, "a2_qkv", env.h_T, [
            (wq, b_rows[:, 0, :], lambda t: qk[:, 0, t, :]),
            (wk, b_rows[:, 1, :], lambda t: qk[:, 1, t, :]),
            (wv, b_rows[:, 2, :], lambda t: v_aug[:, t, :, 0:2 * DH])])
        with signals(nc, "a2_norm", "own sum std normed placed") as (
                own, summed, std_ready, normed, placed):
            with nc.Block() as block:

                @block.gpsimd
                def _(pool):
                    for half in range(KT):
                        nc.gpsimd.tensor_tensor(
                            proj[:, half, :, :], proj[:, half, :, :],
                            env.head_of.unsqueeze(2).broadcast_to([P, HPT, F]),
                            ALU.mult).then_inc(placed, 1)
                    nc.gpsimd.memset(v_aug[:, :, :, 2 * DH:2 * DH + 1], 1.0).then_inc(placed, 1)

                @block.scalar
                def _(act):
                    for n in range(2):
                        act.wait_ge(summed, n + 1)
                        nc.scalar.activation(ssq[:, n, :], ssq[:, n, :], ACT.Sqrt,
                                             bias=env.zero[:, 0:1]).then_inc(std_ready, 1)

                @block.vector
                def _(dve):
                    steps = Steps(dve, own)
                    for n in range(2):
                        steps.done(nc.vector.tensor_tensor(sq[:, n], qk[:, n], qk[:, n], ALU.mult))
                        steps.wait()
                        nc.vector.tensor_reduce(
                            ssq[:, n, :], sq[:, n].rearrange("p t (h d) -> p (t h) d", h=H), AX,
                            ALU.add).then_inc(summed, 1)
                    for n in range(2):
                        dve.wait_ge(std_ready, n + 1)
                        steps.done(nc.vector.tensor_scalar(ssq[:, n, :], ssq[:, n, :], 1e-8, None,
                                                           ALU.add))
                        steps.wait()
                        steps.done(nc.vector.reciprocal(ssq[:, n, :], ssq[:, n, :]))
                        steps.wait()
                        view = qk[:, n].rearrange("p t (h d) -> p (t h) d", h=H)
                        nc.vector.tensor_tensor(
                            view, view, ssq[:, n, :].unsqueeze(2).broadcast_to([P, T * H, DH]),
                            ALU.mult).then_inc(normed, 1)
        turn_rows(nc, env, "a2_qT", qk[:, 0], q_T)
        turn_rows(nc, env, "a2_kT", qk[:, 1], k_T)
        groups = [(0, j, c) for j in range(PAIRS) for c in range(2)] + \
                 [(1, t, c) for t in range(T) for c in range(2)]
        with signals(nc, "a2_feat", "product act_high dve_out act_out") as (
                product, act_high, dve_out, act_out):
            with nc.Block() as block:

                def target(kind, a, c):
                    return (qf_T[:, a, c * NH:(c + 1) * NH] if kind == 0
                            else kf[:, a, c * NH:(c + 1) * NH])

                @block.tensor
                def _(pe):
                    for g, (kind, a, c) in enumerate(groups):
                        if g >= 8:
                            pe.wait_ge((dve_out, act_high)[g % 2], (g - 8) // 2 + 1)
                        if kind == 0:
                            last = nc.tensor.matmul(
                                ps[:, g % 8, :],
                                proj[:, a // 4, 2 * (a % 4):2 * (a % 4) + 2, :],
                                q_T[:, a // 4, c * NH:(c + 1) * NH], start=True, stop=True)
                        else:
                            last = nc.tensor.matmul(
                                ps[:, g % 8, :], k_T[:, c, a * P:(a + 1) * P],
                                proj[:, c, :, :], start=True, stop=True)
                        last.then_inc(product, 1)

                @block.vector
                def _(dve):
                    for g in range(0, len(groups), 2):
                        dve.wait_ge(product, g + 1)
                        nc.vector.tensor_scalar(target(*groups[g]), ps[:, g % 8, :], 0.0, 0.1,
                                                ALU.max, ALU.add).then_inc(dve_out, 1)

                @block.scalar
                def _(act):
                    for g in range(1, len(groups), 2):
                        act.wait_ge(product, g + 1)
                        nc.scalar.activation(target(*groups[g]), ps[:, g % 8, :], ACT.Relu
                                             ).then_inc(act_high, 1)
                        act.wait_ge(act_high, g // 2 + 1)
                        nc.scalar.add(target(*groups[g]), target(*groups[g]), env.tenth
                                      ).then_inc(act_out, 1)

        W = 2 * DH + 1
        with signals(nc, "a2_lin", "own kv_done placed2 o_done o_taken") as (
                own, kv_done, kv_placed, o_done, o_taken):
            with nc.Block() as block:

                @block.tensor
                def _(pe):
                    def key_values(t):
                        if t >= 2:
                            pe.wait_ge(kv_placed, 4 * (t - 1))
                        for b in range(2):
                            rows = slice(b * S, (b + 1) * S)
                            for j in range(PAIRS):
                                last = nc.tensor.matmul(
                                    ps[:, 2 * (t % 2) + b, W * j:W * (j + 1)],
                                    kf[rows, t, 2 * F * j:2 * F * (j + 1)], v_aug[rows, t, j, :],
                                    start=True, stop=True)
                        last.then_inc(kv_done, 1)

                    def outputs(t):
                        pe.wait_ge(kv_placed, 4 * (t + 1))
                        if t >= 2:
                            pe.wait_ge(o_taken, t - 1)
                        for b in range(2):
                            for j in range(PAIRS):
                                last = nc.tensor.matmul(
                                    ps[b * S:(b + 1) * S, 4 + t % 2, (W + 1) * j:(W + 1) * (j + 1)],
                                    qf_T[:, j, t * P + b * S:t * P + (b + 1) * S],
                                    kv[:, t % 2, b, j, :], start=True, stop=True)
                        last.then_inc(o_done, 1)

                    for t in range(T):
                        key_values(t)
                        if t:
                            outputs(t - 1)
                    outputs(T - 1)

                @block.vector
                def _(dve):
                    steps = Steps(dve, own)

                    def place(t):
                        dve.wait_ge(kv_done, t + 1)
                        if t >= 2:
                            dve.wait_ge(o_done, t - 1)
                        for b in range(2):
                            put = ps[:, 2 * (t % 2) + b, 0:W * PAIRS].rearrange(
                                "p (j w) -> p j w", w=W)
                            own_head = env.own_head.unsqueeze(1).broadcast_to([P, PAIRS, 2 * DH])
                            nc.vector.tensor_tensor(kv[:, t % 2, b, :, 0:2 * DH],
                                                    put[:, :, 0:2 * DH], own_head,
                                                    ALU.mult).then_inc(kv_placed, 1)
                            nc.vector.tensor_tensor(
                                kv[:, t % 2, b, :, 2 * DH:2 * DH + 2],
                                put[:, :, 2 * DH:W].broadcast_to([P, PAIRS, 2]),
                                env.which_head.unsqueeze(1).broadcast_to([P, PAIRS, 2]),
                                ALU.mult).then_inc(kv_placed, 1)

                    def divide(t):
                        dve.wait_ge(o_done, t + 1)
                        put = ps[:, 4 + t % 2, 0:(W + 1) * PAIRS].rearrange("p (j w) -> p j w",
                                                                            w=W + 1)
                        steps.done(nc.vector.tensor_scalar(
                            nrm[:, t, :].rearrange("p (j h) -> p j h", h=2),
                            put[:, :, 2 * DH:2 * DH + 2], 1e-6, None, ALU.max))
                        steps.wait()
                        steps.done(nc.vector.reciprocal(nrm[:, t, :], nrm[:, t, :]))
                        steps.wait()
                        nc.vector.tensor_tensor(
                            env.rows[:, t, :].rearrange("p (j h d) -> p j h d", j=PAIRS, h=2),
                            put[:, :, 0:2 * DH].rearrange("p j (h d) -> p j h d", h=2),
                            nrm[:, t, :].rearrange("p (j h) -> p j h", h=2).unsqueeze(3)
                            .broadcast_to([P, PAIRS, 2, DH]), ALU.mult).then_inc(o_taken, 1)

                    for t in range(T):
                        place(t)
                        if t:
                            divide(t - 1)
                    divide(T - 1)
        turn_rows(nc, env, "a2_turn", env.rows, att_T)
        project_add(nc, env, "a2_o", att_T, wo, b_rows[:, 3, :], env.x)


def l2_ffn(nc, env, d):
    E, TOP, ROUTE_SCALE = 16, 8, 2.826
    mem, sb = scoped(nc, "f2")
    with mem:
        gate, bias = sb("gate", [P, KT, E]), sb("bias", [P, E])
        wg, wu, wd = (sb(n, [P, KT, D]) for n in ("wg", "wu", "wd"))
        scores, sel = sb("scores", [P, T, E]), sb("sel", [P, T, E])
        m8, rest, picked = sb("m8", [P, T, TOP]), sb("rest", [P, T, E]), sb("picked", [P, T, E])
        total, comb = sb("total", [P, T]), sb("comb", [P, T, E + 1])
        g_T, h_T = sb("g_T", [P, 2, NH]), sb("hid_T", [P, KT, N])
        ps = env.ps

        def weights_of(e):
            return [(wg[:, :, :], wview(d["L2_w_gate"][e])), (wu[:, :, :], wview(d["L2_w_up"][e]))]

        layernorm(nc, env, "f2_ln", env.x, env.h, env.h_T, loads=[
            (gate[:, :, :], wview(d["L2_ffn_gate_w"])),
            (bias[:, :], d["L2_ffn_expert_bias"].partition_broadcast(P)), *weights_of(0)])
        with signals(nc, "f2_route", "own logits logits_out exped") as (
                own, logits, logits_out, exped):
            with nc.Block() as block:

                @block.tensor
                def _(pe):
                    for t in range(T):
                        for k in range(KT):
                            last = nc.tensor.matmul(ps[:, 0, t * E:(t + 1) * E],
                                                    env.h_T[:, k, t * P:(t + 1) * P],
                                                    gate[:, k, :], start=(k == 0),
                                                    stop=(k == KT - 1))
                    last.then_inc(logits, 1)

                @block.scalar
                def _(act):
                    act.wait_ge(logits, 1)
                    nc.scalar.activation(scores[:, :, :].rearrange("p t e -> p (t e)"),
                                         ps[:, 0, 0:T * E], ACT.Sigmoid).then_inc(exped, 1)

                @block.vector
                def _(dve):
                    steps = Steps(dve, own)
                    dve.wait_ge(exped, 1)
                    steps.done(nc.vector.tensor_tensor(
                        sel[:, :, :], scores[:, :, :],
                        bias[:, :].unsqueeze(1).broadcast_to([P, T, E]), ALU.add))
                    steps.wait()
                    for t in range(T):
                        steps.done(nc.vector.max(m8[:, t, :], sel[:, t, :]))
                    steps.wait()
                    for t in range(T):
                        steps.done(nc.vector.match_replace(rest[:, t, :], m8[:, t, :],
                                                           sel[:, t, :], -3e38))
                    steps.wait()
                    steps.done(nc.vector.tensor_tensor(picked[:, :, :], rest[:, :, :],
                                                       sel[:, :, :], ALU.not_equal))
                    steps.wait()
                    steps.done(nc.vector.tensor_tensor(picked[:, :, :], picked[:, :, :],
                                                       scores[:, :, :], ALU.mult))
                    steps.wait()
                    steps.done(nc.vector.tensor_reduce(total[:, :], picked[:, :, :], AX, ALU.add))
                    steps.wait()
                    steps.done(nc.vector.reciprocal(total[:, :], total[:, :]))
                    steps.wait()
                    steps.done(nc.vector.tensor_tensor(
                        picked[:, :, :], picked[:, :, :],
                        total[:, :].unsqueeze(2).broadcast_to([P, T, E]), ALU.mult))
                    steps.wait()
                    steps.done(nc.vector.tensor_scalar(comb[:, :, 0:E], picked[:, :, :],
                                                       ROUTE_SCALE, None, ALU.mult))
                    steps.done(nc.vector.memset(comb[:, :, E:E + 1], 1.0))

        with nc.Fori(0, E + 1) as e:
            with signals(nc, "f2_up", "loaded product silu_done gated") as (
                    loaded, product, silu_done, gated):
                with nc.Block() as block:

                    @block.sync
                    def _(sp):
                        load_all(sp, [(wd[:, :, :], wview(d["L2_w_down"][e]))], loaded)

                    @block.tensor
                    def _(pe):
                        for g in range(4):
                            m, c = g // 2, g % 2
                            for n, w in ((0, wg), (1, wu)):
                                for k in range(KT):
                                    last = nc.tensor.matmul(ps[:, 2 * g + n, :],
                                                            w[:, k, m * P:(m + 1) * P],
                                                            env.h_T[:, k, c * NH:(c + 1) * NH],
                                                            start=(k == 0), stop=(k == KT - 1))
                                last.then_inc(product, 1)

                    @block.scalar
                    def _(act):
                        for g in range(4):
                            act.wait_ge(product, 2 * g + 1)
                            if g >= 2:
                                act.wait_ge(gated, g - 1)
                            nc.scalar.activation(g_T[:, g % 2, :], ps[:, 2 * g, :], ACT.Silu
                                                 ).then_inc(silu_done, 1)

                    @block.vector
                    def _(dve):
                        for g in range(4):
                            m, c = g // 2, g % 2
                            dve.wait_ge(silu_done, g + 1)
                            dve.wait_ge(product, 2 * g + 2)
                            nc.vector.tensor_tensor(h_T[:, m, c * NH:(c + 1) * NH], g_T[:, g % 2, :],
                                                    ps[:, 2 * g + 1, :], ALU.mult
                                                    ).then_inc(gated, 1)
            project_add(nc, env, "f2_down", h_T, wd, None, env.x,
                        loads=weights_of((e + 1) % (E + 1)),
                        weigh=lambda t, e=e: comb[:, t, bass.ds(e, 1)])


def l3_xattn(nc, env, d):
    SCALE = float(D / H) ** 0.5
    mem, sb = scoped(nc, "x3")
    with mem:
        wq, wk, wv = (sb(n, [P, KT, D]) for n in ("wq", "wk", "wv"))
        bq, bk, bv = sb("bq", [P, KT]), sb("bk", [P, KT]), sb("bv", [1, D])
        q_T, q2_T, att_T = (sb(n, [P, KT, N]) for n in ("q_T", "q2_T", "att_T"))
        ctx_T = [sb(f"ctx_T{r}", [P, 2, KT, SK]) for r in range(1)]
        ctx_n = [sb(f"ctx_n{r}", [P, 2, CT, D]) for r in range(1)]
        q_own, q0_own = sb("q_own", [P, KT, P]), sb("q0_own", [P, KT, P])
        sc, p_T = sb("sc", [P, SK]), sb("p_T", [P, CT, P])
        small = sb("small", [P, 4])
        ps = env.ps
        layernorm(nc, env, "x3_ln", env.x, env.h, env.h_T, loads=[
            (wq[:, :, :], wview(d["L3_xattn_Wq"])), (wk[:, :, :], wview(d["L3_xattn_Wk"])),
            (wv[:, :, :], wview(d["L3_xattn_Wv"])), (bq[:, :], d["L3_xattn_bq"]),
            (bk[:, :], d["L3_xattn_bk"]), (bv[:, :], d["L3_xattn_bv"].unsqueeze(0))])
        linear_T(nc, env, "x3_q", [(env.h_T, wq, q_T, bq, None)])
        linear_T(nc, env, "x3_q2", [(q_T, wk, q2_T, None, None)])
        ctx_T, ctx_n = ctx_T[0], ctx_n[0]
        with signals(nc, "x3_pre", "loaded") as (loaded,):
            with nc.Block() as block:

                @block.sync
                def _(sp):
                    for b in range(2):
                        sp.dma_start(ctx_T[:, b, :, :], d["ctx_T"][b].rearrange(
                            "(k p) n -> p k n", p=P)).then_inc(loaded, 16)
                    sp.wait_ge(loaded, 32)

        with nc.Fori(0, T) as i:
            with signals(nc, "x3_at", "next_T rows_in own q_in s_done shift_ready exped scaled "
                         "turned act_out dve_out u_done u_out") as (
                    next_T, rows_in, own, q_in, s_done, shift_ready, exped, scaled, turned,
                    act_out, dve_out, u_done, u_out):
                with nc.Block() as block:

                    @block.sync
                    def _(sp):
                        for b in range(2):
                            sp.dma_start(ctx_n[:, b, 0:CT - 1, :],
                                         d["ctx"][2 * i + b, 0:(CT - 1) * P, :].rearrange(
                                             "(t p) f -> p t f", p=P)).then_inc(rows_in, 16)
                            sp.dma_start(ctx_n[0:LAST, b, CT - 1, :],
                                         d["ctx"][2 * i + b, (CT - 1) * P:SK, :]
                                         ).then_inc(rows_in, 16)
                        sp.wait_ge(s_done, 1)
                        for b in range(2):
                            sp.dma_start(ctx_T[:, b, :, :], d["ctx_T"][(2 * i + 2) % B + b]
                                         .rearrange("(k p) n -> p k n", p=P)).then_inc(next_T, 16)
                        sp.wait_ge(next_T, 32)

                    @block.tensor
                    def _(pe):
                        pe.wait_ge(q_in, 2)
                        for k in range(KT):
                            nc.tensor.matmul(ps[:, 4, 0:1], q0_own[:, k, :], bk[:, k:k + 1],
                                             start=(k == 0), stop=(k == KT - 1))
                        for b in range(2):
                            for c, (at, n) in enumerate(CHUNKS):
                                for k in range(KT):
                                    last = nc.tensor.matmul(
                                        ps[b * S:(b + 1) * S, c, 0:n],
                                        q_own[:, k, b * S:(b + 1) * S],
                                        ctx_T[:, b, k, at:at + n], start=(k == 0),
                                        stop=(k == KT - 1))
                        last.then_inc(s_done, 1)
                        pe.wait_ge(scaled, 1)
                        for t in range(CT):
                            n = keys_of(t)
                            last = nc.tensor.transpose(ps[0:n, 4 + t // 4, (t % 4) * P:
                                                          (t % 4 + 1) * P],
                                                       sc[:, t * P:t * P + n], env.ident)
                            if t % 4 == 3 or t == CT - 1:
                                last.then_inc(turned, 1)
                        pe.wait_ge(act_out, 2)
                        pe.wait_ge(dve_out, 2)
                        pe.wait_ge(rows_in, 64)
                        for b in range(2):
                            for f in range(KT):
                                for t in range(CT):
                                    n = keys_of(t)
                                    last = nc.tensor.matmul(
                                        ps[:, 0, f * P + b * S:f * P + (b + 1) * S],
                                        ctx_n[0:n, b, t, f * P:(f + 1) * P],
                                        p_T[0:n, t, b * S:(b + 1) * S], start=(t == 0),
                                        stop=(t == CT - 1))
                        last.then_inc(u_done, 1)

                    @block.scalar
                    def _(act):
                        cols = bass.ds(i * P, P)
                        nc.scalar.copy(q_own[:, :, :], q2_T[:, :, cols]).then_inc(q_in, 1)
                        nc.scalar.copy(q0_own[:, :, :], q_T[:, :, cols]).then_inc(q_in, 1)
                        act.wait_ge(shift_ready, 1)
                        nc.scalar.activation(sc[:, :], ps[:, 0:4, :].rearrange(
                            "p c n -> p (c n)")[:, 0:SK], ACT.Exp, scale=SCALE,
                            bias=small[:, 2:3], accum_out=small[:, 3:4]).then_inc(exped, 1)
                        for g in (0, 2):
                            act.wait_ge(turned, g + 1)
                            nc.scalar.copy(p_T[:, 4 * g:4 * g + 4, :].rearrange(
                                "p t n -> p (t n)"), ps[:, 4 + g, :]).then_inc(act_out, 1)
                        act.wait_ge(u_done, 1)
                        nc.scalar.copy(att_T[:, :, cols], ps[:, 0, 0:2 * P].rearrange(
                            "p (k n) -> p k n", k=KT)).then_inc(u_out, 1)

                    @block.vector
                    def _(dve):
                        steps = Steps(dve, own)
                        dve.wait_ge(s_done, 1)
                        steps.done(nc.vector.tensor_reduce(
                            small[:, 0:1], ps[:, 0:4, :].rearrange("p c n -> p (c n)")[:, 0:SK],
                            AX, ALU.max))
                        steps.done(nc.vector.tensor_copy(small[:, 1:2], ps[:, 4, 0:1]))
                        steps.wait()
                        steps.done(nc.vector.tensor_tensor(small[:, 0:1], small[:, 0:1],
                                                           small[:, 1:2], ALU.add))
                        steps.wait()
                        steps.done(nc.vector.tensor_tensor(small[:, 2:3], small[:, 1:2],
                                                           small[:, 0:1], ALU.subtract))
                        steps.wait()
                        nc.vector.tensor_scalar(small[:, 2:3], small[:, 2:3], SCALE, None,
                                                ALU.mult).then_inc(shift_ready, 1)
                        dve.wait_ge(exped, 1)
                        steps.done(nc.vector.reciprocal(small[:, 3:4], small[:, 3:4]))
                        steps.wait()
                        nc.vector.tensor_scalar(sc[:, :], sc[:, :], small[:, 3:4], None,
                                                ALU.mult).then_inc(scaled, 1)
                        dve.wait_ge(turned, 2)
                        nc.vector.tensor_copy(p_T[:, 4:8, :].rearrange("p t n -> p (t n)"),
                                              ps[:, 5, :]).then_inc(dve_out, 1)
                        dve.wait_ge(turned, 4)
                        nc.vector.tensor_copy(p_T[0:LAST, 12, :], ps[0:LAST, 7, 0:P]
                                              ).then_inc(dve_out, 1)
        project_add(nc, env, "x3_v", att_T, wv, bv[:, :], env.x)


def l3_attn(nc, env, d):
    NB = 32
    mem, sb = scoped(nc, "a3")
    with mem:
        w, wo = sb("w", [P, KT, 3 * D]), sb("wo", [P, KT, D])
        b_col, b_row = sb("b_col", [P, 2 * KT]), sb("b_row", [1, 2, D])
        att_T, bias = sb("att_T", [P, KT, N]), sb("bias", [P, H, P])
        rel, onehot = sb("rel", [NB, H]), sb("onehot", [NB, S, P], BF16)
        onehot_f, causal = sb("onehot_f", [NB, 16, P]), sb("causal", [P, P])
        ps = env.ps
        layernorm(nc, env, "a3_ln", env.x, env.h, env.h_T, loads=[
            (w[:, :, :], wview(d["L3_attn_W_attn"])), (wo[:, :, :], wview(d["L3_attn_W_proj"])),
            (b_col[:, :], d["L3_attn_b_qk"]),
            (b_row[:, 0, :], d["L3_attn_b_attn"][2 * D:3 * D].unsqueeze(0)),
            (b_row[:, 1, :], d["L3_attn_b_proj"].unsqueeze(0)),
            (rel[:, :], d["L3_attn_rel_emb"]), (onehot[:, :, :], d["buckets"]),
            (causal[:, :], d["causal"])])
        with signals(nc, "a3_bias", "widened product placed own") as (
                widened, product, placed, own):
            with nc.Block() as block:

                @block.gpsimd
                def _(pool):
                    for g in range(4):
                        if g:
                            pool.wait_ge(product, g)
                        nc.gpsimd.tensor_copy(onehot_f[:, :, :],
                                              onehot[:, 16 * g:16 * g + 16, :]
                                              ).then_inc(widened, 1)

                @block.tensor
                def _(pe):
                    for g in range(4):
                        pe.wait_ge(widened, g + 1)
                        for k in range(16):
                            last = nc.tensor.matmul(ps[:, g // 2, (16 * (g % 2) + k) * H:
                                                       (16 * (g % 2) + k + 1) * H],
                                                    onehot_f[:, k, :], rel[:, :], start=True,
                                                    stop=True)
                        last.then_inc(product, 1)

                @block.vector
                def _(dve):
                    steps = Steps(dve, own)
                    dve.wait_ge(product, 4)
                    for half in range(2):
                        for b in range(2):
                            at = b * S + 32 * half
                            steps.done(nc.vector.tensor_copy(
                                bias[:, :, at:at + 32],
                                ps[:, half, :].rearrange("p (k h) -> p h k", h=H)))
                    steps.wait()
                    nc.vector.tensor_tensor(bias[:, :, :], bias[:, :, :],
                                            causal[:, :].unsqueeze(1).broadcast_to([P, H, P]),
                                            ALU.add).then_inc(placed, 1)
        self_attention(nc, env, "a3", w, b_col, b_row[:, 0, :], att_T, DH ** -0.5, bias, True, sb)
        project_add(nc, env, "a3_o", att_T, wo, b_row[:, 1, :], env.x)


def l3_ffn(nc, env, d):
    MAGIC = 1.5 * 2.0 ** 23
    mem, sb = scoped(nc, "q3")
    with mem:
        w8, w16 = sb("w8", [P, KT, D // 4], I32), sb("w16", [P, KT, D], BF16)
        wscale, bias = sb("wscale", [P, D]), sb("bias", [P, D])
        amax, scale = sb("amax", [P, T]), sb("scale", [P, T])
        xq, xq16 = sb("xq", [P, T, D]), sb("xq16", [P, T, D], BF16)
        x_T, ident16 = sb("x_T", [P, KT, N], BF16), sb("ident16", [P, P], BF16)
        out, sbc = sb("out", [P, T, D]), sb("sbc", [P, T, D])
        ps = env.ps
        layernorm(nc, env, "q3_ln", env.x, env.h, None, loads=[
            (w8[:, :, :], wview(d["L3_ffn_weight_q"])),
            (wscale[:, :], d["L3_ffn_weight_scale"].partition_broadcast(P)),
            (bias[:, :], d["L3_ffn_bias"].partition_broadcast(P))])
        with signals(nc, "q3", "own cast quantised turned x_out product out_ready") as (
                own, cast, quantised, turned, x_out, product, out_ready):
            with nc.Block() as block:

                @block.scalar
                def _(act):
                    nc.scalar.copy(w16[:, :, :], w8[:, :, :].bitcast(I8)).then_inc(cast, 1)
                    nc.scalar.copy(ident16[:, :], env.ident).then_inc(cast, 1)
                    for t in range(T):
                        act.wait_ge(turned, t + 1)
                        nc.scalar.copy(x_T[:, :, t * P:(t + 1) * P],
                                       ps[:, t % 2, :].bitcast(BF16)[:, 0:2 * P].rearrange(
                                           "p (k n) -> p k n", k=KT)).then_inc(x_out, 1)

                @block.tensor
                def _(pe):
                    pe.wait_ge(cast, 2)
                    for t in range(T):
                        pe.wait_ge(quantised, t + 1)
                        if t >= 2:
                            pe.wait_ge(x_out, t - 1)
                        for f in range(KT):
                            last = nc.tensor.transpose(
                                ps[:, t % 2, :].bitcast(BF16)[:, f * P:(f + 1) * P],
                                xq16[:, t, f * P:(f + 1) * P], ident16[:, :])
                        last.then_inc(turned, 1)
                    for t in range(T):
                        pe.wait_ge(x_out, t + 1)
                        if t >= 4:
                            pe.wait_ge(out_ready, t - 3)
                        for k in range(KT):
                            last = nc.tensor.matmul(ps[:, 4 + t % 4, 0:D],
                                                    x_T[:, k, t * P:(t + 1) * P], w16[:, k, :],
                                                    start=(k == 0), stop=(k == KT - 1))
                        last.then_inc(product, 1)

                @block.vector
                def _(dve):
                    steps = Steps(dve, own)
                    steps.done(nc.vector.tensor_reduce(amax[:, :], env.h[:, :, :], AX, ALU.max,
                                                       apply_absolute_value=True))
                    steps.wait()
                    steps.done(nc.vector.tensor_scalar(scale[:, :], amax[:, :], 1e-6, 1.0 / 127.0,
                                                       ALU.max, ALU.mult))
                    steps.wait()
                    steps.done(nc.vector.reciprocal(amax[:, :], scale[:, :]))
                    steps.wait()
                    for t in range(T):
                        steps.done(nc.vector.tensor_scalar(xq[:, t, :], env.h[:, t, :],
                                                           amax[:, t:t + 1], MAGIC, ALU.mult,
                                                           ALU.add))
                    steps.wait()
                    for t in range(T):
                        steps.done(nc.vector.tensor_scalar(xq[:, t, :], xq[:, t, :], MAGIC, None,
                                                           ALU.subtract))
                    steps.wait()
                    for t in range(T):
                        nc.vector.tensor_scalar(xq16[:, t, :], xq[:, t, :], 127.0, -128.0, ALU.min,
                                                ALU.max).then_inc(quantised, 1)
                    for t in range(T):
                        dve.wait_ge(product, t + 1)
                        nc.vector.scalar_tensor_tensor(
                            out=out[:, t, :], in0=ps[:, 4 + t % 4, 0:D], scalar=scale[:, t:t + 1],
                            in1=wscale[:, :], op0=ALU.mult, op1=ALU.mult).then_inc(out_ready, 1)
                    dve.wait_ge(out_ready, T)
                    steps.done(nc.vector.tensor_tensor(
                        out[:, :, :], out[:, :, :],
                        bias[:, :].unsqueeze(1).broadcast_to([P, T, D]), ALU.add))
                    steps.wait()
                    steps.done(nc.vector.tensor_tensor(env.x[:, :, :], env.x[:, :, :],
                                                       out[:, :, :], ALU.add))



SUBLAYERS = {"L0_xattn": l0_xattn, "L0_attn": l0_attn, "L0_ffn": l0_ffn,
             "L1_xattn": l1_xattn, "L1_attn": l1_attn,
             "L1_ffn": l1_ffn,
             "L2_xattn": l2_xattn, "L2_attn": l2_attn, "L2_ffn": l2_ffn,
             "L3_xattn": l3_xattn, "L3_attn": l3_attn, "L3_ffn": l3_ffn}

def constants():
    p = np.arange(P)[:, None]
    c = np.arange(P)[None, :]
    ident = (p == c)
    parts = {
        "ident": ident,
        "fold": ident[:, 0:S] | ident[:, S:P],
        "ones": np.ones((P, P)),
        "same_head": (p // DH == c // DH),
        "own_head": (p // S == c[:, 0:2 * DH] // DH),
        "head_of": (p // DH == c[:, 0:HPT]),
        "tril_min": np.where(c[:, 0:S] <= p % S, -3e38, 0.0),
        "key_le_q": (p <= c[:, 0:S]),
        "zero": np.zeros((P, 1)),
        "iota8": np.tile(np.arange(8), (P, 1)),
        "valid_last": np.repeat(p < LAST, P, 1),
        "cross": np.where(p // S == c // S, 0.0, -1e30),
        "which_head": (p // S == c[:, 0:2]),
        "tenth": np.full((P, 1), 0.1),
        "eps5": np.full((P, 1), 1e-5),
        "eps6": np.full((P, 1), 1e-6),
    }
    at, where, arrays = 0, {}, []
    for name, a in parts.items():
        arrays.append(np.asarray(a, np.float32))
        where[name] = (at, at + a.shape[1])
        at += a.shape[1]
    return np.ascontiguousarray(np.concatenate(arrays, 1)), where


def build(nc, d, out, where, names):
    with ExitStack() as mem:
        def sb(name, shape, dt=F32):
            return mem.enter_context(nc.sbuf_tensor(name, shape, dt))

        env = Env()
        env.x = sb("x", [P, T, D])
        env.h = sb("h", [P, T, D])
        env.h_T = sb("h_T", [P, KT, N])
        env.rows = sb("rows", [P, T, D])
        env.bn, env.mv = sb("bn", [P, T, 6]), sb("mv", [P, T, 2])
        env.std, env.rstd = sb("std", [P, T]), sb("rstd", [P, T])
        consts = sb("consts", [P, d["consts"].shape[1]])
        env.ident = consts[:, where["ident"][0]:where["ident"][1]]
        env.fold = consts[:, where["fold"][0]:where["fold"][1]]
        env.ones = consts[:, where["ones"][0]:where["ones"][1]]
        env.same_head = consts[:, where["same_head"][0]:where["same_head"][1]]
        env.own_head = consts[:, where["own_head"][0]:where["own_head"][1]]
        env.head_of = consts[:, where["head_of"][0]:where["head_of"][1]]
        env.tril_min = consts[:, where["tril_min"][0]:where["tril_min"][1]]
        env.key_le_q = consts[:, where["key_le_q"][0]:where["key_le_q"][1]]
        env.iota8 = consts[:, where["iota8"][0]:where["iota8"][1]]
        env.valid_last = consts[:, where["valid_last"][0]:where["valid_last"][1]]
        env.cross = consts[:, where["cross"][0]:where["cross"][1]]
        env.which_head = consts[:, where["which_head"][0]:where["which_head"][1]]
        env.tenth = consts[:, where["tenth"][0]:where["tenth"][1]]
        env.zero = consts[:, where["zero"][0]:where["zero"][1]]
        env.eps5 = consts[:, where["eps5"][0]:where["eps5"][1]]
        env.eps6 = consts[:, where["eps6"][0]:where["eps6"][1]]
        env.ps = mem.enter_context(nc.psum_tensor("ps", [P, 8, NH], F32))

        with signals(nc, "start", "x_in consts_in") as (x_in, consts_in):
            with nc.Block() as block:

                @block.sync
                def _(sp):
                    sp.dma_start(env.x[:, :, :], d["x"].rearrange("(t b) s n -> (b s) t n", b=2)
                                 ).then_inc(x_in, 16)
                    sp.dma_start(consts[:, :], d["consts"]).then_inc(consts_in, 16)
                    sp.wait_ge(x_in, 16)
                    sp.wait_ge(consts_in, 16)

        for name in names:
            SUBLAYERS[name](nc, env, d)

        with signals(nc, "end", "stored") as (stored,):
            with nc.Block() as block:

                @block.sync
                def _(sp):
                    sp.dma_start(out.rearrange("(t b) s n -> (b s) t n", b=2), env.x[:, :, :]
                                 ).then_inc(stored, 16)
                    sp.wait_ge(stored, 16)


def arrange(inputs):
    a = {}
    for name, v in inputs.items():
        a[name] = np.ascontiguousarray(v)
    a["ctx"] = a.pop("ctx_1024")
    a["ctx_T"] = np.ascontiguousarray(np.transpose(a["ctx"], (0, 2, 1)))
    a["mask_T"] = np.ascontiguousarray(np.transpose(a.pop("mask_BxSxS2_bk0"), (0, 2, 1))
                                       ).view(np.int32)
    def columns(name):
        v = a[name]
        a[name] = np.ascontiguousarray(np.swapaxes(v.reshape(*v.shape[:-1], -1, P), -1, -2))

    for name in ("bq", "b1", "ln1_s", "ln1_b", "ln2_s", "ln2_b"):
        columns("L0_attn_" + name)
    a["L0_ffn_gate_w"] = np.ascontiguousarray(a["L0_ffn_gate_w"].T)
    columns("L0_ffn_b1")
    a["L0_ffn_b1"] = np.ascontiguousarray(np.swapaxes(a["L0_ffn_b1"], 0, 1))
    for name in ("L1_xattn_Wq", "L1_xattn_Wv", "L1_xattn_gru_wih", "L1_xattn_gru_whh",
                 "L1_attn_w_qkv", "L1_attn_w_o", "L2_xattn_Wq", "L2_xattn_Wkv", "L2_xattn_Wo",
                 "L2_ffn_gate_w", "L3_xattn_Wq", "L3_xattn_Wv", "L3_attn_W_attn",
                 "L3_attn_W_proj", "L3_ffn_weight_q"):
        a[name] = np.ascontiguousarray(a[name].T)
    for name in ("slot_norm_w", "input_norm_w", "gru_bih", "gru_bhh"):
        columns("L1_xattn_" + name)
    a["L1_attn_b_qk"] = a["L1_attn_b_qkv"][0:2 * D]
    columns("L1_attn_b_qk")
    a["L1_ffn_expert_w1"] = np.ascontiguousarray(
        np.transpose(a["L1_ffn_expert_w1"], (1, 0, 2))).reshape(2 * D, -1)
    a["L1_ffn_expert_w2"] = a["L1_ffn_expert_w2"].reshape(-1, 3 * D)
    a["L1_ffn_expert_b1"] = a["L1_ffn_expert_b1"].reshape(-1)
    a["L1_ffn_shared_weight"] = a["L1_ffn_shared_weight"].reshape(1)
    columns("L1_ffn_expert_b1")
    columns("L1_ffn_refine_b1")
    proj = np.transpose(a["L2_attn_projection"], (0, 2, 1)).reshape(KT, P, 1, 64)
    a["proj_rows"] = np.ascontiguousarray(np.transpose(
        np.broadcast_to(proj, (KT, P, HPT, 64)), (1, 0, 2, 3)))
    for new, one, shared in (("L2_w_gate", "L2_ffn_w_gate", "L2_ffn_shared_gate_w"),
                             ("L2_w_up", "L2_ffn_w_up", "L2_ffn_shared_up_w"),
                             ("L2_w_down", "L2_ffn_w_down", "L2_ffn_shared_down_w")):
        both = np.concatenate([a.pop(one), a.pop(shared)[None]], 0)
        a[new] = np.ascontiguousarray(np.transpose(both, (0, 2, 1)))
    a["L3_ffn_weight_q"] = a["L3_ffn_weight_q"].view(np.int32)
    columns("L3_xattn_bq")
    columns("L3_xattn_bk")
    a["L3_attn_b_qk"] = a["L3_attn_b_attn"][0:2 * D]
    columns("L3_attn_b_qk")
    rp = -np.minimum(np.arange(S)[None, :] - np.arange(S)[:, None], 0)
    large = 16 + (np.log(rp.astype(np.float32) / np.float32(16) + np.float32(1e-10))
                  / np.float32(np.log(8.0)) * np.float32(16)).astype(np.int32)
    bucket = np.where(rp < 16, rp, np.minimum(large, 31))
    hot = (np.arange(32)[:, None, None] == bucket.T[None, :, :])
    a["buckets"] = np.tile(hot, (1, 1, 2)).astype(mybir.dt.np(BF16))
    at = np.arange(P)
    seen = (at[:, None] // S == at[None, :] // S) & (at[None, :] % S <= at[:, None] % S)
    a["causal"] = np.where(seen, 0.0, -1e30).astype(np.float32)
    a["expert_sel"] = np.ascontiguousarray(
        np.arange(8)[:, None, None] == 2 * np.arange(4)[None, :, None]
        + np.arange(P)[None, None, :] // 64).astype(np.float32)
    half = D // 2
    freq = np.exp(np.arange(half, dtype=np.float32) * np.float32(-np.log(10000.0) / (half - 1)))
    pos = (np.arange(S, dtype=np.float32) + 1.0)[:, None] * freq[None, :]
    a["pos"] = np.tile(np.concatenate([np.sin(pos), np.cos(pos)], -1).astype(np.float32), (2, 1))
    return a


def kernel(**inputs):
    import concourse.bacc as bacc
    from concourse.bass_utils import run_bass_kernel_spmd

    arrays = arrange(inputs)
    arrays["consts"], where = constants()
    nc = bacc.Bacc("TRN2", target_bir_lowering=False, num_devices=1)
    d = {n: nc.dram_tensor(f"in_{n}", a.shape, mybir.dt.from_np(a.dtype),
                           kind="ExternalInput").ap() for n, a in arrays.items()}
    out = nc.dram_tensor("out", (B, S, D), F32, kind="ExternalOutput").ap()
    build(nc, d, out, where, list(SUBLAYERS))
    r = run_bass_kernel_spmd(nc, [{f"in_{n}": a for n, a in arrays.items()}], core_ids=[0])
    return r.results[0]["out"]
```

```python
from contextlib import ExitStack, contextmanager

import numpy as np

import concourse.bass as bass
from concourse import mybir

F32 = mybir.dt.float32
BF16 = mybir.dt.bfloat16
U8 = mybir.dt.uint8
I8 = mybir.dt.int8
I32 = mybir.dt.int32
U32 = mybir.dt.uint32
ACT = mybir.ActivationFunctionType
ALU = mybir.AluOpType
AX = mybir.AxisListType.X

P = 128
B = 16
S = 64
D = 256
KT = D // P
T = B * S // P
N = B * S
NH = 512
H = 16
DH = D // H
HPT = P // DH
PAIRS = H // 2
SK = 1601
CT = -(-SK // P)
LAST = SK - (CT - 1) * P
BANKFULS = [(c, min(NH, SK - c)) for c in range(0, SK, NH)]
CHUNK = -(-SK // len(BANKFULS))
CHUNKS = [(c, min(CHUNK, SK - c)) for c in range(0, SK, CHUNK)]


@contextmanager
def signals(nc, stage, names):
    held = [nc.alloc_semaphore(f"{stage}_{n}") for n in names.split()]
    yield held
    nc.clear_and_free_semaphores(held)
    nc.all_engine_barrier()


class Steps:

    def __init__(self, eng, sem):
        self.eng, self.sem, self.n = eng, sem, 0

    def done(self, ins):
        self.n += 1
        ins.then_inc(self.sem, 1)

    def wait(self):
        self.eng.wait_ge(self.sem, self.n)


class Env:
    pass


def keys_of(k):
    return P if k < CT - 1 else LAST


def load_all(sp, loads, sem):
    for dst, src in loads:
        sp.dma_start(dst, src).then_inc(sem, 16)
    if loads:
        sp.wait_ge(sem, 16 * len(loads))


def wview(ap):
    return ap.rearrange("(k p) n -> p k n", p=P)


def layernorm(nc, env, stage, src, nat, dst_T, affine=None, early=(), loads=()):
    with signals(nc, stage, "loaded early own stats std rows turned act_out dve_out") as (
            loaded, affine_in, own, stats, std_ready, rows_ready, turned, act_out, dve_out):
        with nc.Block() as block:

            @block.sync
            def _(sp):
                load_all(sp, early, affine_in)
                load_all(sp, loads, loaded)

            @block.vector
            def _(dve):
                steps = Steps(dve, own)
                for t in range(T):
                    steps.done(nc.vector.bn_stats(env.bn[:, t, :], src[:, t, :]))
                steps.wait()
                for t in range(T):
                    nc.vector.bn_aggr(env.mv[:, t, :], env.bn[:, t, :]).then_inc(stats, 1)
                dve.wait_ge(std_ready, 1)
                steps.done(nc.vector.reciprocal(env.rstd[:, :], env.std[:, :]))
                steps.wait()
                for t in range(T):
                    nc.vector.tensor_scalar(nat[:, t, :], src[:, t, :], env.mv[:, t, 0:1],
                                            env.rstd[:, t:t + 1], ALU.subtract,
                                            ALU.mult).then_inc(rows_ready, 1)
                if early:
                    dve.wait_ge(affine_in, 16 * len(early))
                for half in range(2 if dst_T is not None else 0):
                    dve.wait_ge(turned, 2 * half + 2)
                    out, put = dst_T[:, 1, half * NH:(half + 1) * NH], env.ps[:, 2 * half + 1, :]
                    if affine is None:
                        nc.vector.tensor_copy(out, put).then_inc(dve_out, 1)
                    else:
                        nc.vector.tensor_scalar(out, put, affine[0][:, 1:2], affine[1][:, 1:2],
                                                ALU.mult, ALU.add).then_inc(dve_out, 1)

            @block.scalar
            def _(act):
                act.wait_ge(stats, T)
                nc.scalar.activation(env.std[:, :], env.mv[:, :, 1], ACT.Sqrt,
                                     bias=env.eps5[:, 0:1]).then_inc(std_ready, 1)
                if early:
                    act.wait_ge(affine_in, 16 * len(early))
                for half in range(2 if dst_T is not None else 0):
                    act.wait_ge(turned, 2 * half + 1)
                    out, put = dst_T[:, 0, half * NH:(half + 1) * NH], env.ps[:, 2 * half, :]
                    if affine is None:
                        nc.scalar.copy(out, put).then_inc(act_out, 1)
                    else:
                        nc.scalar.activation(out, put, ACT.Identity, scale=affine[0][:, 0:1],
                                             bias=affine[1][:, 0:1]).then_inc(act_out, 1)

            @block.tensor
            def _(pe):
                for half in range(2 if dst_T is not None else 0):
                    pe.wait_ge(rows_ready, 4 * half + 4)
                    for f in range(KT):
                        for t in range(4):
                            last = nc.tensor.transpose(
                                env.ps[:, 2 * half + f, t * P:(t + 1) * P],
                                nat[:, 4 * half + t, f * P:(f + 1) * P], env.ident)
                        last.then_inc(turned, 1)


def turn_rows(nc, env, stage, nat, dst_T, loads=()):
    with signals(nc, stage, "loaded turned act_out dve_out") as (loaded, turned, act_out, dve_out):
        with nc.Block() as block:

            @block.sync
            def _(sp):
                load_all(sp, loads, loaded)

            @block.tensor
            def _(pe):
                for half in range(2):
                    for f in range(KT):
                        for t in range(4):
                            last = nc.tensor.transpose(
                                env.ps[:, 2 * half + f, t * P:(t + 1) * P],
                                nat[:, 4 * half + t, f * P:(f + 1) * P], env.ident)
                        last.then_inc(turned, 1)

            @block.vector
            def _(dve):
                for half in range(2):
                    dve.wait_ge(turned, 2 * half + 2)
                    nc.vector.tensor_copy(dst_T[:, 1, half * NH:(half + 1) * NH],
                                          env.ps[:, 2 * half + 1, :]).then_inc(dve_out, 1)

            @block.scalar
            def _(act):
                for half in range(2):
                    act.wait_ge(turned, 2 * half + 1)
                    nc.scalar.copy(dst_T[:, 0, half * NH:(half + 1) * NH],
                                   env.ps[:, 2 * half, :]).then_inc(act_out, 1)


def add_turned(nc, env, stage, src_T, dst):
    with signals(nc, stage, "turned added") as (turned, added):
        with nc.Block() as block:

            @block.tensor
            def _(pe):
                for t in range(T):
                    for f in range(KT):
                        last = nc.tensor.transpose(env.ps[:, t, f * P:(f + 1) * P],
                                                   src_T[:, f, t * P:(t + 1) * P], env.ident)
                    last.then_inc(turned, 1)

            @block.vector
            def _(dve):
                for t in range(T):
                    dve.wait_ge(turned, t + 1)
                    nc.vector.tensor_tensor(dst[:, t, :], dst[:, t, :], env.ps[:, t, 0:D],
                                            ALU.add).then_inc(added, 1)


def linear_T(nc, env, stage, parts, loads=()):
    groups = []
    for in_T, w, out_T, bias, func in parts:
        n_out = w.shape[2]
        for m in range(-(-n_out // P)):
            rows = min(P, n_out - m * P)
            for c in range(2):
                groups.append((in_T, w, out_T, bias, func, m, rows, c))
    on_act = [func not in (None, "relu") or g % 2 == 0
              for g, (_, _, _, _, func, _, _, _) in enumerate(groups)]
    act_before = [sum(on_act[:g]) for g in range(len(groups) + 1)]
    dve_before = [g - a for g, a in enumerate(act_before)]
    with signals(nc, stage, "loaded product act_out dve_out") as (
            loaded, product, act_out, dve_out):
        with nc.Block() as block:

            @block.sync
            def _(sp):
                load_all(sp, loads, loaded)

            @block.tensor
            def _(pe):
                for g, (in_T, w, out_T, bias, func, m, rows, c) in enumerate(groups):
                    if g >= 8:
                        if on_act[g - 8]:
                            pe.wait_ge(act_out, act_before[g - 7])
                        else:
                            pe.wait_ge(dve_out, dve_before[g - 7])
                    kts = w.shape[1]
                    for k in range(kts):
                        last = nc.tensor.matmul(env.ps[0:rows, g % 8, :],
                                                w[:, k, m * P:m * P + rows],
                                                in_T[:, k, c * NH:(c + 1) * NH],
                                                start=(k == 0), stop=(k == kts - 1))
                    last.then_inc(product, 1)

            @block.scalar
            def _(act):
                for g, (in_T, w, out_T, bias, func, m, rows, c) in enumerate(groups):
                    if not on_act[g]:
                        continue
                    act.wait_ge(product, g + 1)
                    kind = {None: ACT.Identity, "relu": ACT.Relu, "gelu": ACT.Gelu}[func]
                    nc.scalar.activation(
                        out_T[0:rows, m, c * NH:(c + 1) * NH], env.ps[0:rows, g % 8, :], kind,
                        bias=bias[0:rows, m:m + 1] if bias is not None else env.zero[0:rows, 0:1],
                    ).then_inc(act_out, 1)

            @block.vector
            def _(dve):
                for g, (in_T, w, out_T, bias, func, m, rows, c) in enumerate(groups):
                    if on_act[g]:
                        continue
                    dve.wait_ge(product, g + 1)
                    out, put = out_T[0:rows, m, c * NH:(c + 1) * NH], env.ps[0:rows, g % 8, :]
                    if func == "relu":
                        ins = nc.vector.tensor_scalar(
                            out, put, bias[0:rows, m:m + 1] if bias is not None else 0.0, 0.0,
                            ALU.add, ALU.max)
                    elif bias is not None:
                        ins = nc.vector.tensor_scalar(out, put, bias[0:rows, m:m + 1], None, ALU.add)
                    else:
                        ins = nc.vector.tensor_copy(out, put)
                    ins.then_inc(dve_out, 1)


def linear_rows(nc, env, stage, in_T, parts, loads=()):
    groups = [(t, w, bias, dst) for w, bias, dst in parts for t in range(T)]
    with signals(nc, stage, "loaded product taken") as (loaded, product, taken):
        with nc.Block() as block:

            @block.sync
            def _(sp):
                load_all(sp, loads, loaded)

            @block.tensor
            def _(pe):
                for g, (t, w, bias, dst) in enumerate(groups):
                    if g >= 8:
                        pe.wait_ge(taken, g - 7)
                    kts = w.shape[1]
                    for k in range(kts):
                        last = nc.tensor.matmul(env.ps[:, g % 8, 0:D], in_T[:, k, t * P:(t + 1) * P],
                                                w[:, k, :], start=(k == 0), stop=(k == kts - 1))
                    last.then_inc(product, 1)

            @block.vector
            def _(dve):
                for g, (t, w, bias, dst) in enumerate(groups):
                    out, put = dst(t), env.ps[:, g % 8, 0:D]
                    if len(out.shape) == 3:
                        put, bias = (x.rearrange("p (a b) -> p a b", a=out.shape[1])
                                     for x in (put, bias))
                    dve.wait_ge(product, g + 1)
                    nc.vector.tensor_tensor(out, put, bias, ALU.add).then_inc(taken, 1)


def project_add(nc, env, stage, act_T, w, bias, dst, loads=(), also=None, scale=None,
                weigh=None):
    kts = w.shape[1]
    with signals(nc, stage, "loaded own product added") as (
            loaded, own, product, added):
        with nc.Block() as block:

            @block.sync
            def _(sp):
                load_all(sp, loads, loaded)

            @block.tensor
            def _(pe):
                for t in range(T):
                    for k in range(kts):
                        last = nc.tensor.matmul(env.ps[:, t, 0:D], act_T[:, k, t * P:(t + 1) * P],
                                                w[:, k, :], start=(k == 0), stop=(k == kts - 1))
                    last.then_inc(product, 1)

            @block.vector
            def _(dve):
                steps = Steps(dve, own)
                if scale is not None and bias is not None:
                    steps.done(nc.vector.tensor_tensor(bias, bias, scale, ALU.mult))
                    steps.wait()
                for t in range(T):
                    if also is not None:
                        steps.done(nc.vector.tensor_tensor(dst[:, t, :], dst[:, t, :],
                                                           also[:, t, :], ALU.add))
                        steps.wait()
                    if bias is not None:
                        steps.done(nc.vector.tensor_tensor(dst[:, t, :], dst[:, t, :], bias,
                                                           ALU.add))
                        steps.wait()
                    put = env.ps[:, t, 0:D]
                    dve.wait_ge(product, t + 1)
                    if weigh is not None:
                        nc.vector.scalar_tensor_tensor(
                            out=dst[:, t, :], in0=put, scalar=weigh(t), in1=dst[:, t, :],
                            op0=ALU.mult, op1=ALU.add).then_inc(added, 1)
                        continue
                    if scale is not None:
                        steps.done(nc.vector.tensor_tensor(env.rows[:, t, :], put, scale, ALU.mult))
                        steps.wait()
                        put = env.rows[:, t, :]
                    nc.vector.tensor_tensor(dst[:, t, :], dst[:, t, :], put,
                                            ALU.add).then_inc(added, 1)


def context_heads(nc, env, stage, ctx, q_T, att_T, w_k, w_v, softmax, notmask=None, nb=None):
    with ExitStack() as mem:
        def sb(name, shape, dt=F32):
            return mem.enter_context(nc.sbuf_tensor(f"{stage}_{name}", shape, dt))

        ctx_T = sb("ctx_T", [P, KT, SK])
        k_T = sb("k_T", [P, KT, SK])
        v = sb("v", [P, CT, D])
        q_bd = sb("q_bd", [P, KT, HPT, S])
        sc = sb("sc", [P, CT, H, S])
        den_parts = sb("den_parts", [P, H, S])
        num, den = sb("num", [P, KT, S]), sb("den", [P, KT, S])
        if softmax:
            zeros = sb("zeros", [S, H, S])
            most = sb("most", [P, H, S])
            top = sb("top", [P, PAIRS])
            diag = sb("diag", [P, PAIRS, P])
            top_bc = sb("top_bc", [P, H, S])
        else:
            mask_in4 = sb("mask_in4", [P, CT, S // 4], I32)
            mask_u8 = mask_in4[:, :, :].bitcast(U8)
            cap = sb("cap", [P, CT, S])
        ps = env.ps
        two_banks = [ps[:, 2 * r:2 * r + 2, :].rearrange("p c n -> p (c n)") for r in range(4)]

        def heads(x):
            return x.rearrange("p (h s) -> p h s", h=H)

        def key_group(g, bank):
            m, (at, n) = g // len(CHUNKS), CHUNKS[g % len(CHUNKS)]
            for k in range(KT):
                last = nc.tensor.matmul(ps[:, bank, 0:n], w_k[:, k, m * P:(m + 1) * P],
                                        ctx_T[:, k, at:at + n], start=(k == 0), stop=(k == KT - 1))
            return last

        def take_keys(copy, g, bank):
            m, (at, n) = g // len(CHUNKS), CHUNKS[g % len(CHUNKS)]
            return copy(k_T[:, m, at:at + n], ps[:, bank, 0:n])

        def value_tile(t):
            n = keys_of(t)
            for k in range(KT):
                last = nc.tensor.matmul(ps[0:n, t % 4, 0:D], ctx_T[:, k, t * P:t * P + n],
                                        w_v[:, k, :], start=(k == 0), stop=(k == KT - 1))
            return last

        def take_values(copy, t):
            return copy(v[0:keys_of(t), t, :], ps[0:keys_of(t), t % 4, 0:D])

        def spread_queries(half, row):
            return nc.gpsimd.tensor_tensor(
                q_bd[:, half, :, :],
                q_T[:, half, bass.ds(row * S, S)].unsqueeze(1).broadcast_to([P, HPT, S]),
                env.head_of.unsqueeze(2).broadcast_to([P, HPT, S]), ALU.mult)

        KG = KT * len(CHUNKS)
        with signals(nc, stage + "_pre", "loaded q_ready k_product k_out v_product v_act v_dve") as (
                loaded, q_ready, k_product, k_out, v_product, v_act, v_dve):
            with nc.Block() as block:

                @block.sync
                def _(sp):
                    sp.dma_start(ctx_T[:, :, :], ctx[0].rearrange("(k p) n -> p k n", p=P)
                                 ).then_inc(loaded, 16)
                    sp.wait_ge(loaded, 16)

                @block.gpsimd
                def _(pool):
                    for half in range(KT):
                        spread_queries(half, 0).then_inc(q_ready, 1)

                @block.tensor
                def _(pe):
                    pe.wait_ge(loaded, 16)
                    for g in range(KG):
                        if g >= 4:
                            pe.wait_ge(k_out, g - 3)
                        key_group(g, g % 4).then_inc(k_product, 1)
                    for t in range(CT):
                        if t < 4:
                            pe.wait_ge(k_out, KG - 3 + t)
                        else:
                            pe.wait_ge((v_act, v_dve)[t % 2], t // 2 - 1)
                        value_tile(t).then_inc(v_product, 1)

                @block.scalar
                def _(act):
                    for g in range(KG):
                        act.wait_ge(k_product, g + 1)
                        take_keys(nc.scalar.copy, g, g % 4).then_inc(k_out, 1)
                    for t in range(0, CT, 2):
                        act.wait_ge(v_product, t + 1)
                        take_values(nc.scalar.copy, t).then_inc(v_act, 1)

                @block.vector
                def _(dve):
                    for t in range(1, CT, 2):
                        dve.wait_ge(v_product, t + 1)
                        take_values(nc.vector.tensor_copy, t).then_inc(v_dve, 1)

        with nc.Fori(0, B) as b:
            with signals(nc, stage, "next_ctx mask_in own s_product s_out p_in p_ready maxima "
                         "turned diag_ready bc_product bc_ready k_product k_act k_dve pv_done "
                         "q_ready den_out den_product v_product v_act v_dve") as (
                    next_ctx, mask_in, own, s_product, s_out, p_in, p_ready, maxima,
                    turned, diag_ready, bc_product, bc_ready, k_product, k_act, k_dve, pv_done,
                    q_ready, den_out, den_product, v_product, v_act, v_dve):

                def keys_taken(pe, g):
                    if softmax:
                        pe.wait_ge(k_act, g + 1)
                    else:
                        pe.wait_ge((k_act, k_dve)[g % 2], g // 2 + 1)

                with nc.Block() as block:

                    @block.sync
                    def _(sp):
                        if not softmax:
                            sp.dma_start(mask_in4[:, 0:CT - 1, :],
                                         notmask[b, 0:(CT - 1) * P, :].rearrange(
                                             "(t p) s -> p t s", p=P)).then_inc(mask_in, 16)
                            sp.dma_start(mask_in4[0:LAST, CT - 1, :],
                                         notmask[b, (CT - 1) * P:SK, :]).then_inc(mask_in, 16)
                        sp.dma_start(ctx_T[:, :, :], ctx[(b + 1) % B].rearrange(
                            "(k p) n -> p k n", p=P)).then_inc(next_ctx, 16)
                        sp.wait_ge(next_ctx, 16)

                    @block.gpsimd
                    def _(pool):
                        pool.wait_ge(s_product, CT)
                        for half in range(KT):
                            spread_queries(half, (b + 1) % B).then_inc(q_ready, 1)

                    @block.tensor
                    def _(pe):
                        def scores(t):
                            if t >= 2:
                                pe.wait_ge(s_out, t - 1)
                            n = keys_of(t)
                            for half in range(2):
                                last = nc.tensor.matmul(ps[0:n, 2 * (t % 2) + half, :],
                                                        k_T[:, half, t * P:t * P + n],
                                                        q_bd[:, half, :, :], start=True, stop=True)
                            last.then_inc(s_product, 1)

                        def values(t):
                            pe.wait_ge(p_ready, t + 1)
                            n = keys_of(t)
                            for j in range(PAIRS):
                                last = nc.tensor.matmul(
                                    ps[32 * (j % 4):32 * (j % 4) + 32, 4 + j // 4, 0:P],
                                    v[0:n, t, 2 * DH * j:2 * DH * (j + 1)],
                                    sc[0:n, t, 2 * j:2 * j + 2, :], start=(t == 0),
                                    stop=(t == CT - 1), skip_group_check=True)
                            g = t % 4
                            for half in range(2 if softmax else 0):
                                last = nc.tensor.matmul(
                                    ps[32 * g:32 * g + 32, 6 + half, :], env.ones[0:n, 0:32],
                                    sc[0:n, t, 8 * half:8 * half + 8, :], start=(t < 4),
                                    stop=(t + 4 >= CT), skip_group_check=True)
                            last.then_inc(pv_done, 1)

                        def next_keys(g):
                            if g < 4:
                                pe.wait_ge(s_out, CT - 1 if g < 2 else CT)
                            else:
                                keys_taken(pe, g - 4)
                            key_group(g, (g + 2) % 4).then_inc(k_product, 1)

                        if softmax:
                            for t in range(CT):
                                scores(t)
                            pe.wait_ge(next_ctx, 16)
                            for g in range(2):
                                next_keys(g)
                            pe.wait_ge(maxima, CT - 1)
                            for j in range(PAIRS):
                                last = nc.tensor.transpose(
                                    two_banks[2][:, j * P:(j + 1) * P],
                                    most[:, 2 * j:2 * j + 2, :].rearrange("p h s -> p (h s)"),
                                    env.ident)
                            last.then_inc(turned, 1)
                            for g in range(2, 4):
                                next_keys(g)
                            pe.wait_ge(diag_ready, 1)
                            for half in range(2):
                                nc.tensor.matmul(ps[:, 6 + half, :], env.ones,
                                                 diag[:, 4 * half:4 * half + 4, :],
                                                 start=True, stop=True).then_inc(bc_product, 1)
                            for g in range(4, KG):
                                next_keys(g)
                            for t in range(CT):
                                values(t)
                        else:
                            for t in range(CT + 2):
                                if t < CT:
                                    scores(t)
                                if t >= 2:
                                    values(t - 2)
                            pe.wait_ge(next_ctx, 16)
                            for g in range(KG):
                                next_keys(g)
                        for t in range(CT):
                            if t < 4:
                                keys_taken(pe, KG - 4 + (t + 2) % 4)
                            else:
                                pe.wait_ge((v_act, v_dve)[t % 2], t // 2 - 1)
                            value_tile(t).then_inc(v_product, 1)
                            if t == 3:
                                pe.wait_ge(den_out, 1 if softmax else CT - 1)
                                for j in range(PAIRS):
                                    last = nc.tensor.matmul(
                                        ps[32 * (j % 4):32 * (j % 4) + 32, 6,
                                           (j // 4) * P:(j // 4 + 1) * P],
                                        env.every32 if softmax else env.ones[:, 0:32],
                                        den_parts[:, 2 * j:2 * j + 2, :], start=True, stop=True)
                                last.then_inc(den_product, 1)

                    @block.scalar
                    def _(act):
                        def take_key_group(g):
                            act.wait_ge(k_product, g + 1)
                            take_keys(nc.scalar.copy, g, (g + 2) % 4).then_inc(k_act, 1)

                        if softmax:
                            for t in range(CT):
                                n = keys_of(t)
                                act.wait_ge(s_product, t + 1)
                                nc.scalar.copy(sc[0:n, t, :, :],
                                               heads(two_banks[t % 2][0:n])).then_inc(s_out, 1)
                            for g in range(4):
                                take_key_group(g)
                            for half in range(2):
                                act.wait_ge(bc_product, half + 1)
                                nc.scalar.copy(top_bc[:, 8 * half:8 * half + 8, :].rearrange(
                                    "p h s -> p (h s)"), ps[:, 6 + half, :]).then_inc(bc_ready, 1)
                        for t in range(CT):
                            n = keys_of(t)
                            if softmax and 4 + t < KG:
                                take_key_group(4 + t)
                            act.wait_ge(p_in if softmax else s_out, t + 1)
                            if softmax:
                                ins = nc.scalar.activation(sc[0:n, t, :, :], sc[0:n, t, :, :],
                                                           ACT.Exp, scale=DH ** -0.5)
                            else:
                                ins = nc.scalar.activation(sc[0:n, t, :, :], sc[0:n, t, :, :],
                                                           ACT.Square, scale=DH ** -0.5,
                                                           bias=nb[0:n, 0:1])
                            ins.then_inc(p_ready, 1)
                        if not softmax:
                            for g in range(0, KG, 2):
                                take_key_group(g)
                        for t in range(0, CT, 2):
                            act.wait_ge(v_product, t + 1)
                            take_values(nc.scalar.copy, t).then_inc(v_act, 1)

                    @block.vector
                    def _(dve):
                        steps = Steps(dve, own)
                        if softmax:
                            for t in range(CT):
                                n = keys_of(t)
                                dve.wait_ge(s_out, t + 1)
                                if t == 0:
                                    steps.done(nc.vector.scalar_tensor_tensor(
                                        out=zeros[:, :, :], in0=sc[0:S, 0, :, :], scalar=0.0,
                                        in1=env.excluded[0:S, :].unsqueeze(1).broadcast_to(
                                            [S, H, S]), op0=ALU.is_equal, op1=ALU.mult))
                                    steps.wait()
                                    steps.done(nc.vector.tensor_tensor(
                                        sc[0:S, 0, :, :], sc[0:S, 0, :, :], zeros[:, :, :],
                                        ALU.add))
                                    continue
                                if t == 1:
                                    steps.wait()
                                else:
                                    dve.wait_ge(maxima, t - 1)
                                nc.vector.tensor_tensor(
                                    most[0:n, :, :], (sc[:, 0] if t == 1 else most)[0:n],
                                    sc[0:n, t, :, :], ALU.max).then_inc(maxima, 1)
                            dve.wait_ge(turned, 1)
                            steps.done(nc.vector.tensor_reduce(
                                top[:, :], two_banks[2].rearrange("p (j k) -> p j k", j=PAIRS),
                                AX, ALU.max))
                            steps.wait()
                            nc.vector.tensor_tensor(
                                diag[:, :, :], env.ident.unsqueeze(1).broadcast_to([P, PAIRS, P]),
                                top[:, :].unsqueeze(2).broadcast_to([P, PAIRS, P]),
                                ALU.mult).then_inc(diag_ready, 1)
                            dve.wait_ge(bc_ready, 2)
                            for t in range(CT):
                                n = keys_of(t)
                                nc.vector.tensor_tensor(sc[0:n, t, :, :], sc[0:n, t, :, :],
                                                        top_bc[0:n, :, :],
                                                        ALU.subtract).then_inc(p_in, 1)
                        else:
                            dve.wait_ge(mask_in, 32)
                            for rows, ts in ((P, slice(0, CT - 1)), (LAST, slice(CT - 1, CT))):
                                steps.done(nc.vector.tensor_scalar(
                                    cap[0:rows, ts, :], mask_u8[0:rows, ts, :], -3e38, 3e38,
                                    ALU.mult, ALU.add))
                                steps.wait()
                                steps.done(nc.vector.tensor_scalar(
                                    cap[0:rows, ts, :], cap[0:rows, ts, :], nb[0:rows, 1:2], None,
                                    ALU.add))
                            steps.wait()
                            for t in range(CT + 1):
                                if t < CT:
                                    n = keys_of(t)
                                    dve.wait_ge(s_product, t + 1)
                                    nc.vector.scalar_tensor_tensor(
                                        out=sc[0:n, t, :, :], in0=heads(two_banks[t % 2][0:n]),
                                        scalar=nb[0:n, 1:2],
                                        in1=cap[0:n, t, :].unsqueeze(1).broadcast_to([n, H, S]),
                                        op0=ALU.max, op1=ALU.min).then_inc(s_out, 1)
                                if t >= 2:
                                    n = keys_of(t - 1)
                                    dve.wait_ge(p_ready, t)
                                    if t >= 3:
                                        dve.wait_ge(den_out, t - 2)
                                    nc.vector.tensor_tensor(
                                        den_parts[0:n, :, :],
                                        (sc[:, 0] if t == 2 else den_parts)[0:n],
                                        sc[0:n, t - 1, :, :], ALU.add).then_inc(den_out, 1)
                        if softmax:
                            dve.wait_ge(pv_done, CT)
                            nc.vector.tensor_copy(den_parts[:, :, :], heads(two_banks[3])
                                                  ).then_inc(den_out, 1)
                        else:
                            for g in range(1, KG, 2):
                                dve.wait_ge(k_product, g + 1)
                                take_keys(nc.vector.tensor_copy, g, (g + 2) % 4).then_inc(k_dve, 1)

                        for t in range(1, CT, 2):
                            dve.wait_ge(v_product, t + 1)
                            take_values(nc.vector.tensor_copy, t).then_inc(v_dve, 1)
                        dve.wait_ge(den_product, 1)
                        for out, in_banks in ((den, ps[:, 6, 0:KT * P].rearrange(
                                "p (k n) -> p k n", k=KT)), (num, ps[:, 4:6, 0:P])):
                            steps.done(nc.vector.tensor_scalar(
                                out[:, :, :], in_banks[:, :, 0:S], env.parity[:, 0:1], None,
                                ALU.mult))
                            steps.wait()
                            steps.done(nc.vector.scalar_tensor_tensor(
                                out=out[:, :, :], in0=in_banks[:, :, S:P],
                                scalar=env.parity[:, 1:2], in1=out[:, :, :], op0=ALU.mult,
                                op1=ALU.add))
                        steps.wait()
                        if not softmax:
                            steps.done(nc.vector.tensor_scalar(den[:, :, :], den[:, :, :], 1e-32,
                                                               None, ALU.add))
                            steps.wait()
                        steps.done(nc.vector.reciprocal(den[:, :, :], den[:, :, :]))
                        steps.wait()
                        steps.done(nc.vector.tensor_tensor(att_T[:, :, bass.ds(b * S, S)],
                                                           num[:, :, :], den[:, :, :], ALU.mult))


def scoped(nc, name):
    mem = ExitStack()

    def sb(n, shape, dt=F32):
        return mem.enter_context(nc.sbuf_tensor(f"{name}_{n}", shape, dt))

    return mem, sb


def l0_xattn(nc, env, d):
    mem, sb = scoped(nc, "x0")
    with mem:
        wq, wk, wv, wo = (sb(n, [P, KT, D]) for n in ("wq", "wk", "wv", "wo"))
        q_T, att_T = sb("q_T", [P, KT, N]), sb("att_T", [P, KT, N])
        layernorm(nc, env, "x0_ln", env.x, env.h, env.h_T, loads=[
            (wq[:, :, :], wview(d["L0_xattn_w_q"])), (wk[:, :, :], wview(d["L0_xattn_w_k"])),
            (wv[:, :, :], wview(d["L0_xattn_w_v"])), (wo[:, :, :], wview(d["L0_xattn_w_o"]))])
        linear_T(nc, env, "x0_q", [(env.h_T, wq, q_T, None, None)])
        context_heads(nc, env, "x0", d["ctx_T"], q_T, att_T, wk, wv, softmax=True)
        project_add(nc, env, "x0_o", att_T, wo, None, env.x)


def l0_attn(nc, env, d):
    mem, sb = scoped(nc, "e0")
    FF = 4 * D
    FT = FF // P
    HALF = T // 2
    with mem:
        y = sb("y", [P, T, D])
        wq, wk, wv, wo = (sb(n, [P, KT, D]) for n in ("wq", "wk", "wv", "wo"))
        w1, w2 = sb("w1", [P, KT, FF]), sb("w2", [P, FT, D])
        ln1, ln2 = sb("ln1", [P, 2, KT]), sb("ln2", [P, 2, KT])
        bq, b1 = sb("bq", [P, KT]), sb("b1", [P, FT])
        bk, bv, bo, b2 = (sb(n, [P, D]) for n in ("bk", "bv", "bo", "b2"))
        pos, lnf = sb("pos", [P, D]), sb("lnf", [P, 2, D])
        q_T, qe_T, att_T = sb("q_T", [P, KT, N]), sb("qe_T", [P, KT, N]), sb("att_T", [P, KT, N])
        den_T = sb("den_T", [P, NH])
        k_nat = sb("k_nat", [P, T, D])
        v_own = sb("v_own", [P, T, KT, 2, P + 1])
        hid_T = sb("hid_T", [P, FT, NH])
        kv_bd = sb("kv_bd", [P, 2 * HALF, KT, P])
        ksum = sb("ksum", [P, KT, 2 * HALF])
        layer_loads = [(wq[:, :, :], lambda i: wview(d["L0_attn_Wq"][i])),
                       (wk[:, :, :], lambda i: wview(d["L0_attn_Wk"][i])),
                       (wv[:, :, :], lambda i: wview(d["L0_attn_Wv"][i])),
                       (bq[:, :], lambda i: d["L0_attn_bq"][i]),
                       (bk[:, :], lambda i: d["L0_attn_bk"][i].partition_broadcast(P)),
                       (bv[:, :], lambda i: d["L0_attn_bv"][i].partition_broadcast(P)),
                       (ln1[:, 0, :], lambda i: d["L0_attn_ln1_s"][i]),
                       (ln1[:, 1, :], lambda i: d["L0_attn_ln1_b"][i])]
        late_loads = [(wo[:, :, :], lambda i: wview(d["L0_attn_Wo"][i])),
                      (bo[:, :], lambda i: d["L0_attn_bo"][i].partition_broadcast(P)),
                      (ln2[:, 0, :], lambda i: d["L0_attn_ln2_s"][i]),
                      (ln2[:, 1, :], lambda i: d["L0_attn_ln2_b"][i]),
                      (b1[:, :], lambda i: d["L0_attn_b1"][i]),
                      (w1[:, :, :], lambda i: wview(d["L0_attn_W1"][i])),
                      (b2[:, :], lambda i: d["L0_attn_b2"][i].partition_broadcast(P)),
                      (w2[:, :, :], lambda i: wview(d["L0_attn_W2"][i]))]
        layernorm(nc, env, "e0_in", env.x, env.h, None, loads=[
            (pos[:, :], d["pos"]),
            (lnf[:, 0, :], d["L0_attn_lnf_s"].partition_broadcast(P)),
            (lnf[:, 1, :], d["L0_attn_lnf_b"].partition_broadcast(P))]
            + [(dst, src(0)) for dst, src in layer_loads])
        with signals(nc, "e0_pos", "zeroed set") as (zeroed, y_set):
            with nc.Block() as block:

                @block.vector
                def _(dve):
                    for t in range(T):
                        nc.vector.scalar_tensor_tensor(
                            out=y[:, t, :], in0=env.h[:, t, :], scalar=float(D) ** 0.5,
                            in1=pos[:, :], op0=ALU.mult, op1=ALU.add).then_inc(y_set, 1)

                @block.gpsimd
                def _(pool):
                    nc.gpsimd.memset(v_own[:, :, :, :, :], 0.0).then_inc(zeroed, 1)
                    pool.wait_ge(zeroed, 1)
                    for b in range(2):
                        nc.gpsimd.memset(v_own[b * S:(b + 1) * S, :, :, b, P:P + 1], 1.0
                                         ).then_inc(zeroed, 1)

        work = [("norm1", c, f, "act") for c in range(2) for f in range(KT)]
        for c in range(2):
            work += [("query", c, m, "act") for m in range(KT)]
            work += [("key_value", t, 0, "dve") for t in range(c * HALF, (c + 1) * HALF)]

        def states(c):
            return [("state", t, f, "dve") for t in range(c * HALF, (c + 1) * HALF)
                    for f in range(KT)]

        def nums_dens(c):
            return [(kind, c, f, "dve") for f in range(KT) for kind in ("den", "num")]

        def outs_turned(c):
            return ([("out", t, 0, "dve") for t in range(c * HALF, (c + 1) * HALF)]
                    + [("norm2", c, f, "act") for f in range(KT)])

        def ups(c):
            return [("up", c, m, "act") for m in range(FT)]

        work += states(0) + nums_dens(0) + states(1) + outs_turned(0) + nums_dens(1)
        work += ups(0)
        work += outs_turned(1)
        work += [("down", t, 0, "dve") for t in range(HALF)]
        work += ups(1)
        work += [("down", t, 0, "dve") for t in range(HALF, T)]
        at = {w[0:3]: g for g, w in enumerate(work)}

        def taken_by(engine, kind, i, j=0):
            return sum(w[3] == engine for w in work[:at[kind, i, j] + 1])

        def bank(kind, i, j=0):
            return env.ps[:, at[kind, i, j] % 8, :]

        with nc.Fori(0, 4) as i:
            with signals(nc, "e0_layer", "late next own stats std rows_ready product act_out "
                         "dve_out k_in q_exped k_exped k_elu k_ready q_ready scaled "
                         "y_biased") as (
                    late, next_in, own, stats, std_ready, rows_ready, product, act_out, dve_out,
                    k_in, q_exped, k_exped, k_elu, k_ready, q_ready, scaled,
                    y_biased):
                with nc.Block() as block:

                    @block.sync
                    def _(sp):
                        for dst, src in late_loads:
                            sp.dma_start(dst, src(i)).then_inc(late, 16)
                        sp.wait_ge(product, at["key_value", T - 1, 0] + 1)
                        sp.wait_ge(act_out, taken_by("act", "query", 1, KT - 1))
                        sp.wait_ge(dve_out, taken_by("dve", "key_value", T - 1))
                        for dst, src in layer_loads:
                            sp.dma_start(dst, src((i + 1) % 4)).then_inc(next_in, 16)
                        sp.wait_ge(late, 16 * len(late_loads))
                        sp.wait_ge(next_in, 16 * len(layer_loads))

                    @block.gpsimd
                    def _(pool):
                        pool.wait_ge(late, 16 * len(late_loads))
                        for norm, bias in ((0, bo), (1, b2)):
                            for c in range(2):
                                pool.wait_ge(rows_ready, 8 * norm + 4 * c + 4)
                                ts = slice(c * HALF, (c + 1) * HALF)
                                nc.gpsimd.tensor_tensor(
                                    y[:, ts, :], y[:, ts, :],
                                    bias[:, :].unsqueeze(1).broadcast_to([P, HALF, D]),
                                    ALU.add).then_inc(y_biased, 1)

                    @block.tensor
                    def _(pe):
                        for g, (kind, a, j, _) in enumerate(work):
                            put = env.ps[:, g % 8, :]
                            if g >= 8:
                                before = work[g - 8]
                                if before[3] == "act":
                                    pe.wait_ge(act_out, taken_by("act", *before[0:3]))
                                else:
                                    pe.wait_ge(dve_out, taken_by("dve", *before[0:3]))
                            if kind in ("norm1", "norm2"):
                                pe.wait_ge(rows_ready, 4 * a + 4 + (T if kind == "norm2" else 0))
                                for t in range(HALF):
                                    last = nc.tensor.transpose(
                                        put[:, t * P:(t + 1) * P],
                                        env.h[:, a * HALF + t, j * P:(j + 1) * P], env.ident)
                            elif kind == "query":
                                pe.wait_ge(act_out, taken_by("act", "norm1", a, KT - 1))
                                for k in range(KT):
                                    last = nc.tensor.matmul(
                                        put, wq[:, k, j * P:(j + 1) * P],
                                        env.h_T[:, k, a * NH:(a + 1) * NH], start=(k == 0),
                                        stop=(k == KT - 1))
                            elif kind == "key_value":
                                for n, w in enumerate((wk, wv)):
                                    for k in range(KT):
                                        last = nc.tensor.matmul(
                                            put[:, n * D:(n + 1) * D],
                                            env.h_T[:, k, a * P:(a + 1) * P], w[:, k, :],
                                            start=(k == 0), stop=(k == KT - 1))
                            elif kind == "state":
                                pe.wait_ge(k_ready, a // HALF + 1)
                                last = nc.tensor.matmul(
                                    put[:, 0:2 * (P + 1)], k_nat[:, a, j * P:(j + 1) * P],
                                    v_own[:, a, j, :, :], start=True, stop=True)
                            elif kind == "den":
                                pe.wait_ge(scaled, a + 1)
                                last = nc.tensor.matmul(
                                    put, env.same_head, qe_T[:, j, a * NH:(a + 1) * NH],
                                    start=True, stop=True)
                            elif kind == "num":
                                for u in range(2 * HALF):
                                    n = 2 * S if u < 2 * HALF - 1 else S
                                    q_at = (2 * HALF * a + u) * S
                                    last = nc.tensor.matmul(
                                        put[:, u * S:u * S + n], kv_bd[:, u, j, :],
                                        q_T[:, j, q_at:q_at + n], start=True, stop=True,
                                        skip_group_check=True)
                            elif kind == "out":
                                pe.wait_ge(dve_out, taken_by("dve", "num", a // HALF, KT - 1))
                                pe.wait_ge(late, 16 * len(late_loads))
                                for k in range(KT):
                                    last = nc.tensor.matmul(
                                        put[:, 0:D], att_T[:, k, a * P:(a + 1) * P], wo[:, k, :],
                                        start=(k == 0), stop=(k == KT - 1))
                            elif kind == "up":
                                pe.wait_ge(act_out, taken_by("act", "norm2", a, KT - 1))
                                for k in range(KT):
                                    last = nc.tensor.matmul(
                                        put, w1[:, k, j * P:(j + 1) * P],
                                        env.h_T[:, k, a * NH:(a + 1) * NH], start=(k == 0),
                                        stop=(k == KT - 1))
                            else:
                                pe.wait_ge(act_out, taken_by("act", "up", a // HALF, FT - 1))
                                for k in range(FT):
                                    t = a % HALF
                                    last = nc.tensor.matmul(
                                        put[:, 0:D], hid_T[:, k, t * P:(t + 1) * P], w2[:, k, :],
                                        start=(k == 0), stop=(k == FT - 1))
                            last.then_inc(product, 1)

                    @block.scalar
                    def _(act):
                        def deviations(norm, c):
                            act.wait_ge(stats, T * norm + HALF * (c + 1))
                            nc.scalar.activation(env.std[:, c * HALF:(c + 1) * HALF],
                                                 env.mv[:, c * HALF:(c + 1) * HALF, 1], ACT.Sqrt,
                                                 bias=env.eps5[:, 0:1]).then_inc(std_ready, 1)

                        def turned(kind, c, affine):
                            for f in range(KT):
                                act.wait_ge(product, at[kind, c, f] + 1)
                                nc.scalar.activation(
                                    env.h_T[:, f, c * NH:(c + 1) * NH], bank(kind, c, f),
                                    ACT.Identity, scale=affine[:, 0, f:f + 1],
                                    bias=affine[:, 1, f:f + 1]).then_inc(act_out, 1)

                        def hidden(c):
                            if c:
                                act.wait_ge(product, at["down", HALF - 1, 0] + 1)
                            for m in range(FT):
                                act.wait_ge(product, at["up", c, m] + 1)
                                nc.scalar.activation(hid_T[:, m, :], bank("up", c, m), ACT.Relu,
                                                     bias=b1[:, m:m + 1]).then_inc(act_out, 1)

                        deviations(0, 0)
                        deviations(0, 1)
                        turned("norm1", 0, ln1)
                        turned("norm1", 1, ln1)
                        for c in range(2):
                            cols, ts = slice(c * NH, (c + 1) * NH), slice(c * HALF, (c + 1) * HALF)
                            for m in range(KT):
                                put = bank("query", c, m)
                                act.wait_ge(product, at["query", c, m] + 1)
                                nc.scalar.activation(qe_T[:, m, cols], put, ACT.Exp,
                                                     bias=bq[:, m:m + 1]).then_inc(q_exped, 1)
                                nc.scalar.activation(q_T[:, m, cols], put, ACT.Relu,
                                                     bias=bq[:, m:m + 1]).then_inc(act_out, 1)
                            act.wait_ge(k_in, HALF * (c + 1))
                            nc.scalar.activation(env.rows[:, ts, :], k_nat[:, ts, :], ACT.Exp
                                                 ).then_inc(k_exped, 1)
                        act.wait_ge(late, 16 * len(late_loads))
                        deviations(1, 0)
                        turned("norm2", 0, ln2)
                        hidden(0)
                        deviations(1, 1)
                        turned("norm2", 1, ln2)
                        hidden(1)

                    @block.vector
                    def _(dve):
                        steps = Steps(dve, own)

                        def normalise(norm, c):
                            ts = range(c * HALF, (c + 1) * HALF)
                            for t in ts:
                                steps.done(nc.vector.bn_stats(env.bn[:, t, :], y[:, t, :]))
                            steps.wait()
                            for t in ts:
                                nc.vector.bn_aggr(env.mv[:, t, :], env.bn[:, t, :]
                                                  ).then_inc(stats, 1)
                            dve.wait_ge(std_ready, 2 * norm + c + 1)
                            half = slice(c * HALF, (c + 1) * HALF)
                            steps.done(nc.vector.reciprocal(env.rstd[:, half], env.std[:, half]))
                            steps.wait()
                            for t in ts:
                                nc.vector.tensor_scalar(
                                    env.h[:, t, :], y[:, t, :], env.mv[:, t, 0:1],
                                    env.rstd[:, t:t + 1], ALU.subtract, ALU.mult
                                ).then_inc(rows_ready, 1)

                        def keys_values(c):
                            for t in range(c * HALF, (c + 1) * HALF):
                                dve.wait_ge(product, at["key_value", t, 0] + 1)
                                put = bank("key_value", t)
                                nc.vector.tensor_tensor(k_nat[:, t, :], put[:, 0:D], bk[:, :],
                                                        ALU.add).then_inc(k_in, 1)
                                for b in range(2):
                                    own_rows = slice(b * S, (b + 1) * S)
                                    ins = nc.vector.tensor_tensor(
                                        v_own[own_rows, t, :, b, 0:P],
                                        put[own_rows, D:2 * D].rearrange("p (f n) -> p f n", f=KT),
                                        bv[own_rows, :].rearrange("p (f n) -> p f n", f=KT),
                                        ALU.add)
                                    steps.done(ins) if b == 0 else ins.then_inc(dve_out, 1)
                            ts = slice(c * HALF, (c + 1) * HALF)
                            dve.wait_ge(k_exped, c + 1)
                            nc.vector.tensor_scalar(env.rows[:, ts, :], env.rows[:, ts, :], 1.0,
                                                    None, ALU.min).then_inc(k_elu, 1)
                            dve.wait_ge(k_elu, c + 1)
                            nc.vector.scalar_tensor_tensor(
                                out=k_nat[:, ts, :], in0=k_nat[:, ts, :], scalar=0.0,
                                in1=env.rows[:, ts, :], op0=ALU.max, op1=ALU.add
                            ).then_inc(k_ready, 1)

                        def take_states(c):
                            if c:
                                dve.wait_ge(product, at["num", 0, KT - 1] + 1)
                            for t in range(c * HALF, (c + 1) * HALF):
                                for f in range(KT):
                                    u = 2 * (t % HALF)
                                    dve.wait_ge(product, at["state", t, f] + 1)
                                    put = bank("state", t, f)[:, 0:2 * (P + 1)].rearrange(
                                        "p (b n) -> p b n", b=2)
                                    steps.done(nc.vector.tensor_copy(ksum[:, f, u:u + 2],
                                                                     put[:, :, P]))
                                    nc.vector.tensor_tensor(
                                        kv_bd[:, u:u + 2, f, :], put[:, :, 0:P],
                                        env.same_head.unsqueeze(1).broadcast_to([P, 2, P]),
                                        ALU.mult).then_inc(dve_out, 1)
                            cols = slice(c * NH, (c + 1) * NH)
                            dve.wait_ge(act_out, taken_by("act", "query", c, KT - 1))
                            dve.wait_ge(q_exped, KT * (c + 1))
                            nc.vector.scalar_tensor_tensor(
                                out=q_T[:, :, cols], in0=qe_T[:, :, cols], scalar=1.0,
                                in1=q_T[:, :, cols], op0=ALU.min, op1=ALU.add
                            ).then_inc(q_ready, 1)
                            dve.wait_ge(q_ready, c + 1)
                            steps.wait()
                            for f in range(KT):
                                ins = nc.vector.tensor_tensor(
                                    qe_T[:, f, cols].rearrange("p (u s) -> p u s", s=S),
                                    q_T[:, f, cols].rearrange("p (u s) -> p u s", s=S),
                                    ksum[:, f, :].unsqueeze(2).broadcast_to([P, 2 * HALF, S]),
                                    ALU.mult)
                                steps.done(ins) if f == 0 else ins.then_inc(scaled, 1)

                        def attention(c):
                            for f in range(KT):
                                dve.wait_ge(product, at["den", c, f] + 1)
                                nc.vector.tensor_scalar(den_T[:, :], bank("den", c, f), 1e-6,
                                                        None, ALU.add).then_inc(dve_out, 1)
                                dve.wait_ge(dve_out, taken_by("dve", "den", c, f))
                                steps.done(nc.vector.reciprocal(den_T[:, :], den_T[:, :]))
                                dve.wait_ge(product, at["num", c, f] + 1)
                                steps.wait()
                                nc.vector.tensor_tensor(
                                    att_T[:, f, c * NH:(c + 1) * NH], bank("num", c, f),
                                    den_T[:, :], ALU.mult).then_inc(dve_out, 1)
                                dve.wait_ge(dve_out, taken_by("dve", "num", c, f))

                        def add_rows(kind, c):
                            dve.wait_ge(y_biased, c + 1 + (2 if kind == "down" else 0))
                            for t in range(c * HALF, (c + 1) * HALF):
                                dve.wait_ge(product, at[kind, t, 0] + 1)
                                nc.vector.tensor_tensor(y[:, t, :], y[:, t, :],
                                                        bank(kind, t)[:, 0:D], ALU.add
                                                        ).then_inc(dve_out, 1)
                            dve.wait_ge(dve_out, taken_by("dve", kind, (c + 1) * HALF - 1))

                        normalise(0, 0)
                        normalise(0, 1)
                        keys_values(0)
                        keys_values(1)
                        take_states(0)
                        attention(0)
                        take_states(1)
                        add_rows("out", 0)
                        normalise(1, 0)
                        attention(1)
                        add_rows("out", 1)
                        normalise(1, 1)
                        add_rows("down", 0)
                        add_rows("down", 1)

        layernorm(nc, env, "e0_lnf", y, env.h, None)
        with signals(nc, "e0_add", "scaled moved added") as (scaled, moved, added):
            with nc.Block() as block:

                @block.vector
                def _(dve):
                    for t in range(T):
                        nc.vector.tensor_tensor(env.h[:, t, :], env.h[:, t, :], lnf[:, 0, :],
                                                ALU.mult).then_inc(scaled, 1)
                    for t in range(T):
                        dve.wait_ge(scaled, t + 1)
                        nc.vector.tensor_tensor(env.h[:, t, :], env.h[:, t, :], lnf[:, 1, :],
                                                ALU.add).then_inc(moved, 1)
                    for t in range(T):
                        dve.wait_ge(moved, t + 1)
                        nc.vector.tensor_tensor(env.x[:, t, :], env.x[:, t, :], env.h[:, t, :],
                                                ALU.add).then_inc(added, 1)


def top2(nc, env, dve, probs, experts, weights, chosen, m8, i8, i_f, steps):
    for t in range(T):
        steps.done(nc.vector.max(m8[:, t, :], probs[:, t, :]))
    steps.wait()
    for t in range(T):
        steps.done(nc.vector.max_index(i8[:, t, :], m8[:, t, :], probs[:, t, :]))
    steps.done(nc.vector.tensor_copy(weights, m8[:, :, 0:2]))
    steps.wait()
    steps.done(nc.vector.tensor_copy(i_f[:, :, :], i8[:, :, 0:2]))
    steps.wait()
    for k in range(2):
        steps.done(nc.vector.tensor_tensor(
            chosen[:, :, k, :], env.iota8.unsqueeze(1).broadcast_to([P, T, experts]),
            i_f[:, :, k:k + 1].broadcast_to([P, T, experts]), ALU.is_equal))
    steps.wait()


def row_softmax(nc, dve, logits, top, total, n, exped, shifted, steps):
    steps.done(nc.vector.tensor_reduce(top, logits, AX, ALU.max))
    steps.wait()
    nc.vector.tensor_tensor(logits, logits, top.unsqueeze(2).broadcast_to([P, T, n]),
                            ALU.subtract).then_inc(shifted, 1)
    dve.wait_ge(exped, 1)
    steps.done(nc.vector.tensor_reduce(total, logits, AX, ALU.add))
    steps.wait()
    steps.done(nc.vector.reciprocal(total, total))
    steps.wait()
    steps.done(nc.vector.tensor_tensor(logits, logits, total.unsqueeze(2).broadcast_to([P, T, n]),
                                       ALU.mult))
    steps.wait()


def l0_ffn(nc, env, d):
    E = 8
    CAP = int(1.25 * N / E)
    mem, sb = scoped(nc, "f0")
    with mem:
        gate = sb("gate", [P, KT, E])
        w1, w2 = sb("w1", [P, 2, KT, D]), sb("w2", [P, 2, KT, D])
        b1, b2 = sb("b1", [P, E, KT]), sb("b2", [E, D])
        probs, comb = sb("probs", [P, T, E]), sb("comb", [P, T, E])
        chosen, weights = sb("chosen", [P, T, 2, E]), sb("weights", [P, T, 2])
        m8, i8, i_f = sb("m8", [P, T, 8]), sb("i8", [P, T, 8], U32), sb("i_f", [P, T, 2])
        top, total, keep = sb("top", [P, T]), sb("total", [P, T]), sb("keep", [P, E])
        both, tmp = sb("both", [P, T, E]), sb("tmp", [P, T, E])
        hid_T, comb_T = sb("hid_T", [P, KT, N]), sb("comb_T", [E, N])
        layernorm(nc, env, "f0_ln", env.x, env.h, env.h_T, loads=[
            (gate[:, :, :], wview(d["L0_ffn_gate_w"])), (b1[:, :, :], d["L0_ffn_b1"]),
            (b2[:, :], d["L0_ffn_b2"]),
            (w1[:, 0, :, :], wview(d["L0_ffn_W1"][0])), (w2[:, 0, :, :], wview(d["L0_ffn_W2"][0]))])
        with signals(nc, "f0_route", "logits own shifted exped picked counted weighed turned "
                     "turned_out biases added") as (
                logits, own, shifted, exped, picked, counted, weighed, turned, turned_out,
                biases, added):
            with nc.Block() as block:

                @block.tensor
                def _(pe):
                    for t in range(T):
                        for k in range(KT):
                            last = nc.tensor.matmul(env.ps[:, 0, t * E:(t + 1) * E],
                                                    env.h_T[:, k, t * P:(t + 1) * P],
                                                    gate[:, k, :], start=(k == 0),
                                                    stop=(k == KT - 1))
                    last.then_inc(logits, 1)
                    pe.wait_ge(picked, 1)
                    for t in range(T):
                        last = nc.tensor.matmul(env.ps[:, 1, 0:E], env.ones, both[:, t, :],
                                                start=(t == 0), stop=(t == T - 1))
                    last.then_inc(counted, 1)
                    pe.wait_ge(weighed, 1)
                    for t in range(T):
                        last = nc.tensor.transpose(
                            env.ps[0:E, 2 + t // 4, (t % 4) * P:(t % 4 + 1) * P], comb[:, t, :],
                            env.ident)
                    last.then_inc(turned, 1)
                    pe.wait_ge(turned_out, 1)
                    for t in range(T):
                        nc.tensor.matmul(env.ps[:, 4 + t // 2, (t % 2) * D:(t % 2 + 1) * D],
                                         comb_T[:, t * P:(t + 1) * P], b2[:, :], start=True,
                                         stop=True).then_inc(biases, 1)

                @block.scalar
                def _(act):
                    act.wait_ge(shifted, 1)
                    nc.scalar.activation(probs[:, :, :], probs[:, :, :], ACT.Exp).then_inc(exped, 1)

                @block.vector
                def _(dve):
                    steps = Steps(dve, own)
                    dve.wait_ge(logits, 1)
                    steps.done(nc.vector.tensor_copy(
                        probs[:, :, :], env.ps[:, 0, 0:T * E].rearrange("p (t e) -> p t e", t=T)))
                    steps.wait()
                    row_softmax(nc, dve, probs[:, :, :], top[:, :], total[:, :], E, exped, shifted,
                                steps)
                    top2(nc, env, dve, probs, E, weights[:, :, :], chosen, m8, i8, i_f, steps)
                    nc.vector.tensor_tensor(both[:, :, :], chosen[:, :, 0, :], chosen[:, :, 1, :],
                                            ALU.add).then_inc(picked, 1)
                    for k, dst in ((0, comb), (1, tmp)):
                        steps.done(nc.vector.tensor_tensor(
                            dst[:, :, :], chosen[:, :, k, :],
                            weights[:, :, k:k + 1].broadcast_to([P, T, E]), ALU.mult))
                    steps.wait()
                    steps.done(nc.vector.tensor_tensor(comb[:, :, :], comb[:, :, :], tmp[:, :, :],
                                                       ALU.add))
                    dve.wait_ge(counted, 1)
                    steps.done(nc.vector.tensor_scalar(keep[:, :], env.ps[:, 1, 0:E], float(CAP),
                                                       None, ALU.is_le))
                    steps.wait()
                    nc.vector.tensor_tensor(
                        comb[:, :, :], comb[:, :, :],
                        keep[:, :].unsqueeze(1).broadcast_to([P, T, E]), ALU.mult
                    ).then_inc(weighed, 1)
                    dve.wait_ge(turned, 1)
                    nc.vector.tensor_copy(comb_T[:, :].rearrange("e (c n) -> e c n", c=2),
                                          env.ps[0:E, 2:4, :]).then_inc(turned_out, 1)
                    for t in range(0, T, 2):
                        dve.wait_ge(biases, t + 2)
                        nc.vector.tensor_tensor(
                            env.x[:, t:t + 2, :], env.x[:, t:t + 2, :],
                            env.ps[:, 4 + t // 2, :].rearrange("p (t n) -> p t n", t=2), ALU.add
                        ).then_inc(added, 1)

        with nc.Fori(0, E // 2) as i:
            for r in range(2):
                e = 2 * i + r
                nxt = (e + 1) % E
                experts = [(w1[:, 1 - r, :, :], wview(d["L0_ffn_W1"][nxt])),
                           (w2[:, 1 - r, :, :], wview(d["L0_ffn_W2"][nxt]))]
                expert_bias = b1[:, bass.ds(e, 1), :].squeeze(1)
                linear_T(nc, env, f"f0_up{r}", [(env.h_T, w1[:, r], hid_T, expert_bias, "relu")],
                         loads=experts)
                project_add(nc, env, f"f0_down{r}", hid_T, w2[:, r],
                            None, env.x,
                            weigh=lambda t, e=e: comb[:, t, bass.ds(e, 1)])


def l1_xattn(nc, env, d):
    G3 = 3 * KT
    PAD = CT * P
    mem, sb = scoped(nc, "s1")
    with mem:
        wq, wk, wv = (sb(n, [P, KT, D]) for n in ("wq", "wk", "wv"))
        wih, whh = sb("wih", [P, KT, 3 * D]), sb("whh", [P, KT, 3 * D])
        norm = sb("norm", [P, 2, KT])
        gb = sb("gb", [P, 2, G3])
        gb2 = sb("gb2", [P, 4])
        res_T = sb("res_T", [P, KT, N])
        ctx_T = [sb(f"ctx_T{r}", [P, 2, KT, PAD]) for r in range(2)]
        ctx_n = [sb(f"ctx_n{r}", [P, 2, CT, D + 1]) for r in range(2)]
        ssq, rs_c = sb("ssq", [P, 2, CT]), sb("rs_c", [P, 2, CT])
        junk = sb("junk", [P, 2, D])
        sl = sb("sl", [P, KT, P])
        sq, sn, q1, q2, upd = (sb(n, [P, KT, P]) for n in ("sq", "sn", "q1", "q2", "upd"))
        std, rs = sb("std", [P, P]), sb("rs", [P, P])
        att = sb("att", [P, 2, CT, S])
        top, tot = sb("top", [P, 2, CT]), sb("tot", [P, 2, CT])
        rden = sb("rden", [P, 1])
        u_n, u_T = sb("u_n", [P, D]), sb("u_T", [P, KT, P])
        rz, n_T, hn = sb("rz", [P, 4, P]), sb("n_T", [P, KT, P]), sb("hn", [P, KT, P])
        tiny = sb("tiny", [P, 1])
        ps = env.ps
        layernorm(nc, env, "s1_ln", env.x, env.h, env.h_T, loads=[
            (wq[:, :, :], wview(d["L1_xattn_Wq"])), (wk[:, :, :], wview(d["L1_xattn_Wk"])),
            (wv[:, :, :], wview(d["L1_xattn_Wv"])), (wih[:, :, :], wview(d["L1_xattn_gru_wih"])),
            (whh[:, :, :], wview(d["L1_xattn_gru_whh"])),
            (norm[:, 0, :], d["L1_xattn_slot_norm_w"]), (norm[:, 1, :], d["L1_xattn_input_norm_w"]),
            (gb[:, 0, :], d["L1_xattn_gru_bih"]), (gb[:, 1, :], d["L1_xattn_gru_bhh"])])

        def load_context(sp, r, pair, sem):
            for b in range(2):
                row = 2 * pair + b
                sp.dma_start(ctx_T[r][:, b, :, 0:SK],
                             d["ctx_T"][row].rearrange("(k p) n -> p k n", p=P)).then_inc(sem, 16)
                sp.dma_start(ctx_n[r][:, b, 0:CT - 1, 0:D],
                             d["ctx"][row, 0:(CT - 1) * P, :].rearrange(
                                 "(t p) f -> p t f", p=P)).then_inc(sem, 16)
                sp.dma_start(ctx_n[r][0:LAST, b, CT - 1, 0:D],
                             d["ctx"][row, (CT - 1) * P:SK, :]).then_inc(sem, 16)

        with signals(nc, "s1_pre", "cleared loaded own") as (cleared, loaded, own):
            with nc.Block() as block:

                @block.vector
                def _(dve):
                    for r in range(2):
                        nc.vector.memset(ctx_T[r][:, :, :, SK:PAD], 0.0).then_inc(cleared, 1)
                        nc.vector.memset(ctx_n[r][S:P, :, CT - 1, :], 0.0).then_inc(cleared, 1)
                    steps = Steps(dve, own)
                    steps.done(nc.vector.tensor_tensor(gb2[:, :], gb[:, 0, 0:4], gb[:, 1, 0:4],
                                                       ALU.add))
                    steps.wait()
                    steps.done(nc.vector.tensor_scalar(gb2[:, :], gb2[:, :], 0.5, None, ALU.mult))

                @block.sync
                def _(sp):
                    sp.wait_ge(cleared, 4)
                    load_context(sp, 0, 0, loaded)
                    sp.wait_ge(loaded, 6 * 16)

        def prepare(r, pair, loads):
            with signals(nc, f"s1_prep{r}", "squared std taken own") as (
                    squared, std_ready, taken, own):
                with nc.Block() as block:

                    @block.sync
                    def _(sp):
                        loads(sp)

                    @block.scalar
                    def _(act):
                        for t in range(CT):
                            nc.scalar.activation(junk[:, 0, :], ctx_n[r][:, 0, t, 0:D], ACT.Square,
                                                 accum_out=ssq[:, 0, t:t + 1]).then_inc(squared, 1)
                            act.wait_ge(squared, t + 1)
                        act.wait_ge(own, CT)
                        nc.scalar.activation(rs_c[:, :, :], ssq[:, :, :], ACT.Sqrt, scale=1.0 / D,
                                             bias=env.eps6[:, 0:1]).then_inc(std_ready, 1)

                    @block.vector
                    def _(dve):
                        steps = Steps(dve, own)
                        for t in range(CT):
                            steps.done(nc.vector.tensor_tensor_reduce(
                                junk[:, 1, :], ctx_n[r][:, 1, t, 0:D], ctx_n[r][:, 1, t, 0:D], 1.0,
                                0.0, ALU.mult, ALU.add, ssq[:, 1, t:t + 1]))
                            steps.wait()
                        nc.vector.tensor_copy(sl[:, :, :], env.h_T[:, :, bass.ds(pair * P, P)]
                                              ).then_inc(taken, 1)
                        dve.wait_ge(std_ready, 1)
                        steps.done(nc.vector.tensor_copy(ctx_n[r][:, :, 0:CT - 1, D],
                                                         rs_c[:, :, 0:CT - 1]))
                        steps.done(nc.vector.tensor_scalar(
                            ctx_n[r][:, :, CT - 1, D], rs_c[:, :, CT - 1], env.valid_last[:, 0:1],
                            None, ALU.mult))
                        steps.wait()
                        steps.done(nc.vector.reciprocal(rs_c[:, :, :], rs_c[:, :, :]))

        PER = 7
        units = [(b, c, range(PER * c, min(PER * (c + 1), CT))) for b in range(2) for c in range(2)]

        def attend(r):
            with signals(nc, f"s1_it{r}", "own squares ssq_done std normed q1_done q1_out q2_done "
                         "q2_out s_done shifted exped weights u_done u_ready u_turned u_out "
                         "upd_done upd_out hid_done r_done n_done z_done gates n_in n_out") as (
                    own, squares, ssq_done, std_ready, normed, q1_done, q1_out, q2_done, q2_out,
                    s_done, shifted, exped, weights, u_done, u_ready, u_turned, u_out,
                    upd_done, upd_out, hid_done, r_done, n_done, z_done, gates, n_in, n_out):
                with nc.Block() as block:

                    @block.tensor
                    def _(pe):
                        def project(put, w, in_T, m, **flags):
                            for k in range(KT):
                                last = nc.tensor.matmul(put, w[:, k, m * P:(m + 1) * P],
                                                        in_T[:, k, :],
                                                        **(flags or dict(start=(k == 0),
                                                                         stop=(k == KT - 1))))
                            return last

                        pe.wait_ge(squares, 1)
                        for k in range(KT):
                            last = nc.tensor.matmul(ps[:, 5, 0:P], env.ones, sq[:, k, :],
                                                    start=(k == 0), stop=(k == KT - 1))
                        last.then_inc(ssq_done, 1)

                        def hidden(bank, at, first):
                            for i in range(2):
                                for k in range(KT):
                                    m = first + i
                                    last = nc.tensor.matmul(
                                        ps[:, bank, at + i * P:at + (i + 1) * P],
                                        whh[:, k, m * P:(m + 1) * P], sl[:, k, :],
                                        start=(i == 0 and k == 0), stop=False,
                                        skip_group_check=True)
                            return last

                        hidden(6, 0, 0)
                        hidden(7, 2 * P, 4).then_inc(hid_done, 1)
                        pe.wait_ge(normed, KT)
                        for m in range(KT):
                            last = project(ps[:, 5, (1 + m) * P:(2 + m) * P], wq, sn, m)
                        last.then_inc(q1_done, 1)
                        pe.wait_ge(q1_out, 2)
                        for m in range(KT):
                            last = project(ps[:, 5, m * P:(m + 1) * P], wk, q1, m)
                        last.then_inc(q2_done, 1)
                        pe.wait_ge(q2_out, 1)
                        for b, c, tiles in units:
                            for t in tiles if b == 0 else reversed(tiles):
                                at = (t - tiles[0]) * S
                                for k in range(KT):
                                    last = nc.tensor.matmul(
                                        ps[:, 2 * b + c, at:at + P],
                                        ctx_T[r][:, b, k, t * P:(t + 1) * P], q2[:, k, :],
                                        start=(k == 0), stop=(k == KT - 1))
                            last.then_inc(s_done, 1)
                        pe.wait_ge(shifted, 1)
                        hidden(0, 0, 2)
                        for u, (b, c, tiles) in enumerate(units):
                            pe.wait_ge(weights, u + 1)
                            for t in tiles:
                                last = nc.tensor.matmul(
                                    ps[b * S:(b + 1) * S, 4, 0:D + 1], att[:, b, t, :],
                                    ctx_n[r][:, b, t, :], start=(t == 0), stop=(t == CT - 1))
                        last.then_inc(u_done, 1)
                        pe.wait_ge(u_ready, 1)
                        for f in range(KT):
                            last = nc.tensor.transpose(ps[:, 5, f * P:(f + 1) * P],
                                                       u_n[:, f * P:(f + 1) * P], env.ident)
                        last.then_inc(u_turned, 1)
                        pe.wait_ge(u_out, 1)
                        for m in range(KT):
                            last = project(ps[:, 5, (2 + m) * P:(3 + m) * P], wv, u_T, m)
                        last.then_inc(upd_done, 1)
                        pe.wait_ge(upd_out, 1)
                        for bank, first, done in ((6, 0, r_done), (7, 4, n_done), (0, 2, z_done)):
                            for i in range(2):
                                last = project(ps[:, bank, i * P:(i + 1) * P], wih, upd, first + i,
                                               start=False, stop=True, skip_group_check=True)
                            last.then_inc(done, 1)

                    @block.scalar
                    def _(act):
                        act.wait_ge(ssq_done, 1)
                        nc.scalar.activation(std[:, :], ps[:, 5, 0:P], ACT.Sqrt, scale=1.0 / D,
                                             bias=env.eps6[:, 0:1]).then_inc(std_ready, 1)
                        nc.scalar.activation(tiny[:, :], env.zero[:, 0:1], ACT.Exp
                                             ).then_inc(q1_out, 1)
                        act.wait_ge(q1_done, 1)
                        nc.scalar.copy(q1[:, :, :].rearrange("p k n -> p (k n)"),
                                       ps[:, 5, P:3 * P]).then_inc(q1_out, 1)
                        for u, (b, c, tiles) in enumerate(units):
                            ts = slice(tiles[0], tiles[-1] + 1)
                            act.wait_ge(shifted, u + 1)
                            nc.scalar.activation(att[:, b, ts, :], att[:, b, ts, :], ACT.Exp,
                                                 scale=D ** -0.5).then_inc(exped, 1)
                        act.wait_ge(upd_done, 1)
                        nc.scalar.copy(upd[:, :, :].rearrange("p k n -> p (k n)"),
                                       ps[:, 5, 2 * P:4 * P]).then_inc(upd_out, 1)
                        for ms, done in (((0, 1), r_done), ((2, 3), z_done)):
                            if ms[0]:
                                act.wait_ge(n_in, 1)
                                for m in range(KT):
                                    nc.scalar.activation(n_T[:, m, :], n_T[:, m, :], ACT.Tanh,
                                                         bias=gb[:, 0, 4 + m:5 + m]
                                                         ).then_inc(n_out, 1)
                            act.wait_ge(done, 1)
                            for m in ms:
                                nc.scalar.activation(rz[:, m, :],
                                                     ps[:, 0 if m > 1 else 6,
                                                        (m % 2) * P:(m % 2 + 1) * P],
                                                     ACT.Tanh, scale=0.5, bias=gb2[:, m:m + 1]
                                                     ).then_inc(gates, 1)
                        nc.scalar.activation(tiny[:, :], env.ones[:, 0:1], ACT.Sqrt
                                             ).then_inc(gates, 1)

                    @block.vector
                    def _(dve):
                        steps = Steps(dve, own)
                        first_256 = ps[:, 5, 0:2 * P].rearrange("p (k n) -> p k n", k=KT)
                        norm_by_feature = norm[:, 1, :].unsqueeze(2).broadcast_to([P, KT, P])
                        nc.vector.tensor_tensor(sq[:, :, :], sl[:, :, :], sl[:, :, :],
                                                ALU.mult).then_inc(squares, 1)
                        dve.wait_ge(std_ready, 1)
                        steps.done(nc.vector.reciprocal(rs[:, :], std[:, :]))
                        steps.wait()
                        for k in range(KT):
                            nc.vector.scalar_tensor_tensor(
                                out=sn[:, k, :], in0=sl[:, k, :], scalar=norm[:, 0, k:k + 1],
                                in1=rs[:, :], op0=ALU.mult, op1=ALU.mult).then_inc(normed, 1)
                        dve.wait_ge(hid_done, 1)
                        for m in range(KT):
                            steps.done(nc.vector.tensor_scalar(
                                hn[:, m, :], ps[:, 7, (2 + m) * P:(3 + m) * P],
                                gb[:, 1, 4 + m:5 + m], 0.5, ALU.add, ALU.mult))
                        dve.wait_ge(q2_done, 1)
                        nc.vector.tensor_tensor(q2[:, :, :], first_256, norm_by_feature,
                                                ALU.mult).then_inc(q2_out, 1)

                        def unit_views(u):
                            b, c, tiles = units[u]
                            n, ts = len(tiles), slice(tiles[0], tiles[-1] + 1)
                            put = ps[:, 2 * b + c, b * S:(b + n) * S].rearrange(
                                "p (t s) -> p t s", t=n)

                            def over_slots(x):
                                return x[:, b, ts].unsqueeze(2).broadcast_to([P, n, S])

                            return put, att[:, b, ts, :], (b, ts), over_slots

                        def shift(u):
                            put, w, (b, ts), over_slots = unit_views(u)
                            dve.wait_ge(s_done, u + 1)
                            steps.done(nc.vector.tensor_reduce(top[:, b, ts], put, AX, ALU.max))
                            steps.wait()
                            steps.done(nc.vector.tensor_tensor(w, put, over_slots(top),
                                                               ALU.subtract))
                            steps.wait()
                            nc.vector.tensor_tensor(w, w, over_slots(rs_c), ALU.mult
                                                    ).then_inc(shifted, 1)

                        def weigh(u):
                            put, w, (b, ts), over_slots = unit_views(u)
                            dve.wait_ge(exped, u + 1)
                            steps.done(nc.vector.tensor_reduce(tot[:, b, ts], w, AX, ALU.add))
                            steps.wait()
                            steps.done(nc.vector.reciprocal(tot[:, b, ts], tot[:, b, ts]))
                            steps.wait()
                            steps.done(nc.vector.tensor_tensor(tot[:, b, ts], tot[:, b, ts],
                                                               rs_c[:, b, ts], ALU.mult))
                            steps.wait()
                            nc.vector.tensor_tensor(w, w, over_slots(tot), ALU.mult
                                                    ).then_inc(weights, 1)

                        for u in range(5):
                            if u < 4:
                                shift(u)
                            if u >= 1:
                                weigh(u - 1)
                        dve.wait_ge(u_done, 1)
                        steps.done(nc.vector.tensor_scalar(rden[:, :], ps[:, 4, D:D + 1], 1e-6,
                                                           None, ALU.add))
                        steps.wait()
                        steps.done(nc.vector.reciprocal(rden[:, :], rden[:, :]))
                        steps.wait()
                        nc.vector.tensor_scalar(u_n[:, :], ps[:, 4, 0:D], rden[:, 0:1], None,
                                                ALU.mult).then_inc(u_ready, 1)
                        dve.wait_ge(u_turned, 1)
                        nc.vector.tensor_tensor(u_T[:, :, :], first_256, norm_by_feature,
                                                ALU.mult).then_inc(u_out, 1)
                        dve.wait_ge(gates, 2)
                        steps.done(nc.vector.scalar_tensor_tensor(
                            out=hn[:, :, :], in0=rz[:, 0:2, :], scalar=1.0, in1=hn[:, :, :],
                            op0=ALU.add, op1=ALU.mult))
                        steps.wait()
                        dve.wait_ge(n_done, 1)
                        nc.vector.tensor_tensor(
                            n_T[:, :, :], hn[:, :, :],
                            ps[:, 7, 0:2 * P].rearrange("p (m n) -> p m n", m=KT),
                            ALU.add).then_inc(n_in, 1)
                        dve.wait_ge(n_out, KT)
                        steps.done(nc.vector.tensor_tensor(hn[:, :, :], sl[:, :, :], n_T[:, :, :],
                                                           ALU.subtract))
                        steps.wait()
                        dve.wait_ge(gates, 4)
                        steps.done(nc.vector.scalar_tensor_tensor(
                            out=hn[:, :, :], in0=rz[:, 2:4, :], scalar=1.0, in1=hn[:, :, :],
                            op0=ALU.add, op1=ALU.mult))
                        steps.wait()
                        steps.done(nc.vector.scalar_tensor_tensor(
                            out=sl[:, :, :], in0=hn[:, :, :], scalar=0.5, in1=n_T[:, :, :],
                            op0=ALU.mult, op1=ALU.add))

        def keep_slots(r, pair, loads):
            with signals(nc, f"s1_keep{r}", "kept") as (kept,):
                with nc.Block() as block:

                    @block.sync
                    def _(sp):
                        loads(sp)

                    @block.vector
                    def _(dve):
                        nc.vector.tensor_copy(res_T[:, :, bass.ds(pair * P, P)],
                                              sl[:, :, :]).then_inc(kept, 1)

        with nc.Fori(0, T // 2) as i:
            with signals(nc, "s1_ctx", "second_in first_in") as (second_in, first_in):
                prepare(0, 2 * i, lambda sp: load_context(sp, 1, 2 * i + 1, second_in))
                with nc.Fori(0, 3):
                    attend(0)
                keep_slots(0, 2 * i, lambda sp: sp.wait_ge(second_in, 6 * 16))
                prepare(1, 2 * i + 1, lambda sp: load_context(sp, 0, (2 * i + 2) % T, first_in))
                with nc.Fori(0, 3):
                    attend(1)
                keep_slots(1, 2 * i + 1, lambda sp: sp.wait_ge(first_in, 6 * 16))
        add_turned(nc, env, "s1_add", res_T, env.x)


def self_attention(nc, env, stage, w, b_col, b_row, att_T, scale, bias, per_head, sb):
    q_T, k_T, v_nat = sb("q_T", [P, KT, N]), sb("k_T", [P, KT, N]), sb("v_nat", [P, T, D])
    q_own, v_own = sb("q_own", [P, KT, 2 * P]), sb("v_own", [P, 2, D])
    k_bd = sb("k_bd", [P, 2, KT, HPT, P])
    sc, p_T = sb("sc", [P, 2, H, P]), sb("p_T", [P, 2, H, P])
    top, tot = sb("top", [P, 2, H]), sb("tot", [P, 2, H])
    halves = sb("halves", [P, KT, P])
    ps = env.ps
    linear_T(nc, env, f"{stage}_qk", [(env.h_T, w[:, :, 0:D], q_T, b_col[:, 0:KT], None),
                                      (env.h_T, w[:, :, D:2 * D], k_T, b_col[:, KT:2 * KT], None)])
    linear_rows(nc, env, f"{stage}_v", env.h_T, [(w[:, :, 2 * D:3 * D], b_row,
                                                  lambda t: v_nat[:, t, :])])
    with nc.Fori(0, T // 2) as i:
        with signals(nc, f"{stage}_at", "own taken k_in s_done top_ready exped normed p_turned "
                     "act_out dve_out o_done o_out") as (
                own, taken, k_in, s_done, top_ready, exped, normed, p_turned, act_out, dve_out,
                o_done, o_out):
            with nc.Block() as block:

                @block.gpsimd
                def _(pool):
                    for j in range(2):
                        for half in range(KT):
                            nc.gpsimd.tensor_tensor(
                                k_bd[:, j, half, :, :],
                                k_T[:, half, bass.ds(i * (2 * P) + j * P, P)].unsqueeze(1)
                                .broadcast_to([P, HPT, P]),
                                env.head_of.unsqueeze(2).broadcast_to([P, HPT, P]),
                                ALU.mult).then_inc(k_in, 1)

                @block.tensor
                def _(pe):
                    pe.wait_ge(taken, 1)
                    for j in range(2):
                        for g in range(4):
                            if g % 2 == 0:
                                pe.wait_ge(k_in, 2 * j + g // 2 + 1)
                            nc.tensor.matmul(ps[:, 4 * j + g, :],
                                             q_own[:, g // 2, j * P:(j + 1) * P],
                                             k_bd[:, j, g // 2, 4 * (g % 2):4 * (g % 2) + 4, :],
                                             start=True, stop=True).then_inc(s_done, 1)
                    for j in range(2):
                        for g in range(4):
                            pe.wait_ge(normed, 4 * j + g + 1)
                            for h in range(4 * g, 4 * g + 4):
                                last = nc.tensor.transpose(
                                    ps[:, 4 * j + g, (h % 4) * P:(h % 4 + 1) * P],
                                    sc[:, j, h, :], env.ident)
                            last.then_inc(p_turned, 1)
                    pe.wait_ge(taken, 2)
                    for j in range(2):
                        pe.wait_ge(act_out, 2 * j + 2)
                        pe.wait_ge(dve_out, 2 * j + 2)
                        for pair in range(PAIRS):
                            rows = slice(32 * (pair % 4), 32 * (pair % 4) + 32)
                            last = nc.tensor.matmul(
                                ps[rows, 4 * j, (pair // 4) * D:(pair // 4 + 1) * D],
                                v_own[:, j, 2 * DH * pair:2 * DH * (pair + 1)],
                                p_T[:, j, 2 * pair:2 * pair + 2, :], start=True, stop=True)
                        last.then_inc(o_done, 1)

                @block.scalar
                def _(act):
                    nc.scalar.copy(q_own[:, :, :], q_T[:, :, bass.ds(i * (2 * P), 2 * P)]
                                   ).then_inc(taken, 1)
                    nc.scalar.copy(v_own[:, :, :], v_nat[:, bass.ds(2 * i, 2), :]
                                   ).then_inc(taken, 1)
                    for j in range(2):
                        act.wait_ge(top_ready, j + 1)
                        for h in range(H):
                            nc.scalar.activation(sc[:, j, h, :], sc[:, j, h, :], ACT.Exp,
                                                 bias=top[:, j, h:h + 1],
                                                 accum_out=tot[:, j, h:h + 1]).then_inc(exped, 1)
                    for j in range(2):
                        for g in (0, 2):
                            act.wait_ge(p_turned, 4 * j + g + 1)
                            nc.scalar.copy(
                                p_T[:, j, 4 * g:4 * g + 4, :].rearrange("p h n -> p (h n)"),
                                ps[:, 4 * j + g, :]).then_inc(act_out, 1)

                @block.vector
                def _(dve):
                    steps = Steps(dve, own)
                    for j in range(2):
                        for g in range(4):
                            hs = slice(4 * g, 4 * g + 4)
                            dve.wait_ge(s_done, 4 * j + g + 1)
                            steps.done(nc.vector.scalar_tensor_tensor(
                                out=sc[:, j, hs, :],
                                in0=ps[:, 4 * j + g, :].rearrange("p (h n) -> p h n", h=4),
                                scalar=scale,
                                in1=bias[:, hs, :] if per_head else
                                bias.unsqueeze(1).broadcast_to([P, 4, P]),
                                op0=ALU.mult, op1=ALU.add))
                        steps.wait()
                        steps.done(nc.vector.tensor_reduce(top[:, j, :], sc[:, j, :, :], AX,
                                                           ALU.max))
                        steps.wait()
                        nc.vector.tensor_scalar(top[:, j, :], top[:, j, :], -1.0, None, ALU.mult
                                                ).then_inc(top_ready, 1)
                    for j in range(2):
                        for g in range(4):
                            hs = slice(4 * g, 4 * g + 4)
                            dve.wait_ge(exped, H * j + 4 * g + 4)
                            steps.done(nc.vector.reciprocal(tot[:, j, hs], tot[:, j, hs]))
                            steps.wait()
                            nc.vector.tensor_tensor(
                                sc[:, j, hs, :], sc[:, j, hs, :],
                                tot[:, j, hs].unsqueeze(2).broadcast_to([P, 4, P]), ALU.mult
                            ).then_inc(normed, 1)
                    for j in range(2):
                        for g in (1, 3):
                            dve.wait_ge(p_turned, 4 * j + g + 1)
                            nc.vector.tensor_copy(
                                p_T[:, j, 4 * g:4 * g + 4, :].rearrange("p h n -> p (h n)"),
                                ps[:, 4 * j + g, :]).then_inc(dve_out, 1)
                    for j in range(2):
                        dve.wait_ge(o_done, j + 1)
                        put = ps[:, 4 * j, :].rearrange("p (k h n) -> p k h n", k=KT, h=2)
                        steps.done(nc.vector.tensor_scalar(
                            halves[:, :, :], put[:, :, 0, :], env.parity[:, 0:1], None, ALU.mult))
                        steps.wait()
                        nc.vector.scalar_tensor_tensor(
                            out=att_T[:, :, bass.ds(i * (2 * P) + j * P, P)],
                            in0=put[:, :, 1, :], scalar=env.parity[:, 1:2], in1=halves[:, :, :],
                            op0=ALU.mult, op1=ALU.add).then_inc(o_out, 1)
                        dve.wait_ge(o_out, j + 1)


def l1_attn(nc, env, d):
    mem, sb = scoped(nc, "a1")
    with mem:
        w, wo = sb("w", [P, KT, 3 * D]), sb("wo", [P, KT, D])
        b_col, b_row = sb("b_col", [P, 2 * KT]), sb("b_row", [P, 2, D])
        att_T = sb("att_T", [P, KT, N])
        layernorm(nc, env, "a1_ln", env.x, env.h, env.h_T, loads=[
            (w[:, :, :], wview(d["L1_attn_w_qkv"])), (wo[:, :, :], wview(d["L1_attn_w_o"])),
            (b_col[:, :], d["L1_attn_b_qk"]),
            (b_row[:, 0, :], d["L1_attn_b_qkv"][2 * D:3 * D].partition_broadcast(P)),
            (b_row[:, 1, :], d["L1_attn_b_o"].partition_broadcast(P))])
        self_attention(nc, env, "a1", w, b_col, b_row[:, 0, :], att_T, D ** -0.5, env.cross, False,
                       sb)
        project_add(nc, env, "a1_o", att_T, wo, b_row[:, 1, :], env.x, also=env.h)


def l1_ffn(nc, env, d):
    E, HD, ITERS, G = 8, 64, 2, 4
    STEP = 4
    mem, sb = scoped(nc, "g1")
    with mem:
        rw1, hw1 = sb("rw1", [P, KT, HD]), sb("hw1", [P, KT, HD])
        rw2, hw2 = sb("rw2", [HD, 1, E]), sb("hw2", [HD, 1, 1])
        rb1, hb1, sb1 = (sb(n, [HD, 1]) for n in ("rb1", "hb1", "sb1"))
        rb2, fb2 = sb("rb2", [1, E]), sb("fb2", [P, D])
        hb2 = sb("hb2", [P, 1])
        ew1, eb1 = sb("ew1", [P, 2 * KT, E * HD]), sb("eb1", [P, G])
        ew2, eb2 = sb("ew2", [P, G, 3 * D]), sb("eb2", [P, 3 * D])
        sw1, sw2 = sb("sw1", [P, 2 * KT, HD]), sb("sw2", [P, 3 * D])
        fw1, fb1, fw2 = sb("fw1", [P, KT, 2 * D]), sb("fb1", [P, 2 * KT]), sb("fw2", [P, 2 * KT, D])
        mu, iw, sw = sb("mu", [P, D]), sb("iw", [P, D]), sb("sw", [P, 2])
        r_T, sh_T = sb("r_T", [HD, 1, N]), sb("sh_T", [P, 1, N])
        hid_T = sb("hid_T", [P, G, N])
        sel = sb("sel", [E, G, P])
        masks = sb("masks", [P, 2, G, N], BF16)
        probs, chosen = sb("probs", [P, T, E]), sb("chosen", [P, T, 2, E])
        chosen_T = sb("chosen_T", [P, 2, N])
        weights, coef, wsum = sb("weights", [P, T, 2]), sb("coef", [P, T, 3]), sb("wsum", [P, T])
        m8, i8, i_f = sb("m8", [P, T, 8]), sb("i8", [P, T, 8], U32), sb("i_f", [P, T, 2])
        top, total, halt = sb("top", [P, T]), sb("total", [P, T]), sb("halt", [P, T])
        cur, vel = sb("cur", [P, T, D]), sb("vel", [P, T, D])
        cv_T = sb("cv_T", [P, 2 * KT, N])
        hm = sb("hm", [P, 2, 2, G, P])
        sh_own, ch_own = sb("sh_own", [P, STEP * P]), sb("ch_own", [P, 2, STEP * P])
        th, sp_ = sb("th", [P, 2, 3, 2, D]), sb("sp", [P, 2, 3, D])
        lg = sb("lg", [P, 2, 3, D])
        v3, x3 = sb("v3", [P, 3, D]), sb("x3", [P, 3, D])
        away, acc = sb("away", [P, D]), sb("acc", [P, 2, D])
        ps = env.ps
        with signals(nc, "g1_pad", "own") as (own,):
            with nc.Block() as block:

                @block.vector
                def _(dve):
                    steps = Steps(dve, own)
                    for a in (chosen_T, eb2):
                        steps.done(nc.vector.memset(a[tuple([slice(None)] * len(a.shape))], 0.0))
                    steps.done(nc.vector.memset(sw2[HD:P, :], 0.0))
                    steps.done(nc.vector.memset(sh_T[HD:P, 0, :], 0.0))
                    steps.wait()
                    steps.done(nc.vector.memset(sh_T[HD:HD + 1, 0, :], 1.0))

        layernorm(nc, env, "g1_ln", env.x, env.h, env.h_T, loads=[
            (rw1[:, :, :], wview(d["L1_ffn_router_w1"])), (hw1[:, :, :], wview(d["L1_ffn_halt_w1"])),
            (rw2[:, 0, :], d["L1_ffn_router_w2"]), (hw2[:, 0, :], d["L1_ffn_halt_w2"]),
            (rb1[:, :], d["L1_ffn_router_b1"].unsqueeze(1)),
            (hb1[:, :], d["L1_ffn_halt_b1"].unsqueeze(1)),
            (sb1[:, :], d["L1_ffn_shared_b1"].unsqueeze(1)),
            (rb2[:, :], d["L1_ffn_router_b2"].unsqueeze(0)),
            (sw2[HD:HD + 1, :], d["L1_ffn_shared_b2"].unsqueeze(0)),
            (fb2[:, :], d["L1_ffn_refine_b2"].partition_broadcast(P)),
            (hb2[:, :], d["L1_ffn_halt_b2"].partition_broadcast(P)),
            (sw[:, 0:1], d["L1_ffn_shared_weight"].partition_broadcast(P)),
            (ew1[:, :, :], wview(d["L1_ffn_expert_w1"])), (eb1[:, :], d["L1_ffn_expert_b1"]),
            (ew2[:, :, :], wview(d["L1_ffn_expert_w2"])), (eb2[0:E, :], d["L1_ffn_expert_b2"]),
            (sw1[:, :, :], wview(d["L1_ffn_shared_w1"])), (sw2[0:HD, :], d["L1_ffn_shared_w2"]),
            (fw1[:, :, :], wview(d["L1_ffn_refine_w1"])), (fb1[:, :], d["L1_ffn_refine_b1"]),
            (fw2[:, :, :], wview(d["L1_ffn_refine_w2"])),
            (mu[:, :], d["L1_ffn_mu"].partition_broadcast(P)),
            (iw[:, :], d["L1_ffn_integration_weight"].partition_broadcast(P)),
            (sel[:, :, :], d["expert_sel"])])
        linear_T(nc, env, "g1_r", [(env.h_T, rw1, r_T, rb1, "gelu")])
        with signals(nc, "g1_route", "own logits shifted exped neg state picked turned turned_out "
                     "spread spread_out") as (own, logits, shifted, exped, neg, state, picked,
                                              turned, turned_out, spread, spread_out):
            with nc.Block() as block:

                @block.gpsimd
                def _(pool):
                    nc.gpsimd.memset(vel[:, :, :], 0.0).then_inc(state, 1)
                    nc.gpsimd.memset(cv_T[:, KT:2 * KT, :], 0.0).then_inc(state, 1)
                    nc.gpsimd.tensor_copy(cur[:, :, :], env.h[:, :, :]).then_inc(state, 1)
                    nc.gpsimd.tensor_copy(cv_T[:, 0:KT, :], env.h_T[:, :, :]).then_inc(state, 1)

                @block.tensor
                def _(pe):
                    for t in range(T):
                        put = ps[:, 0, t * E:(t + 1) * E]
                        nc.tensor.matmul(put, r_T[:, 0, t * P:(t + 1) * P], rw2[:, 0, :],
                                         start=True, stop=False)
                        last = nc.tensor.matmul(put, env.ones[0:1, :], rb2[:, :],
                                                start=False, stop=True)
                    last.then_inc(logits, 1)
                    pe.wait_ge(picked, 1)
                    for k in range(2):
                        for t in range(T):
                            last = nc.tensor.transpose(
                                ps[0:E, 1 + 2 * k + t // 4, (t % 4) * P:(t % 4 + 1) * P],
                                chosen[:, t, k, :], env.ident)
                        last.then_inc(turned, 1)
                    pe.wait_ge(turned_out, 2)
                    n = 0
                    for k in range(2):
                        for g in range(G):
                            for c in range(2):
                                if n >= 8:
                                    pe.wait_ge(spread_out, n - 7)
                                nc.tensor.matmul(ps[:, n % 8, :], sel[:, g, :],
                                                 chosen_T[0:E, k, c * NH:(c + 1) * NH], start=True,
                                                 stop=True).then_inc(spread, 1)
                                n += 1

                @block.scalar
                def _(act):
                    act.wait_ge(shifted, 1)
                    nc.scalar.activation(probs[:, :, :], probs[:, :, :], ACT.Exp).then_inc(exped, 1)
                    nc.scalar.activation(sw[:, 1:2], sw[:, 0:1], ACT.Exp, scale=-1.0
                                         ).then_inc(neg, 1)

                @block.vector
                def _(dve):
                    steps = Steps(dve, own)
                    dve.wait_ge(logits, 1)
                    steps.done(nc.vector.tensor_copy(
                        probs[:, :, :], ps[:, 0, 0:T * E].rearrange("p (t e) -> p t e", t=T)))
                    steps.wait()
                    row_softmax(nc, dve, probs[:, :, :], top[:, :], total[:, :], E, exped, shifted,
                                steps)
                    top2(nc, env, dve, probs, E, weights[:, :, :], chosen, m8, i8, i_f, steps)
                    steps.done(nc.vector.tensor_reduce(wsum[:, :], weights[:, :, :], AX, ALU.add))
                    steps.wait()
                    steps.done(nc.vector.reciprocal(wsum[:, :], wsum[:, :]))
                    dve.wait_ge(neg, 1)
                    steps.done(nc.vector.tensor_scalar(sw[:, 1:2], sw[:, 1:2], 1.0, None, ALU.add))
                    steps.wait()
                    steps.done(nc.vector.reciprocal(sw[:, 0:1], sw[:, 1:2]))
                    steps.wait()
                    steps.done(nc.vector.tensor_scalar(sw[:, 1:2], sw[:, 0:1], -1.0, 1.0, ALU.mult,
                                                       ALU.add))
                    steps.done(nc.vector.tensor_copy(
                        coef[:, :, 0:1], sw[:, 0:1].unsqueeze(1).broadcast_to([P, T, 1])))
                    steps.done(nc.vector.tensor_tensor(
                        weights[:, :, :], weights[:, :, :],
                        wsum[:, :].unsqueeze(2).broadcast_to([P, T, 2]), ALU.mult))
                    steps.wait()
                    nc.vector.tensor_scalar(coef[:, :, 1:3], weights[:, :, :], sw[:, 1:2], None,
                                            ALU.mult).then_inc(picked, 1)
                    for k in range(2):
                        dve.wait_ge(turned, k + 1)
                        nc.vector.tensor_copy(
                            chosen_T[0:E, k, :].rearrange("e (c n) -> e c n", c=2),
                            ps[0:E, 1 + 2 * k:3 + 2 * k, :]).then_inc(turned_out, 1)
                    n = 0
                    for k in range(2):
                        for g in range(G):
                            for c in range(2):
                                dve.wait_ge(spread, n + 1)
                                nc.vector.tensor_copy(masks[:, k, g, c * NH:(c + 1) * NH],
                                                      ps[:, n % 8, :]).then_inc(spread_out, 1)
                                n += 1

        with nc.Fori(0, ITERS):
            linear_T(nc, env, "g1_hid", [(cv_T, ew1, hid_T, eb1, "gelu"),
                                         (cv_T, sw1, sh_T, sb1, "gelu"),
                                         (cv_T[:, 0:KT], hw1, r_T, hb1, "gelu")])
            with signals(nc, "g1_halt", "own product exped") as (own, product, exped):
                with nc.Block() as block:

                    @block.tensor
                    def _(pe):
                        for t in range(T):
                            last = nc.tensor.matmul(ps[:, 0, t:t + 1], r_T[:, 0, t * P:(t + 1) * P],
                                                    hw2[:, 0, :], start=True, stop=True)
                        last.then_inc(product, 1)

                    @block.scalar
                    def _(act):
                        act.wait_ge(own, 1)
                        nc.scalar.activation(halt[:, :], halt[:, :], ACT.Tanh, scale=0.5
                                             ).then_inc(exped, 1)

                    @block.vector
                    def _(dve):
                        steps = Steps(dve, own)
                        dve.wait_ge(product, 1)
                        steps.done(nc.vector.tensor_scalar(halt[:, :], ps[:, 0, 0:T], hb2[:, 0:1],
                                                           None, ALU.add))
                        dve.wait_ge(exped, 1)
                        steps.done(nc.vector.tensor_scalar(halt[:, :], halt[:, :], 0.5, 0.5,
                                                           ALU.mult, ALU.add))

            with nc.Fori(0, T // STEP) as i:
                with signals(nc, "g1_step", "own taken masked ctrl emptied logged used "
                             "new_state") as (
                        own, taken, masked, ctrl, emptied, logged, used, new_state):
                    group = bass.ds(i * (STEP * P), STEP * P)
                    with nc.Block() as block:

                        @block.gpsimd
                        def _(pool):
                            nc.gpsimd.tensor_copy(sh_own[:, :], sh_T[:, 0, group]
                                                  ).then_inc(taken, 1)
                            for j in range(STEP):
                                tile = bass.ds(i * (STEP * P) + j * P, P)
                                if j >= 2:
                                    pool.wait_ge(ctrl, 3 * (j - 1))
                                for k in range(2):
                                    nc.gpsimd.tensor_tensor(hm[:, j % 2, k, :, :],
                                                            hid_T[:, :, tile],
                                                            masks[:, k, :, tile],
                                                            ALU.mult).then_inc(masked, 1)
                                    if j == 0:
                                        nc.gpsimd.tensor_copy(ch_own[:, k, :],
                                                              chosen_T[:, k, group]
                                                              ).then_inc(taken, 1)

                        @block.tensor
                        def _(pe):
                            for j in range(STEP):
                                cols = slice(j * P, (j + 1) * P)
                                for s in range(3):
                                    n = 3 * j + s
                                    if n >= 4:
                                        pe.wait_ge(emptied, n - 3)
                                    if n < 3:
                                        pe.wait_ge(taken, n + 1)
                                    if s:
                                        pe.wait_ge(masked, 2 * j + s)
                                    for bank, part in ((2 * (n % 4), slice(0, 2 * D)),
                                                       (2 * (n % 4) + 1, slice(2 * D, 3 * D))):
                                        put = ps[:, bank, 0:part.stop - part.start]
                                        if s == 0:
                                            last = nc.tensor.matmul(
                                                put, sh_own[:, cols], sw2[:, part],
                                                start=True, stop=True)
                                            continue
                                        for g in range(G):
                                            nc.tensor.matmul(put, hm[:, j % 2, s - 1, g, :],
                                                             ew2[:, g, part],
                                                             start=(g == 0), stop=False)
                                        last = nc.tensor.matmul(put, ch_own[:, s - 1, cols],
                                                                eb2[:, part], start=False,
                                                                stop=True)
                                    last.then_inc(ctrl, 1)

                        @block.scalar
                        def _(act):
                            for j in range(STEP):
                                if j >= 2:
                                    act.wait_ge(used, j - 1)
                                r = j % 2
                                for s in range(3):
                                    n = 3 * j + s
                                    pair = ps[:, 2 * (n % 4):2 * (n % 4) + 2, 0:D]
                                    b_part = ps[:, 2 * (n % 4), D:2 * D]
                                    act.wait_ge(ctrl, n + 1)
                                    nc.scalar.activation(th[:, r, s, :, :], pair, ACT.Tanh,
                                                         scale=0.5)
                                    nc.scalar.activation(sp_[:, r, s, :], b_part, ACT.Relu)
                                    nc.scalar.activation(lg[:, r, s, :], b_part, ACT.Abs
                                                         ).then_inc(emptied, 1)
                                act.wait_ge(emptied, 3 * j + 3)
                                nc.scalar.activation(lg[:, r, :, :], lg[:, r, :, :], ACT.Exp,
                                                     scale=-1.0).then_inc(logged, 1)
                                act.wait_ge(logged, 2 * j + 1)
                                nc.scalar.activation(lg[:, r, :, :], lg[:, r, :, :], ACT.Ln,
                                                     bias=env.ones[:, 0:1]).then_inc(logged, 1)

                        @block.vector
                        def _(dve):
                            steps = Steps(dve, own)
                            for j in range(STEP):
                                r, tile = j % 2, bass.ds(i * STEP + j, 1)
                                cur_own, vel_own = cur[:, tile, :], vel[:, tile, :]
                                steps.done(nc.vector.tensor_tensor(
                                    away[:, :], cur_own.squeeze(1), mu[:, :], ALU.subtract))

                                def three(x):
                                    return x.broadcast_to([P, 3, D])

                                dve.wait_ge(emptied, 3 * j + 3)
                                steps.done(nc.vector.scalar_tensor_tensor(
                                    out=v3[:, :, :], in0=th[:, r, :, 0, :], scalar=1.0,
                                    in1=three(vel_own), op0=ALU.add, op1=ALU.mult))
                                dve.wait_ge(logged, 2 * j + 2)
                                steps.done(nc.vector.tensor_tensor(
                                    sp_[:, r, :, :], sp_[:, r, :, :], lg[:, r, :, :], ALU.add))
                                steps.wait()
                                steps.done(nc.vector.tensor_tensor(
                                    sp_[:, r, :, :], sp_[:, r, :, :],
                                    three(away[:, :].unsqueeze(1)), ALU.mult))
                                steps.wait()
                                steps.done(nc.vector.scalar_tensor_tensor(
                                    out=v3[:, :, :], in0=v3[:, :, :], scalar=0.5,
                                    in1=sp_[:, r, :, :], op0=ALU.mult, op1=ALU.subtract))
                                steps.wait()
                                nc.vector.scalar_tensor_tensor(
                                    out=x3[:, :, :], in0=th[:, r, :, 1, :], scalar=1.0,
                                    in1=v3[:, :, :], op0=ALU.add, op1=ALU.mult).then_inc(used, 1)
                                dve.wait_ge(used, j + 1)
                                steps.done(nc.vector.scalar_tensor_tensor(
                                    out=x3[:, :, :], in0=x3[:, :, :], scalar=0.05,
                                    in1=three(cur_own), op0=ALU.mult, op1=ALU.add))
                                steps.wait()
                                for s in range(3):
                                    c = coef[:, tile, s:s + 1].squeeze(1)
                                    for n, src in ((0, x3), (1, v3)):
                                        if s == 0:
                                            steps.done(nc.vector.tensor_scalar(
                                                acc[:, n, :], src[:, s, :], c, None, ALU.mult))
                                        else:
                                            steps.done(nc.vector.scalar_tensor_tensor(
                                                out=acc[:, n, :], in0=src[:, s, :], scalar=c,
                                                in1=acc[:, n, :], op0=ALU.mult, op1=ALU.add))
                                    steps.wait()
                                for n, state in ((0, cur_own), (1, vel_own)):
                                    steps.done(nc.vector.tensor_tensor(
                                        acc[:, n, :], acc[:, n, :], state.squeeze(1),
                                        ALU.subtract))
                                steps.wait()
                                for n, state in ((0, cur_own), (1, vel_own)):
                                    nc.vector.scalar_tensor_tensor(
                                        out=state.squeeze(1), in0=acc[:, n, :],
                                        scalar=halt[:, tile], in1=state.squeeze(1),
                                        op0=ALU.mult, op1=ALU.add).then_inc(new_state, 1)
                                dve.wait_ge(new_state, 2 * j + 2)
            turn_rows(nc, env, "g1_cur", cur, cv_T[:, 0:KT])
            turn_rows(nc, env, "g1_vel", vel, cv_T[:, KT:2 * KT])
        linear_T(nc, env, "g1_ref", [(cv_T[:, 0:KT], fw1, hid_T, fb1, "gelu")])
        project_add(nc, env, "g1_out", hid_T, fw2, fb2[:, :], env.x, also=env.h, scale=iw[:, :])



def l2_xattn(nc, env, d):
    mem, sb = scoped(nc, "x2")
    with mem:
        wq, wk, wv, wo = (sb(n, [P, KT, D]) for n in ("wq", "wk", "wv", "wo"))
        q_T, att_T, nb = sb("q_T", [P, KT, N]), sb("att_T", [P, KT, N]), sb("nb", [P, 2])
        kv = wview(d["L2_xattn_Wkv"])
        layernorm(nc, env, "x2_ln", env.x, env.h, env.h_T, loads=[
            (wq[:, :, :], wview(d["L2_xattn_Wq"])), (wk[:, :, :], kv[:, :, 0:D]),
            (wv[:, :, :], kv[:, :, D:2 * D]), (wo[:, :, :], wview(d["L2_xattn_Wo"])),
            (nb[:, 0:1], d["L2_xattn_nbias"].partition_broadcast(P))])
        with signals(nc, "x2_nb", "ready") as (ready,):
            with nc.Block() as block:

                @block.vector
                def _(dve):
                    nc.vector.tensor_scalar(nb[:, 1:2], nb[:, 0:1], -float(DH) ** 0.5, None,
                                            ALU.mult).then_inc(ready, 1)
        linear_T(nc, env, "x2_q", [(env.h_T, wq, q_T, None, None)])
        context_heads(nc, env, "x2", d["ctx_T"], q_T, att_T, wk, wv, softmax=False,
                      notmask=d["mask_T"], nb=nb)
        project_add(nc, env, "x2_o", att_T, wo, None, env.x)


def l2_attn(nc, env, d):
    F = 64
    mem, sb = scoped(nc, "a2")
    with mem:
        wq, wk, wv, wo = (sb(n, [P, KT, D]) for n in ("wq", "wk", "wv", "wo"))
        b_rows = sb("b_rows", [P, 4, D])
        proj = sb("proj", [P, KT, HPT, F])
        qk, v_aug = sb("qk", [P, 2, T, D]), sb("v_aug", [P, T, PAIRS, 2 * DH + 1])
        sq, ssq = sb("sq", [P, 2, T, D]), sb("ssq", [P, 2, T * H])
        q_T, k_T = sb("q_T", [P, KT, N]), sb("k_T", [P, KT, N])
        qf_T, kf = sb("qf_T", [P, PAIRS, N]), sb("kf", [P, T, H * F])
        kv = sb("kv", [P, 2, 2, PAIRS, 2 * DH + 2])
        nrm, att_T = sb("nrm", [P, T, H]), sb("att_T", [P, KT, N])
        o_own = sb("o_own", [P, H])
        ps = env.ps
        layernorm(nc, env, "a2_ln", env.x, env.h, env.h_T, loads=[
            (wq[:, :, :], wview(d["L2_attn_Wq"])), (wk[:, :, :], wview(d["L2_attn_Wk"])),
            (wv[:, :, :], wview(d["L2_attn_Wv"])), (wo[:, :, :], wview(d["L2_attn_Wo"])),
            (b_rows[:, 0, :], d["L2_attn_bq"].partition_broadcast(P)),
            (b_rows[:, 1, :], d["L2_attn_bk"].partition_broadcast(P)),
            (b_rows[:, 2, :], d["L2_attn_bv"].partition_broadcast(P)),
            (b_rows[:, 3, :], d["L2_attn_bo"].partition_broadcast(P)),
            (proj[:, :, :, :], d["proj_rows"])])
        linear_rows(nc, env, "a2_qkv", env.h_T, [
            (wq, b_rows[:, 0, :], lambda t: qk[:, 0, t, :]),
            (wk, b_rows[:, 1, :], lambda t: qk[:, 1, t, :]),
            (wv, b_rows[:, 2, :], lambda t: v_aug[:, t, :, 0:2 * DH])])
        with signals(nc, "a2_norm", "own sum std normed placed") as (
                own, summed, std_ready, normed, placed):
            with nc.Block() as block:

                @block.gpsimd
                def _(pool):
                    for half in range(KT):
                        nc.gpsimd.tensor_tensor(
                            proj[:, half, :, :], proj[:, half, :, :],
                            env.head_of.unsqueeze(2).broadcast_to([P, HPT, F]),
                            ALU.mult).then_inc(placed, 1)
                    nc.gpsimd.memset(v_aug[:, :, :, 2 * DH:2 * DH + 1], 1.0).then_inc(placed, 1)

                @block.scalar
                def _(act):
                    for n in range(2):
                        act.wait_ge(summed, n + 1)
                        nc.scalar.activation(ssq[:, n, :], ssq[:, n, :], ACT.Sqrt,
                                             bias=env.zero[:, 0:1]).then_inc(std_ready, 1)

                @block.vector
                def _(dve):
                    steps = Steps(dve, own)
                    for n in range(2):
                        steps.done(nc.vector.tensor_tensor(sq[:, n], qk[:, n], qk[:, n], ALU.mult))
                        steps.wait()
                        nc.vector.tensor_reduce(
                            ssq[:, n, :], sq[:, n].rearrange("p t (h d) -> p (t h) d", h=H), AX,
                            ALU.add).then_inc(summed, 1)
                    for n in range(2):
                        dve.wait_ge(std_ready, n + 1)
                        steps.done(nc.vector.tensor_scalar(ssq[:, n, :], ssq[:, n, :], 1e-8, None,
                                                           ALU.add))
                        steps.wait()
                        steps.done(nc.vector.reciprocal(ssq[:, n, :], ssq[:, n, :]))
                        steps.wait()
                        view = qk[:, n].rearrange("p t (h d) -> p (t h) d", h=H)
                        nc.vector.tensor_tensor(
                            view, view, ssq[:, n, :].unsqueeze(2).broadcast_to([P, T * H, DH]),
                            ALU.mult).then_inc(normed, 1)
        turn_rows(nc, env, "a2_qT", qk[:, 0], q_T)
        turn_rows(nc, env, "a2_kT", qk[:, 1], k_T)
        groups = [(0, j, c) for j in range(PAIRS) for c in range(2)] + \
                 [(1, t, c) for t in range(T) for c in range(2)]
        with signals(nc, "a2_feat", "product act_high dve_out act_out") as (
                product, act_high, dve_out, act_out):
            with nc.Block() as block:

                def target(kind, a, c):
                    return (qf_T[:, a, c * NH:(c + 1) * NH] if kind == 0
                            else kf[:, a, c * NH:(c + 1) * NH])

                @block.tensor
                def _(pe):
                    for g, (kind, a, c) in enumerate(groups):
                        if g >= 8:
                            pe.wait_ge((dve_out, act_high)[g % 2], (g - 8) // 2 + 1)
                        if kind == 0:
                            last = nc.tensor.matmul(
                                ps[:, g % 8, :],
                                proj[:, a // 4, 2 * (a % 4):2 * (a % 4) + 2, :],
                                q_T[:, a // 4, c * NH:(c + 1) * NH], start=True, stop=True)
                        else:
                            last = nc.tensor.matmul(
                                ps[:, g % 8, :], k_T[:, c, a * P:(a + 1) * P],
                                proj[:, c, :, :], start=True, stop=True)
                        last.then_inc(product, 1)

                @block.vector
                def _(dve):
                    for g in range(0, len(groups), 2):
                        dve.wait_ge(product, g + 1)
                        nc.vector.tensor_scalar(target(*groups[g]), ps[:, g % 8, :], 0.0, 0.1,
                                                ALU.max, ALU.add).then_inc(dve_out, 1)

                @block.scalar
                def _(act):
                    for g in range(1, len(groups), 2):
                        act.wait_ge(product, g + 1)
                        nc.scalar.activation(target(*groups[g]), ps[:, g % 8, :], ACT.Relu
                                             ).then_inc(act_high, 1)
                        act.wait_ge(act_high, g // 2 + 1)
                        nc.scalar.add(target(*groups[g]), target(*groups[g]), env.tenth
                                      ).then_inc(act_out, 1)

        W = 2 * DH + 1
        with signals(nc, "a2_lin", "own kv_done placed2 o_done o_taken") as (
                own, kv_done, kv_placed, o_done, o_taken):
            with nc.Block() as block:

                @block.tensor
                def _(pe):
                    def key_values(t):
                        if t >= 2:
                            pe.wait_ge(kv_placed, 4 * (t - 1))
                        for b in range(2):
                            rows = slice(b * S, (b + 1) * S)
                            for j in range(PAIRS):
                                last = nc.tensor.matmul(
                                    ps[:, 2 * (t % 2) + b, W * j:W * (j + 1)],
                                    kf[rows, t, 2 * F * j:2 * F * (j + 1)], v_aug[rows, t, j, :],
                                    start=True, stop=True)
                        last.then_inc(kv_done, 1)

                    def outputs(t):
                        pe.wait_ge(kv_placed, 4 * (t + 1))
                        if t >= 2:
                            pe.wait_ge(o_taken, t - 1)
                        for b in range(2):
                            for j in range(PAIRS):
                                last = nc.tensor.matmul(
                                    ps[b * S:(b + 1) * S, 4 + t % 2, (W + 1) * j:(W + 1) * (j + 1)],
                                    qf_T[:, j, t * P + b * S:t * P + (b + 1) * S],
                                    kv[:, t % 2, b, j, :], start=True, stop=True)
                        last.then_inc(o_done, 1)

                    for t in range(T):
                        key_values(t)
                        if t:
                            outputs(t - 1)
                    outputs(T - 1)

                @block.vector
                def _(dve):
                    steps = Steps(dve, own)

                    def place(t):
                        dve.wait_ge(kv_done, t + 1)
                        if t >= 2:
                            dve.wait_ge(o_done, t - 1)
                        for b in range(2):
                            put = ps[:, 2 * (t % 2) + b, 0:W * PAIRS].rearrange(
                                "p (j w) -> p j w", w=W)
                            own_head = env.own_head.unsqueeze(1).broadcast_to([P, PAIRS, 2 * DH])
                            nc.vector.tensor_tensor(kv[:, t % 2, b, :, 0:2 * DH],
                                                    put[:, :, 0:2 * DH], own_head,
                                                    ALU.mult).then_inc(kv_placed, 1)
                            nc.vector.tensor_tensor(
                                kv[:, t % 2, b, :, 2 * DH:2 * DH + 2],
                                put[:, :, 2 * DH:W].broadcast_to([P, PAIRS, 2]),
                                env.which_head.unsqueeze(1).broadcast_to([P, PAIRS, 2]),
                                ALU.mult).then_inc(kv_placed, 1)

                    def divide(t):
                        dve.wait_ge(o_done, t + 1)
                        put = ps[:, 4 + t % 2, 0:(W + 1) * PAIRS].rearrange("p (j w) -> p j w",
                                                                            w=W + 1)
                        steps.done(nc.vector.tensor_scalar(
                            nrm[:, t, :].rearrange("p (j h) -> p j h", h=2),
                            put[:, :, 2 * DH:2 * DH + 2], 1e-6, None, ALU.max))
                        steps.wait()
                        steps.done(nc.vector.reciprocal(nrm[:, t, :], nrm[:, t, :]))
                        steps.wait()
                        nc.vector.tensor_tensor(
                            env.rows[:, t, :].rearrange("p (j h d) -> p j h d", j=PAIRS, h=2),
                            put[:, :, 0:2 * DH].rearrange("p j (h d) -> p j h d", h=2),
                            nrm[:, t, :].rearrange("p (j h) -> p j h", h=2).unsqueeze(3)
                            .broadcast_to([P, PAIRS, 2, DH]), ALU.mult).then_inc(o_taken, 1)

                    for t in range(T):
                        place(t)
                        if t:
                            divide(t - 1)
                    divide(T - 1)
        turn_rows(nc, env, "a2_turn", env.rows, att_T)
        project_add(nc, env, "a2_o", att_T, wo, b_rows[:, 3, :], env.x)


def l2_ffn(nc, env, d):
    E, TOP, ROUTE_SCALE = 16, 8, 2.826
    mem, sb = scoped(nc, "f2")
    with mem:
        gate, bias = sb("gate", [P, KT, E]), sb("bias", [P, E])
        wg, wu, wd = (sb(n, [P, KT, D]) for n in ("wg", "wu", "wd"))
        scores, sel = sb("scores", [P, T, E]), sb("sel", [P, T, E])
        m8, rest, picked = sb("m8", [P, T, TOP]), sb("rest", [P, T, E]), sb("picked", [P, T, E])
        total, comb = sb("total", [P, T]), sb("comb", [P, T, E + 1])
        g_T, h_T = sb("g_T", [P, 2, NH]), sb("hid_T", [P, KT, N])
        ps = env.ps

        def weights_of(e):
            return [(wg[:, :, :], wview(d["L2_w_gate"][e])), (wu[:, :, :], wview(d["L2_w_up"][e]))]

        layernorm(nc, env, "f2_ln", env.x, env.h, env.h_T, loads=[
            (gate[:, :, :], wview(d["L2_ffn_gate_w"])),
            (bias[:, :], d["L2_ffn_expert_bias"].partition_broadcast(P)), *weights_of(0)])
        with signals(nc, "f2_route", "own logits logits_out exped") as (
                own, logits, logits_out, exped):
            with nc.Block() as block:

                @block.tensor
                def _(pe):
                    for t in range(T):
                        for k in range(KT):
                            last = nc.tensor.matmul(ps[:, 0, t * E:(t + 1) * E],
                                                    env.h_T[:, k, t * P:(t + 1) * P],
                                                    gate[:, k, :], start=(k == 0),
                                                    stop=(k == KT - 1))
                    last.then_inc(logits, 1)

                @block.scalar
                def _(act):
                    act.wait_ge(logits, 1)
                    nc.scalar.activation(scores[:, :, :].rearrange("p t e -> p (t e)"),
                                         ps[:, 0, 0:T * E], ACT.Sigmoid).then_inc(exped, 1)

                @block.vector
                def _(dve):
                    steps = Steps(dve, own)
                    dve.wait_ge(exped, 1)
                    steps.done(nc.vector.tensor_tensor(
                        sel[:, :, :], scores[:, :, :],
                        bias[:, :].unsqueeze(1).broadcast_to([P, T, E]), ALU.add))
                    steps.wait()
                    for t in range(T):
                        steps.done(nc.vector.max(m8[:, t, :], sel[:, t, :]))
                    steps.wait()
                    for t in range(T):
                        steps.done(nc.vector.match_replace(rest[:, t, :], m8[:, t, :],
                                                           sel[:, t, :], -3e38))
                    steps.wait()
                    steps.done(nc.vector.tensor_tensor(picked[:, :, :], rest[:, :, :],
                                                       sel[:, :, :], ALU.not_equal))
                    steps.wait()
                    steps.done(nc.vector.tensor_tensor(picked[:, :, :], picked[:, :, :],
                                                       scores[:, :, :], ALU.mult))
                    steps.wait()
                    steps.done(nc.vector.tensor_reduce(total[:, :], picked[:, :, :], AX, ALU.add))
                    steps.wait()
                    steps.done(nc.vector.reciprocal(total[:, :], total[:, :]))
                    steps.wait()
                    steps.done(nc.vector.tensor_tensor(
                        picked[:, :, :], picked[:, :, :],
                        total[:, :].unsqueeze(2).broadcast_to([P, T, E]), ALU.mult))
                    steps.wait()
                    steps.done(nc.vector.tensor_scalar(comb[:, :, 0:E], picked[:, :, :],
                                                       ROUTE_SCALE, None, ALU.mult))
                    steps.done(nc.vector.memset(comb[:, :, E:E + 1], 1.0))

        with nc.Fori(0, E + 1) as e:
            with signals(nc, "f2_up", "loaded product silu_done gated") as (
                    loaded, product, silu_done, gated):
                with nc.Block() as block:

                    @block.sync
                    def _(sp):
                        load_all(sp, [(wd[:, :, :], wview(d["L2_w_down"][e]))], loaded)

                    @block.tensor
                    def _(pe):
                        for g in range(4):
                            m, c = g // 2, g % 2
                            for n, w in ((0, wg), (1, wu)):
                                for k in range(KT):
                                    last = nc.tensor.matmul(ps[:, 2 * g + n, :],
                                                            w[:, k, m * P:(m + 1) * P],
                                                            env.h_T[:, k, c * NH:(c + 1) * NH],
                                                            start=(k == 0), stop=(k == KT - 1))
                                last.then_inc(product, 1)

                    @block.scalar
                    def _(act):
                        for g in range(4):
                            act.wait_ge(product, 2 * g + 1)
                            if g >= 2:
                                act.wait_ge(gated, g - 1)
                            nc.scalar.activation(g_T[:, g % 2, :], ps[:, 2 * g, :], ACT.Silu
                                                 ).then_inc(silu_done, 1)

                    @block.vector
                    def _(dve):
                        for g in range(4):
                            m, c = g // 2, g % 2
                            dve.wait_ge(silu_done, g + 1)
                            dve.wait_ge(product, 2 * g + 2)
                            nc.vector.tensor_tensor(h_T[:, m, c * NH:(c + 1) * NH], g_T[:, g % 2, :],
                                                    ps[:, 2 * g + 1, :], ALU.mult
                                                    ).then_inc(gated, 1)
            project_add(nc, env, "f2_down", h_T, wd, None, env.x,
                        loads=weights_of((e + 1) % (E + 1)),
                        weigh=lambda t, e=e: comb[:, t, bass.ds(e, 1)])


def l3_xattn(nc, env, d):
    SCALE = float(D / H) ** 0.5
    mem, sb = scoped(nc, "x3")
    with mem:
        wq, wk, wv = (sb(n, [P, KT, D]) for n in ("wq", "wk", "wv"))
        bq, bk, bv = sb("bq", [P, KT]), sb("bk", [P, KT]), sb("bv", [P, D])
        q_T, q2_T, att_T = (sb(n, [P, KT, N]) for n in ("q_T", "q2_T", "att_T"))
        ctx_T, ctx_n = sb("ctx_T", [P, 2, KT, SK]), sb("ctx_n", [P, 2, CT, D])
        q_own, q0_own = sb("q_own", [P, KT, P]), sb("q0_own", [P, KT, P])
        sc, p_T = sb("sc", [P, SK]), sb("p_T", [P, CT, P])
        small, u_n = sb("small", [P, 4]), sb("u_n", [P, D])
        ps = env.ps
        layernorm(nc, env, "x3_ln", env.x, env.h, env.h_T, loads=[
            (wq[:, :, :], wview(d["L3_xattn_Wq"])), (wk[:, :, :], wview(d["L3_xattn_Wk"])),
            (wv[:, :, :], wview(d["L3_xattn_Wv"])), (bq[:, :], d["L3_xattn_bq"]),
            (bk[:, :], d["L3_xattn_bk"]), (bv[:, :], d["L3_xattn_bv"].partition_broadcast(P))])
        linear_T(nc, env, "x3_q", [(env.h_T, wq, q_T, bq, None)])
        linear_T(nc, env, "x3_q2", [(q_T, wk, q2_T, None, None)])
        with signals(nc, "x3_pre", "loaded") as (loaded,):
            with nc.Block() as block:

                @block.sync
                def _(sp):
                    for b in range(2):
                        sp.dma_start(ctx_T[:, b, :, :], d["ctx_T"][b].rearrange(
                            "(k p) n -> p k n", p=P)).then_inc(loaded, 16)
                    sp.wait_ge(loaded, 32)

        with nc.Fori(0, T) as i:
            with signals(nc, "x3_at", "next_T rows_in own q_in s_done shift_ready exped "
                         "turned act_out dve_out u_done u_ready u_turned u_out") as (
                    next_T, rows_in, own, q_in, s_done, shift_ready, exped, turned,
                    act_out, dve_out, u_done, u_ready, u_turned, u_out):
                with nc.Block() as block:

                    @block.sync
                    def _(sp):
                        for b in range(2):
                            sp.dma_start(ctx_n[:, b, 0:CT - 1, :],
                                         d["ctx"][2 * i + b, 0:(CT - 1) * P, :].rearrange(
                                             "(t p) f -> p t f", p=P)).then_inc(rows_in, 16)
                            sp.dma_start(ctx_n[0:LAST, b, CT - 1, :],
                                         d["ctx"][2 * i + b, (CT - 1) * P:SK, :]
                                         ).then_inc(rows_in, 16)
                        sp.wait_ge(s_done, 1)
                        for b in range(2):
                            sp.dma_start(ctx_T[:, b, :, :], d["ctx_T"][(2 * i + 2) % B + b]
                                         .rearrange("(k p) n -> p k n", p=P)).then_inc(next_T, 16)
                        sp.wait_ge(next_T, 32)

                    @block.tensor
                    def _(pe):
                        pe.wait_ge(q_in, 2)
                        for k in range(KT):
                            nc.tensor.matmul(ps[:, 4, 0:1], q0_own[:, k, :], bk[:, k:k + 1],
                                             start=(k == 0), stop=(k == KT - 1))
                        for b in range(2):
                            for c, (at, n) in enumerate(BANKFULS):
                                for k in range(KT):
                                    last = nc.tensor.matmul(
                                        ps[b * S:(b + 1) * S, c, 0:n],
                                        q_own[:, k, b * S:(b + 1) * S],
                                        ctx_T[:, b, k, at:at + n], start=(k == 0),
                                        stop=(k == KT - 1))
                        last.then_inc(s_done, 1)
                        pe.wait_ge(exped, 1)
                        for t in range(CT):
                            n = keys_of(t)
                            last = nc.tensor.transpose(ps[0:n, 4 + t // 4, (t % 4) * P:
                                                          (t % 4 + 1) * P],
                                                       sc[:, t * P:t * P + n], env.ident)
                            if t % 4 == 3 or t == CT - 1:
                                last.then_inc(turned, 1)
                        pe.wait_ge(act_out, 2)
                        pe.wait_ge(dve_out, 2)
                        pe.wait_ge(rows_in, 64)
                        for b in range(2):
                            for t in range(CT):
                                n = keys_of(t)
                                last = nc.tensor.matmul(
                                    ps[b * S:(b + 1) * S, 0, 0:D],
                                    p_T[0:n, t, b * S:(b + 1) * S], ctx_n[0:n, b, t, :],
                                    start=(t == 0), stop=(t == CT - 1))
                        last.then_inc(u_done, 1)
                        pe.wait_ge(u_ready, 1)
                        for k in range(KT):
                            last = nc.tensor.transpose(ps[:, 1, k * P:(k + 1) * P],
                                                       u_n[:, k * P:(k + 1) * P], env.ident)
                        last.then_inc(u_turned, 1)

                    @block.scalar
                    def _(act):
                        cols = bass.ds(i * P, P)
                        nc.scalar.copy(q_own[:, :, :], q2_T[:, :, cols]).then_inc(q_in, 1)
                        nc.scalar.copy(q0_own[:, :, :], q_T[:, :, cols]).then_inc(q_in, 1)
                        act.wait_ge(shift_ready, 1)
                        nc.scalar.activation(sc[:, :], ps[:, 0:4, :].rearrange(
                            "p c n -> p (c n)")[:, 0:SK], ACT.Exp, scale=SCALE,
                            bias=small[:, 2:3], accum_out=small[:, 3:4]).then_inc(exped, 1)
                        for g in (0, 2):
                            act.wait_ge(turned, g + 1)
                            nc.scalar.copy(p_T[:, 4 * g:4 * g + 4, :].rearrange(
                                "p t n -> p (t n)"), ps[:, 4 + g, :]).then_inc(act_out, 1)
                        act.wait_ge(u_turned, 1)
                        nc.scalar.copy(att_T[:, :, cols], ps[:, 1, 0:2 * P].rearrange(
                            "p (k n) -> p k n", k=KT)).then_inc(u_out, 1)

                    @block.vector
                    def _(dve):
                        steps = Steps(dve, own)
                        dve.wait_ge(s_done, 1)
                        steps.done(nc.vector.tensor_reduce(
                            small[:, 0:1], ps[:, 0:4, :].rearrange("p c n -> p (c n)")[:, 0:SK],
                            AX, ALU.max))
                        steps.done(nc.vector.tensor_copy(small[:, 1:2], ps[:, 4, 0:1]))
                        steps.wait()
                        steps.done(nc.vector.tensor_tensor(small[:, 0:1], small[:, 0:1],
                                                           small[:, 1:2], ALU.add))
                        steps.wait()
                        steps.done(nc.vector.tensor_tensor(small[:, 2:3], small[:, 1:2],
                                                           small[:, 0:1], ALU.subtract))
                        steps.wait()
                        nc.vector.tensor_scalar(small[:, 2:3], small[:, 2:3], SCALE, None,
                                                ALU.mult).then_inc(shift_ready, 1)
                        dve.wait_ge(exped, 1)
                        steps.done(nc.vector.reciprocal(small[:, 3:4], small[:, 3:4]))
                        dve.wait_ge(turned, 2)
                        nc.vector.tensor_copy(p_T[:, 4:8, :].rearrange("p t n -> p (t n)"),
                                              ps[:, 5, :]).then_inc(dve_out, 1)
                        dve.wait_ge(turned, 4)
                        nc.vector.tensor_copy(p_T[0:LAST, 12, :], ps[0:LAST, 7, 0:P]
                                              ).then_inc(dve_out, 1)
                        dve.wait_ge(u_done, 1)
                        steps.wait()
                        nc.vector.tensor_scalar(u_n[:, :], ps[:, 0, 0:D], small[:, 3:4], None,
                                                ALU.mult).then_inc(u_ready, 1)
        project_add(nc, env, "x3_v", att_T, wv, bv[:, :], env.x)


def l3_attn(nc, env, d):
    NB = 32
    mem, sb = scoped(nc, "a3")
    with mem:
        w, wo = sb("w", [P, KT, 3 * D]), sb("wo", [P, KT, D])
        b_col, b_row = sb("b_col", [P, 2 * KT]), sb("b_row", [P, 2, D])
        att_T, bias = sb("att_T", [P, KT, N]), sb("bias", [P, H, P])
        rel, onehot = sb("rel", [NB, H]), sb("onehot", [NB, S, P], BF16)
        onehot_f, causal = sb("onehot_f", [NB, 16, P]), sb("causal", [P, P])
        ps = env.ps
        layernorm(nc, env, "a3_ln", env.x, env.h, env.h_T, loads=[
            (w[:, :, :], wview(d["L3_attn_W_attn"])), (wo[:, :, :], wview(d["L3_attn_W_proj"])),
            (b_col[:, :], d["L3_attn_b_qk"]),
            (b_row[:, 0, :], d["L3_attn_b_attn"][2 * D:3 * D].partition_broadcast(P)),
            (b_row[:, 1, :], d["L3_attn_b_proj"].partition_broadcast(P)),
            (rel[:, :], d["L3_attn_rel_emb"]), (onehot[:, :, :], d["buckets"]),
            (causal[:, :], d["causal"])])
        with signals(nc, "a3_bias", "widened product placed own") as (
                widened, product, placed, own):
            with nc.Block() as block:

                @block.gpsimd
                def _(pool):
                    for g in range(4):
                        if g:
                            pool.wait_ge(product, g)
                        nc.gpsimd.tensor_copy(onehot_f[:, :, :],
                                              onehot[:, 16 * g:16 * g + 16, :]
                                              ).then_inc(widened, 1)

                @block.tensor
                def _(pe):
                    for g in range(4):
                        pe.wait_ge(widened, g + 1)
                        for k in range(16):
                            last = nc.tensor.matmul(ps[:, g // 2, (16 * (g % 2) + k) * H:
                                                       (16 * (g % 2) + k + 1) * H],
                                                    onehot_f[:, k, :], rel[:, :], start=True,
                                                    stop=True)
                        last.then_inc(product, 1)

                @block.vector
                def _(dve):
                    steps = Steps(dve, own)
                    dve.wait_ge(product, 4)
                    for half in range(2):
                        for b in range(2):
                            at = b * S + 32 * half
                            steps.done(nc.vector.tensor_copy(
                                bias[:, :, at:at + 32],
                                ps[:, half, :].rearrange("p (k h) -> p h k", h=H)))
                    steps.wait()
                    nc.vector.tensor_tensor(bias[:, :, :], bias[:, :, :],
                                            causal[:, :].unsqueeze(1).broadcast_to([P, H, P]),
                                            ALU.add).then_inc(placed, 1)
        self_attention(nc, env, "a3", w, b_col, b_row[:, 0, :], att_T, DH ** -0.5, bias, True, sb)
        project_add(nc, env, "a3_o", att_T, wo, b_row[:, 1, :], env.x)


def l3_ffn(nc, env, d):
    MAGIC = 1.5 * 2.0 ** 23
    mem, sb = scoped(nc, "q3")
    with mem:
        w8, w16 = sb("w8", [P, KT, D // 4], I32), sb("w16", [P, KT, D], BF16)
        wscale, bias = sb("wscale", [P, D]), sb("bias", [P, D])
        amax, scale = sb("amax", [P, T]), sb("scale", [P, T])
        xq, xq16 = sb("xq", [P, T, D]), sb("xq16", [P, T, D], BF16)
        x_T, ident16 = sb("x_T", [P, KT, N], BF16), sb("ident16", [P, P], BF16)
        out, sbc = sb("out", [P, T, D]), sb("sbc", [P, T, D])
        ps = env.ps
        layernorm(nc, env, "q3_ln", env.x, env.h, None, loads=[
            (w8[:, :, :], wview(d["L3_ffn_weight_q"])),
            (wscale[:, :], d["L3_ffn_weight_scale"].partition_broadcast(P)),
            (bias[:, :], d["L3_ffn_bias"].partition_broadcast(P))])
        with signals(nc, "q3", "own cast quantised turned x_out product out_ready") as (
                own, cast, quantised, turned, x_out, product, out_ready):
            with nc.Block() as block:

                @block.scalar
                def _(act):
                    nc.scalar.copy(w16[:, :, :], w8[:, :, :].bitcast(I8)).then_inc(cast, 1)
                    nc.scalar.copy(ident16[:, :], env.ident).then_inc(cast, 1)
                    for t in range(T):
                        act.wait_ge(turned, t + 1)
                        nc.scalar.copy(x_T[:, :, t * P:(t + 1) * P],
                                       ps[:, t % 2, :].bitcast(BF16)[:, 0:2 * P].rearrange(
                                           "p (k n) -> p k n", k=KT)).then_inc(x_out, 1)

                @block.tensor
                def _(pe):
                    pe.wait_ge(cast, 2)
                    for t in range(T):
                        pe.wait_ge(quantised, t + 1)
                        if t >= 2:
                            pe.wait_ge(x_out, t - 1)
                        for f in range(KT):
                            last = nc.tensor.transpose(
                                ps[:, t % 2, :].bitcast(BF16)[:, f * P:(f + 1) * P],
                                xq16[:, t, f * P:(f + 1) * P], ident16[:, :])
                        last.then_inc(turned, 1)
                    for t in range(T):
                        pe.wait_ge(x_out, t + 1)
                        if t >= 4:
                            pe.wait_ge(out_ready, t - 3)
                        for k in range(KT):
                            last = nc.tensor.matmul(ps[:, 4 + t % 4, 0:D],
                                                    x_T[:, k, t * P:(t + 1) * P], w16[:, k, :],
                                                    start=(k == 0), stop=(k == KT - 1))
                        last.then_inc(product, 1)

                @block.vector
                def _(dve):
                    steps = Steps(dve, own)
                    steps.done(nc.vector.tensor_reduce(amax[:, :], env.h[:, :, :], AX, ALU.max,
                                                       apply_absolute_value=True))
                    steps.wait()
                    steps.done(nc.vector.tensor_scalar(scale[:, :], amax[:, :], 1e-6, 1.0 / 127.0,
                                                       ALU.max, ALU.mult))
                    steps.wait()
                    steps.done(nc.vector.reciprocal(amax[:, :], scale[:, :]))
                    steps.wait()
                    for t in range(T):
                        steps.done(nc.vector.tensor_scalar(xq[:, t, :], env.h[:, t, :],
                                                           amax[:, t:t + 1], MAGIC, ALU.mult,
                                                           ALU.add))
                    steps.wait()
                    for t in range(T):
                        steps.done(nc.vector.tensor_scalar(xq[:, t, :], xq[:, t, :], MAGIC, None,
                                                           ALU.subtract))
                    steps.wait()
                    for t in range(T):
                        nc.vector.tensor_scalar(xq16[:, t, :], xq[:, t, :], 127.0, -128.0, ALU.min,
                                                ALU.max).then_inc(quantised, 1)
                    for t in range(T):
                        dve.wait_ge(product, t + 1)
                        nc.vector.scalar_tensor_tensor(
                            out=out[:, t, :], in0=ps[:, 4 + t % 4, 0:D], scalar=scale[:, t:t + 1],
                            in1=wscale[:, :], op0=ALU.mult, op1=ALU.mult).then_inc(out_ready, 1)
                    dve.wait_ge(out_ready, T)
                    steps.done(nc.vector.tensor_tensor(
                        out[:, :, :], out[:, :, :],
                        bias[:, :].unsqueeze(1).broadcast_to([P, T, D]), ALU.add))
                    steps.wait()
                    steps.done(nc.vector.tensor_tensor(env.x[:, :, :], env.x[:, :, :],
                                                       out[:, :, :], ALU.add))



SUBLAYERS = {"L0_xattn": l0_xattn, "L0_attn": l0_attn, "L0_ffn": l0_ffn,
             "L1_xattn": l1_xattn, "L1_attn": l1_attn,
             "L1_ffn": l1_ffn,
             "L2_xattn": l2_xattn, "L2_attn": l2_attn, "L2_ffn": l2_ffn,
             "L3_xattn": l3_xattn, "L3_attn": l3_attn, "L3_ffn": l3_ffn}

def constants():
    p = np.arange(P)[:, None]
    c = np.arange(P)[None, :]
    ident = (p == c)
    parts = {
        "ident": ident,
        "fold": ident[:, 0:S] | ident[:, S:P],
        "ones": np.ones((P, P)),
        "same_head": (p // DH == c // DH),
        "own_head": (p // S == c[:, 0:2 * DH] // DH),
        "head_of": (p // DH == c[:, 0:HPT]),
        "tril_min": np.where(c[:, 0:S] <= p % S, -3e38, 0.0),
        "excluded": np.where(p <= c[:, 0:S], -3e38, 0.0),
        "every32": np.repeat(p % 32 == 0, 32, 1),
        "parity": (p // DH % 2 == c[:, 0:2]),
        "zero": np.zeros((P, 1)),
        "iota8": np.tile(np.arange(8), (P, 1)),
        "valid_last": np.repeat(p < LAST, P, 1),
        "cross": np.where(p // S == c // S, 0.0, -1e30),
        "which_head": (p // S == c[:, 0:2]),
        "tenth": np.full((P, 1), 0.1),
        "eps5": np.full((P, 1), 1e-5),
        "eps6": np.full((P, 1), 1e-6),
    }
    at, where, arrays = 0, {}, []
    for name, a in parts.items():
        arrays.append(np.asarray(a, np.float32))
        where[name] = (at, at + a.shape[1])
        at += a.shape[1]
    return np.ascontiguousarray(np.concatenate(arrays, 1)), where


def build(nc, d, out, where, names):
    with ExitStack() as mem:
        def sb(name, shape, dt=F32):
            return mem.enter_context(nc.sbuf_tensor(name, shape, dt))

        env = Env()
        env.x = sb("x", [P, T, D])
        env.h = sb("h", [P, T, D])
        env.h_T = sb("h_T", [P, KT, N])
        env.rows = sb("rows", [P, T, D])
        env.bn, env.mv = sb("bn", [P, T, 6]), sb("mv", [P, T, 2])
        env.std, env.rstd = sb("std", [P, T]), sb("rstd", [P, T])
        consts = sb("consts", [P, d["consts"].shape[1]])
        env.ident = consts[:, where["ident"][0]:where["ident"][1]]
        env.fold = consts[:, where["fold"][0]:where["fold"][1]]
        env.ones = consts[:, where["ones"][0]:where["ones"][1]]
        env.same_head = consts[:, where["same_head"][0]:where["same_head"][1]]
        env.own_head = consts[:, where["own_head"][0]:where["own_head"][1]]
        env.head_of = consts[:, where["head_of"][0]:where["head_of"][1]]
        env.tril_min = consts[:, where["tril_min"][0]:where["tril_min"][1]]
        env.excluded = consts[:, where["excluded"][0]:where["excluded"][1]]
        env.every32 = consts[:, where["every32"][0]:where["every32"][1]]
        env.parity = consts[:, where["parity"][0]:where["parity"][1]]
        env.iota8 = consts[:, where["iota8"][0]:where["iota8"][1]]
        env.valid_last = consts[:, where["valid_last"][0]:where["valid_last"][1]]
        env.cross = consts[:, where["cross"][0]:where["cross"][1]]
        env.which_head = consts[:, where["which_head"][0]:where["which_head"][1]]
        env.tenth = consts[:, where["tenth"][0]:where["tenth"][1]]
        env.zero = consts[:, where["zero"][0]:where["zero"][1]]
        env.eps5 = consts[:, where["eps5"][0]:where["eps5"][1]]
        env.eps6 = consts[:, where["eps6"][0]:where["eps6"][1]]
        env.ps = mem.enter_context(nc.psum_tensor("ps", [P, 8, NH], F32))

        with signals(nc, "start", "x_in consts_in") as (x_in, consts_in):
            with nc.Block() as block:

                @block.sync
                def _(sp):
                    sp.dma_start(env.x[:, :, :], d["x"].rearrange("(t b) s n -> (b s) t n", b=2)
                                 ).then_inc(x_in, 16)
                    sp.dma_start(consts[:, :], d["consts"]).then_inc(consts_in, 16)
                    sp.wait_ge(x_in, 16)
                    sp.wait_ge(consts_in, 16)

        for name in names:
            SUBLAYERS[name](nc, env, d)

        with signals(nc, "end", "stored") as (stored,):
            with nc.Block() as block:

                @block.sync
                def _(sp):
                    sp.dma_start(out.rearrange("(t b) s n -> (b s) t n", b=2), env.x[:, :, :]
                                 ).then_inc(stored, 16)
                    sp.wait_ge(stored, 16)


def arrange(inputs):
    a = {}
    for name, v in inputs.items():
        a[name] = np.ascontiguousarray(v)
    a["ctx"] = a.pop("ctx_1024")
    a["ctx_T"] = np.ascontiguousarray(np.transpose(a["ctx"], (0, 2, 1)))
    a["mask_T"] = np.ascontiguousarray(np.transpose(a.pop("mask_BxSxS2_bk0"), (0, 2, 1))
                                       ).view(np.int32)
    def columns(name):
        v = a[name]
        a[name] = np.ascontiguousarray(np.swapaxes(v.reshape(*v.shape[:-1], -1, P), -1, -2))

    for name in ("bq", "b1", "ln1_s", "ln1_b", "ln2_s", "ln2_b"):
        columns("L0_attn_" + name)
    a["L0_ffn_gate_w"] = np.ascontiguousarray(a["L0_ffn_gate_w"].T)
    columns("L0_ffn_b1")
    a["L0_ffn_b1"] = np.ascontiguousarray(np.swapaxes(a["L0_ffn_b1"], 0, 1))
    for name in ("L1_xattn_Wq", "L1_xattn_Wv", "L1_xattn_gru_wih", "L1_xattn_gru_whh",
                 "L1_attn_w_qkv", "L1_attn_w_o", "L2_xattn_Wq", "L2_xattn_Wkv", "L2_xattn_Wo",
                 "L2_ffn_gate_w", "L3_xattn_Wq", "L3_xattn_Wv", "L3_attn_W_attn",
                 "L3_attn_W_proj", "L3_ffn_weight_q"):
        a[name] = np.ascontiguousarray(a[name].T)
    for name in ("slot_norm_w", "input_norm_w", "gru_bih", "gru_bhh"):
        columns("L1_xattn_" + name)
    a["L1_attn_b_qk"] = a["L1_attn_b_qkv"][0:2 * D]
    columns("L1_attn_b_qk")
    a["L1_ffn_expert_w1"] = np.ascontiguousarray(
        np.transpose(a["L1_ffn_expert_w1"], (1, 0, 2))).reshape(2 * D, -1)
    a["L1_ffn_expert_w2"] = a["L1_ffn_expert_w2"].reshape(-1, 3 * D)
    a["L1_ffn_expert_b1"] = a["L1_ffn_expert_b1"].reshape(-1)
    a["L1_ffn_shared_weight"] = a["L1_ffn_shared_weight"].reshape(1)
    columns("L1_ffn_expert_b1")
    columns("L1_ffn_refine_b1")
    proj = np.transpose(a["L2_attn_projection"], (0, 2, 1)).reshape(KT, P, 1, 64)
    a["proj_rows"] = np.ascontiguousarray(np.transpose(
        np.broadcast_to(proj, (KT, P, HPT, 64)), (1, 0, 2, 3)))
    for new, one, shared in (("L2_w_gate", "L2_ffn_w_gate", "L2_ffn_shared_gate_w"),
                             ("L2_w_up", "L2_ffn_w_up", "L2_ffn_shared_up_w"),
                             ("L2_w_down", "L2_ffn_w_down", "L2_ffn_shared_down_w")):
        both = np.concatenate([a.pop(one), a.pop(shared)[None]], 0)
        a[new] = np.ascontiguousarray(np.transpose(both, (0, 2, 1)))
    a["L3_ffn_weight_q"] = a["L3_ffn_weight_q"].view(np.int32)
    columns("L3_xattn_bq")
    columns("L3_xattn_bk")
    a["L3_attn_b_qk"] = a["L3_attn_b_attn"][0:2 * D]
    columns("L3_attn_b_qk")
    rp = -np.minimum(np.arange(S)[None, :] - np.arange(S)[:, None], 0)
    large = 16 + (np.log(rp.astype(np.float32) / np.float32(16) + np.float32(1e-10))
                  / np.float32(np.log(8.0)) * np.float32(16)).astype(np.int32)
    bucket = np.where(rp < 16, rp, np.minimum(large, 31))
    hot = (np.arange(32)[:, None, None] == bucket.T[None, :, :])
    a["buckets"] = np.tile(hot, (1, 1, 2)).astype(mybir.dt.np(BF16))
    at = np.arange(P)
    seen = (at[:, None] // S == at[None, :] // S) & (at[None, :] % S <= at[:, None] % S)
    a["causal"] = np.where(seen, 0.0, -1e30).astype(np.float32)
    a["expert_sel"] = np.ascontiguousarray(
        np.arange(8)[:, None, None] == 2 * np.arange(4)[None, :, None]
        + np.arange(P)[None, None, :] // 64).astype(np.float32)
    half = D // 2
    freq = np.exp(np.arange(half, dtype=np.float32) * np.float32(-np.log(10000.0) / (half - 1)))
    pos = (np.arange(S, dtype=np.float32) + 1.0)[:, None] * freq[None, :]
    a["pos"] = np.tile(np.concatenate([np.sin(pos), np.cos(pos)], -1).astype(np.float32), (2, 1))
    return a


def kernel(**inputs):
    import concourse.bacc as bacc
    from concourse.bass_utils import run_bass_kernel_spmd

    arrays = arrange(inputs)
    arrays["consts"], where = constants()
    nc = bacc.Bacc("TRN2", target_bir_lowering=False, num_devices=1)
    d = {n: nc.dram_tensor(f"in_{n}", a.shape, mybir.dt.from_np(a.dtype),
                           kind="ExternalInput").ap() for n, a in arrays.items()}
    out = nc.dram_tensor("out", (B, S, D), F32, kind="ExternalOutput").ap()
    build(nc, d, out, where, list(SUBLAYERS))
    r = run_bass_kernel_spmd(nc, [{f"in_{n}": a for n, a in arrays.items()}], core_ids=[0])
    return r.results[0]["out"]
```

```python
from contextlib import ExitStack, contextmanager

import numpy as np

import concourse.bass as bass
from concourse import mybir

F32 = mybir.dt.float32
BF16 = mybir.dt.bfloat16
U8 = mybir.dt.uint8
I8 = mybir.dt.int8
I32 = mybir.dt.int32
U32 = mybir.dt.uint32
ACT = mybir.ActivationFunctionType
ALU = mybir.AluOpType
AX = mybir.AxisListType.X

P = 128
B = 16
S = 64
D = 256
KT = D // P
T = B * S // P
N = B * S
NH = 512
H = 16
DH = D // H
HPT = P // DH
PAIRS = H // 2
SK = 1601
CT = -(-SK // P)
LAST = SK - (CT - 1) * P
BANKFULS = [(c, min(NH, SK - c)) for c in range(0, SK, NH)]
CHUNK = -(-SK // len(BANKFULS))
CHUNKS = [(c, min(CHUNK, SK - c)) for c in range(0, SK, CHUNK)]


@contextmanager
def signals(nc, stage, names):
    held = [nc.alloc_semaphore(f"{stage}_{n}") for n in names.split()]
    yield held
    nc.clear_and_free_semaphores(held)
    nc.all_engine_barrier()


class Steps:

    def __init__(self, eng, sem):
        self.eng, self.sem, self.n = eng, sem, 0

    def done(self, ins):
        self.n += 1
        ins.then_inc(self.sem, 1)

    def wait(self):
        self.eng.wait_ge(self.sem, self.n)


class Env:
    pass


def keys_of(k):
    return P if k < CT - 1 else LAST


def load_all(sp, loads, sem):
    for dst, src in loads:
        sp.dma_start(dst, src).then_inc(sem, 16)
    if loads:
        sp.wait_ge(sem, 16 * len(loads))


def wview(ap):
    return ap.rearrange("(k p) n -> p k n", p=P)


def layernorm(nc, env, stage, src, nat, dst_T, affine=None, early=(), loads=()):
    with signals(nc, stage, "loaded early own stats std rows turned act_out dve_out") as (
            loaded, affine_in, own, stats, std_ready, rows_ready, turned, act_out, dve_out):
        with nc.Block() as block:

            @block.sync
            def _(sp):
                load_all(sp, early, affine_in)
                load_all(sp, loads, loaded)

            @block.vector
            def _(dve):
                steps = Steps(dve, own)
                for t in range(T):
                    steps.done(nc.vector.bn_stats(env.bn[:, t, :], src[:, t, :]))
                steps.wait()
                for t in range(T):
                    nc.vector.bn_aggr(env.mv[:, t, :], env.bn[:, t, :]).then_inc(stats, 1)
                dve.wait_ge(std_ready, 1)
                steps.done(nc.vector.reciprocal(env.rstd[:, :], env.std[:, :]))
                steps.wait()
                for t in range(T):
                    nc.vector.tensor_scalar(nat[:, t, :], src[:, t, :], env.mv[:, t, 0:1],
                                            env.rstd[:, t:t + 1], ALU.subtract,
                                            ALU.mult).then_inc(rows_ready, 1)
                if early:
                    dve.wait_ge(affine_in, 16 * len(early))
                for half in range(2 if dst_T is not None else 0):
                    dve.wait_ge(turned, 2 * half + 2)
                    out, put = dst_T[:, 1, half * NH:(half + 1) * NH], env.ps[:, 2 * half + 1, :]
                    if affine is None:
                        nc.vector.tensor_copy(out, put).then_inc(dve_out, 1)
                    else:
                        nc.vector.tensor_scalar(out, put, affine[0][:, 1:2], affine[1][:, 1:2],
                                                ALU.mult, ALU.add).then_inc(dve_out, 1)

            @block.scalar
            def _(act):
                act.wait_ge(stats, T)
                nc.scalar.activation(env.std[:, :], env.mv[:, :, 1], ACT.Sqrt,
                                     bias=env.eps5[:, 0:1]).then_inc(std_ready, 1)
                if early:
                    act.wait_ge(affine_in, 16 * len(early))
                for half in range(2 if dst_T is not None else 0):
                    act.wait_ge(turned, 2 * half + 1)
                    out, put = dst_T[:, 0, half * NH:(half + 1) * NH], env.ps[:, 2 * half, :]
                    if affine is None:
                        nc.scalar.copy(out, put).then_inc(act_out, 1)
                    else:
                        nc.scalar.activation(out, put, ACT.Identity, scale=affine[0][:, 0:1],
                                             bias=affine[1][:, 0:1]).then_inc(act_out, 1)

            @block.tensor
            def _(pe):
                for half in range(2 if dst_T is not None else 0):
                    pe.wait_ge(rows_ready, 4 * half + 4)
                    for f in range(KT):
                        for t in range(4):
                            last = nc.tensor.transpose(
                                env.ps[:, 2 * half + f, t * P:(t + 1) * P],
                                nat[:, 4 * half + t, f * P:(f + 1) * P], env.ident)
                        last.then_inc(turned, 1)


def turn_rows(nc, env, stage, nat, dst_T, loads=()):
    with signals(nc, stage, "loaded turned act_out dve_out") as (loaded, turned, act_out, dve_out):
        with nc.Block() as block:

            @block.sync
            def _(sp):
                load_all(sp, loads, loaded)

            @block.tensor
            def _(pe):
                for half in range(2):
                    for f in range(KT):
                        for t in range(4):
                            last = nc.tensor.transpose(
                                env.ps[:, 2 * half + f, t * P:(t + 1) * P],
                                nat[:, 4 * half + t, f * P:(f + 1) * P], env.ident)
                        last.then_inc(turned, 1)

            @block.vector
            def _(dve):
                for half in range(2):
                    dve.wait_ge(turned, 2 * half + 2)
                    nc.vector.tensor_copy(dst_T[:, 1, half * NH:(half + 1) * NH],
                                          env.ps[:, 2 * half + 1, :]).then_inc(dve_out, 1)

            @block.scalar
            def _(act):
                for half in range(2):
                    act.wait_ge(turned, 2 * half + 1)
                    nc.scalar.copy(dst_T[:, 0, half * NH:(half + 1) * NH],
                                   env.ps[:, 2 * half, :]).then_inc(act_out, 1)


def add_turned(nc, env, stage, src_T, dst):
    with signals(nc, stage, "turned added") as (turned, added):
        with nc.Block() as block:

            @block.tensor
            def _(pe):
                for t in range(T):
                    for f in range(KT):
                        last = nc.tensor.transpose(env.ps[:, t, f * P:(f + 1) * P],
                                                   src_T[:, f, t * P:(t + 1) * P], env.ident)
                    last.then_inc(turned, 1)

            @block.vector
            def _(dve):
                for t in range(T):
                    dve.wait_ge(turned, t + 1)
                    nc.vector.tensor_tensor(dst[:, t, :], dst[:, t, :], env.ps[:, t, 0:D],
                                            ALU.add).then_inc(added, 1)


def linear_T(nc, env, stage, parts, loads=()):
    groups = []
    for in_T, w, out_T, bias, func in parts:
        n_out = w.shape[2]
        for m in range(-(-n_out // P)):
            rows = min(P, n_out - m * P)
            for c in range(2):
                groups.append((in_T, w, out_T, bias, func, m, rows, c))
    on_act = [func not in (None, "relu") or g % 2 == 0
              for g, (_, _, _, _, func, _, _, _) in enumerate(groups)]
    act_before = [sum(on_act[:g]) for g in range(len(groups) + 1)]
    dve_before = [g - a for g, a in enumerate(act_before)]
    with signals(nc, stage, "loaded product act_out dve_out") as (
            loaded, product, act_out, dve_out):
        with nc.Block() as block:

            @block.sync
            def _(sp):
                load_all(sp, loads, loaded)

            @block.tensor
            def _(pe):
                for g, (in_T, w, out_T, bias, func, m, rows, c) in enumerate(groups):
                    if g >= 8:
                        if on_act[g - 8]:
                            pe.wait_ge(act_out, act_before[g - 7])
                        else:
                            pe.wait_ge(dve_out, dve_before[g - 7])
                    kts = w.shape[1]
                    for k in range(kts):
                        last = nc.tensor.matmul(env.ps[0:rows, g % 8, :],
                                                w[:, k, m * P:m * P + rows],
                                                in_T[:, k, c * NH:(c + 1) * NH],
                                                start=(k == 0), stop=(k == kts - 1))
                    last.then_inc(product, 1)

            @block.scalar
            def _(act):
                for g, (in_T, w, out_T, bias, func, m, rows, c) in enumerate(groups):
                    if not on_act[g]:
                        continue
                    act.wait_ge(product, g + 1)
                    kind = {None: ACT.Identity, "relu": ACT.Relu, "gelu": ACT.Gelu}[func]
                    nc.scalar.activation(
                        out_T[0:rows, m, c * NH:(c + 1) * NH], env.ps[0:rows, g % 8, :], kind,
                        bias=bias[0:rows, m:m + 1] if bias is not None else env.zero[0:rows, 0:1],
                    ).then_inc(act_out, 1)

            @block.vector
            def _(dve):
                for g, (in_T, w, out_T, bias, func, m, rows, c) in enumerate(groups):
                    if on_act[g]:
                        continue
                    dve.wait_ge(product, g + 1)
                    out, put = out_T[0:rows, m, c * NH:(c + 1) * NH], env.ps[0:rows, g % 8, :]
                    if func == "relu":
                        ins = nc.vector.tensor_scalar(
                            out, put, bias[0:rows, m:m + 1] if bias is not None else 0.0, 0.0,
                            ALU.add, ALU.max)
                    elif bias is not None:
                        ins = nc.vector.tensor_scalar(out, put, bias[0:rows, m:m + 1], None, ALU.add)
                    else:
                        ins = nc.vector.tensor_copy(out, put)
                    ins.then_inc(dve_out, 1)


def linear_rows(nc, env, stage, in_T, parts, loads=()):
    groups = [(t, w, bias, dst) for w, bias, dst in parts for t in range(T)]
    with signals(nc, stage, "loaded product taken") as (loaded, product, taken):
        with nc.Block() as block:

            @block.sync
            def _(sp):
                load_all(sp, loads, loaded)

            @block.tensor
            def _(pe):
                for g, (t, w, bias, dst) in enumerate(groups):
                    if g >= 8:
                        pe.wait_ge(taken, g - 7)
                    kts = w.shape[1]
                    for k in range(kts):
                        last = nc.tensor.matmul(env.ps[:, g % 8, 0:D], in_T[:, k, t * P:(t + 1) * P],
                                                w[:, k, :], start=(k == 0), stop=(k == kts - 1))
                    last.then_inc(product, 1)

            @block.vector
            def _(dve):
                for g, (t, w, bias, dst) in enumerate(groups):
                    out, put = dst(t), env.ps[:, g % 8, 0:D]
                    if len(out.shape) == 3:
                        put, bias = (x.rearrange("p (a b) -> p a b", a=out.shape[1])
                                     for x in (put, bias))
                    dve.wait_ge(product, g + 1)
                    nc.vector.tensor_tensor(out, put, bias, ALU.add).then_inc(taken, 1)


def project_add(nc, env, stage, act_T, w, bias, dst, loads=(), also=None, scale=None):
    kts = w.shape[1]
    with signals(nc, stage, "loaded own product added") as (
            loaded, own, product, added):
        with nc.Block() as block:

            @block.sync
            def _(sp):
                load_all(sp, loads, loaded)

            @block.tensor
            def _(pe):
                for t in range(T):
                    for k in range(kts):
                        last = nc.tensor.matmul(env.ps[:, t, 0:D], act_T[:, k, t * P:(t + 1) * P],
                                                w[:, k, :], start=(k == 0), stop=(k == kts - 1))
                    last.then_inc(product, 1)

            @block.vector
            def _(dve):
                steps = Steps(dve, own)
                if scale is not None and bias is not None:
                    steps.done(nc.vector.tensor_tensor(bias, bias, scale, ALU.mult))
                    steps.wait()
                for t in range(T):
                    if also is not None:
                        steps.done(nc.vector.tensor_tensor(dst[:, t, :], dst[:, t, :],
                                                           also[:, t, :], ALU.add))
                        steps.wait()
                    if bias is not None:
                        steps.done(nc.vector.tensor_tensor(dst[:, t, :], dst[:, t, :], bias,
                                                           ALU.add))
                        steps.wait()
                    put = env.ps[:, t, 0:D]
                    dve.wait_ge(product, t + 1)
                    if scale is not None:
                        steps.done(nc.vector.tensor_tensor(env.rows[:, t, :], put, scale, ALU.mult))
                        steps.wait()
                        put = env.rows[:, t, :]
                    nc.vector.tensor_tensor(dst[:, t, :], dst[:, t, :], put,
                                            ALU.add).then_inc(added, 1)


def expert(nc, env, stage, w_in, bias, hid_T, w_out, weigh, now, after):
    n_in, half = len(w_in), T // 2
    groups = [(c, m) for c in range(2) for m in range(KT)]
    with signals(nc, stage, "now after product silu hidden down added") as (
            now_in, after_in, product, silu, hidden, down, added):
        with nc.Block() as block:

            @block.sync
            def _(sp):
                for dst, src in now:
                    sp.dma_start(dst, src).then_inc(now_in, 16)
                sp.wait_ge(product, n_in * len(groups))
                for dst, src in after:
                    sp.dma_start(dst, src).then_inc(after_in, 16)
                sp.wait_ge(now_in, 16 * len(now))
                sp.wait_ge(after_in, 16 * len(after))

            def down_bank(t):
                return t if n_in == 2 else (t + 4) % 8

            @block.tensor
            def _(pe):
                for g, (c, m) in enumerate(groups):
                    for n, w in enumerate(w_in):
                        for k in range(KT):
                            last = nc.tensor.matmul(env.ps[:, n_in * g + n, :],
                                                    w[:, k, m * P:(m + 1) * P],
                                                    env.h_T[:, k, c * NH:(c + 1) * NH],
                                                    start=(k == 0), stop=(k == KT - 1))
                        last.then_inc(product, 1)
                pe.wait_ge(now_in, 16 * len(now))
                for t in range(T):
                    pe.wait_ge(hidden, KT * (t // half + 1))
                    for k in range(KT):
                        last = nc.tensor.matmul(env.ps[:, down_bank(t), 0:D],
                                                hid_T[:, k, t * P:(t + 1) * P], w_out[:, k, :],
                                                start=(k == 0), stop=(k == KT - 1))
                    last.then_inc(down, 1)

            @block.scalar
            def _(act):
                for g, (c, m) in enumerate(groups):
                    out = hid_T[:, m, c * NH:(c + 1) * NH]
                    act.wait_ge(product, n_in * g + 1)
                    if n_in == 2:
                        nc.scalar.activation(out, env.ps[:, 2 * g, :], ACT.Silu).then_inc(silu, 1)
                    else:
                        nc.scalar.activation(out, env.ps[:, g, :], ACT.Relu, bias=bias[:, m:m + 1]
                                             ).then_inc(hidden, 1)

            @block.vector
            def _(dve):
                for g, (c, m) in enumerate(groups if n_in == 2 else ()):
                    out = hid_T[:, m, c * NH:(c + 1) * NH]
                    dve.wait_ge(silu, g + 1)
                    dve.wait_ge(product, 2 * g + 2)
                    nc.vector.tensor_tensor(out, out, env.ps[:, 2 * g + 1, :], ALU.mult
                                            ).then_inc(hidden, 1)
                for t in range(T):
                    dve.wait_ge(down, t + 1)
                    nc.vector.scalar_tensor_tensor(
                        out=env.x[:, t, :], in0=env.ps[:, down_bank(t), 0:D], scalar=weigh(t),
                        in1=env.x[:, t, :], op0=ALU.mult, op1=ALU.add).then_inc(added, 1)


def context_heads(nc, env, stage, ctx, ctx_T, q_T, att_T, w_k, w_v, softmax, notmask=None,
                  nb=None):
    with ExitStack() as mem:
        def sb(name, shape, dt=F32):
            return mem.enter_context(nc.sbuf_tensor(f"{stage}_{name}", shape, dt))

        k_T = sb("k_T", [P, KT, SK])
        v = sb("v", [P, CT, D])
        q_bd = sb("q_bd", [P, KT, HPT, S])
        sc = sb("sc", [P, CT, H, S])
        den_parts = sb("den_parts", [P, 2, H, S])
        POOL_TILES = range(0, 5 if softmax else 0)
        DVE_TILES = range(len(POOL_TILES), CT)
        POOL_SHIFTS = (3, 7, 11)
        sum_kinds = [r for r, tiles in enumerate((POOL_TILES, DVE_TILES)) if tiles]
        num, den = sb("num", [P, KT, S]), sb("den", [P, KT, S])
        if softmax:
            zeros = sb("zeros", [S, H, S])
            most = sb("most", [P, H, S])
            top = sb("top", [P, PAIRS])
            diag = sb("diag", [P, PAIRS, P])
            top_bc = sb("top_bc", [P, H, S])
        else:
            mask_in4 = sb("mask_in4", [P, CT, S // 4], I32)
            mask_u8 = mask_in4[:, :, :].bitcast(U8)
            cap = sb("cap", [P, CT, S])
        ps = env.ps
        two_banks = [ps[:, 2 * r:2 * r + 2, :].rearrange("p c n -> p (c n)") for r in range(4)]

        def heads(x):
            return x.rearrange("p (h s) -> p h s", h=H)

        def key_group(g, bank):
            m, (at, n) = g // len(CHUNKS), CHUNKS[g % len(CHUNKS)]
            for k in range(KT):
                last = nc.tensor.matmul(ps[:, bank, 0:n], w_k[:, k, m * P:(m + 1) * P],
                                        ctx_T[:, k, at:at + n], start=(k == 0), stop=(k == KT - 1))
            return last

        def take_keys(copy, g, bank):
            m, (at, n) = g // len(CHUNKS), CHUNKS[g % len(CHUNKS)]
            return copy(k_T[:, m, at:at + n], ps[:, bank, 0:n])

        def value_tile(t):
            n = keys_of(t)
            for k in range(KT):
                last = nc.tensor.matmul(ps[0:n, t % 4, 0:D], ctx_T[:, k, t * P:t * P + n],
                                        w_v[:, k, :], start=(k == 0), stop=(k == KT - 1))
            return last

        def take_values(copy, t):
            return copy(v[0:keys_of(t), t, :], ps[0:keys_of(t), t % 4, 0:D])

        def spread_queries(half, row):
            return nc.gpsimd.tensor_tensor(
                q_bd[:, half, :, :],
                q_T[:, half, bass.ds(row * S, S)].unsqueeze(1).broadcast_to([P, HPT, S]),
                env.head_of.unsqueeze(2).broadcast_to([P, HPT, S]), ALU.mult)

        def load_mask(sp, row, sem):
            sp.dma_start(mask_in4[:, 0:CT - 1, :], notmask[row, 0:(CT - 1) * P, :].rearrange(
                "(t p) s -> p t s", p=P)).then_inc(sem, 16)
            sp.dma_start(mask_in4[0:LAST, CT - 1, :], notmask[row, (CT - 1) * P:SK, :]
                         ).then_inc(sem, 16)

        def set_cap(pool, sem):
            parts = ((P, slice(0, CT - 1)), (LAST, slice(CT - 1, CT)))
            for rows, ts in parts:
                nc.gpsimd.tensor_scalar(cap[0:rows, ts, :], mask_u8[0:rows, ts, :], -3e38, 3e38,
                                        ALU.mult, ALU.add).then_inc(sem, 1)
            pool.wait_ge(sem, 2)
            for rows, ts in parts:
                nc.gpsimd.tensor_scalar(cap[0:rows, ts, :], cap[0:rows, ts, :], nb[0:rows, 1:2],
                                        None, ALU.add).then_inc(sem, 1)

        KG = KT * len(CHUNKS)
        with signals(nc, stage + "_pre", "mask_in cap_ready q_ready k_product k_out v_product "
                     "v_act v_dve") as (
                mask_in, cap_ready, q_ready, k_product, k_out, v_product, v_act, v_dve):
            with nc.Block() as block:

                @block.sync
                def _(sp):
                    if not softmax:
                        load_mask(sp, 0, mask_in)

                @block.gpsimd
                def _(pool):
                    for half in range(KT):
                        spread_queries(half, 0).then_inc(q_ready, 1)
                    if not softmax:
                        pool.wait_ge(mask_in, 32)
                        set_cap(pool, cap_ready)

                @block.tensor
                def _(pe):
                    for g in range(KG):
                        if g >= 4:
                            pe.wait_ge(k_out, g - 3)
                        key_group(g, g % 4).then_inc(k_product, 1)
                    for t in range(CT):
                        if t < 4:
                            pe.wait_ge(k_out, KG - 3 + t)
                        else:
                            pe.wait_ge((v_act, v_dve)[t % 2], t // 2 - 1)
                        value_tile(t).then_inc(v_product, 1)

                @block.scalar
                def _(act):
                    for g in range(KG):
                        act.wait_ge(k_product, g + 1)
                        take_keys(nc.scalar.copy, g, g % 4).then_inc(k_out, 1)
                    for t in range(0, CT, 2):
                        act.wait_ge(v_product, t + 1)
                        take_values(nc.scalar.copy, t).then_inc(v_act, 1)

                @block.vector
                def _(dve):
                    for t in range(1, CT, 2):
                        dve.wait_ge(v_product, t + 1)
                        take_values(nc.vector.tensor_copy, t).then_inc(v_dve, 1)

        with nc.Fori(0, B) as b:
            with signals(nc, stage, "cap_ready next_ctx mask_in own s_product s_out p_dve "
                         "p_pool p_ready maxima "
                         "turned diag_ready bc_product bc_ready k_product k_act k_dve "
                         "q_ready pool_sums dve_sums den_product v_product v_act v_dve") as (
                    cap_ready, next_ctx, mask_in, own, s_product, s_out, p_dve, p_pool,
                    p_ready, maxima,
                    turned, diag_ready, bc_product, bc_ready, k_product, k_act, k_dve,
                    q_ready, pool_sums, dve_sums, den_product, v_product, v_act, v_dve):

                act_values = range(0, CT, 1 if softmax else 2)

                def values_taken(pe, t):
                    if softmax:
                        pe.wait_ge(v_act, t + 1)
                    else:
                        pe.wait_ge((v_act, v_dve)[t % 2], t // 2 + 1)

                def keys_taken(pe, g):
                    if softmax:
                        pe.wait_ge(k_act, g + 1)
                    else:
                        pe.wait_ge((k_act, k_dve)[g % 2], g // 2 + 1)

                with nc.Block() as block:

                    @block.sync
                    def _(sp):
                        if not softmax:
                            load_mask(sp, (b + 1) % B, mask_in)
                        sp.dma_start(ctx_T[:, :, :], ctx[(b + 1) % B].rearrange(
                            "(k p) n -> p k n", p=P)).then_inc(next_ctx, 16)
                        sp.wait_ge(next_ctx, 16)

                    def shift(eng, t):
                        n = keys_of(t)
                        return eng.tensor_tensor(sc[0:n, t, :, :], sc[0:n, t, :, :],
                                                 top_bc[0:n, :, :], ALU.subtract)

                    def add_weights(eng, r, tiles, sums, t):
                        eng.wait_ge(p_ready, t + 1)
                        if t == tiles[0]:
                            return
                        if t > tiles[1]:
                            eng.wait_ge(sums, t - tiles[1])
                        n = keys_of(t)
                        first = sc[:, tiles[0]] if t == tiles[1] else den_parts[:, r]
                        eng.tensor_tensor(den_parts[0:n, r, :, :], first[0:n], sc[0:n, t, :, :],
                                          ALU.add).then_inc(sums, 1)

                    @block.gpsimd
                    def _(pool):
                        pool.wait_ge(s_product, CT)
                        for half in range(KT):
                            spread_queries(half, (b + 1) % B).then_inc(q_ready, 1)
                        if not softmax:
                            pool.wait_ge(mask_in, 32)
                            pool.wait_ge(s_out, CT)
                            set_cap(pool, cap_ready)
                        if softmax:
                            pool.wait_ge(bc_ready, 2)
                            for t in POOL_SHIFTS:
                                shift(nc.gpsimd, t).then_inc(p_pool, 1)
                        for t in POOL_TILES:
                            add_weights(nc.gpsimd, 0, POOL_TILES, pool_sums, t)

                    @block.tensor
                    def _(pe):
                        def scores(t):
                            if t >= 2:
                                pe.wait_ge(s_out, t - 1)
                            n = keys_of(t)
                            for half in range(2):
                                last = nc.tensor.matmul(ps[0:n, 2 * (t % 2) + half, :],
                                                        k_T[:, half, t * P:t * P + n],
                                                        q_bd[:, half, :, :], start=True, stop=True)
                            last.then_inc(s_product, 1)

                        def values(t):
                            pe.wait_ge(p_ready, t + 1)
                            n = keys_of(t)
                            for j in range(PAIRS):
                                nc.tensor.matmul(
                                    ps[32 * (j % 4):32 * (j % 4) + 32, 4 + j // 4, 0:P],
                                    v[0:n, t, 2 * DH * j:2 * DH * (j + 1)],
                                    sc[0:n, t, 2 * j:2 * j + 2, :], start=(t == 0),
                                    stop=(t == CT - 1), skip_group_check=True)

                        def next_keys(g):
                            if g < 4:
                                pe.wait_ge(s_out, CT - 1 if g < 2 else CT)
                            else:
                                keys_taken(pe, g - 4)
                            key_group(g, (g + 2) % 4).then_inc(k_product, 1)

                        if softmax:
                            for t in range(CT):
                                scores(t)
                            pe.wait_ge(next_ctx, 16)
                            for g in range(2):
                                next_keys(g)
                            pe.wait_ge(maxima, CT - 1)
                            for j in range(PAIRS):
                                last = nc.tensor.transpose(
                                    two_banks[2][:, j * P:(j + 1) * P],
                                    most[:, 2 * j:2 * j + 2, :].rearrange("p h s -> p (h s)"),
                                    env.ident)
                            last.then_inc(turned, 1)
                            for g in range(2, 4):
                                next_keys(g)
                            pe.wait_ge(diag_ready, 1)
                            for half in range(2):
                                nc.tensor.matmul(ps[:, 6 + half, :], env.ones,
                                                 diag[:, 4 * half:4 * half + 4, :],
                                                 start=True, stop=True).then_inc(bc_product, 1)
                            for g in range(4, KG):
                                next_keys(g)
                            for t in range(CT):
                                values(t)
                        else:
                            for t in range(CT + 2):
                                if t < CT:
                                    scores(t)
                                if t >= 2:
                                    values(t - 2)
                            pe.wait_ge(next_ctx, 16)
                            for g in range(KG):
                                next_keys(g)
                        for t in range(CT):
                            if t < 4:
                                keys_taken(pe, KG - 4 + (t + 2) % 4)
                            else:
                                values_taken(pe, t - 4)
                            value_tile(t).then_inc(v_product, 1)
                            if t == (9 if softmax else 3):
                                if POOL_TILES:
                                    pe.wait_ge(pool_sums, len(POOL_TILES) - 1)
                                pe.wait_ge(dve_sums, len(DVE_TILES) - 1)
                                for j in range(PAIRS):
                                    for r in sum_kinds:
                                        last = nc.tensor.matmul(
                                            ps[32 * (j % 4):32 * (j % 4) + 32, 6,
                                               (j // 4) * P:(j // 4 + 1) * P],
                                            env.ones[:, 0:32],
                                            den_parts[:, r, 2 * j:2 * j + 2, :],
                                            start=(r == sum_kinds[0]), stop=(r == 1))
                                last.then_inc(den_product, 1)

                    @block.scalar
                    def _(act):
                        def take_key_group(g):
                            act.wait_ge(k_product, g + 1)
                            take_keys(nc.scalar.copy, g, (g + 2) % 4).then_inc(k_act, 1)

                        if softmax:
                            for t in range(CT):
                                n = keys_of(t)
                                act.wait_ge(s_product, t + 1)
                                nc.scalar.copy(sc[0:n, t, :, :],
                                               heads(two_banks[t % 2][0:n])).then_inc(s_out, 1)
                            for g in range(4):
                                take_key_group(g)
                            for half in range(2):
                                act.wait_ge(bc_product, half + 1)
                                nc.scalar.copy(top_bc[:, 8 * half:8 * half + 8, :].rearrange(
                                    "p h s -> p (h s)"), ps[:, 6 + half, :]).then_inc(bc_ready, 1)
                        for t in range(CT):
                            n = keys_of(t)
                            if softmax and 4 + t < KG:
                                take_key_group(4 + t)
                            if not softmax:
                                act.wait_ge(s_out, t + 1)
                            elif t in POOL_SHIFTS:
                                act.wait_ge(p_pool, POOL_SHIFTS.index(t) + 1)
                            else:
                                act.wait_ge(p_dve, sum(u not in POOL_SHIFTS
                                                       for u in range(t + 1)))
                            if softmax:
                                ins = nc.scalar.activation(sc[0:n, t, :, :], sc[0:n, t, :, :],
                                                           ACT.Exp, scale=DH ** -0.5)
                            else:
                                ins = nc.scalar.activation(sc[0:n, t, :, :], sc[0:n, t, :, :],
                                                           ACT.Square, scale=DH ** -0.5,
                                                           bias=nb[0:n, 0:1])
                            ins.then_inc(p_ready, 1)
                        if not softmax:
                            for g in range(0, KG, 2):
                                take_key_group(g)
                        for t in act_values:
                            act.wait_ge(v_product, t + 1)
                            take_values(nc.scalar.copy, t).then_inc(v_act, 1)

                    @block.vector
                    def _(dve):
                        steps = Steps(dve, own)
                        if softmax:
                            for t in range(CT):
                                n = keys_of(t)
                                dve.wait_ge(s_out, t + 1)
                                if t == 0:
                                    steps.done(nc.vector.scalar_tensor_tensor(
                                        out=zeros[:, :, :], in0=sc[0:S, 0, :, :], scalar=0.0,
                                        in1=env.excluded[0:S, :].unsqueeze(1).broadcast_to(
                                            [S, H, S]), op0=ALU.is_equal, op1=ALU.mult))
                                    steps.wait()
                                    steps.done(nc.vector.tensor_tensor(
                                        sc[0:S, 0, :, :], sc[0:S, 0, :, :], zeros[:, :, :],
                                        ALU.add))
                                    continue
                                if t == 1:
                                    steps.wait()
                                else:
                                    dve.wait_ge(maxima, t - 1)
                                nc.vector.tensor_tensor(
                                    most[0:n, :, :], (sc[:, 0] if t == 1 else most)[0:n],
                                    sc[0:n, t, :, :], ALU.max).then_inc(maxima, 1)
                            dve.wait_ge(turned, 1)
                            steps.done(nc.vector.tensor_reduce(
                                top[:, :], two_banks[2].rearrange("p (j k) -> p j k", j=PAIRS),
                                AX, ALU.max))
                            steps.wait()
                            nc.vector.tensor_tensor(
                                diag[:, :, :], env.ident.unsqueeze(1).broadcast_to([P, PAIRS, P]),
                                top[:, :].unsqueeze(2).broadcast_to([P, PAIRS, P]),
                                ALU.mult).then_inc(diag_ready, 1)
                            dve.wait_ge(bc_ready, 2)
                            for t in range(CT):
                                if t not in POOL_SHIFTS:
                                    shift(nc.vector, t).then_inc(p_dve, 1)
                        else:
                            for t in range(CT + 1):
                                if t < CT:
                                    n = keys_of(t)
                                    dve.wait_ge(s_product, t + 1)
                                    nc.vector.scalar_tensor_tensor(
                                        out=sc[0:n, t, :, :], in0=heads(two_banks[t % 2][0:n]),
                                        scalar=nb[0:n, 1:2],
                                        in1=cap[0:n, t, :].unsqueeze(1).broadcast_to([n, H, S]),
                                        op0=ALU.max, op1=ALU.min).then_inc(s_out, 1)
                                if t >= 1:
                                    add_weights(nc.vector, 1, DVE_TILES, dve_sums, t - 1)
                        if softmax:
                            for t in DVE_TILES:
                                add_weights(nc.vector, 1, DVE_TILES, dve_sums, t)
                        else:
                            for g in range(1, KG, 2):
                                dve.wait_ge(k_product, g + 1)
                                take_keys(nc.vector.tensor_copy, g, (g + 2) % 4).then_inc(k_dve, 1)

                        def combine():
                            dve.wait_ge(den_product, 1)
                            for out, in_banks in ((den, ps[:, 6, 0:KT * P].rearrange(
                                    "p (k n) -> p k n", k=KT)), (num, ps[:, 4:6, 0:P])):
                                steps.done(nc.vector.tensor_scalar(
                                    out[:, :, :], in_banks[:, :, 0:S], env.parity[:, 0:1], None,
                                    ALU.mult))
                                steps.wait()
                                steps.done(nc.vector.scalar_tensor_tensor(
                                    out=out[:, :, :], in0=in_banks[:, :, S:P],
                                    scalar=env.parity[:, 1:2], in1=out[:, :, :], op0=ALU.mult,
                                    op1=ALU.add))
                            steps.wait()
                            if not softmax:
                                steps.done(nc.vector.tensor_scalar(den[:, :, :], den[:, :, :], 1e-32,
                                                                   None, ALU.add))
                                steps.wait()
                            steps.done(nc.vector.reciprocal(den[:, :, :], den[:, :, :]))
                            steps.wait()
                            steps.done(nc.vector.tensor_tensor(att_T[:, :, bass.ds(b * S, S)],
                                                               num[:, :, :], den[:, :, :], ALU.mult))

                        for t in range(CT):
                            if t not in act_values:
                                dve.wait_ge(v_product, t + 1)
                                take_values(nc.vector.tensor_copy, t).then_inc(v_dve, 1)
                            if t == (CT - 1 if softmax else 5):
                                combine()


def scoped(nc, name):
    mem = ExitStack()

    def sb(n, shape, dt=F32):
        return mem.enter_context(nc.sbuf_tensor(f"{name}_{n}", shape, dt))

    return mem, sb


def l0_xattn(nc, env, d):
    mem, sb = scoped(nc, "x0")
    with mem:
        wq, wk, wv, wo = (sb(n, [P, KT, D]) for n in ("wq", "wk", "wv", "wo"))
        q_T, att_T = sb("q_T", [P, KT, N]), sb("att_T", [P, KT, N])
        ctx_T = sb("ctx_T", [P, KT, SK])
        layernorm(nc, env, "x0_ln", env.x, env.h, env.h_T, loads=[
            (ctx_T[:, :, :], wview(d["ctx_T"][0])),
            (wq[:, :, :], wview(d["L0_xattn_w_q"])), (wk[:, :, :], wview(d["L0_xattn_w_k"])),
            (wv[:, :, :], wview(d["L0_xattn_w_v"])), (wo[:, :, :], wview(d["L0_xattn_w_o"]))])
        linear_T(nc, env, "x0_q", [(env.h_T, wq, q_T, None, None)])
        context_heads(nc, env, "x0", d["ctx_T"], ctx_T, q_T, att_T, wk, wv, softmax=True)
        project_add(nc, env, "x0_o", att_T, wo, None, env.x)


def l0_attn(nc, env, d):
    mem, sb = scoped(nc, "e0")
    FF = 4 * D
    FT = FF // P
    HALF = T // 2
    with mem:
        y = sb("y", [P, T, D])
        wq, wk, wv, wo = (sb(n, [P, KT, D]) for n in ("wq", "wk", "wv", "wo"))
        w1, w2 = sb("w1", [P, KT, FF]), sb("w2", [P, FT, D])
        ln1, ln2 = sb("ln1", [P, 2, KT]), sb("ln2", [P, 2, KT])
        bq, b1 = sb("bq", [P, KT]), sb("b1", [P, FT])
        bk, bv, bo, b2 = (sb(n, [P, D]) for n in ("bk", "bv", "bo", "b2"))
        pos, lnf = sb("pos", [P, D]), sb("lnf", [P, 2, D])
        q_T, qe_T, att_T = sb("q_T", [P, KT, N]), sb("qe_T", [P, KT, N]), sb("att_T", [P, KT, N])
        den_T = sb("den_T", [P, NH])
        k_nat = sb("k_nat", [P, T, D])
        v_own = sb("v_own", [P, T, KT, 2, P + 1])
        hid_T = sb("hid_T", [P, FT, NH])
        kv_bd = sb("kv_bd", [P, 2 * HALF, KT, P])
        ksum = sb("ksum", [P, KT, 2 * HALF])
        layer_loads = [(wq[:, :, :], lambda i: wview(d["L0_attn_Wq"][i])),
                       (wk[:, :, :], lambda i: wview(d["L0_attn_Wk"][i])),
                       (wv[:, :, :], lambda i: wview(d["L0_attn_Wv"][i])),
                       (bq[:, :], lambda i: d["L0_attn_bq"][i]),
                       (bk[:, :], lambda i: d["L0_attn_bk"][i].partition_broadcast(P)),
                       (bv[:, :], lambda i: d["L0_attn_bv"][i].partition_broadcast(P)),
                       (ln1[:, 0, :], lambda i: d["L0_attn_ln1_s"][i]),
                       (ln1[:, 1, :], lambda i: d["L0_attn_ln1_b"][i])]
        late_loads = [(wo[:, :, :], lambda i: wview(d["L0_attn_Wo"][i])),
                      (bo[:, :], lambda i: d["L0_attn_bo"][i].partition_broadcast(P)),
                      (ln2[:, 0, :], lambda i: d["L0_attn_ln2_s"][i]),
                      (ln2[:, 1, :], lambda i: d["L0_attn_ln2_b"][i]),
                      (b1[:, :], lambda i: d["L0_attn_b1"][i]),
                      (w1[:, :, :], lambda i: wview(d["L0_attn_W1"][i])),
                      (b2[:, :], lambda i: d["L0_attn_b2"][i].partition_broadcast(P)),
                      (w2[:, :, :], lambda i: wview(d["L0_attn_W2"][i]))]
        layernorm(nc, env, "e0_in", env.x, env.h, None, loads=[
            (pos[:, :], d["pos"]),
            (lnf[:, 0, :], d["L0_attn_lnf_s"].partition_broadcast(P)),
            (lnf[:, 1, :], d["L0_attn_lnf_b"].partition_broadcast(P))]
            + [(dst, src(0)) for dst, src in layer_loads])
        with signals(nc, "e0_pos", "zeroed set") as (zeroed, y_set):
            with nc.Block() as block:

                @block.vector
                def _(dve):
                    for t in range(T):
                        nc.vector.scalar_tensor_tensor(
                            out=y[:, t, :], in0=env.h[:, t, :], scalar=float(D) ** 0.5,
                            in1=pos[:, :], op0=ALU.mult, op1=ALU.add).then_inc(y_set, 1)

                @block.gpsimd
                def _(pool):
                    nc.gpsimd.memset(v_own[:, :, :, :, :], 0.0).then_inc(zeroed, 1)
                    pool.wait_ge(zeroed, 1)
                    for b in range(2):
                        nc.gpsimd.memset(v_own[b * S:(b + 1) * S, :, :, b, P:P + 1], 1.0
                                         ).then_inc(zeroed, 1)

        work = [("norm1", c, f, "act") for c in range(2) for f in range(KT)]
        for c in range(2):
            work += [("query", c, m, "act") for m in range(KT)]
            work += [("key_value", t, 0, "dve") for t in range(c * HALF, (c + 1) * HALF)]

        def states(c):
            return [("state", t, f, "dve") for t in range(c * HALF, (c + 1) * HALF)
                    for f in range(KT)]

        def nums_dens(c):
            return [(kind, c, f, "dve") for f in range(KT) for kind in ("den", "num")]

        def rows_of(kind, c):
            return [(kind, t, 0, "dve") for t in range(c * HALF, (c + 1) * HALF)]

        def turned_ups(c):
            return ([("norm2", c, f, "act") for f in range(KT)]
                    + [("up", c, m, "act") for m in range(FT)])

        work += states(0) + nums_dens(0) + states(1) + rows_of("out", 0) + nums_dens(1)
        work += turned_ups(0) + rows_of("out", 1) + rows_of("down", 0)
        work += turned_ups(1) + rows_of("down", 1)
        at = {w[0:3]: g for g, w in enumerate(work)}

        def taken_by(engine, kind, i, j=0):
            return sum(w[3] == engine for w in work[:at[kind, i, j] + 1])

        def bank(kind, i, j=0):
            return env.ps[:, at[kind, i, j] % 8, :]

        with nc.Fori(0, 4) as i:
            with signals(nc, "e0_layer", "late next own stats std rows_ready product act_out "
                         "dve_out k_in q_exped k_exped k_elu k_ready q_ready scaled "
                         "y_biased") as (
                    late, next_in, own, stats, std_ready, rows_ready, product, act_out, dve_out,
                    k_in, q_exped, k_exped, k_elu, k_ready, q_ready, scaled,
                    y_biased):
                with nc.Block() as block:

                    @block.sync
                    def _(sp):
                        for dst, src in late_loads:
                            sp.dma_start(dst, src(i)).then_inc(late, 16)
                        sp.wait_ge(product, at["key_value", T - 1, 0] + 1)
                        sp.wait_ge(act_out, taken_by("act", "query", 1, KT - 1))
                        sp.wait_ge(dve_out, taken_by("dve", "key_value", T - 1))
                        for dst, src in layer_loads:
                            sp.dma_start(dst, src((i + 1) % 4)).then_inc(next_in, 16)
                        sp.wait_ge(late, 16 * len(late_loads))
                        sp.wait_ge(next_in, 16 * len(layer_loads))

                    @block.gpsimd
                    def _(pool):
                        pool.wait_ge(late, 16 * len(late_loads))
                        for norm, bias in ((0, bo), (1, b2)):
                            for c in range(2):
                                pool.wait_ge(rows_ready, 8 * norm + 4 * c + 4)
                                ts = slice(c * HALF, (c + 1) * HALF)
                                nc.gpsimd.tensor_tensor(
                                    y[:, ts, :], y[:, ts, :],
                                    bias[:, :].unsqueeze(1).broadcast_to([P, HALF, D]),
                                    ALU.add).then_inc(y_biased, 1)

                    @block.tensor
                    def _(pe):
                        for g, (kind, a, j, _) in enumerate(work):
                            put = env.ps[:, g % 8, :]
                            if g >= 8:
                                before = work[g - 8]
                                if before[3] == "act":
                                    pe.wait_ge(act_out, taken_by("act", *before[0:3]))
                                else:
                                    pe.wait_ge(dve_out, taken_by("dve", *before[0:3]))
                            if kind in ("norm1", "norm2"):
                                pe.wait_ge(rows_ready, 4 * a + 4 + (T if kind == "norm2" else 0))
                                for t in range(HALF):
                                    last = nc.tensor.transpose(
                                        put[:, t * P:(t + 1) * P],
                                        env.h[:, a * HALF + t, j * P:(j + 1) * P], env.ident)
                            elif kind == "query":
                                pe.wait_ge(act_out, taken_by("act", "norm1", a, KT - 1))
                                for k in range(KT):
                                    last = nc.tensor.matmul(
                                        put, wq[:, k, j * P:(j + 1) * P],
                                        env.h_T[:, k, a * NH:(a + 1) * NH], start=(k == 0),
                                        stop=(k == KT - 1))
                            elif kind == "key_value":
                                for n, w in enumerate((wk, wv)):
                                    for k in range(KT):
                                        last = nc.tensor.matmul(
                                            put[:, n * D:(n + 1) * D],
                                            env.h_T[:, k, a * P:(a + 1) * P], w[:, k, :],
                                            start=(k == 0), stop=(k == KT - 1))
                            elif kind == "state":
                                pe.wait_ge(k_ready, a // HALF + 1)
                                last = nc.tensor.matmul(
                                    put[:, 0:2 * (P + 1)], k_nat[:, a, j * P:(j + 1) * P],
                                    v_own[:, a, j, :, :], start=True, stop=True)
                            elif kind == "den":
                                pe.wait_ge(scaled, a + 1)
                                last = nc.tensor.matmul(
                                    put, env.same_head, qe_T[:, j, a * NH:(a + 1) * NH],
                                    start=True, stop=True)
                            elif kind == "num":
                                for u in range(2 * HALF):
                                    n = 2 * S if u < 2 * HALF - 1 else S
                                    q_at = (2 * HALF * a + u) * S
                                    last = nc.tensor.matmul(
                                        put[:, u * S:u * S + n], kv_bd[:, u, j, :],
                                        q_T[:, j, q_at:q_at + n], start=True, stop=True,
                                        skip_group_check=True)
                            elif kind == "out":
                                pe.wait_ge(dve_out, taken_by("dve", "num", a // HALF, KT - 1))
                                pe.wait_ge(late, 16 * len(late_loads))
                                for k in range(KT):
                                    last = nc.tensor.matmul(
                                        put[:, 0:D], att_T[:, k, a * P:(a + 1) * P], wo[:, k, :],
                                        start=(k == 0), stop=(k == KT - 1))
                            elif kind == "up":
                                pe.wait_ge(act_out, taken_by("act", "norm2", a, KT - 1))
                                for k in range(KT):
                                    last = nc.tensor.matmul(
                                        put, w1[:, k, j * P:(j + 1) * P],
                                        env.h_T[:, k, a * NH:(a + 1) * NH], start=(k == 0),
                                        stop=(k == KT - 1))
                            else:
                                pe.wait_ge(act_out, taken_by("act", "up", a // HALF, FT - 1))
                                for k in range(FT):
                                    t = a % HALF
                                    last = nc.tensor.matmul(
                                        put[:, 0:D], hid_T[:, k, t * P:(t + 1) * P], w2[:, k, :],
                                        start=(k == 0), stop=(k == FT - 1))
                            last.then_inc(product, 1)

                    @block.scalar
                    def _(act):
                        def deviations(norm, c):
                            act.wait_ge(stats, T * norm + HALF * (c + 1))
                            nc.scalar.activation(env.std[:, c * HALF:(c + 1) * HALF],
                                                 env.mv[:, c * HALF:(c + 1) * HALF, 1], ACT.Sqrt,
                                                 bias=env.eps5[:, 0:1]).then_inc(std_ready, 1)

                        def turned(kind, c, affine):
                            for f in range(KT):
                                act.wait_ge(product, at[kind, c, f] + 1)
                                nc.scalar.activation(
                                    env.h_T[:, f, c * NH:(c + 1) * NH], bank(kind, c, f),
                                    ACT.Identity, scale=affine[:, 0, f:f + 1],
                                    bias=affine[:, 1, f:f + 1]).then_inc(act_out, 1)

                        def hidden(c):
                            if c:
                                act.wait_ge(product, at["down", HALF - 1, 0] + 1)
                            for m in range(FT):
                                act.wait_ge(product, at["up", c, m] + 1)
                                nc.scalar.activation(hid_T[:, m, :], bank("up", c, m), ACT.Relu,
                                                     bias=b1[:, m:m + 1]).then_inc(act_out, 1)

                        deviations(0, 0)
                        deviations(0, 1)
                        turned("norm1", 0, ln1)
                        turned("norm1", 1, ln1)
                        for c in range(2):
                            cols, ts = slice(c * NH, (c + 1) * NH), slice(c * HALF, (c + 1) * HALF)
                            for m in range(KT):
                                put = bank("query", c, m)
                                act.wait_ge(product, at["query", c, m] + 1)
                                nc.scalar.activation(qe_T[:, m, cols], put, ACT.Exp,
                                                     bias=bq[:, m:m + 1]).then_inc(q_exped, 1)
                                nc.scalar.activation(q_T[:, m, cols], put, ACT.Relu,
                                                     bias=bq[:, m:m + 1]).then_inc(act_out, 1)
                            act.wait_ge(k_in, HALF * (c + 1))
                            nc.scalar.activation(env.rows[:, ts, :], k_nat[:, ts, :], ACT.Exp
                                                 ).then_inc(k_exped, 1)
                        act.wait_ge(late, 16 * len(late_loads))
                        deviations(1, 0)
                        turned("norm2", 0, ln2)
                        hidden(0)
                        deviations(1, 1)
                        turned("norm2", 1, ln2)
                        hidden(1)

                    @block.vector
                    def _(dve):
                        steps = Steps(dve, own)

                        def normalise(norm, c):
                            ts = range(c * HALF, (c + 1) * HALF)
                            for t in ts:
                                steps.done(nc.vector.bn_stats(env.bn[:, t, :], y[:, t, :]))
                            steps.wait()
                            for t in ts:
                                nc.vector.bn_aggr(env.mv[:, t, :], env.bn[:, t, :]
                                                  ).then_inc(stats, 1)
                            dve.wait_ge(std_ready, 2 * norm + c + 1)
                            half = slice(c * HALF, (c + 1) * HALF)
                            steps.done(nc.vector.reciprocal(env.rstd[:, half], env.std[:, half]))
                            steps.wait()
                            for t in ts:
                                nc.vector.tensor_scalar(
                                    env.h[:, t, :], y[:, t, :], env.mv[:, t, 0:1],
                                    env.rstd[:, t:t + 1], ALU.subtract, ALU.mult
                                ).then_inc(rows_ready, 1)

                        def keys_values(c):
                            for t in range(c * HALF, (c + 1) * HALF):
                                dve.wait_ge(product, at["key_value", t, 0] + 1)
                                put = bank("key_value", t)
                                nc.vector.tensor_tensor(k_nat[:, t, :], put[:, 0:D], bk[:, :],
                                                        ALU.add).then_inc(k_in, 1)
                                for b in range(2):
                                    own_rows = slice(b * S, (b + 1) * S)
                                    ins = nc.vector.tensor_tensor(
                                        v_own[own_rows, t, :, b, 0:P],
                                        put[own_rows, D:2 * D].rearrange("p (f n) -> p f n", f=KT),
                                        bv[own_rows, :].rearrange("p (f n) -> p f n", f=KT),
                                        ALU.add)
                                    steps.done(ins) if b == 0 else ins.then_inc(dve_out, 1)

                        def elu(c):
                            cols = slice(c * NH, (c + 1) * NH)
                            dve.wait_ge(act_out, taken_by("act", "query", c, KT - 1))
                            dve.wait_ge(q_exped, KT * (c + 1))
                            nc.vector.scalar_tensor_tensor(
                                out=q_T[:, :, cols], in0=qe_T[:, :, cols], scalar=1.0,
                                in1=q_T[:, :, cols], op0=ALU.min, op1=ALU.add
                            ).then_inc(q_ready, 1)
                            ts = slice(c * HALF, (c + 1) * HALF)
                            dve.wait_ge(k_exped, c + 1)
                            nc.vector.tensor_scalar(env.rows[:, ts, :], env.rows[:, ts, :], 1.0,
                                                    None, ALU.min).then_inc(k_elu, 1)
                            dve.wait_ge(k_elu, c + 1)
                            nc.vector.scalar_tensor_tensor(
                                out=k_nat[:, ts, :], in0=k_nat[:, ts, :], scalar=0.0,
                                in1=env.rows[:, ts, :], op0=ALU.max, op1=ALU.add
                            ).then_inc(k_ready, 1)

                        def take_states(c):
                            if c:
                                dve.wait_ge(product, at["num", 0, KT - 1] + 1)
                            for t in range(c * HALF, (c + 1) * HALF):
                                for f in range(KT):
                                    u = 2 * (t % HALF)
                                    dve.wait_ge(product, at["state", t, f] + 1)
                                    put = bank("state", t, f)[:, 0:2 * (P + 1)].rearrange(
                                        "p (b n) -> p b n", b=2)
                                    steps.done(nc.vector.tensor_copy(ksum[:, f, u:u + 2],
                                                                     put[:, :, P]))
                                    nc.vector.tensor_tensor(
                                        kv_bd[:, u:u + 2, f, :], put[:, :, 0:P],
                                        env.same_head.unsqueeze(1).broadcast_to([P, 2, P]),
                                        ALU.mult).then_inc(dve_out, 1)
                            cols = slice(c * NH, (c + 1) * NH)
                            dve.wait_ge(q_ready, c + 1)
                            steps.wait()
                            for f in range(KT):
                                ins = nc.vector.tensor_tensor(
                                    qe_T[:, f, cols].rearrange("p (u s) -> p u s", s=S),
                                    q_T[:, f, cols].rearrange("p (u s) -> p u s", s=S),
                                    ksum[:, f, :].unsqueeze(2).broadcast_to([P, 2 * HALF, S]),
                                    ALU.mult)
                                steps.done(ins) if f == 0 else ins.then_inc(scaled, 1)

                        def attention(c):
                            for f in range(KT):
                                dve.wait_ge(product, at["den", c, f] + 1)
                                nc.vector.tensor_scalar(den_T[:, :], bank("den", c, f), 1e-6,
                                                        None, ALU.add).then_inc(dve_out, 1)
                                dve.wait_ge(dve_out, taken_by("dve", "den", c, f))
                                steps.done(nc.vector.reciprocal(den_T[:, :], den_T[:, :]))
                                dve.wait_ge(product, at["num", c, f] + 1)
                                steps.wait()
                                nc.vector.tensor_tensor(
                                    att_T[:, f, c * NH:(c + 1) * NH], bank("num", c, f),
                                    den_T[:, :], ALU.mult).then_inc(dve_out, 1)
                                dve.wait_ge(dve_out, taken_by("dve", "num", c, f))

                        def add_rows(kind, c):
                            dve.wait_ge(y_biased, c + 1 + (2 if kind == "down" else 0))
                            for t in range(c * HALF, (c + 1) * HALF):
                                dve.wait_ge(product, at[kind, t, 0] + 1)
                                nc.vector.tensor_tensor(y[:, t, :], y[:, t, :],
                                                        bank(kind, t)[:, 0:D], ALU.add
                                                        ).then_inc(dve_out, 1)
                            dve.wait_ge(dve_out, taken_by("dve", kind, (c + 1) * HALF - 1))

                        normalise(0, 0)
                        normalise(0, 1)
                        keys_values(0)
                        elu(0)
                        keys_values(1)
                        take_states(0)
                        elu(1)
                        attention(0)
                        take_states(1)
                        add_rows("out", 0)
                        normalise(1, 0)
                        attention(1)
                        add_rows("out", 1)
                        normalise(1, 1)
                        add_rows("down", 0)
                        add_rows("down", 1)

        layernorm(nc, env, "e0_lnf", y, env.h, None)
        with signals(nc, "e0_add", "scaled moved added") as (scaled, moved, added):
            with nc.Block() as block:

                @block.vector
                def _(dve):
                    for t in range(T):
                        nc.vector.tensor_tensor(env.h[:, t, :], env.h[:, t, :], lnf[:, 0, :],
                                                ALU.mult).then_inc(scaled, 1)
                    for t in range(T):
                        dve.wait_ge(scaled, t + 1)
                        nc.vector.tensor_tensor(env.h[:, t, :], env.h[:, t, :], lnf[:, 1, :],
                                                ALU.add).then_inc(moved, 1)
                    for t in range(T):
                        dve.wait_ge(moved, t + 1)
                        nc.vector.tensor_tensor(env.x[:, t, :], env.x[:, t, :], env.h[:, t, :],
                                                ALU.add).then_inc(added, 1)


def top2(nc, env, dve, probs, experts, weights, chosen, m8, i8, i_f, steps):
    for t in range(T):
        steps.done(nc.vector.max(m8[:, t, :], probs[:, t, :]))
    steps.wait()
    for t in range(T):
        steps.done(nc.vector.max_index(i8[:, t, :], m8[:, t, :], probs[:, t, :]))
    steps.done(nc.vector.tensor_copy(weights, m8[:, :, 0:2]))
    steps.wait()
    steps.done(nc.vector.tensor_copy(i_f[:, :, :], i8[:, :, 0:2]))
    steps.wait()
    for k in range(2):
        steps.done(nc.vector.tensor_tensor(
            chosen[:, :, k, :], env.iota8.unsqueeze(1).broadcast_to([P, T, experts]),
            i_f[:, :, k:k + 1].broadcast_to([P, T, experts]), ALU.is_equal))
    steps.wait()


def row_softmax(nc, dve, logits, top, total, n, exped, shifted, steps):
    steps.done(nc.vector.tensor_reduce(top, logits, AX, ALU.max))
    steps.wait()
    nc.vector.tensor_tensor(logits, logits, top.unsqueeze(2).broadcast_to([P, T, n]),
                            ALU.subtract).then_inc(shifted, 1)
    dve.wait_ge(exped, 1)
    steps.done(nc.vector.tensor_reduce(total, logits, AX, ALU.add))
    steps.wait()
    steps.done(nc.vector.reciprocal(total, total))
    steps.wait()
    steps.done(nc.vector.tensor_tensor(logits, logits, total.unsqueeze(2).broadcast_to([P, T, n]),
                                       ALU.mult))
    steps.wait()


def l0_ffn(nc, env, d):
    E = 8
    CAP = int(1.25 * N / E)
    mem, sb = scoped(nc, "f0")
    with mem:
        gate = sb("gate", [P, KT, E])
        w1, w2 = sb("w1", [P, KT, D]), sb("w2", [P, KT, D])
        b1, b2 = sb("b1", [P, E, KT]), sb("b2", [E, D])
        probs, comb = sb("probs", [P, T, E]), sb("comb", [P, T, E])
        chosen, weights = sb("chosen", [P, T, 2, E]), sb("weights", [P, T, 2])
        m8, i8, i_f = sb("m8", [P, T, 8]), sb("i8", [P, T, 8], U32), sb("i_f", [P, T, 2])
        top, total, keep = sb("top", [P, T]), sb("total", [P, T]), sb("keep", [P, E])
        both, tmp = sb("both", [P, T, E]), sb("tmp", [P, T, E])
        hid_T, comb_T = sb("hid_T", [P, KT, N]), sb("comb_T", [E, N])
        layernorm(nc, env, "f0_ln", env.x, env.h, env.h_T, loads=[
            (gate[:, :, :], wview(d["L0_ffn_gate_w"])), (b1[:, :, :], d["L0_ffn_b1"]),
            (b2[:, :], d["L0_ffn_b2"]),
            (w1[:, :, :], wview(d["L0_ffn_W1"][0]))])
        with signals(nc, "f0_route", "logits own shifted exped picked counted weighed turned "
                     "turned_out biases added") as (
                logits, own, shifted, exped, picked, counted, weighed, turned, turned_out,
                biases, added):
            with nc.Block() as block:

                @block.tensor
                def _(pe):
                    for t in range(T):
                        for k in range(KT):
                            last = nc.tensor.matmul(env.ps[:, 0, t * E:(t + 1) * E],
                                                    env.h_T[:, k, t * P:(t + 1) * P],
                                                    gate[:, k, :], start=(k == 0),
                                                    stop=(k == KT - 1))
                    last.then_inc(logits, 1)
                    pe.wait_ge(picked, 1)
                    for t in range(T):
                        last = nc.tensor.matmul(env.ps[:, 1, 0:E], env.ones, both[:, t, :],
                                                start=(t == 0), stop=(t == T - 1))
                    last.then_inc(counted, 1)
                    pe.wait_ge(weighed, 1)
                    for t in range(T):
                        last = nc.tensor.transpose(
                            env.ps[0:E, 2 + t // 4, (t % 4) * P:(t % 4 + 1) * P], comb[:, t, :],
                            env.ident)
                    last.then_inc(turned, 1)
                    pe.wait_ge(turned_out, 1)
                    for t in range(T):
                        nc.tensor.matmul(env.ps[:, 4 + t // 2, (t % 2) * D:(t % 2 + 1) * D],
                                         comb_T[:, t * P:(t + 1) * P], b2[:, :], start=True,
                                         stop=True).then_inc(biases, 1)

                @block.scalar
                def _(act):
                    act.wait_ge(shifted, 1)
                    nc.scalar.activation(probs[:, :, :], probs[:, :, :], ACT.Exp).then_inc(exped, 1)

                @block.vector
                def _(dve):
                    steps = Steps(dve, own)
                    dve.wait_ge(logits, 1)
                    steps.done(nc.vector.tensor_copy(
                        probs[:, :, :], env.ps[:, 0, 0:T * E].rearrange("p (t e) -> p t e", t=T)))
                    steps.wait()
                    row_softmax(nc, dve, probs[:, :, :], top[:, :], total[:, :], E, exped, shifted,
                                steps)
                    top2(nc, env, dve, probs, E, weights[:, :, :], chosen, m8, i8, i_f, steps)
                    nc.vector.tensor_tensor(both[:, :, :], chosen[:, :, 0, :], chosen[:, :, 1, :],
                                            ALU.add).then_inc(picked, 1)
                    for k, dst in ((0, comb), (1, tmp)):
                        steps.done(nc.vector.tensor_tensor(
                            dst[:, :, :], chosen[:, :, k, :],
                            weights[:, :, k:k + 1].broadcast_to([P, T, E]), ALU.mult))
                    steps.wait()
                    steps.done(nc.vector.tensor_tensor(comb[:, :, :], comb[:, :, :], tmp[:, :, :],
                                                       ALU.add))
                    dve.wait_ge(counted, 1)
                    steps.done(nc.vector.tensor_scalar(keep[:, :], env.ps[:, 1, 0:E], float(CAP),
                                                       None, ALU.is_le))
                    steps.wait()
                    nc.vector.tensor_tensor(
                        comb[:, :, :], comb[:, :, :],
                        keep[:, :].unsqueeze(1).broadcast_to([P, T, E]), ALU.mult
                    ).then_inc(weighed, 1)
                    dve.wait_ge(turned, 1)
                    nc.vector.tensor_copy(comb_T[:, :].rearrange("e (c n) -> e c n", c=2),
                                          env.ps[0:E, 2:4, :]).then_inc(turned_out, 1)
                    for t in range(0, T, 2):
                        dve.wait_ge(biases, t + 2)
                        nc.vector.tensor_tensor(
                            env.x[:, t:t + 2, :], env.x[:, t:t + 2, :],
                            env.ps[:, 4 + t // 2, :].rearrange("p (t n) -> p t n", t=2), ALU.add
                        ).then_inc(added, 1)

        with nc.Fori(0, E) as e:
            expert(nc, env, "f0_expert", [w1], b1[:, bass.ds(e, 1), :].squeeze(1), hid_T, w2,
                   lambda t: comb[:, t, bass.ds(e, 1)],
                   now=[(w2[:, :, :], wview(d["L0_ffn_W2"][e]))],
                   after=[(w1[:, :, :], wview(d["L0_ffn_W1"][(e + 1) % E]))])


def l1_xattn(nc, env, d):
    G3 = 3 * KT
    PAD = CT * P
    mem, sb = scoped(nc, "s1")
    with mem:
        wq, wk, wv = (sb(n, [P, KT, D]) for n in ("wq", "wk", "wv"))
        wih, whh = sb("wih", [P, KT, 3 * D]), sb("whh", [P, KT, 3 * D])
        norm = sb("norm", [P, 2, KT])
        gb = sb("gb", [P, 2, G3])
        gb2 = sb("gb2", [P, 4])
        res_T = sb("res_T", [P, KT, N])
        ctx_T = [sb(f"ctx_T{r}", [P, 2, KT, PAD]) for r in range(2)]
        ctx_n = [sb(f"ctx_n{r}", [P, 2, CT, D + 1]) for r in range(2)]
        ssq, rms, rs_c = (sb(n, [P, 2, CT]) for n in ("ssq", "rms", "rs_c"))
        junk = sb("junk", [P, 2, D])
        sl = sb("sl", [P, KT, P])
        carry, wup = sb("carry", [P, KT, D]), sb("wup", [P, KT, 3 * D])
        sq, rs_norm, q2 = (sb(n, [P, KT, P]) for n in ("sq", "rs_norm", "q2"))
        std, rs = sb("std", [P, P]), sb("rs", [P, P])
        att = sb("att", [P, 2, CT, S])
        top, tot = sb("top", [P, 2, CT]), sb("tot", [P, 2, CT])
        rden = sb("rden", [P, 1])
        u_n, u_T = sb("u_n", [P, D]), sb("u_T", [P, KT, P])
        rz, n_T, hn = sb("rz", [P, 4, P]), sb("n_T", [P, KT, P]), sb("hn", [P, KT, P])
        tiny = sb("tiny", [P, 1])
        ps = env.ps
        layernorm(nc, env, "s1_ln", env.x, env.h, env.h_T, loads=[
            (wq[:, :, :], wview(d["L1_xattn_Wq"])), (wk[:, :, :], wview(d["L1_xattn_Wk"])),
            (wv[:, :, :], wview(d["L1_xattn_Wv"])), (wih[:, :, :], wview(d["L1_xattn_gru_wih"])),
            (whh[:, :, :], wview(d["L1_xattn_gru_whh"])),
            (norm[:, 0, :], d["L1_xattn_slot_norm_w"]), (norm[:, 1, :], d["L1_xattn_input_norm_w"]),
            (gb[:, 0, :], d["L1_xattn_gru_bih"]), (gb[:, 1, :], d["L1_xattn_gru_bhh"])]
            + [load for row in range(2) for load in (
                (ctx_T[0][:, row, :, 0:SK], wview(d["ctx_T"][row])),
                (ctx_n[0][:, row, 0:CT - 1, 0:D], wview(d["ctx"][row, 0:(CT - 1) * P, :])))])

        def load_context(sp, r, pair, sem):
            for b in range(2):
                row = 2 * pair + b
                sp.dma_start(ctx_T[r][:, b, :, 0:SK],
                             d["ctx_T"][row].rearrange("(k p) n -> p k n", p=P)).then_inc(sem, 16)
                sp.dma_start(ctx_n[r][:, b, 0:CT - 1, 0:D],
                             d["ctx"][row, 0:(CT - 1) * P, :].rearrange(
                                 "(t p) f -> p t f", p=P)).then_inc(sem, 16)
                sp.dma_start(ctx_n[r][0:LAST, b, CT - 1, 0:D],
                             d["ctx"][row, (CT - 1) * P:SK, :]).then_inc(sem, 16)

        with signals(nc, "s1_pre", "cleared loaded own product combined") as (
                cleared, loaded, own, product, combined):
            with nc.Block() as block:

                @block.tensor
                def _(pe):
                    for m in range(KT):
                        for k in range(KT):
                            last = nc.tensor.matmul(ps[:, m, 0:D], wq[:, k, m * P:(m + 1) * P],
                                                    wk[:, k, :], start=(k == 0),
                                                    stop=(k == KT - 1))
                    last.then_inc(product, 1)
                    for m in range(KT):
                        for bank, cols in ((0, slice(0, NH)), (1, slice(NH, 3 * D))):
                            for k in range(KT):
                                last = nc.tensor.matmul(
                                    ps[:, 2 + 2 * m + bank, 0:cols.stop - cols.start],
                                    wv[:, k, m * P:(m + 1) * P], wih[:, k, cols],
                                    start=(k == 0), stop=(k == KT - 1))
                    last.then_inc(product, 1)

                @block.scalar
                def _(act):
                    act.wait_ge(product, 1)
                    for m in range(KT):
                        nc.scalar.activation(carry[:, m, :], ps[:, m, 0:D], ACT.Identity,
                                             scale=norm[:, 0, m:m + 1], bias=env.zero[:, 0:1]
                                             ).then_inc(combined, 1)
                    act.wait_ge(product, 2)
                    for m in range(KT):
                        nc.scalar.activation(
                            wup[:, m, :], ps[:, 2 + 2 * m:4 + 2 * m, :].rearrange(
                                "p c n -> p (c n)")[:, 0:3 * D], ACT.Identity,
                            scale=norm[:, 1, m:m + 1], bias=env.zero[:, 0:1]
                            ).then_inc(combined, 1)

                @block.vector
                def _(dve):
                    for r in range(2):
                        nc.vector.memset(ctx_T[r][:, :, :, SK:PAD], 0.0).then_inc(cleared, 1)
                        nc.vector.memset(ctx_n[r][S:P, :, CT - 1, :], 0.0).then_inc(cleared, 1)
                    steps = Steps(dve, own)
                    steps.done(nc.vector.tensor_tensor(gb2[:, :], gb[:, 0, 0:4], gb[:, 1, 0:4],
                                                       ALU.add))
                    steps.wait()
                    steps.done(nc.vector.tensor_scalar(gb2[:, :], gb2[:, :], 0.5, None, ALU.mult))

                @block.sync
                def _(sp):
                    sp.wait_ge(cleared, 4)
                    for row in range(2):
                        sp.dma_start(ctx_n[0][0:LAST, row, CT - 1, 0:D],
                                     d["ctx"][row, (CT - 1) * P:SK, :]).then_inc(loaded, 16)
                    sp.wait_ge(loaded, 2 * 16)

        def square_act(r, t):
            return nc.scalar.activation(junk[:, 0, :], ctx_n[r][:, 0, t, 0:D], ACT.Square,
                                        accum_out=ssq[:, 0, t:t + 1])

        def square_dve(r, t):
            return nc.vector.tensor_tensor_reduce(
                junk[:, 1, :], ctx_n[r][:, 1, t, 0:D], ctx_n[r][:, 1, t, 0:D], 1.0, 0.0,
                ALU.mult, ALU.add, ssq[:, 1, t:t + 1])

        with signals(nc, "s1_squares", "squared_act squared_dve") as (squared_act, squared_dve):
            with nc.Block() as block:

                @block.scalar
                def _(act):
                    for t in range(CT):
                        square_act(0, t).then_inc(squared_act, 1)
                        act.wait_ge(squared_act, t + 1)

                @block.vector
                def _(dve):
                    for t in range(CT):
                        square_dve(0, t).then_inc(squared_dve, 1)
                        dve.wait_ge(squared_dve, t + 1)

        def take_pair(r, pair, next_pair, next_in):
            with signals(nc, f"s1_take{r}", "rms taken own") as (rms_ready, taken, own):
                with nc.Block() as block:

                    @block.sync
                    def _(sp):
                        load_context(sp, 1 - r, next_pair, next_in)

                    @block.scalar
                    def _(act):
                        nc.scalar.activation(rms[:, :, :], ssq[:, :, :], ACT.Sqrt, scale=1.0 / D,
                                             bias=env.eps6[:, 0:1]).then_inc(rms_ready, 1)

                    @block.vector
                    def _(dve):
                        steps = Steps(dve, own)
                        nc.vector.tensor_copy(sl[:, :, :], env.h_T[:, :, bass.ds(pair * P, P)]
                                              ).then_inc(taken, 1)
                        dve.wait_ge(rms_ready, 1)
                        steps.done(nc.vector.reciprocal(rs_c[:, :, :], rms[:, :, :]))
                        steps.done(nc.vector.tensor_copy(ctx_n[r][:, :, 0:CT - 1, D],
                                                         rms[:, :, 0:CT - 1]))
                        steps.done(nc.vector.tensor_scalar(
                            ctx_n[r][:, :, CT - 1, D], rms[:, :, CT - 1], env.valid_last[:, 0:1],
                            None, ALU.mult))

        PER = 7
        units = [(b, c, range(PER * c, min(PER * (c + 1), CT))) for b in range(2) for c in range(2)]

        def attend(r, result=None, next_in=None):
            last_round = result is not None
            with signals(nc, f"s1_it{r}{'last' if last_round else ''}",
                         "squared_act squared_dve own squares ssq_done std q2_done q2_out s_done "
                         "shifted "
                         "exped weights u_done u_ready u_turned u_out hid_done r_done n_done "
                         "z_done gates n_in n_out tables") as (
                    squared_act, squared_dve, own, squares, ssq_done, std_ready, q2_done,
                    q2_out, s_done, shifted,
                    exped, weights, u_done, u_ready, u_turned, u_out, hid_done, r_done, n_done,
                    z_done, gates, n_in, n_out, tables):
                with nc.Block() as block:

                    @block.tensor
                    def _(pe):
                        def project(put, w, in_T, m, **flags):
                            for k in range(KT):
                                last = nc.tensor.matmul(put, w[:, k, m * P:(m + 1) * P],
                                                        in_T[:, k, :],
                                                        **(flags or dict(start=(k == 0),
                                                                         stop=(k == KT - 1))))
                            return last

                        for m in range(KT):
                            last = project(ps[:, 5, m * P:(m + 1) * P], carry, sl, m)
                        last.then_inc(q2_done, 1)
                        pe.wait_ge(squares, 1)
                        for k in range(KT):
                            last = nc.tensor.matmul(ps[:, 4, 0:P], env.ones, sq[:, k, :],
                                                    start=(k == 0), stop=(k == KT - 1))
                        last.then_inc(ssq_done, 1)

                        def hidden(bank, at, first):
                            for i in range(2):
                                for k in range(KT):
                                    m = first + i
                                    last = nc.tensor.matmul(
                                        ps[:, bank, at + i * P:at + (i + 1) * P],
                                        whh[:, k, m * P:(m + 1) * P], sl[:, k, :],
                                        start=(i == 0 and k == 0), stop=False,
                                        skip_group_check=True)
                            return last

                        hidden(6, 0, 0)
                        hidden(7, 2 * P, 4).then_inc(hid_done, 1)
                        pe.wait_ge(q2_out, 1)
                        for b, c, tiles in units:
                            for t in tiles if b == 0 else reversed(tiles):
                                at = (t - tiles[0]) * S
                                for k in range(KT):
                                    last = nc.tensor.matmul(
                                        ps[:, 2 * b + c, at:at + P],
                                        ctx_T[r][:, b, k, t * P:(t + 1) * P], q2[:, k, :],
                                        start=(k == 0), stop=(k == KT - 1))
                            last.then_inc(s_done, 1)
                        pe.wait_ge(shifted, 1)
                        hidden(0, 0, 2)
                        for u, (b, c, tiles) in enumerate(units):
                            pe.wait_ge(weights, u + 1)
                            for t in tiles:
                                last = nc.tensor.matmul(
                                    ps[b * S:(b + 1) * S, 4, 0:D + 1], att[:, b, t, :],
                                    ctx_n[r][:, b, t, :], start=(t == 0), stop=(t == CT - 1))
                        last.then_inc(u_done, 1)
                        pe.wait_ge(u_ready, 1)
                        for f in range(KT):
                            last = nc.tensor.transpose(ps[:, 5, f * P:(f + 1) * P],
                                                       u_n[:, f * P:(f + 1) * P], env.ident)
                        last.then_inc(u_turned, 1)
                        pe.wait_ge(u_out, 1)
                        for bank, first, done in ((6, 0, r_done), (7, 4, n_done), (0, 2, z_done)):
                            for i in range(2):
                                last = project(ps[:, bank, i * P:(i + 1) * P], wup, u_T, first + i,
                                               start=False, stop=True, skip_group_check=True)
                            last.then_inc(done, 1)

                    @block.scalar
                    def _(act):
                        act.wait_ge(ssq_done, 1)
                        nc.scalar.activation(std[:, :], ps[:, 4, 0:P], ACT.Sqrt, scale=1.0 / D,
                                             bias=env.eps6[:, 0:1]).then_inc(std_ready, 1)
                        nc.scalar.activation(tiny[:, :], env.zero[:, 0:1], ACT.Exp
                                             ).then_inc(tables, 1)

                        def next_squares(tiles):
                            for t in tiles if last_round else ():
                                if t == 0:
                                    act.wait_ge(next_in, 6 * 16)
                                else:
                                    act.wait_ge(squared_act, t)
                                square_act(1 - r, t).then_inc(squared_act, 1)

                        next_squares(range(0, 5))
                        for u, (b, c, tiles) in enumerate(units):
                            ts = slice(tiles[0], tiles[-1] + 1)
                            if u:
                                next_squares(range(3 + 2 * u, 5 + 2 * u))
                            act.wait_ge(shifted, u + 1)
                            nc.scalar.activation(att[:, b, ts, :], att[:, b, ts, :], ACT.Exp,
                                                 scale=D ** -0.5).then_inc(exped, 1)
                        next_squares(range(11, CT))
                        for ms, done in (((0, 1), r_done), ((2, 3), z_done)):
                            if ms[0]:
                                act.wait_ge(n_in, 1)
                                for m in range(KT):
                                    nc.scalar.activation(n_T[:, m, :], n_T[:, m, :], ACT.Tanh,
                                                         bias=gb[:, 0, 4 + m:5 + m]
                                                         ).then_inc(n_out, 1)
                            act.wait_ge(done, 1)
                            for m in ms:
                                nc.scalar.activation(rz[:, m, :],
                                                     ps[:, 0 if m > 1 else 6,
                                                        (m % 2) * P:(m % 2 + 1) * P],
                                                     ACT.Tanh, scale=0.5, bias=gb2[:, m:m + 1]
                                                     ).then_inc(gates, 1)
                        nc.scalar.activation(tiny[:, :], env.ones[:, 0:1], ACT.Sqrt
                                             ).then_inc(tables, 1)

                    @block.vector
                    def _(dve):
                        steps = Steps(dve, own)
                        first_256 = ps[:, 5, 0:2 * P].rearrange("p (k n) -> p k n", k=KT)
                        norm_by_feature = norm[:, 1, :].unsqueeze(2).broadcast_to([P, KT, P])
                        nc.vector.tensor_tensor(sq[:, :, :], sl[:, :, :], sl[:, :, :],
                                                ALU.mult).then_inc(squares, 1)
                        dve.wait_ge(std_ready, 1)
                        steps.done(nc.vector.reciprocal(rs[:, :], std[:, :]))
                        steps.wait()
                        steps.done(nc.vector.tensor_tensor(
                            rs_norm[:, :, :], norm_by_feature,
                            rs[:, :].unsqueeze(1).broadcast_to([P, KT, P]), ALU.mult))
                        steps.wait()
                        dve.wait_ge(q2_done, 1)
                        nc.vector.tensor_tensor(q2[:, :, :], first_256, rs_norm[:, :, :],
                                                ALU.mult).then_inc(q2_out, 1)
                        dve.wait_ge(hid_done, 1)
                        for m in range(KT):
                            steps.done(nc.vector.tensor_scalar(
                                hn[:, m, :], ps[:, 7, (2 + m) * P:(3 + m) * P],
                                gb[:, 1, 4 + m:5 + m], 0.5, ALU.add, ALU.mult))

                        def unit_views(u):
                            b, c, tiles = units[u]
                            n, ts = len(tiles), slice(tiles[0], tiles[-1] + 1)
                            put = ps[:, 2 * b + c, b * S:(b + n) * S].rearrange(
                                "p (t s) -> p t s", t=n)

                            def over_slots(x):
                                return x[:, b, ts].unsqueeze(2).broadcast_to([P, n, S])

                            return put, att[:, b, ts, :], (b, ts), over_slots

                        def shift(u):
                            put, w, (b, ts), over_slots = unit_views(u)
                            dve.wait_ge(s_done, u + 1)
                            steps.done(nc.vector.tensor_reduce(top[:, b, ts], put, AX, ALU.max))
                            steps.wait()
                            steps.done(nc.vector.tensor_tensor(w, put, over_slots(top),
                                                               ALU.subtract))
                            steps.wait()
                            nc.vector.tensor_tensor(w, w, over_slots(rs_c), ALU.mult
                                                    ).then_inc(shifted, 1)

                        def weigh(u):
                            put, w, (b, ts), over_slots = unit_views(u)
                            dve.wait_ge(exped, u + 1)
                            steps.done(nc.vector.tensor_reduce(tot[:, b, ts], w, AX, ALU.add))
                            steps.wait()
                            steps.done(nc.vector.reciprocal(tot[:, b, ts], tot[:, b, ts]))
                            steps.wait()
                            steps.done(nc.vector.tensor_tensor(tot[:, b, ts], tot[:, b, ts],
                                                               rs_c[:, b, ts], ALU.mult))
                            steps.wait()
                            nc.vector.tensor_tensor(w, w, over_slots(tot), ALU.mult
                                                    ).then_inc(weights, 1)

                        def next_squares(tiles):
                            for t in tiles if last_round else ():
                                if t == 0:
                                    dve.wait_ge(next_in, 6 * 16)
                                else:
                                    dve.wait_ge(squared_dve, t)
                                square_dve(1 - r, t).then_inc(squared_dve, 1)

                        next_squares(range(0, 7))
                        for u in range(5):
                            if u < 4:
                                shift(u)
                            if u >= 1:
                                weigh(u - 1)
                        next_squares(range(7, CT))
                        dve.wait_ge(u_done, 1)
                        steps.done(nc.vector.tensor_scalar(rden[:, :], ps[:, 4, D:D + 1], 1e-6,
                                                           None, ALU.add))
                        steps.wait()
                        steps.done(nc.vector.reciprocal(rden[:, :], rden[:, :]))
                        steps.wait()
                        nc.vector.tensor_scalar(u_n[:, :], ps[:, 4, 0:D], rden[:, 0:1], None,
                                                ALU.mult).then_inc(u_ready, 1)
                        dve.wait_ge(u_turned, 1)
                        nc.vector.tensor_copy(u_T[:, :, :], first_256).then_inc(u_out, 1)
                        dve.wait_ge(gates, 2)
                        steps.done(nc.vector.scalar_tensor_tensor(
                            out=hn[:, :, :], in0=rz[:, 0:2, :], scalar=1.0, in1=hn[:, :, :],
                            op0=ALU.add, op1=ALU.mult))
                        steps.wait()
                        dve.wait_ge(n_done, 1)
                        nc.vector.tensor_tensor(
                            n_T[:, :, :], hn[:, :, :],
                            ps[:, 7, 0:2 * P].rearrange("p (m n) -> p m n", m=KT),
                            ALU.add).then_inc(n_in, 1)
                        dve.wait_ge(n_out, KT)
                        steps.done(nc.vector.tensor_tensor(hn[:, :, :], sl[:, :, :], n_T[:, :, :],
                                                           ALU.subtract))
                        steps.wait()
                        dve.wait_ge(gates, 4)
                        steps.done(nc.vector.scalar_tensor_tensor(
                            out=hn[:, :, :], in0=rz[:, 2:4, :], scalar=1.0, in1=hn[:, :, :],
                            op0=ALU.add, op1=ALU.mult))
                        steps.wait()
                        steps.done(nc.vector.scalar_tensor_tensor(
                            out=result if last_round else sl[:, :, :], in0=hn[:, :, :],
                            scalar=0.5, in1=n_T[:, :, :],
                            op0=ALU.mult, op1=ALU.add))

        with nc.Fori(0, T // 2) as i:
            with signals(nc, "s1_ctx", "second_in first_in") as next_ins:
                for r, next_in in enumerate(next_ins):
                    pair = 2 * i + r
                    take_pair(r, pair, (pair + 1) % T, next_in)
                    with nc.Fori(0, 2):
                        attend(r)
                    attend(r, res_T[:, :, bass.ds(pair * P, P)], next_in)
        add_turned(nc, env, "s1_add", res_T, env.x)


def self_attention(nc, env, stage, w, b_col, b_row, att_T, scale, bias, per_head, sb):
    q_T, k_T, v_nat = sb("q_T", [P, KT, N]), sb("k_T", [P, KT, N]), sb("v_nat", [P, T, D])
    q_own, v_own = sb("q_own", [P, KT, 2 * P]), sb("v_own", [P, 2, D])
    k_bd = sb("k_bd", [P, 2, KT, HPT, P])
    sc, p_T = sb("sc", [P, 2, H, P]), sb("p_T", [P, 2, H, P])
    top, tot = sb("top", [P, 2, H]), sb("tot", [P, 2, H])
    halves = sb("halves", [P, KT, P])
    ps = env.ps
    linear_T(nc, env, f"{stage}_qk", [(env.h_T, w[:, :, 0:D], q_T, b_col[:, 0:KT], None),
                                      (env.h_T, w[:, :, D:2 * D], k_T, b_col[:, KT:2 * KT], None)])
    linear_rows(nc, env, f"{stage}_v", env.h_T, [(w[:, :, 2 * D:3 * D], b_row,
                                                  lambda t: v_nat[:, t, :])])
    def place(eng, i):
        yield eng.tensor_copy(q_own[:, :, :], q_T[:, :, bass.ds(i * (2 * P), 2 * P)])
        for j in range(2):
            for half in range(KT):
                yield eng.tensor_tensor(
                    k_bd[:, j, half, :, :],
                    k_T[:, half, bass.ds(i * (2 * P) + j * P, P)].unsqueeze(1)
                    .broadcast_to([P, HPT, P]),
                    env.head_of.unsqueeze(2).broadcast_to([P, HPT, P]), ALU.mult)

    with signals(nc, f"{stage}_first", "placed") as (placed,):
        with nc.Block() as block:

            @block.vector
            def _(dve):
                for ins in place(nc.vector, 0):
                    ins.then_inc(placed, 1)

    with nc.Fori(0, T // 2) as i:
        with signals(nc, f"{stage}_at", "own taken placed s_done top_ready exped normed p_turned "
                     "act_out dve_out o_done o_out") as (
                own, taken, placed, s_done, top_ready, exped, normed, p_turned, act_out, dve_out,
                o_done, o_out):
            with nc.Block() as block:

                @block.gpsimd
                def _(pool):
                    pool.wait_ge(s_done, 8)
                    for ins in place(nc.gpsimd, (i + 1) % (T // 2)):
                        ins.then_inc(placed, 1)

                @block.tensor
                def _(pe):
                    for j in range(2):
                        for g in range(4):
                            nc.tensor.matmul(ps[:, 4 * j + g, :],
                                             q_own[:, g // 2, j * P:(j + 1) * P],
                                             k_bd[:, j, g // 2, 4 * (g % 2):4 * (g % 2) + 4, :],
                                             start=True, stop=True).then_inc(s_done, 1)
                    for j in range(2):
                        for g in range(4):
                            pe.wait_ge(normed, 4 * j + g + 1)
                            for h in range(4 * g, 4 * g + 4):
                                last = nc.tensor.transpose(
                                    ps[:, 4 * j + g, (h % 4) * P:(h % 4 + 1) * P],
                                    sc[:, j, h, :], env.ident)
                            last.then_inc(p_turned, 1)
                    pe.wait_ge(taken, 1)
                    for j in range(2):
                        pe.wait_ge(act_out, 2 * j + 2)
                        pe.wait_ge(dve_out, 2 * j + 2)
                        for pair in range(PAIRS):
                            rows = slice(32 * (pair % 4), 32 * (pair % 4) + 32)
                            last = nc.tensor.matmul(
                                ps[rows, 4 * j, (pair // 4) * D:(pair // 4 + 1) * D],
                                v_own[:, j, 2 * DH * pair:2 * DH * (pair + 1)],
                                p_T[:, j, 2 * pair:2 * pair + 2, :], start=True, stop=True)
                        last.then_inc(o_done, 1)

                @block.scalar
                def _(act):
                    nc.scalar.copy(v_own[:, :, :], v_nat[:, bass.ds(2 * i, 2), :]
                                   ).then_inc(taken, 1)
                    for j in range(2):
                        act.wait_ge(top_ready, j + 1)
                        for h in range(H):
                            nc.scalar.activation(sc[:, j, h, :], sc[:, j, h, :], ACT.Exp,
                                                 bias=top[:, j, h:h + 1],
                                                 accum_out=tot[:, j, h:h + 1]).then_inc(exped, 1)
                    for j in range(2):
                        for g in (0, 2):
                            act.wait_ge(p_turned, 4 * j + g + 1)
                            nc.scalar.copy(
                                p_T[:, j, 4 * g:4 * g + 4, :].rearrange("p h n -> p (h n)"),
                                ps[:, 4 * j + g, :]).then_inc(act_out, 1)

                @block.vector
                def _(dve):
                    steps = Steps(dve, own)
                    for j in range(2):
                        for g in range(4):
                            hs = slice(4 * g, 4 * g + 4)
                            dve.wait_ge(s_done, 4 * j + g + 1)
                            steps.done(nc.vector.scalar_tensor_tensor(
                                out=sc[:, j, hs, :],
                                in0=ps[:, 4 * j + g, :].rearrange("p (h n) -> p h n", h=4),
                                scalar=scale,
                                in1=bias[:, hs, :] if per_head else
                                bias.unsqueeze(1).broadcast_to([P, 4, P]),
                                op0=ALU.mult, op1=ALU.add))
                        steps.wait()
                        steps.done(nc.vector.tensor_reduce(top[:, j, :], sc[:, j, :, :], AX,
                                                           ALU.max))
                        steps.wait()
                        nc.vector.tensor_scalar(top[:, j, :], top[:, j, :], -1.0, None, ALU.mult
                                                ).then_inc(top_ready, 1)
                    for j in range(2):
                        for g in range(4):
                            hs = slice(4 * g, 4 * g + 4)
                            dve.wait_ge(exped, H * j + 4 * g + 4)
                            steps.done(nc.vector.reciprocal(tot[:, j, hs], tot[:, j, hs]))
                            steps.wait()
                            nc.vector.tensor_tensor(
                                sc[:, j, hs, :], sc[:, j, hs, :],
                                tot[:, j, hs].unsqueeze(2).broadcast_to([P, 4, P]), ALU.mult
                            ).then_inc(normed, 1)
                    for j in range(2):
                        for g in (1, 3):
                            dve.wait_ge(p_turned, 4 * j + g + 1)
                            nc.vector.tensor_copy(
                                p_T[:, j, 4 * g:4 * g + 4, :].rearrange("p h n -> p (h n)"),
                                ps[:, 4 * j + g, :]).then_inc(dve_out, 1)
                    for j in range(2):
                        dve.wait_ge(o_done, j + 1)
                        put = ps[:, 4 * j, :].rearrange("p (k h n) -> p k h n", k=KT, h=2)
                        steps.done(nc.vector.tensor_scalar(
                            halves[:, :, :], put[:, :, 0, :], env.parity[:, 0:1], None, ALU.mult))
                        steps.wait()
                        nc.vector.scalar_tensor_tensor(
                            out=att_T[:, :, bass.ds(i * (2 * P) + j * P, P)],
                            in0=put[:, :, 1, :], scalar=env.parity[:, 1:2], in1=halves[:, :, :],
                            op0=ALU.mult, op1=ALU.add).then_inc(o_out, 1)
                        dve.wait_ge(o_out, j + 1)


def l1_attn(nc, env, d):
    mem, sb = scoped(nc, "a1")
    with mem:
        w, wo = sb("w", [P, KT, 3 * D]), sb("wo", [P, KT, D])
        b_col, b_row = sb("b_col", [P, 2 * KT]), sb("b_row", [P, 2, D])
        att_T = sb("att_T", [P, KT, N])
        layernorm(nc, env, "a1_ln", env.x, env.h, env.h_T, loads=[
            (w[:, :, :], wview(d["L1_attn_w_qkv"])), (wo[:, :, :], wview(d["L1_attn_w_o"])),
            (b_col[:, :], d["L1_attn_b_qk"]),
            (b_row[:, 0, :], d["L1_attn_b_qkv"][2 * D:3 * D].partition_broadcast(P)),
            (b_row[:, 1, :], d["L1_attn_b_o"].partition_broadcast(P))])
        self_attention(nc, env, "a1", w, b_col, b_row[:, 0, :], att_T, D ** -0.5, env.cross, False,
                       sb)
        project_add(nc, env, "a1_o", att_T, wo, b_row[:, 1, :], env.x, also=env.h)


def l1_ffn(nc, env, d):
    E, HD, ITERS, G = 8, 64, 2, 4
    STEP = 4
    mem, sb = scoped(nc, "g1")
    with mem:
        rw1, hw1 = sb("rw1", [P, KT, HD]), sb("hw1", [P, KT, HD])
        rw2, hw2 = sb("rw2", [HD, 1, E]), sb("hw2", [HD, 1, 1])
        rb1, hb1, sb1 = (sb(n, [HD, 1]) for n in ("rb1", "hb1", "sb1"))
        rb2, fb2 = sb("rb2", [1, E]), sb("fb2", [P, D])
        hb2 = sb("hb2", [P, 1])
        ew1, eb1 = sb("ew1", [P, 2 * KT, E * HD]), sb("eb1", [P, G])
        ew2, eb2 = sb("ew2", [P, G, 3 * D]), sb("eb2", [P, 3 * D])
        sw1, sw2 = sb("sw1", [P, 2 * KT, HD]), sb("sw2", [P, 3 * D])
        fw1, fb1, fw2 = sb("fw1", [P, KT, 2 * D]), sb("fb1", [P, 2 * KT]), sb("fw2", [P, 2 * KT, D])
        mu, iw, sw = sb("mu", [P, D]), sb("iw", [P, D]), sb("sw", [P, 2])
        r_T, sh_T = sb("r_T", [HD, 1, N]), sb("sh_T", [P, 1, N])
        hid_T = sb("hid_T", [P, G, N])
        sel = sb("sel", [E, G, P], BF16)
        picked_T = env.rows[0:E, 0:T // 2, :].bitcast(BF16).rearrange(
            "e a b -> e (a b)").rearrange("e (k n) -> e k n", k=2)
        masks = sb("masks", [P, 2, G, N], BF16)
        probs, chosen = sb("probs", [P, T, E]), sb("chosen", [P, T, 2, E])
        chosen_T = sb("chosen_T", [P, 2, N])
        weights, coef, wsum = sb("weights", [P, T, 2]), sb("coef", [P, T, 3]), sb("wsum", [P, T])
        m8, i8, i_f = sb("m8", [P, T, 8]), sb("i8", [P, T, 8], U32), sb("i_f", [P, T, 2])
        top, total, halt = sb("top", [P, T]), sb("total", [P, T]), sb("halt", [P, T])
        cur, vel = sb("cur", [P, T, D]), sb("vel", [P, T, D])
        cv_T = sb("cv_T", [P, 2 * KT, N])
        hm = sb("hm", [P, 2, 2, G, P])
        sh_own, ch_own = sb("sh_own", [P, STEP * P]), sb("ch_own", [P, 2, STEP * P])
        th, sp_ = sb("th", [P, 2, 3, 2, D]), sb("sp", [P, 2, 3, D])
        lg = sb("lg", [P, 2, 3, D])
        v3, x3 = sb("v3", [P, 3, D]), sb("x3", [P, 3, D])
        away, acc = sb("away", [P, D]), sb("acc", [P, 2, D])
        ps = env.ps
        with signals(nc, "g1_pad", "own") as (own,):
            with nc.Block() as block:

                @block.vector
                def _(dve):
                    steps = Steps(dve, own)
                    for a in (chosen_T, eb2):
                        steps.done(nc.vector.memset(a[tuple([slice(None)] * len(a.shape))], 0.0))
                    steps.done(nc.vector.memset(sw2[HD:P, :], 0.0))
                    steps.done(nc.vector.memset(sh_T[HD:P, 0, :], 0.0))
                    steps.wait()
                    steps.done(nc.vector.memset(sh_T[HD:HD + 1, 0, :], 1.0))

        layernorm(nc, env, "g1_ln", env.x, env.h, env.h_T, loads=[
            (rw1[:, :, :], wview(d["L1_ffn_router_w1"])), (hw1[:, :, :], wview(d["L1_ffn_halt_w1"])),
            (rw2[:, 0, :], d["L1_ffn_router_w2"]), (hw2[:, 0, :], d["L1_ffn_halt_w2"]),
            (rb1[:, :], d["L1_ffn_router_b1"].unsqueeze(1)),
            (hb1[:, :], d["L1_ffn_halt_b1"].unsqueeze(1)),
            (sb1[:, :], d["L1_ffn_shared_b1"].unsqueeze(1)),
            (rb2[:, :], d["L1_ffn_router_b2"].unsqueeze(0)),
            (sw2[HD:HD + 1, :], d["L1_ffn_shared_b2"].unsqueeze(0)),
            (fb2[:, :], d["L1_ffn_refine_b2"].partition_broadcast(P)),
            (hb2[:, :], d["L1_ffn_halt_b2"].partition_broadcast(P)),
            (sw[:, 0:1], d["L1_ffn_shared_weight"].partition_broadcast(P)),
            (sw1[:, :, :], wview(d["L1_ffn_shared_w1"])), (sw2[0:HD, :], d["L1_ffn_shared_w2"]),
            (mu[:, :], d["L1_ffn_mu"].partition_broadcast(P)),
            (iw[:, :], d["L1_ffn_integration_weight"].partition_broadcast(P)),
            (sel[:, :, :], d["expert_sel"])])
        linear_T(nc, env, "g1_r", [(env.h_T, rw1, r_T, rb1, "gelu")])

        def mask_part(n):
            k, g, c = n // (2 * G), n // 2 % G, n % 2
            return masks[:, k, g, c * NH:(c + 1) * NH]

        later = [
            (ew1[:, :, :], wview(d["L1_ffn_expert_w1"])), (eb1[:, :], d["L1_ffn_expert_b1"]),
            (ew2[:, :, :], wview(d["L1_ffn_expert_w2"])), (eb2[0:E, :], d["L1_ffn_expert_b2"]),
            (fw1[:, :, :], wview(d["L1_ffn_refine_w1"])), (fb1[:, :], d["L1_ffn_refine_b1"]),
            (fw2[:, :, :], wview(d["L1_ffn_refine_w2"]))
        ]
        with signals(nc, "g1_route", "own logits shifted exped neg state picked turned turned_out "
                     "spread act_out dve_out loaded") as (
                own, logits, shifted, exped, neg, state, picked, turned, turned_out, spread,
                act_out, dve_out, loaded):
            with nc.Block() as block:

                @block.sync
                def _(sp):
                    load_all(sp, later, loaded)

                @block.gpsimd
                def _(pool):
                    nc.gpsimd.memset(vel[:, :, :], 0.0).then_inc(state, 1)
                    nc.gpsimd.memset(cv_T[:, KT:2 * KT, :], 0.0).then_inc(state, 1)
                    nc.gpsimd.tensor_copy(cur[:, :, :], env.h[:, :, :]).then_inc(state, 1)
                    nc.gpsimd.tensor_copy(cv_T[:, 0:KT, :], env.h_T[:, :, :]).then_inc(state, 1)

                @block.tensor
                def _(pe):
                    for t in range(T):
                        put = ps[:, 0, t * E:(t + 1) * E]
                        nc.tensor.matmul(put, r_T[:, 0, t * P:(t + 1) * P], rw2[:, 0, :],
                                         start=True, stop=False)
                        last = nc.tensor.matmul(put, env.ones[0:1, :], rb2[:, :],
                                                start=False, stop=True)
                    last.then_inc(logits, 1)
                    pe.wait_ge(picked, 1)
                    for k in range(2):
                        for t in range(T):
                            last = nc.tensor.transpose(
                                ps[0:E, 1 + 2 * k + t // 4, (t % 4) * P:(t % 4 + 1) * P],
                                chosen[:, t, k, :], env.ident)
                        last.then_inc(turned, 1)
                    pe.wait_ge(turned_out, 4)
                    n = 0
                    for k in range(2):
                        for g in range(G):
                            for c in range(2):
                                if n >= 8:
                                    pe.wait_ge((act_out, dve_out)[n % 2], (n - 8) // 2 + 1)
                                nc.tensor.matmul(ps[:, n % 8, :], sel[:, g, :],
                                                 picked_T[:, k, c * NH:(c + 1) * NH], start=True,
                                                 stop=True).then_inc(spread, 1)
                                n += 1

                @block.scalar
                def _(act):
                    act.wait_ge(shifted, 1)
                    nc.scalar.activation(probs[:, :, :], probs[:, :, :], ACT.Exp).then_inc(exped, 1)
                    nc.scalar.activation(sw[:, 1:2], sw[:, 0:1], ACT.Exp, scale=-1.0
                                         ).then_inc(neg, 1)
                    for n in range(0, 4 * G, 2):
                        act.wait_ge(spread, n + 1)
                        nc.scalar.copy(mask_part(n), ps[:, n % 8, :]).then_inc(act_out, 1)

                @block.vector
                def _(dve):
                    steps = Steps(dve, own)
                    dve.wait_ge(logits, 1)
                    steps.done(nc.vector.tensor_copy(
                        probs[:, :, :], ps[:, 0, 0:T * E].rearrange("p (t e) -> p t e", t=T)))
                    steps.wait()
                    row_softmax(nc, dve, probs[:, :, :], top[:, :], total[:, :], E, exped, shifted,
                                steps)
                    top2(nc, env, dve, probs, E, weights[:, :, :], chosen, m8, i8, i_f, steps)
                    steps.done(nc.vector.tensor_reduce(wsum[:, :], weights[:, :, :], AX, ALU.add))
                    steps.wait()
                    steps.done(nc.vector.reciprocal(wsum[:, :], wsum[:, :]))
                    dve.wait_ge(neg, 1)
                    steps.done(nc.vector.tensor_scalar(sw[:, 1:2], sw[:, 1:2], 1.0, None, ALU.add))
                    steps.wait()
                    steps.done(nc.vector.reciprocal(sw[:, 0:1], sw[:, 1:2]))
                    steps.wait()
                    steps.done(nc.vector.tensor_scalar(sw[:, 1:2], sw[:, 0:1], -1.0, 1.0, ALU.mult,
                                                       ALU.add))
                    steps.done(nc.vector.tensor_copy(
                        coef[:, :, 0:1], sw[:, 0:1].unsqueeze(1).broadcast_to([P, T, 1])))
                    steps.done(nc.vector.tensor_tensor(
                        weights[:, :, :], weights[:, :, :],
                        wsum[:, :].unsqueeze(2).broadcast_to([P, T, 2]), ALU.mult))
                    steps.wait()
                    nc.vector.tensor_scalar(coef[:, :, 1:3], weights[:, :, :], sw[:, 1:2], None,
                                            ALU.mult).then_inc(picked, 1)
                    for k in range(2):
                        dve.wait_ge(turned, k + 1)
                        for dst in (chosen_T[0:E], picked_T):
                            nc.vector.tensor_copy(
                                dst[:, k, :].rearrange("e (c n) -> e c n", c=2),
                                ps[0:E, 1 + 2 * k:3 + 2 * k, :]).then_inc(turned_out, 1)
                    for n in range(1, 4 * G, 2):
                        dve.wait_ge(spread, n + 1)
                        nc.vector.tensor_copy(mask_part(n), ps[:, n % 8, :]).then_inc(dve_out, 1)

        with nc.Fori(0, ITERS):
            linear_T(nc, env, "g1_hid", [(cv_T, ew1, hid_T, eb1, "gelu"),
                                         (cv_T, sw1, sh_T, sb1, "gelu"),
                                         (cv_T[:, 0:KT], hw1, r_T, hb1, "gelu")])
            with signals(nc, "g1_halt", "own product exped") as (own, product, exped):
                with nc.Block() as block:

                    @block.tensor
                    def _(pe):
                        for t in range(T):
                            last = nc.tensor.matmul(ps[:, 0, t:t + 1], r_T[:, 0, t * P:(t + 1) * P],
                                                    hw2[:, 0, :], start=True, stop=True)
                        last.then_inc(product, 1)

                    @block.scalar
                    def _(act):
                        act.wait_ge(own, 1)
                        nc.scalar.activation(halt[:, :], halt[:, :], ACT.Tanh, scale=0.5
                                             ).then_inc(exped, 1)

                    @block.vector
                    def _(dve):
                        steps = Steps(dve, own)
                        dve.wait_ge(product, 1)
                        steps.done(nc.vector.tensor_scalar(halt[:, :], ps[:, 0, 0:T], hb2[:, 0:1],
                                                           None, ALU.add))
                        dve.wait_ge(exped, 1)
                        steps.done(nc.vector.tensor_scalar(halt[:, :], halt[:, :], 0.5, 0.5,
                                                           ALU.mult, ALU.add))

            with nc.Fori(0, T // STEP) as i:
                with signals(nc, "g1_step", "own taken masked ctrl emptied logged used "
                             "new_state") as (
                        own, taken, masked, ctrl, emptied, logged, used, new_state):
                    group = bass.ds(i * (STEP * P), STEP * P)
                    with nc.Block() as block:

                        @block.gpsimd
                        def _(pool):
                            nc.gpsimd.tensor_copy(sh_own[:, :], sh_T[:, 0, group]
                                                  ).then_inc(taken, 1)
                            for j in range(STEP):
                                tile = bass.ds(i * (STEP * P) + j * P, P)
                                if j >= 2:
                                    pool.wait_ge(ctrl, 3 * (j - 1))
                                for k in range(2):
                                    nc.gpsimd.tensor_tensor(hm[:, j % 2, k, :, :],
                                                            hid_T[:, :, tile],
                                                            masks[:, k, :, tile],
                                                            ALU.mult).then_inc(masked, 1)
                                    if j == 0:
                                        nc.gpsimd.tensor_copy(ch_own[:, k, :],
                                                              chosen_T[:, k, group]
                                                              ).then_inc(taken, 1)

                        @block.tensor
                        def _(pe):
                            for j in range(STEP):
                                cols = slice(j * P, (j + 1) * P)
                                for s in range(3):
                                    n = 3 * j + s
                                    if n >= 4:
                                        pe.wait_ge(emptied, n - 3)
                                    if n < 3:
                                        pe.wait_ge(taken, n + 1)
                                    if s:
                                        pe.wait_ge(masked, 2 * j + s)
                                    for bank, part in ((2 * (n % 4), slice(0, 2 * D)),
                                                       (2 * (n % 4) + 1, slice(2 * D, 3 * D))):
                                        put = ps[:, bank, 0:part.stop - part.start]
                                        if s == 0:
                                            last = nc.tensor.matmul(
                                                put, sh_own[:, cols], sw2[:, part],
                                                start=True, stop=True)
                                            continue
                                        for g in range(G):
                                            nc.tensor.matmul(put, hm[:, j % 2, s - 1, g, :],
                                                             ew2[:, g, part],
                                                             start=(g == 0), stop=False)
                                        last = nc.tensor.matmul(put, ch_own[:, s - 1, cols],
                                                                eb2[:, part], start=False,
                                                                stop=True)
                                    last.then_inc(ctrl, 1)

                        @block.scalar
                        def _(act):
                            for j in range(STEP):
                                if j >= 2:
                                    act.wait_ge(used, j - 1)
                                r = j % 2
                                for s in range(3):
                                    n = 3 * j + s
                                    pair = ps[:, 2 * (n % 4):2 * (n % 4) + 2, 0:D]
                                    b_part = ps[:, 2 * (n % 4), D:2 * D]
                                    act.wait_ge(ctrl, n + 1)
                                    nc.scalar.activation(th[:, r, s, :, :], pair, ACT.Tanh,
                                                         scale=0.5)
                                    nc.scalar.activation(sp_[:, r, s, :], b_part, ACT.Relu)
                                    nc.scalar.activation(lg[:, r, s, :], b_part, ACT.Abs
                                                         ).then_inc(emptied, 1)
                                act.wait_ge(emptied, 3 * j + 3)
                                nc.scalar.activation(lg[:, r, :, :], lg[:, r, :, :], ACT.Exp,
                                                     scale=-1.0).then_inc(logged, 1)
                                act.wait_ge(logged, 2 * j + 1)
                                nc.scalar.activation(lg[:, r, :, :], lg[:, r, :, :], ACT.Ln,
                                                     bias=env.ones[:, 0:1]).then_inc(logged, 1)

                        @block.vector
                        def _(dve):
                            steps = Steps(dve, own)
                            for j in range(STEP):
                                r, tile = j % 2, bass.ds(i * STEP + j, 1)
                                cur_own, vel_own = cur[:, tile, :], vel[:, tile, :]
                                steps.done(nc.vector.tensor_tensor(
                                    away[:, :], cur_own.squeeze(1), mu[:, :], ALU.subtract))

                                def three(x):
                                    return x.broadcast_to([P, 3, D])

                                dve.wait_ge(emptied, 3 * j + 3)
                                steps.done(nc.vector.scalar_tensor_tensor(
                                    out=v3[:, :, :], in0=th[:, r, :, 0, :], scalar=1.0,
                                    in1=three(vel_own), op0=ALU.add, op1=ALU.mult))
                                dve.wait_ge(logged, 2 * j + 2)
                                steps.done(nc.vector.tensor_tensor(
                                    sp_[:, r, :, :], sp_[:, r, :, :], lg[:, r, :, :], ALU.add))
                                steps.wait()
                                steps.done(nc.vector.tensor_tensor(
                                    sp_[:, r, :, :], sp_[:, r, :, :],
                                    three(away[:, :].unsqueeze(1)), ALU.mult))
                                steps.wait()
                                steps.done(nc.vector.scalar_tensor_tensor(
                                    out=v3[:, :, :], in0=v3[:, :, :], scalar=0.5,
                                    in1=sp_[:, r, :, :], op0=ALU.mult, op1=ALU.subtract))
                                steps.wait()
                                nc.vector.scalar_tensor_tensor(
                                    out=x3[:, :, :], in0=th[:, r, :, 1, :], scalar=1.0,
                                    in1=v3[:, :, :], op0=ALU.add, op1=ALU.mult).then_inc(used, 1)
                                dve.wait_ge(used, j + 1)
                                steps.done(nc.vector.scalar_tensor_tensor(
                                    out=x3[:, :, :], in0=x3[:, :, :], scalar=0.05,
                                    in1=three(cur_own), op0=ALU.mult, op1=ALU.add))
                                steps.wait()
                                for s in range(3):
                                    c = coef[:, tile, s:s + 1].squeeze(1)
                                    for n, src in ((0, x3), (1, v3)):
                                        if s == 0:
                                            steps.done(nc.vector.tensor_scalar(
                                                acc[:, n, :], src[:, s, :], c, None, ALU.mult))
                                        else:
                                            steps.done(nc.vector.scalar_tensor_tensor(
                                                out=acc[:, n, :], in0=src[:, s, :], scalar=c,
                                                in1=acc[:, n, :], op0=ALU.mult, op1=ALU.add))
                                    steps.wait()
                                for n, state in ((0, cur_own), (1, vel_own)):
                                    steps.done(nc.vector.tensor_tensor(
                                        acc[:, n, :], acc[:, n, :], state.squeeze(1),
                                        ALU.subtract))
                                steps.wait()
                                for n, state in ((0, cur_own), (1, vel_own)):
                                    nc.vector.scalar_tensor_tensor(
                                        out=state.squeeze(1), in0=acc[:, n, :],
                                        scalar=halt[:, tile], in1=state.squeeze(1),
                                        op0=ALU.mult, op1=ALU.add).then_inc(new_state, 1)
                                dve.wait_ge(new_state, 2 * j + 2)
            turn_rows(nc, env, "g1_cur", cur, cv_T[:, 0:KT])
            turn_rows(nc, env, "g1_vel", vel, cv_T[:, KT:2 * KT])
        linear_T(nc, env, "g1_ref", [(cv_T[:, 0:KT], fw1, hid_T, fb1, "gelu")])
        project_add(nc, env, "g1_out", hid_T, fw2, fb2[:, :], env.x, also=env.h, scale=iw[:, :])



def l2_xattn(nc, env, d):
    mem, sb = scoped(nc, "x2")
    with mem:
        wq, wk, wv, wo = (sb(n, [P, KT, D]) for n in ("wq", "wk", "wv", "wo"))
        q_T, att_T, nb = sb("q_T", [P, KT, N]), sb("att_T", [P, KT, N]), sb("nb", [P, 2])
        kv = wview(d["L2_xattn_Wkv"])
        ctx_T = sb("ctx_T", [P, KT, SK])
        layernorm(nc, env, "x2_ln", env.x, env.h, env.h_T, loads=[
            (ctx_T[:, :, :], wview(d["ctx_T"][0])),
            (wq[:, :, :], wview(d["L2_xattn_Wq"])), (wk[:, :, :], kv[:, :, 0:D]),
            (wv[:, :, :], kv[:, :, D:2 * D]), (wo[:, :, :], wview(d["L2_xattn_Wo"])),
            (nb[:, 0:1], d["L2_xattn_nbias"].partition_broadcast(P))])
        with signals(nc, "x2_nb", "ready") as (ready,):
            with nc.Block() as block:

                @block.vector
                def _(dve):
                    nc.vector.tensor_scalar(nb[:, 1:2], nb[:, 0:1], -float(DH) ** 0.5, None,
                                            ALU.mult).then_inc(ready, 1)
        linear_T(nc, env, "x2_q", [(env.h_T, wq, q_T, None, None)])
        context_heads(nc, env, "x2", d["ctx_T"], ctx_T, q_T, att_T, wk, wv, softmax=False,
                      notmask=d["mask_T"], nb=nb)
        project_add(nc, env, "x2_o", att_T, wo, None, env.x)


def l2_attn(nc, env, d):
    F = 64
    mem, sb = scoped(nc, "a2")
    with mem:
        wq, wk, wv, wo = (sb(n, [P, KT, D]) for n in ("wq", "wk", "wv", "wo"))
        b_rows = sb("b_rows", [P, 4, D])
        proj = sb("proj", [P, KT, HPT, F])
        qk, v_aug = sb("qk", [P, 2, T, D]), sb("v_aug", [P, T, PAIRS, 2 * DH + 1])
        sq, ssq = sb("sq", [P, 2, T, D]), sb("ssq", [P, 2, T * H])
        q_T, k_T = sb("q_T", [P, KT, N]), sb("k_T", [P, KT, N])
        qf_T, kf = sb("qf_T", [P, PAIRS, N]), sb("kf", [P, T, H * F])
        kv = sb("kv", [P, 2, 2, PAIRS, 2 * DH + 2])
        nrm, att_T = sb("nrm", [P, T, H]), sb("att_T", [P, KT, N])
        ps = env.ps
        layernorm(nc, env, "a2_ln", env.x, env.h, env.h_T, loads=[
            (wq[:, :, :], wview(d["L2_attn_Wq"])), (wk[:, :, :], wview(d["L2_attn_Wk"])),
            (wv[:, :, :], wview(d["L2_attn_Wv"])), (wo[:, :, :], wview(d["L2_attn_Wo"])),
            (b_rows[:, 0, :], d["L2_attn_bq"].partition_broadcast(P)),
            (b_rows[:, 1, :], d["L2_attn_bk"].partition_broadcast(P)),
            (b_rows[:, 2, :], d["L2_attn_bv"].partition_broadcast(P)),
            (b_rows[:, 3, :], d["L2_attn_bo"].partition_broadcast(P)),
            (proj[:, :, :, :], d["proj_rows"])])
        linear_rows(nc, env, "a2_qkv", env.h_T, [
            (wq, b_rows[:, 0, :], lambda t: qk[:, 0, t, :]),
            (wk, b_rows[:, 1, :], lambda t: qk[:, 1, t, :]),
            (wv, b_rows[:, 2, :], lambda t: v_aug[:, t, :, 0:2 * DH])])
        with signals(nc, "a2_norm", "own sum std normed placed") as (
                own, summed, std_ready, normed, placed):
            with nc.Block() as block:

                @block.gpsimd
                def _(pool):
                    for half in range(KT):
                        nc.gpsimd.tensor_tensor(
                            proj[:, half, :, :], proj[:, half, :, :],
                            env.head_of.unsqueeze(2).broadcast_to([P, HPT, F]),
                            ALU.mult).then_inc(placed, 1)
                    nc.gpsimd.memset(v_aug[:, :, :, 2 * DH:2 * DH + 1], 1.0).then_inc(placed, 1)

                @block.scalar
                def _(act):
                    for n in range(2):
                        act.wait_ge(summed, n + 1)
                        nc.scalar.activation(ssq[:, n, :], ssq[:, n, :], ACT.Sqrt,
                                             bias=env.zero[:, 0:1]).then_inc(std_ready, 1)

                @block.vector
                def _(dve):
                    steps = Steps(dve, own)
                    for n in range(2):
                        steps.done(nc.vector.tensor_tensor(sq[:, n], qk[:, n], qk[:, n], ALU.mult))
                        steps.wait()
                        nc.vector.tensor_reduce(
                            ssq[:, n, :], sq[:, n].rearrange("p t (h d) -> p (t h) d", h=H), AX,
                            ALU.add).then_inc(summed, 1)
                    for n in range(2):
                        dve.wait_ge(std_ready, n + 1)
                        steps.done(nc.vector.tensor_scalar(ssq[:, n, :], ssq[:, n, :], 1e-8, None,
                                                           ALU.add))
                        steps.wait()
                        steps.done(nc.vector.reciprocal(ssq[:, n, :], ssq[:, n, :]))
                        steps.wait()
                        view = qk[:, n].rearrange("p t (h d) -> p (t h) d", h=H)
                        nc.vector.tensor_tensor(
                            view, view, ssq[:, n, :].unsqueeze(2).broadcast_to([P, T * H, DH]),
                            ALU.mult).then_inc(normed, 1)
        turn_rows(nc, env, "a2_qT", qk[:, 0], q_T)
        turn_rows(nc, env, "a2_kT", qk[:, 1], k_T)
        groups = [(0, j, c) for j in range(PAIRS) for c in range(2)] + \
                 [(1, t, c) for t in range(T) for c in range(2)]
        with signals(nc, "a2_feat", "product act_high dve_out act_out") as (
                product, act_high, dve_out, act_out):
            with nc.Block() as block:

                def target(kind, a, c):
                    return (qf_T[:, a, c * NH:(c + 1) * NH] if kind == 0
                            else kf[:, a, c * NH:(c + 1) * NH])

                @block.tensor
                def _(pe):
                    for g, (kind, a, c) in enumerate(groups):
                        if g >= 8:
                            pe.wait_ge((dve_out, act_high)[g % 2], (g - 8) // 2 + 1)
                        if kind == 0:
                            last = nc.tensor.matmul(
                                ps[:, g % 8, :],
                                proj[:, a // 4, 2 * (a % 4):2 * (a % 4) + 2, :],
                                q_T[:, a // 4, c * NH:(c + 1) * NH], start=True, stop=True)
                        else:
                            last = nc.tensor.matmul(
                                ps[:, g % 8, :], k_T[:, c, a * P:(a + 1) * P],
                                proj[:, c, :, :], start=True, stop=True)
                        last.then_inc(product, 1)

                @block.vector
                def _(dve):
                    for g in range(0, len(groups), 2):
                        dve.wait_ge(product, g + 1)
                        nc.vector.tensor_scalar(target(*groups[g]), ps[:, g % 8, :], 0.0, 0.1,
                                                ALU.max, ALU.add).then_inc(dve_out, 1)

                @block.scalar
                def _(act):
                    for g in range(1, len(groups), 2):
                        act.wait_ge(product, g + 1)
                        nc.scalar.activation(target(*groups[g]), ps[:, g % 8, :], ACT.Relu
                                             ).then_inc(act_high, 1)
                        act.wait_ge(act_high, g // 2 + 1)
                        nc.scalar.add(target(*groups[g]), target(*groups[g]), env.tenth
                                      ).then_inc(act_out, 1)

        W = 2 * DH + 1
        with signals(nc, "a2_lin", "own kv_done placed2 o_done o_taken") as (
                own, kv_done, kv_placed, o_done, o_taken):
            with nc.Block() as block:

                @block.tensor
                def _(pe):
                    def key_values(t):
                        if t >= 2:
                            pe.wait_ge(kv_placed, 4 * (t - 1))
                        for b in range(2):
                            rows = slice(b * S, (b + 1) * S)
                            for j in range(PAIRS):
                                last = nc.tensor.matmul(
                                    ps[:, 2 * (t % 2) + b, W * j:W * (j + 1)],
                                    kf[rows, t, 2 * F * j:2 * F * (j + 1)], v_aug[rows, t, j, :],
                                    start=True, stop=True)
                        last.then_inc(kv_done, 1)

                    def outputs(t):
                        pe.wait_ge(kv_placed, 4 * (t + 1))
                        if t >= 2:
                            pe.wait_ge(o_taken, t - 1)
                        for b in range(2):
                            for j in range(PAIRS):
                                last = nc.tensor.matmul(
                                    ps[b * S:(b + 1) * S, 4 + t % 2, (W + 1) * j:(W + 1) * (j + 1)],
                                    qf_T[:, j, t * P + b * S:t * P + (b + 1) * S],
                                    kv[:, t % 2, b, j, :], start=True, stop=True)
                        last.then_inc(o_done, 1)

                    for t in range(T):
                        key_values(t)
                        if t:
                            outputs(t - 1)
                    outputs(T - 1)

                @block.vector
                def _(dve):
                    steps = Steps(dve, own)

                    def place(t):
                        dve.wait_ge(kv_done, t + 1)
                        if t >= 2:
                            dve.wait_ge(o_done, t - 1)
                        for b in range(2):
                            put = ps[:, 2 * (t % 2) + b, 0:W * PAIRS].rearrange(
                                "p (j w) -> p j w", w=W)
                            own_head = env.own_head.unsqueeze(1).broadcast_to([P, PAIRS, 2 * DH])
                            nc.vector.tensor_tensor(kv[:, t % 2, b, :, 0:2 * DH],
                                                    put[:, :, 0:2 * DH], own_head,
                                                    ALU.mult).then_inc(kv_placed, 1)
                            nc.vector.tensor_tensor(
                                kv[:, t % 2, b, :, 2 * DH:2 * DH + 2],
                                put[:, :, 2 * DH:W].broadcast_to([P, PAIRS, 2]),
                                env.which_head.unsqueeze(1).broadcast_to([P, PAIRS, 2]),
                                ALU.mult).then_inc(kv_placed, 1)

                    def divide(t):
                        dve.wait_ge(o_done, t + 1)
                        put = ps[:, 4 + t % 2, 0:(W + 1) * PAIRS].rearrange("p (j w) -> p j w",
                                                                            w=W + 1)
                        steps.done(nc.vector.tensor_scalar(
                            nrm[:, t, :].rearrange("p (j h) -> p j h", h=2),
                            put[:, :, 2 * DH:2 * DH + 2], 1e-6, None, ALU.max))
                        steps.wait()
                        steps.done(nc.vector.reciprocal(nrm[:, t, :], nrm[:, t, :]))
                        steps.wait()
                        nc.vector.tensor_tensor(
                            env.rows[:, t, :].rearrange("p (j h d) -> p j h d", j=PAIRS, h=2),
                            put[:, :, 0:2 * DH].rearrange("p j (h d) -> p j h d", h=2),
                            nrm[:, t, :].rearrange("p (j h) -> p j h", h=2).unsqueeze(3)
                            .broadcast_to([P, PAIRS, 2, DH]), ALU.mult).then_inc(o_taken, 1)

                    for t in range(T):
                        place(t)
                        if t:
                            divide(t - 1)
                    divide(T - 1)
        turn_rows(nc, env, "a2_turn", env.rows, att_T)
        project_add(nc, env, "a2_o", att_T, wo, b_rows[:, 3, :], env.x)


def l2_ffn(nc, env, d):
    E, TOP, ROUTE_SCALE = 16, 8, 2.826
    mem, sb = scoped(nc, "f2")
    with mem:
        gate, bias = sb("gate", [P, KT, E]), sb("bias", [P, E])
        wg, wu, wd = (sb(n, [P, KT, D]) for n in ("wg", "wu", "wd"))
        scores, sel = sb("scores", [P, T, E]), sb("sel", [P, T, E])
        m8, rest, picked = sb("m8", [P, T, TOP]), sb("rest", [P, T, E]), sb("picked", [P, T, E])
        total, comb = sb("total", [P, T]), sb("comb", [P, T, E + 1])
        hid_T = sb("hid_T", [P, KT, N])
        ps = env.ps

        def weights_of(e):
            return [(wg[:, :, :], wview(d["L2_w_gate"][e])), (wu[:, :, :], wview(d["L2_w_up"][e]))]

        layernorm(nc, env, "f2_ln", env.x, env.h, env.h_T, loads=[
            (gate[:, :, :], wview(d["L2_ffn_gate_w"])),
            (bias[:, :], d["L2_ffn_expert_bias"].partition_broadcast(P)), *weights_of(0)])
        with signals(nc, "f2_route", "own logits exped") as (
                own, logits, exped):
            with nc.Block() as block:

                @block.tensor
                def _(pe):
                    for t in range(T):
                        for k in range(KT):
                            last = nc.tensor.matmul(ps[:, 0, t * E:(t + 1) * E],
                                                    env.h_T[:, k, t * P:(t + 1) * P],
                                                    gate[:, k, :], start=(k == 0),
                                                    stop=(k == KT - 1))
                    last.then_inc(logits, 1)

                @block.scalar
                def _(act):
                    act.wait_ge(logits, 1)
                    nc.scalar.activation(scores[:, :, :].rearrange("p t e -> p (t e)"),
                                         ps[:, 0, 0:T * E], ACT.Sigmoid).then_inc(exped, 1)

                @block.vector
                def _(dve):
                    steps = Steps(dve, own)
                    dve.wait_ge(exped, 1)
                    steps.done(nc.vector.tensor_tensor(
                        sel[:, :, :], scores[:, :, :],
                        bias[:, :].unsqueeze(1).broadcast_to([P, T, E]), ALU.add))
                    steps.wait()
                    for t in range(T):
                        steps.done(nc.vector.max(m8[:, t, :], sel[:, t, :]))
                    steps.wait()
                    for t in range(T):
                        steps.done(nc.vector.match_replace(rest[:, t, :], m8[:, t, :],
                                                           sel[:, t, :], -3e38))
                    steps.wait()
                    steps.done(nc.vector.tensor_tensor(picked[:, :, :], rest[:, :, :],
                                                       sel[:, :, :], ALU.not_equal))
                    steps.wait()
                    steps.done(nc.vector.tensor_tensor(picked[:, :, :], picked[:, :, :],
                                                       scores[:, :, :], ALU.mult))
                    steps.wait()
                    steps.done(nc.vector.tensor_reduce(total[:, :], picked[:, :, :], AX, ALU.add))
                    steps.wait()
                    steps.done(nc.vector.reciprocal(total[:, :], total[:, :]))
                    steps.wait()
                    steps.done(nc.vector.tensor_tensor(
                        picked[:, :, :], picked[:, :, :],
                        total[:, :].unsqueeze(2).broadcast_to([P, T, E]), ALU.mult))
                    steps.wait()
                    steps.done(nc.vector.tensor_scalar(comb[:, :, 0:E], picked[:, :, :],
                                                       ROUTE_SCALE, None, ALU.mult))
                    steps.done(nc.vector.memset(comb[:, :, E:E + 1], 1.0))

        with nc.Fori(0, E + 1) as e:
            expert(nc, env, "f2_expert", [wg, wu], None, hid_T, wd,
                   lambda t: comb[:, t, bass.ds(e, 1)],
                   now=[(wd[:, :, :], wview(d["L2_w_down"][e]))],
                   after=weights_of((e + 1) % (E + 1)))


def l3_xattn(nc, env, d):
    SCALE = float(D / H) ** 0.5
    mem, sb = scoped(nc, "x3")
    with mem:
        wq, wk, wv = (sb(n, [P, KT, D]) for n in ("wq", "wk", "wv"))
        bq, bk, bv = sb("bq", [P, KT]), sb("bk", [P, KT]), sb("bv", [P, D])
        q_T, q2_T, att_T = (sb(n, [P, KT, N]) for n in ("q_T", "q2_T", "att_T"))
        ctx_Ts = [sb(f"ctx_T{r}", [P, 2, KT, SK]) for r in range(2)]
        ctx_ns = [sb(f"ctx_n{r}", [P, 2, CT, D]) for r in range(2)]
        q_own, q0_own = sb("q_own", [P, KT, P]), sb("q0_own", [P, KT, P])
        sc, p_T = sb("sc", [P, SK]), sb("p_T", [P, CT, P])
        small, u_n = sb("small", [P, 4]), sb("u_n", [P, D])
        ps = env.ps

        def row_loads(r, row):
            return [load for b in range(2) for load in (
                (ctx_ns[r][:, b, 0:CT - 1, :], wview(d["ctx"][row + b, 0:(CT - 1) * P, :])),
                (ctx_ns[r][0:LAST, b, CT - 1, :], d["ctx"][row + b, (CT - 1) * P:SK, :]))]

        layernorm(nc, env, "x3_ln", env.x, env.h, env.h_T, loads=[
            (wq[:, :, :], wview(d["L3_xattn_Wq"])), (wk[:, :, :], wview(d["L3_xattn_Wk"])),
            (wv[:, :, :], wview(d["L3_xattn_Wv"])), (bq[:, :], d["L3_xattn_bq"]),
            (bk[:, :], d["L3_xattn_bk"]), (bv[:, :], d["L3_xattn_bv"].partition_broadcast(P))]
            + [(ctx_Ts[0][:, b, :, :], wview(d["ctx_T"][b])) for b in range(2)])
        linear_T(nc, env, "x3_q", [(env.h_T, wq, q_T, bq, None)], loads=row_loads(0, 0))
        linear_T(nc, env, "x3_q2", [(q_T, wk, q2_T, None, None)])
        def attend(r, pair):
            ctx_T, ctx_n = ctx_Ts[r], ctx_ns[r]
            with signals(nc, f"x3_at{r}", "next_in own q_in s_done shift_ready exped "
                         "turned act_out dve_out u_done u_ready u_turned u_out") as (
                    next_in, own, q_in, s_done, shift_ready, exped, turned,
                    act_out, dve_out, u_done, u_ready, u_turned, u_out):
                with nc.Block() as block:

                    @block.sync
                    def _(sp):
                        row = (2 * pair + 2) % B
                        load_all(sp, [(ctx_Ts[1 - r][:, b, :, :], wview(d["ctx_T"][row + b]))
                                      for b in range(2)] + row_loads(1 - r, row), next_in)

                    @block.tensor
                    def _(pe):
                        pe.wait_ge(q_in, 2)
                        for k in range(KT):
                            nc.tensor.matmul(ps[:, 4, 0:1], q0_own[:, k, :], bk[:, k:k + 1],
                                             start=(k == 0), stop=(k == KT - 1))
                        for c, (at, n) in enumerate(BANKFULS):
                            for k in range(KT):
                                for b in range(2):
                                    last = nc.tensor.matmul(
                                        ps[b * S:(b + 1) * S, c, 0:n],
                                        q_own[:, k, b * S:(b + 1) * S],
                                        ctx_T[:, b, k, at:at + n], start=(k == 0),
                                        stop=(k == KT - 1))
                        last.then_inc(s_done, 1)
                        pe.wait_ge(exped, 1)
                        for t in range(CT):
                            n = keys_of(t)
                            last = nc.tensor.transpose(ps[0:n, 4 + t // 4, (t % 4) * P:
                                                          (t % 4 + 1) * P],
                                                       sc[:, t * P:t * P + n], env.ident)
                            if t % 4 == 3 or t == CT - 1:
                                last.then_inc(turned, 1)
                        pe.wait_ge(act_out, 2)
                        pe.wait_ge(dve_out, 2)
                        for t in range(CT):
                            for b in range(2):
                                n = keys_of(t)
                                last = nc.tensor.matmul(
                                    ps[b * S:(b + 1) * S, 0, 0:D],
                                    p_T[0:n, t, b * S:(b + 1) * S], ctx_n[0:n, b, t, :],
                                    start=(t == 0), stop=(t == CT - 1))
                        last.then_inc(u_done, 1)
                        pe.wait_ge(u_ready, 1)
                        for k in range(KT):
                            last = nc.tensor.transpose(ps[:, 1, k * P:(k + 1) * P],
                                                       u_n[:, k * P:(k + 1) * P], env.ident)
                        last.then_inc(u_turned, 1)

                    @block.scalar
                    def _(act):
                        cols = bass.ds(pair * P, P)
                        nc.scalar.copy(q_own[:, :, :], q2_T[:, :, cols]).then_inc(q_in, 1)
                        nc.scalar.copy(q0_own[:, :, :], q_T[:, :, cols]).then_inc(q_in, 1)
                        act.wait_ge(shift_ready, 1)
                        nc.scalar.activation(sc[:, :], ps[:, 0:4, :].rearrange(
                            "p c n -> p (c n)")[:, 0:SK], ACT.Exp, scale=SCALE,
                            bias=small[:, 2:3], accum_out=small[:, 3:4]).then_inc(exped, 1)
                        for g in (0, 2):
                            act.wait_ge(turned, g + 1)
                            nc.scalar.copy(p_T[:, 4 * g:4 * g + 4, :].rearrange(
                                "p t n -> p (t n)"), ps[:, 4 + g, :]).then_inc(act_out, 1)
                        act.wait_ge(u_turned, 1)
                        nc.scalar.copy(att_T[:, :, cols], ps[:, 1, 0:2 * P].rearrange(
                            "p (k n) -> p k n", k=KT)).then_inc(u_out, 1)

                    @block.vector
                    def _(dve):
                        steps = Steps(dve, own)
                        dve.wait_ge(s_done, 1)
                        steps.done(nc.vector.tensor_reduce(
                            small[:, 0:1], ps[:, 0:4, :].rearrange("p c n -> p (c n)")[:, 0:SK],
                            AX, ALU.max))
                        steps.done(nc.vector.tensor_copy(small[:, 1:2], ps[:, 4, 0:1]))
                        steps.wait()
                        steps.done(nc.vector.tensor_tensor(small[:, 0:1], small[:, 0:1],
                                                           small[:, 1:2], ALU.add))
                        steps.wait()
                        steps.done(nc.vector.tensor_tensor(small[:, 2:3], small[:, 1:2],
                                                           small[:, 0:1], ALU.subtract))
                        steps.wait()
                        nc.vector.tensor_scalar(small[:, 2:3], small[:, 2:3], SCALE, None,
                                                ALU.mult).then_inc(shift_ready, 1)
                        dve.wait_ge(exped, 1)
                        steps.done(nc.vector.reciprocal(small[:, 3:4], small[:, 3:4]))
                        dve.wait_ge(turned, 2)
                        nc.vector.tensor_copy(p_T[:, 4:8, :].rearrange("p t n -> p (t n)"),
                                              ps[:, 5, :]).then_inc(dve_out, 1)
                        dve.wait_ge(turned, 4)
                        nc.vector.tensor_copy(p_T[0:LAST, 12, :], ps[0:LAST, 7, 0:P]
                                              ).then_inc(dve_out, 1)
                        dve.wait_ge(u_done, 1)
                        steps.wait()
                        nc.vector.tensor_scalar(u_n[:, :], ps[:, 0, 0:D], small[:, 3:4], None,
                                                ALU.mult).then_inc(u_ready, 1)
        with nc.Fori(0, T // 2) as i:
            for r in range(2):
                attend(r, 2 * i + r)
        project_add(nc, env, "x3_v", att_T, wv, bv[:, :], env.x)


def l3_attn(nc, env, d):
    NB = 32
    mem, sb = scoped(nc, "a3")
    with mem:
        w, wo = sb("w", [P, KT, 3 * D]), sb("wo", [P, KT, D])
        b_col, b_row = sb("b_col", [P, 2 * KT]), sb("b_row", [P, 2, D])
        att_T, bias = sb("att_T", [P, KT, N]), sb("bias", [P, H, P])
        onehot, rel_bd = sb("onehot", [P, S // 4, P]), sb("rel_bd", [P, 4, H])
        causal = sb("causal", [P, P])
        ps = env.ps
        layernorm(nc, env, "a3_ln", env.x, env.h, env.h_T, loads=[
            (w[:, :, :], wview(d["L3_attn_W_attn"])), (wo[:, :, :], wview(d["L3_attn_W_proj"])),
            (b_col[:, :], d["L3_attn_b_qk"]),
            (b_row[:, 0, :], d["L3_attn_b_attn"][2 * D:3 * D].partition_broadcast(P)),
            (b_row[:, 1, :], d["L3_attn_b_proj"].partition_broadcast(P)),
            (onehot[:, :, :], d["buckets"]), (causal[:, :], d["causal"])])
        with signals(nc, "a3_bias", "zeroed table product placed own") as (
                zeroed, table, product, placed, own):
            with nc.Block() as block:

                @block.gpsimd
                def _(pool):
                    nc.gpsimd.memset(rel_bd[:, :, :], 0.0).then_inc(zeroed, 1)

                @block.sync
                def _(sp):
                    sp.wait_ge(zeroed, 1)
                    for r in range(4):
                        sp.dma_start(rel_bd[r * NB:(r + 1) * NB, r, :],
                                     d["L3_attn_rel_emb"]).then_inc(table, 16)

                @block.tensor
                def _(pe):
                    pe.wait_ge(table, 4 * 16)
                    for g in range(S // 4):
                        last = nc.tensor.matmul(ps[:, g // 8, (g % 8) * 4 * H:(g % 8 + 1) * 4 * H],
                                                onehot[:, g, :], rel_bd[:, :, :], start=True,
                                                stop=True)
                    last.then_inc(product, 1)

                @block.vector
                def _(dve):
                    steps = Steps(dve, own)
                    dve.wait_ge(product, 1)
                    for half in range(2):
                        for b in range(2):
                            at = b * S + 32 * half
                            steps.done(nc.vector.tensor_copy(
                                bias[:, :, at:at + 32],
                                ps[:, half, :].rearrange("p (k h) -> p h k", h=H)))
                    steps.wait()
                    nc.vector.tensor_tensor(bias[:, :, :], bias[:, :, :],
                                            causal[:, :].unsqueeze(1).broadcast_to([P, H, P]),
                                            ALU.add).then_inc(placed, 1)
        self_attention(nc, env, "a3", w, b_col, b_row[:, 0, :], att_T, DH ** -0.5, bias, True, sb)
        project_add(nc, env, "a3_o", att_T, wo, b_row[:, 1, :], env.x)


def l3_ffn(nc, env, d):
    MAGIC = 1.5 * 2.0 ** 23
    mem, sb = scoped(nc, "q3")
    with mem:
        w8, w16 = sb("w8", [P, KT, D // 4], I32), sb("w16", [P, KT, D], BF16)
        wscale, bias = sb("wscale", [P, D]), sb("bias", [P, D])
        amax, scale = sb("amax", [P, T]), sb("scale", [P, T])
        xq, xq16 = sb("xq", [P, T, D]), sb("xq16", [P, T, D], BF16)
        x_T, ident16 = sb("x_T", [P, KT, N], BF16), sb("ident16", [P, P], BF16)
        out = sb("out", [P, T, D])
        ps = env.ps
        layernorm(nc, env, "q3_ln", env.x, env.h, None, loads=[
            (w8[:, :, :], wview(d["L3_ffn_weight_q"])),
            (wscale[:, :], d["L3_ffn_weight_scale"].partition_broadcast(P)),
            (bias[:, :], d["L3_ffn_bias"].partition_broadcast(P))])
        with signals(nc, "q3", "own cast quantised turned x_out product out_ready") as (
                own, cast, quantised, turned, x_out, product, out_ready):
            with nc.Block() as block:

                @block.scalar
                def _(act):
                    nc.scalar.copy(w16[:, :, :], w8[:, :, :].bitcast(I8)).then_inc(cast, 1)
                    nc.scalar.copy(ident16[:, :], env.ident).then_inc(cast, 1)
                    for t in range(T):
                        act.wait_ge(turned, t + 1)
                        nc.scalar.copy(x_T[:, :, t * P:(t + 1) * P],
                                       ps[:, t % 2, :].bitcast(BF16)[:, 0:2 * P].rearrange(
                                           "p (k n) -> p k n", k=KT)).then_inc(x_out, 1)

                @block.tensor
                def _(pe):
                    pe.wait_ge(cast, 2)
                    for t in range(T):
                        pe.wait_ge(quantised, t + 1)
                        if t >= 2:
                            pe.wait_ge(x_out, t - 1)
                        for f in range(KT):
                            last = nc.tensor.transpose(
                                ps[:, t % 2, :].bitcast(BF16)[:, f * P:(f + 1) * P],
                                xq16[:, t, f * P:(f + 1) * P], ident16[:, :])
                        last.then_inc(turned, 1)
                    for t in range(T):
                        pe.wait_ge(x_out, t + 1)
                        if t >= 4:
                            pe.wait_ge(out_ready, t - 3)
                        for k in range(KT):
                            last = nc.tensor.matmul(ps[:, 4 + t % 4, 0:D],
                                                    x_T[:, k, t * P:(t + 1) * P], w16[:, k, :],
                                                    start=(k == 0), stop=(k == KT - 1))
                        last.then_inc(product, 1)

                @block.vector
                def _(dve):
                    steps = Steps(dve, own)
                    steps.done(nc.vector.tensor_reduce(amax[:, :], env.h[:, :, :], AX, ALU.max,
                                                       apply_absolute_value=True))
                    steps.wait()
                    steps.done(nc.vector.tensor_scalar(scale[:, :], amax[:, :], 1e-6, 1.0 / 127.0,
                                                       ALU.max, ALU.mult))
                    steps.wait()
                    steps.done(nc.vector.reciprocal(amax[:, :], scale[:, :]))
                    steps.wait()
                    for t in range(T):
                        steps.done(nc.vector.tensor_scalar(xq[:, t, :], env.h[:, t, :],
                                                           amax[:, t:t + 1], MAGIC, ALU.mult,
                                                           ALU.add))
                    steps.wait()
                    for t in range(T):
                        steps.done(nc.vector.tensor_scalar(xq[:, t, :], xq[:, t, :], MAGIC, None,
                                                           ALU.subtract))
                    steps.wait()
                    for t in range(T):
                        nc.vector.tensor_scalar(xq16[:, t, :], xq[:, t, :], 127.0, -128.0, ALU.min,
                                                ALU.max).then_inc(quantised, 1)
                    for t in range(T):
                        dve.wait_ge(product, t + 1)
                        nc.vector.scalar_tensor_tensor(
                            out=out[:, t, :], in0=ps[:, 4 + t % 4, 0:D], scalar=scale[:, t:t + 1],
                            in1=wscale[:, :], op0=ALU.mult, op1=ALU.mult).then_inc(out_ready, 1)
                    dve.wait_ge(out_ready, T)
                    steps.done(nc.vector.tensor_tensor(
                        out[:, :, :], out[:, :, :],
                        bias[:, :].unsqueeze(1).broadcast_to([P, T, D]), ALU.add))
                    steps.wait()
                    steps.done(nc.vector.tensor_tensor(env.x[:, :, :], env.x[:, :, :],
                                                       out[:, :, :], ALU.add))



SUBLAYERS = {"L0_xattn": l0_xattn, "L0_attn": l0_attn, "L0_ffn": l0_ffn,
             "L1_xattn": l1_xattn, "L1_attn": l1_attn,
             "L1_ffn": l1_ffn,
             "L2_xattn": l2_xattn, "L2_attn": l2_attn, "L2_ffn": l2_ffn,
             "L3_xattn": l3_xattn, "L3_attn": l3_attn, "L3_ffn": l3_ffn}

def constants():
    p = np.arange(P)[:, None]
    c = np.arange(P)[None, :]
    ident = (p == c)
    parts = {
        "ident": ident,
        "ones": np.ones((P, P)),
        "same_head": (p // DH == c // DH),
        "own_head": (p // S == c[:, 0:2 * DH] // DH),
        "head_of": (p // DH == c[:, 0:HPT]),
        "excluded": np.where(p <= c[:, 0:S], -3e38, 0.0),
        "parity": (p // DH % 2 == c[:, 0:2]),
        "zero": np.zeros((P, 1)),
        "iota8": np.tile(np.arange(8), (P, 1)),
        "valid_last": np.repeat(p < LAST, P, 1),
        "cross": np.where(p // S == c // S, 0.0, -1e30),
        "which_head": (p // S == c[:, 0:2]),
        "tenth": np.full((P, 1), 0.1),
        "eps5": np.full((P, 1), 1e-5),
        "eps6": np.full((P, 1), 1e-6),
    }
    at, where, arrays = 0, {}, []
    for name, a in parts.items():
        arrays.append(np.asarray(a, np.float32))
        where[name] = (at, at + a.shape[1])
        at += a.shape[1]
    return np.ascontiguousarray(np.concatenate(arrays, 1)), where


def build(nc, d, out, where, names):
    with ExitStack() as mem:
        def sb(name, shape, dt=F32):
            return mem.enter_context(nc.sbuf_tensor(name, shape, dt))

        env = Env()
        env.x = sb("x", [P, T, D])
        env.h = sb("h", [P, T, D])
        env.h_T = sb("h_T", [P, KT, N])
        env.rows = sb("rows", [P, T, D])
        env.bn, env.mv = sb("bn", [P, T, 6]), sb("mv", [P, T, 2])
        env.std, env.rstd = sb("std", [P, T]), sb("rstd", [P, T])
        consts = sb("consts", [P, d["consts"].shape[1]])
        env.ident = consts[:, where["ident"][0]:where["ident"][1]]
        env.ones = consts[:, where["ones"][0]:where["ones"][1]]
        env.same_head = consts[:, where["same_head"][0]:where["same_head"][1]]
        env.own_head = consts[:, where["own_head"][0]:where["own_head"][1]]
        env.head_of = consts[:, where["head_of"][0]:where["head_of"][1]]
        env.excluded = consts[:, where["excluded"][0]:where["excluded"][1]]
        env.parity = consts[:, where["parity"][0]:where["parity"][1]]
        env.iota8 = consts[:, where["iota8"][0]:where["iota8"][1]]
        env.valid_last = consts[:, where["valid_last"][0]:where["valid_last"][1]]
        env.cross = consts[:, where["cross"][0]:where["cross"][1]]
        env.which_head = consts[:, where["which_head"][0]:where["which_head"][1]]
        env.tenth = consts[:, where["tenth"][0]:where["tenth"][1]]
        env.zero = consts[:, where["zero"][0]:where["zero"][1]]
        env.eps5 = consts[:, where["eps5"][0]:where["eps5"][1]]
        env.eps6 = consts[:, where["eps6"][0]:where["eps6"][1]]
        env.ps = mem.enter_context(nc.psum_tensor("ps", [P, 8, NH], F32))

        with signals(nc, "start", "x_in consts_in") as (x_in, consts_in):
            with nc.Block() as block:

                @block.sync
                def _(sp):
                    sp.dma_start(env.x[:, :, :], d["x"].rearrange("(t b) s n -> (b s) t n", b=2)
                                 ).then_inc(x_in, 16)
                    sp.dma_start(consts[:, :], d["consts"]).then_inc(consts_in, 16)
                    sp.wait_ge(x_in, 16)
                    sp.wait_ge(consts_in, 16)

        for name in names:
            SUBLAYERS[name](nc, env, d)

        with signals(nc, "end", "stored") as (stored,):
            with nc.Block() as block:

                @block.sync
                def _(sp):
                    sp.dma_start(out.rearrange("(t b) s n -> (b s) t n", b=2), env.x[:, :, :]
                                 ).then_inc(stored, 16)
                    sp.wait_ge(stored, 16)


def arrange(inputs):
    a = {}
    for name, v in inputs.items():
        a[name] = np.ascontiguousarray(v)
    a["ctx"] = a.pop("ctx_1024")
    a["ctx_T"] = np.ascontiguousarray(np.transpose(a["ctx"], (0, 2, 1)))
    a["mask_T"] = np.ascontiguousarray(np.transpose(a.pop("mask_BxSxS2_bk0"), (0, 2, 1))
                                       ).view(np.int32)
    def columns(name):
        v = a[name]
        a[name] = np.ascontiguousarray(np.swapaxes(v.reshape(*v.shape[:-1], -1, P), -1, -2))

    for name in ("bq", "b1", "ln1_s", "ln1_b", "ln2_s", "ln2_b"):
        columns("L0_attn_" + name)
    a["L0_ffn_gate_w"] = np.ascontiguousarray(a["L0_ffn_gate_w"].T)
    columns("L0_ffn_b1")
    a["L0_ffn_b1"] = np.ascontiguousarray(np.swapaxes(a["L0_ffn_b1"], 0, 1))
    for name in ("L1_xattn_gru_wih", "L1_xattn_gru_whh",
                 "L1_attn_w_qkv", "L1_attn_w_o", "L2_xattn_Wq", "L2_xattn_Wkv", "L2_xattn_Wo",
                 "L2_ffn_gate_w", "L3_xattn_Wq", "L3_xattn_Wv", "L3_attn_W_attn",
                 "L3_attn_W_proj", "L3_ffn_weight_q"):
        a[name] = np.ascontiguousarray(a[name].T)
    for name in ("slot_norm_w", "input_norm_w", "gru_bih", "gru_bhh"):
        columns("L1_xattn_" + name)
    a["L1_attn_b_qk"] = a["L1_attn_b_qkv"][0:2 * D]
    columns("L1_attn_b_qk")
    a["L1_ffn_expert_w1"] = np.ascontiguousarray(
        np.transpose(a["L1_ffn_expert_w1"], (1, 0, 2))).reshape(2 * D, -1)
    a["L1_ffn_expert_w2"] = a["L1_ffn_expert_w2"].reshape(-1, 3 * D)
    a["L1_ffn_expert_b1"] = a["L1_ffn_expert_b1"].reshape(-1)
    a["L1_ffn_shared_weight"] = a["L1_ffn_shared_weight"].reshape(1)
    columns("L1_ffn_expert_b1")
    columns("L1_ffn_refine_b1")
    proj = np.transpose(a["L2_attn_projection"], (0, 2, 1)).reshape(KT, P, 1, 64)
    a["proj_rows"] = np.ascontiguousarray(np.transpose(
        np.broadcast_to(proj, (KT, P, HPT, 64)), (1, 0, 2, 3)))
    for new, one, shared in (("L2_w_gate", "L2_ffn_w_gate", "L2_ffn_shared_gate_w"),
                             ("L2_w_up", "L2_ffn_w_up", "L2_ffn_shared_up_w"),
                             ("L2_w_down", "L2_ffn_w_down", "L2_ffn_shared_down_w")):
        both = np.concatenate([a.pop(one), a.pop(shared)[None]], 0)
        a[new] = np.ascontiguousarray(np.transpose(both, (0, 2, 1)))
    a["L3_ffn_weight_q"] = a["L3_ffn_weight_q"].view(np.int32)
    columns("L3_xattn_bq")
    columns("L3_xattn_bk")
    a["L3_attn_b_qk"] = a["L3_attn_b_attn"][0:2 * D]
    columns("L3_attn_b_qk")
    rp = -np.minimum(np.arange(S)[None, :] - np.arange(S)[:, None], 0)
    large = 16 + (np.log(rp.astype(np.float32) / np.float32(16) + np.float32(1e-10))
                  / np.float32(np.log(8.0)) * np.float32(16)).astype(np.int32)
    bucket = np.where(rp < 16, rp, np.minimum(large, 31))
    hot = (np.arange(32)[:, None, None] == bucket.T[None, :, :])
    hot = np.tile(hot, (1, 1, 2)).reshape(32, S // 4, 4, P)
    a["buckets"] = np.ascontiguousarray(np.transpose(hot, (2, 0, 1, 3)).reshape(P, S // 4, P)
                                        ).astype(np.float32)
    at = np.arange(P)
    seen = (at[:, None] // S == at[None, :] // S) & (at[None, :] % S <= at[:, None] % S)
    a["causal"] = np.where(seen, 0.0, -1e30).astype(np.float32)
    a["expert_sel"] = np.ascontiguousarray(
        np.arange(8)[:, None, None] == 2 * np.arange(4)[None, :, None]
        + np.arange(P)[None, None, :] // 64).astype(mybir.dt.np(BF16))
    half = D // 2
    freq = np.exp(np.arange(half, dtype=np.float32) * np.float32(-np.log(10000.0) / (half - 1)))
    pos = (np.arange(S, dtype=np.float32) + 1.0)[:, None] * freq[None, :]
    a["pos"] = np.tile(np.concatenate([np.sin(pos), np.cos(pos)], -1).astype(np.float32), (2, 1))
    return a


def kernel(**inputs):
    import concourse.bacc as bacc
    from concourse.bass_utils import run_bass_kernel_spmd

    arrays = arrange(inputs)
    arrays["consts"], where = constants()
    nc = bacc.Bacc("TRN2", target_bir_lowering=False, num_devices=1)
    d = {n: nc.dram_tensor(f"in_{n}", a.shape, mybir.dt.from_np(a.dtype),
                           kind="ExternalInput").ap() for n, a in arrays.items()}
    out = nc.dram_tensor("out", (B, S, D), F32, kind="ExternalOutput").ap()
    build(nc, d, out, where, list(SUBLAYERS))
    r = run_bass_kernel_spmd(nc, [{f"in_{n}": a for n, a in arrays.items()}], core_ids=[0])
    return r.results[0]["out"]
```
